# Optimizing a Trainium2 kernel written in Bass

```python
import numpy as np
import jax
import jax.numpy as jnp

def _softmax(x, axis=-1):
    return jax.nn.softmax(x, axis=axis)

def _gelu(x):
    return jax.nn.gelu(x, approximate=True)

def _silu(x):
    return jax.nn.silu(x)

def _sigmoid(x):
    return jax.nn.sigmoid(x)

def _layernorm(x, axis=-1, eps=1e-05):
    m = jnp.mean(x, axis=axis, keepdims=True)
    v = jnp.var(x, axis=axis, keepdims=True)
    return (x - m) / jnp.sqrt(v + eps)

def _scatter_add(tgt, idx, src, axis=0):
    return tgt.at[idx].add(src)

def _segment_sum(src, seg, n):
    return jax.ops.segment_sum(src, seg, n)
kernel_name = 'mk_decoder_postln_d4_seqx_r8_e36999'

def setup_inputs(seed: int=0):
    np.random.seed(seed)
    _w = jnp.asarray

    def _rec_inputs():
        import jax
        import jax.numpy as jnp
        _rk = jax.random.key(seed)
        x = -0.0002928 + 1 * jax.random.normal(jax.random.fold_in(_rk, 1), (2, 512, 128), jnp.float32)
        _lenS = 512 - jax.random.randint(jax.random.fold_in(_rk, 7), (2,), 0, max(1, 512 // 4) + 1, jnp.int32)
        _lenS2 = 77 - jax.random.randint(jax.random.fold_in(_rk, 8), (2,), 0, max(1, 77 // 4) + 1, jnp.int32)
        _ctx_512P = jax.random.normal(jax.random.fold_in(_rk, 11), (2, 16, 64), jnp.float32)
        _ctx_512c = jax.random.dirichlet(jax.random.fold_in(_rk, 511), 0.3 * jnp.ones((16,), jnp.float32), (2, 77))
        _ctx_512t = jnp.einsum('bsk,bkd->bsd', _ctx_512c, _ctx_512P)
        _ctx_512t = _ctx_512t * jax.lax.rsqrt(jnp.mean(jnp.square(_ctx_512t)) + 1e-12) * 0.953939
        ctx_512 = -0.000514642 + 1.00011 * (_ctx_512t + 0.3 * jax.random.normal(jax.random.fold_in(_rk, 611), (2, 77, 64), jnp.float32))
        return (x, ctx_512)
    x, ctx_512 = _rec_inputs()

    def _L0_attn_setup():
        import jax, jax.numpy as jnp
        import numpy as np
        import math
        H = 16

        def quant4(x):
            xs = jax.lax.stop_gradient(x)
            ma = jnp.maximum(jnp.max(jnp.abs(xs), axis=-1, keepdims=True), 1e-06)
            q = jnp.clip(jnp.round(xs / ma * 7.0), -8.0, 7.0)
            return x + jax.lax.stop_gradient(q * ma / 7.0 - xs)

        def ternary_weight(w):
            thresh = jax.lax.stop_gradient(0.05 * jnp.mean(jnp.abs(w)))
            sign = jnp.where(jnp.abs(w) < thresh, 0.0, jnp.sign(w))
            alpha = jnp.mean(jnp.abs(w), axis=1, keepdims=True)
            return sign * alpha + (w - jax.lax.stop_gradient(w))

        def rotary(t, n):
            half = t.shape[-1] // 2
            inv = 1.0 / 10000.0 ** (jnp.arange(half, dtype=t.dtype) / half)
            ang = jnp.arange(n, dtype=t.dtype)[:, None] * inv
            c, s = (jnp.cos(ang), jnp.sin(ang))
            t1, t2 = (t[..., ::2], t[..., 1::2])
            return jnp.concatenate([t1 * c - t2 * s, t1 * s + t2 * c], axis=-1)
        key = jax.random.key(seed)
        k1, k2, k3, k4 = jax.random.split(key, 4)
        B, N, d, r = (2, 256, 128, 32)
        dk = d // H
        x = jax.random.normal(k1, (B, N, d), dtype=jnp.float32)
        Wqkv_w = jax.random.normal(k2, (d, d), dtype=jnp.float32) / math.sqrt(d)
        Wqkv_b = jnp.zeros((d,), dtype=jnp.float32)
        U = jax.random.normal(k3, (dk, r), dtype=jnp.float32) / math.sqrt(dk)
        Wo_w = jax.random.normal(k4, (d, d), dtype=jnp.float32) / math.sqrt(d)
        return {'x': x, 'Wqkv_w': Wqkv_w, 'Wqkv_b': Wqkv_b, 'U': U, 'Wo_w': Wo_w}
    _L0_attn_all = _L0_attn_setup()
    _L0_attn_in = {k: v for k, v in _L0_attn_all.items() if k in ('Wqkv_w', 'Wqkv_b', 'U', 'Wo_w')}
    del _L0_attn_all

    def _L0_xattn_setup():
        import jax, jax.numpy as jnp
        import numpy as np
        DIM = 128
        LATENT_DIM = 64
        NUM_HEADS = 16
        HEAD_DIM = DIM // NUM_HEADS
        SCALE = HEAD_DIM ** (-0.5)
        key = jax.random.key(seed)
        k1, k2, k3, k4, k5 = jax.random.split(key, 5)
        B, xN, zN = (2, 256, 256)
        x = jax.random.normal(k1, (B, xN, DIM), dtype=jnp.float32)
        z = jax.random.normal(k2, (B, zN, LATENT_DIM), dtype=jnp.float32)
        Wq = jax.random.normal(k3, (DIM, DIM), dtype=jnp.float32) * DIM ** (-0.5)
        Wkv = jax.random.normal(k4, (2 * DIM, LATENT_DIM), dtype=jnp.float32) * LATENT_DIM ** (-0.5)
        Wo = jax.random.normal(k5, (DIM, DIM), dtype=jnp.float32) * DIM ** (-0.5)
        return {'x': x, 'z': z, 'Wq': Wq, 'Wkv': Wkv, 'Wo': Wo}
    _L0_xattn_all = _L0_xattn_setup()
    _L0_xattn_in = {k: v for k, v in _L0_xattn_all.items() if k in ('Wq', 'Wkv', 'Wo')}
    del _L0_xattn_all

    def _L0_ffn_setup():
        import jax, jax.numpy as jnp
        import numpy as np
        TOP_K = 2
        ROUTE_SCALE = 1.0
        EPS = 1e-20
        key = jax.random.key(seed)
        ks = jax.random.split(key, 8)
        dim, hid, E, X = (128, 352, 8, 1)
        std = 0.02
        x = jax.random.normal(ks[0], (2, 256, dim), dtype=jnp.float32)
        w1 = jax.random.normal(ks[1], (E, hid, dim), dtype=jnp.float32) * std
        w2 = jax.random.normal(ks[2], (E, dim, hid), dtype=jnp.float32) * std
        w3 = jax.random.normal(ks[3], (E, hid, dim), dtype=jnp.float32) * std
        new_w1 = jax.random.normal(ks[4], (X, hid, dim), dtype=jnp.float32) * std
        new_w2 = jnp.zeros((X, dim, hid), dtype=jnp.float32)
        new_w3 = jax.random.normal(ks[5], (X, hid, dim), dtype=jnp.float32) * std
        gate_weight = jax.random.normal(ks[6], (E, dim), dtype=jnp.float32) * std
        new_gate_weight = jax.random.normal(ks[7], (X, dim), dtype=jnp.float32) * std
        gate_bias = jnp.zeros((X,), dtype=jnp.float32)
        return dict(x=x, w1=w1, w2=w2, w3=w3, new_w1=new_w1, new_w2=new_w2, new_w3=new_w3, gate_weight=gate_weight, new_gate_weight=new_gate_weight, gate_bias=gate_bias)
    _L0_ffn_all = _L0_ffn_setup()
    _L0_ffn_in = {k: v for k, v in _L0_ffn_all.items() if k in ('w1', 'w2', 'w3', 'new_w1', 'new_w2', 'new_w3', 'gate_weight', 'new_gate_weight', 'gate_bias')}
    del _L0_ffn_all

    def _L1_attn_setup():
        import jax, jax.numpy as jnp
        import numpy as np
        Bsz, L, D, N = (2, 256, 128, 16)
        LN_EPS = 1e-05
        key = jax.random.key(seed)
        ks = jax.random.split(key, 5)
        A_log = -jnp.broadcast_to(jnp.log(jnp.arange(1, N + 1, dtype=jnp.float32))[None, :], (D, N))
        return {'x': jax.random.normal(ks[0], (Bsz, L, D), jnp.float32), 'W_dt': jax.random.normal(ks[1], (D, D), jnp.float32) * 0.02, 'b_dt': jnp.zeros((D,), jnp.float32), 'W_B': jax.random.normal(ks[2], (N, D), jnp.float32) * 0.02, 'W_C': jax.random.normal(ks[3], (N, D), jnp.float32) * 0.02, 'D_param': jnp.ones((D,), jnp.float32), 'A_log': A_log, 'gamma': jnp.ones((D,), jnp.float32), 'beta': jnp.zeros((D,), jnp.float32)}
    _L1_attn_all = _L1_attn_setup()
    _L1_attn_in = {k: v for k, v in _L1_attn_all.items() if k in ('W_dt', 'b_dt', 'W_B', 'W_C', 'D_param', 'A_log', 'gamma', 'beta')}
    del _L1_attn_all

    def _L1_xattn_setup():
        import jax, jax.numpy as jnp
        import numpy as np
        HEADS = 16
        D_MODEL = 128
        IMG_MODEL = 64
        D_K = D_MODEL // HEADS
        key = jax.random.key(seed)
        ks = jax.random.split(key, 12)
        B, LQ, LKV = (8, 256, 128)
        s_dm = 1.0 / np.sqrt(D_MODEL)
        s_im = 1.0 / np.sqrt(IMG_MODEL)
        return {'q': jax.random.normal(ks[0], (B, LQ, D_MODEL), jnp.float32), 'k': jax.random.normal(ks[1], (B, LKV, IMG_MODEL), jnp.float32), 'v': jax.random.normal(ks[2], (B, LKV, IMG_MODEL), jnp.float32), 'Wq': jax.random.normal(ks[3], (D_MODEL, D_MODEL), jnp.float32) * s_dm, 'bq': jnp.zeros((D_MODEL,), jnp.float32), 'Wk': jax.random.normal(ks[4], (IMG_MODEL, D_MODEL), jnp.float32) * s_im, 'bk': jnp.zeros((D_MODEL,), jnp.float32), 'Wv': jax.random.normal(ks[5], (IMG_MODEL, D_MODEL), jnp.float32) * s_im, 'bv': jnp.zeros((D_MODEL,), jnp.float32), 'Wo': jax.random.normal(ks[6], (D_MODEL, D_MODEL), jnp.float32) * s_dm, 'bo': jnp.zeros((D_MODEL,), jnp.float32)}
    _L1_xattn_all = _L1_xattn_setup()
    _L1_xattn_in = {k: v for k, v in _L1_xattn_all.items() if k in ('Wq', 'bq', 'Wk', 'bk', 'Wv', 'bv', 'Wo', 'bo')}
    del _L1_xattn_all

    def _L1_ffn_setup():
        import jax, jax.numpy as jnp
        import numpy as np
        D = 128
        HQ = 16
        HKV = 4
        G = HQ // HKV
        K = 64
        V = 64
        E = 8
        TOPK = 2
        HID = 256
        CAP_FRAC = 0.125
        EPS = 1e-06

        def _rmsnorm(x, g):
            return x * jax.lax.rsqrt(jnp.mean(x * x, axis=-1, keepdims=True) + EPS) * g

        def _rotary_tables(t, dim):
            thetas = 10000.0 ** (-np.arange(0, dim, 2, dtype=np.float32) / dim)
            ticks = np.outer(np.arange(t, dtype=np.float32), thetas)
            ticks = np.tile(ticks, (1, 2))[None, :, None, :]
            return (jnp.asarray(np.cos(ticks)), jnp.asarray(np.sin(ticks)))

        def _neg_half(x):
            x1, x2 = jnp.split(x, 2, axis=-1)
            return jnp.concatenate([-x2, x1], axis=-1)

        def _attention(x, wq, wk, wv, wo):
            b, t, _ = x.shape
            q = (x @ wq).reshape(b, t, HQ, K)
            k = (x @ wk).reshape(b, t, HKV, K)
            v = (x @ wv).reshape(b, t, HKV, V)
            cos, sin = _rotary_tables(t, K)
            q = q * cos + _neg_half(q) * sin
            k = k * cos + _neg_half(k) * sin
            qg = q.reshape(b, t, G, HKV, K)
            scores = jnp.einsum('btghk,bThk->bghtT', qg, k)
            mask = jnp.tril(jnp.ones((t, t), bool))
            scores = jnp.where(mask, scores, -jnp.inf) / np.float32(np.sqrt(K))
            p = jax.nn.softmax(scores, axis=-1)
            out = jnp.einsum('bghtT,bThv->btghv', p, v).reshape(b, t, HQ * V)
            return out @ wo

        def _moe(x, router_w, router_b, w1, w2, w3):
            b, t, d = x.shape
            n = b * t
            xf = x.reshape(n, d)
            logits = xf @ router_w + router_b
            vals, idx = jax.lax.top_k(logits, TOPK)
            scores = jax.nn.softmax(vals, axis=-1)
            cap = int(np.floor(n * CAP_FRAC))
            oh = jax.nn.one_hot(idx, E, dtype=jnp.float32)
            pos = jnp.cumsum(jnp.cumsum(oh, axis=0), axis=1).astype(jnp.int32)
            emask = oh * (pos < cap)
            tmask = jnp.sum(emask, axis=-1)
            assign = jnp.einsum('tke,e->tk', emask, jnp.arange(E, dtype=jnp.float32)).astype(jnp.int32)
            m = jnp.max(assign, axis=-1)

            def ff(w1e, w2e, w3e):
                h = jax.nn.gelu(xf @ w2e * (xf @ w1e), approximate=False)
                return h @ w3e
            y_all = jax.vmap(ff)(w1, w2, w3)
            y = y_all[m, jnp.arange(n)]
            slot = jnp.where(tmask[..., None] > 0, y[:, None, :], xf[:, None, :])
            out = jnp.einsum('tkD,tk->tD', slot, scores)
            return out.reshape(b, t, d)
        key = jax.random.key(seed)
        ks = jax.random.split(key, 10)
        w = lambda k, shape: jax.random.normal(k, shape, jnp.float32) * 0.02
        return {'x': jax.random.normal(ks[0], (4, 64, D), jnp.float32), 'g1': jnp.ones((D,), jnp.float32), 'g2': jnp.ones((D,), jnp.float32), 'wq': w(ks[1], (D, HQ * K)), 'wk': w(ks[2], (D, HKV * K)), 'wv': w(ks[3], (D, HKV * V)), 'wo': w(ks[4], (HQ * V, D)), 'router_w': w(ks[5], (D, E)), 'router_b': jnp.zeros((E,), jnp.float32), 'w1': w(ks[6], (E, D, HID)), 'w2': w(ks[7], (E, D, HID)), 'w3': w(ks[8], (E, HID, D))}
    _L1_ffn_all = _L1_ffn_setup()
    _L1_ffn_in = {k: v for k, v in _L1_ffn_all.items() if k in ('g1', 'g2', 'wq', 'wk', 'wv', 'wo', 'router_w', 'router_b', 'w1', 'w2', 'w3')}
    del _L1_ffn_all

    def _L2_attn_setup():
        import jax, jax.numpy as jnp
        import numpy as np
        import math
        D_MODEL, N_HEADS, RANK = (128, 16, 16)
        D_K = D_MODEL // N_HEADS
        BATCH, N = (2, 256)
        key = jax.random.key(seed)
        ks = jax.random.split(key, 8)
        s = 1.0 / math.sqrt(D_MODEL)
        sr = 1.0 / math.sqrt(D_K)
        return {'x': jax.random.normal(ks[0], (BATCH, N, D_MODEL), jnp.float32), 'WQ': jax.random.normal(ks[1], (D_MODEL, D_MODEL), jnp.float32) * s, 'bQ': jnp.zeros((D_MODEL,), jnp.float32), 'WK': jax.random.normal(ks[2], (D_MODEL, D_MODEL), jnp.float32) * s, 'bK': jnp.zeros((D_MODEL,), jnp.float32), 'WV': jax.random.normal(ks[3], (D_MODEL, D_MODEL), jnp.float32) * s, 'bV': jnp.zeros((D_MODEL,), jnp.float32), 'WO': jax.random.normal(ks[4], (D_MODEL, D_MODEL), jnp.float32) * s, 'bO': jnp.zeros((D_MODEL,), jnp.float32), 'WQr': jax.random.normal(ks[5], (D_K, RANK), jnp.float32) * sr, 'WKr': jax.random.normal(ks[6], (D_K, RANK), jnp.float32) * sr}
    _L2_attn_all = _L2_attn_setup()
    _L2_attn_in = {k: v for k, v in _L2_attn_all.items() if k in ('WQ', 'bQ', 'WK', 'bK', 'WV', 'bV', 'WO', 'bO', 'WQr', 'WKr')}
    del _L2_attn_all

    def _L2_xattn_setup():
        import jax, jax.numpy as jnp
        import numpy as np
        NUM_HEADS = 16
        HEAD_DIM = 64
        Q_DIM = 128
        KV_DIM = 64
        INNER = NUM_HEADS * HEAD_DIM
        key = jax.random.key(seed)
        ks = jax.random.split(key, 7)
        B, N, M = (32, 128, 256)
        q = jax.random.normal(ks[0], (B, N, Q_DIM), dtype=jnp.float32)
        kv = jax.random.normal(ks[1], (B, M, KV_DIM), dtype=jnp.float32)
        Wq = jax.random.normal(ks[2], (Q_DIM, INNER), dtype=jnp.float32) / np.sqrt(Q_DIM)
        Wk = jax.random.normal(ks[3], (KV_DIM, INNER), dtype=jnp.float32) / np.sqrt(KV_DIM)
        Wv = jax.random.normal(ks[4], (KV_DIM, INNER), dtype=jnp.float32) / np.sqrt(KV_DIM)
        Wo = jax.random.normal(ks[5], (INNER, Q_DIM), dtype=jnp.float32) / np.sqrt(INNER)
        bo = jax.random.normal(ks[6], (Q_DIM,), dtype=jnp.float32) * 0.01
        return {'q': q, 'kv': kv, 'Wq': Wq, 'Wk': Wk, 'Wv': Wv, 'Wo': Wo, 'bo': bo}
    _L2_xattn_all = _L2_xattn_setup()
    _L2_xattn_in = {k: v for k, v in _L2_xattn_all.items() if k in ('Wq', 'Wk', 'Wv', 'Wo', 'bo')}
    del _L2_xattn_all

    def _L2_ffn_setup():
        import jax, jax.numpy as jnp
        import numpy as np
        from jax import lax
        B, S, H = (2, 128, 128)
        I = 64
        E = 32
        TOP_K = 4
        N_GROUP = 4
        TOPK_GROUP = 2
        SCALE = 2.5
        N_SHARED = 2
        SH_I = I * N_SHARED

        def _route(tokens, router_weight, router_bias):
            logits = tokens.astype(jnp.float32) @ router_weight.astype(jnp.float32).T
            scores = jax.nn.sigmoid(logits)
            sfc = scores + router_bias[None, :]
            T = tokens.shape[0]
            grp = sfc.reshape(T, N_GROUP, E // N_GROUP)
            group_scores = lax.top_k(grp, 2)[0].sum(-1)
            _, gidx = lax.top_k(group_scores, TOPK_GROUP)
            gmask = jax.nn.one_hot(gidx, N_GROUP, dtype=sfc.dtype).sum(1)
            smask = jnp.broadcast_to(gmask[:, :, None], (T, N_GROUP, E // N_GROUP)).reshape(T, E)
            tmp = jnp.where(smask > 0, sfc, 0.0)
            _, topk_idx = lax.top_k(tmp, TOP_K)
            topk_w = jnp.take_along_axis(scores, topk_idx, axis=1)
            topk_w = topk_w / (topk_w.sum(-1, keepdims=True) + 1e-20)
            topk_w = topk_w * SCALE
            return (topk_idx, topk_w)
        key = jax.random.key(seed)
        ks = jax.random.split(key, 10)
        std = 0.02
        return {'hidden_states': jax.random.normal(ks[0], (B, S, H), jnp.float32), 'router_weight': jax.random.normal(ks[1], (E, H), jnp.float32) * std, 'router_bias': jnp.zeros((E,), jnp.float32), 'gate_w': jax.random.normal(ks[2], (E, I, H), jnp.float32) * std, 'up_w': jax.random.normal(ks[3], (E, I, H), jnp.float32) * std, 'down_w': jax.random.normal(ks[4], (E, H, I), jnp.float32) * std, 'shared_gate_w': jax.random.normal(ks[5], (SH_I, H), jnp.float32) * std, 'shared_up_w': jax.random.normal(ks[6], (SH_I, H), jnp.float32) * std, 'shared_down_w': jax.random.normal(ks[7], (H, SH_I), jnp.float32) * std}
    _L2_ffn_all = _L2_ffn_setup()
    _L2_ffn_in = {k: v for k, v in _L2_ffn_all.items() if k in ('router_weight', 'router_bias', 'gate_w', 'up_w', 'down_w', 'shared_gate_w', 'shared_up_w', 'shared_down_w')}
    del _L2_ffn_all

    def _L3_attn_setup():
        import jax, jax.numpy as jnp
        import numpy as np
        B, N, D = (4, 512, 128)
        H, F = (16, 32)
        HD = D // H
        EPS_ATTN = 1e-08
        EPS_LN = 1e-05

        def _layernorm(x, gamma, beta):
            mu = jnp.mean(x, axis=-1, keepdims=True)
            var = jnp.var(x, axis=-1, keepdims=True)
            return (x - mu) * jax.lax.rsqrt(var + EPS_LN) * gamma + beta
        key = jax.random.key(seed)
        ks = jax.random.split(key, 10)

        def kaiming(k, shape):
            fan_in = shape[1]
            return jax.random.normal(k, shape, jnp.float32) * jnp.sqrt(2.0 / fan_in)
        pm = jax.random.normal(ks[0], (H, HD, F), jnp.float32)
        return {'x': jax.random.normal(ks[1], (B, N, D), jnp.float32), 'proj': pm, 'w_qkv': kaiming(ks[2], (3 * D, D)), 'w_out': kaiming(ks[3], (D, D)), 'b_out': jnp.zeros((D,), jnp.float32), 'gamma': jnp.ones((D,), jnp.float32), 'beta': jnp.zeros((D,), jnp.float32), 'w1': kaiming(ks[4], (4 * D, D)), 'b1': jnp.zeros((4 * D,), jnp.float32), 'w2': kaiming(ks[5], (D, 4 * D)), 'b2': jnp.zeros((D,), jnp.float32)}
    _L3_attn_all = _L3_attn_setup()
    _L3_attn_in = {k: v for k, v in _L3_attn_all.items() if k in ('proj', 'w_qkv', 'w_out', 'b_out', 'gamma', 'beta', 'w1', 'b1', 'w2', 'b2')}
    del _L3_attn_all

    def _L3_xattn_setup():
        import jax, jax.numpy as jnp
        import numpy as np
        H, D, C1, C2, S, M, B, W = (16, 32, 128, 64, 256, 64, 2, 4)

        def _ln(x, g, b):
            m = jnp.mean(x, -1, keepdims=True)
            v = jnp.var(x, -1, keepdims=True)
            return (x - m) * jax.lax.rsqrt(v + 1e-05) * g + b

        def _mha(x, y, wq, wk, wv, li1_w, li1_b, lnx_g, lnx_b, lny_g, lny_b, ln3_g, ln3_b, li2_w, li2_b, li3_w, li3_b, causal):
            xn = _ln(x, lnx_g, lnx_b)
            yn = _ln(y, lny_g, lny_b)
            q = jnp.einsum('bsc,hcd->bhsd', xn, wq)
            k = jnp.einsum('btc,hcd->bhtd', yn, wk)
            v = jnp.einsum('btc,hcd->bhtd', yn, wv)
            a = jax.nn.softmax(jnp.einsum('bhsd,bhtd->bhst', q, k) * D ** (-0.5), axis=-1)
            if causal:
                s, t = (a.shape[-2], a.shape[-1])
                mask = (jnp.arange(t)[None, :] > jnp.arange(s)[:, None]).astype(a.dtype)
                a = a * mask
            o = jnp.einsum('bhst,bhtd->bhsd', a, v)
            o = o.transpose(0, 2, 1, 3).reshape(x.shape[0], x.shape[1], H * D)
            x_out = x + o @ li1_w + li1_b
            h = jax.nn.gelu(_ln(x_out, ln3_g, ln3_b) @ li2_w + li2_b, approximate=False)
            return x_out + h @ li3_w + li3_b
        key = jax.random.key(seed)
        ks = iter(jax.random.split(key, 64))

        def w(shape, scale=0.02):
            return jax.random.normal(next(ks), shape, jnp.float32) * scale
        inp = {'xx': jax.random.normal(next(ks), (B, S, C1), jnp.float32), 'ee': jax.random.normal(next(ks), (B, M, C2), jnp.float32), 'ln1_g': jnp.ones(C1, jnp.float32), 'ln1_b': jnp.zeros(C1, jnp.float32), 'ln2_g': jnp.ones(C1, jnp.float32), 'ln2_b': jnp.zeros(C1, jnp.float32)}
        for pfx, cy in (('a1', C1), ('a2', C2)):
            inp[pfx + '_wq'] = w((H, C1, D))
            inp[pfx + '_wk'] = w((H, cy, D))
            inp[pfx + '_wv'] = w((H, cy, D))
            inp[pfx + '_li1_w'] = w((H * D, C1))
            inp[pfx + '_li1_b'] = jnp.zeros(C1, jnp.float32)
            inp[pfx + '_lnx_g'] = jnp.ones(C1, jnp.float32)
            inp[pfx + '_lnx_b'] = jnp.zeros(C1, jnp.float32)
            inp[pfx + '_lny_g'] = jnp.ones(cy, jnp.float32)
            inp[pfx + '_lny_b'] = jnp.zeros(cy, jnp.float32)
            inp[pfx + '_ln3_g'] = jnp.ones(C1, jnp.float32)
            inp[pfx + '_ln3_b'] = jnp.zeros(C1, jnp.float32)
            inp[pfx + '_li2_w'] = w((C1, C1 * W))
            inp[pfx + '_li2_b'] = jnp.zeros(C1 * W, jnp.float32)
            inp[pfx + '_li3_w'] = w((C1 * W, C1))
            inp[pfx + '_li3_b'] = jnp.zeros(C1, jnp.float32)
        inp['training'] = 0
        return inp
    _L3_xattn_all = _L3_xattn_setup()
    _L3_xattn_in = {k: v for k, v in _L3_xattn_all.items() if k in ('ln1_g', 'ln1_b', 'ln2_g', 'ln2_b', 'a1_wq', 'a1_wk', 'a1_wv', 'a1_li1_w', 'a1_li1_b', 'a1_lnx_g', 'a1_lnx_b', 'a1_lny_g', 'a1_lny_b', 'a1_ln3_g', 'a1_ln3_b', 'a1_li2_w', 'a1_li2_b', 'a1_li3_w', 'a1_li3_b', 'a2_wq', 'a2_wk', 'a2_wv', 'a2_li1_w', 'a2_li1_b', 'a2_lnx_g', 'a2_lnx_b', 'a2_lny_g', 'a2_lny_b', 'a2_ln3_g', 'a2_ln3_b', 'a2_li2_w', 'a2_li2_b', 'a2_li3_w', 'a2_li3_b')}
    del _L3_xattn_all

    def _L3_ffn_setup():
        import jax, jax.numpy as jnp
        import numpy as np
        DIM = 128

        def _reference_tuple_inner(x, W_r, W_k, W_v, mu_r, mu_k):
            B, T, C = x.shape
            x_prev = jnp.concatenate([jnp.zeros((B, 1, C), x.dtype), x[:, :-1, :]], axis=1)
            xr = mu_r * x + (1.0 - mu_r) * x_prev
            xk = mu_k * x + (1.0 - mu_k) * x_prev
            r = jax.nn.sigmoid(jnp.einsum('btc,dc->btd', xr, W_r))
            k = jnp.einsum('btc,dc->btd', xk, W_k)
            k_act = jnp.square(jax.nn.relu(k))
            out = r * jnp.einsum('btc,dc->btd', k_act, W_v)
            new_state = x[:, -1, :]
            return (out, new_state)
        key = jax.random.key(seed)
        ks = jax.random.split(key, 6)
        B, T, C = (8, 256, DIM)
        x = jax.random.normal(ks[0], (B, T, C), dtype=jnp.float32)
        s = 1.0 / np.sqrt(C)
        W_r = jax.random.uniform(ks[1], (C, C), jnp.float32, -s, s)
        W_k = jax.random.uniform(ks[2], (C, C), jnp.float32, -s, s)
        W_v = jax.random.uniform(ks[3], (C, C), jnp.float32, -s, s)
        mu_r = jax.random.uniform(ks[4], (C,), jnp.float32)
        mu_k = jax.random.uniform(ks[5], (C,), jnp.float32)
        return {'x': x, 'W_r': W_r, 'W_k': W_k, 'W_v': W_v, 'mu_r': mu_r, 'mu_k': mu_k}
    _L3_ffn_all = _L3_ffn_setup()
    _L3_ffn_in = {k: v for k, v in _L3_ffn_all.items() if k in ('W_r', 'W_k', 'W_v', 'mu_r', 'mu_k')}
    del _L3_ffn_all
    return {'x': x, 'ctx_512': ctx_512, 'L0_attn_Wqkv_w': _L0_attn_in['Wqkv_w'], 'L0_attn_Wqkv_b': _L0_attn_in['Wqkv_b'], 'L0_attn_U': _L0_attn_in['U'], 'L0_attn_Wo_w': _L0_attn_in['Wo_w'], 'L0_xattn_Wq': _L0_xattn_in['Wq'], 'L0_xattn_Wkv': _L0_xattn_in['Wkv'], 'L0_xattn_Wo': _L0_xattn_in['Wo'], 'L0_ffn_w1': _L0_ffn_in['w1'], 'L0_ffn_w2': _L0_ffn_in['w2'], 'L0_ffn_w3': _L0_ffn_in['w3'], 'L0_ffn_new_w1': _L0_ffn_in['new_w1'], 'L0_ffn_new_w2': _L0_ffn_in['new_w2'], 'L0_ffn_new_w3': _L0_ffn_in['new_w3'], 'L0_ffn_gate_weight': _L0_ffn_in['gate_weight'], 'L0_ffn_new_gate_weight': _L0_ffn_in['new_gate_weight'], 'L0_ffn_gate_bias': _L0_ffn_in['gate_bias'], 'L1_attn_W_dt': _L1_attn_in['W_dt'], 'L1_attn_b_dt': _L1_attn_in['b_dt'], 'L1_attn_W_B': _L1_attn_in['W_B'], 'L1_attn_W_C': _L1_attn_in['W_C'], 'L1_attn_D_param': _L1_attn_in['D_param'], 'L1_attn_A_log': _L1_attn_in['A_log'], 'L1_attn_gamma': _L1_attn_in['gamma'], 'L1_attn_beta': _L1_attn_in['beta'], 'L1_xattn_Wq': _L1_xattn_in['Wq'], 'L1_xattn_bq': _L1_xattn_in['bq'], 'L1_xattn_Wk': _L1_xattn_in['Wk'], 'L1_xattn_bk': _L1_xattn_in['bk'], 'L1_xattn_Wv': _L1_xattn_in['Wv'], 'L1_xattn_bv': _L1_xattn_in['bv'], 'L1_xattn_Wo': _L1_xattn_in['Wo'], 'L1_xattn_bo': _L1_xattn_in['bo'], 'L1_ffn_g1': _L1_ffn_in['g1'], 'L1_ffn_g2': _L1_ffn_in['g2'], 'L1_ffn_wq': _L1_ffn_in['wq'], 'L1_ffn_wk': _L1_ffn_in['wk'], 'L1_ffn_wv': _L1_ffn_in['wv'], 'L1_ffn_wo': _L1_ffn_in['wo'], 'L1_ffn_router_w': _L1_ffn_in['router_w'], 'L1_ffn_router_b': _L1_ffn_in['router_b'], 'L1_ffn_w1': _L1_ffn_in['w1'], 'L1_ffn_w2': _L1_ffn_in['w2'], 'L1_ffn_w3': _L1_ffn_in['w3'], 'L2_attn_WQ': _L2_attn_in['WQ'], 'L2_attn_bQ': _L2_attn_in['bQ'], 'L2_attn_WK': _L2_attn_in['WK'], 'L2_attn_bK': _L2_attn_in['bK'], 'L2_attn_WV': _L2_attn_in['WV'], 'L2_attn_bV': _L2_attn_in['bV'], 'L2_attn_WO': _L2_attn_in['WO'], 'L2_attn_bO': _L2_attn_in['bO'], 'L2_attn_WQr': _L2_attn_in['WQr'], 'L2_attn_WKr': _L2_attn_in['WKr'], 'L2_xattn_Wq': _L2_xattn_in['Wq'], 'L2_xattn_Wk': _L2_xattn_in['Wk'], 'L2_xattn_Wv': _L2_xattn_in['Wv'], 'L2_xattn_Wo': _L2_xattn_in['Wo'], 'L2_xattn_bo': _L2_xattn_in['bo'], 'L2_ffn_router_weight': _L2_ffn_in['router_weight'], 'L2_ffn_router_bias': _L2_ffn_in['router_bias'], 'L2_ffn_gate_w': _L2_ffn_in['gate_w'], 'L2_ffn_up_w': _L2_ffn_in['up_w'], 'L2_ffn_down_w': _L2_ffn_in['down_w'], 'L2_ffn_shared_gate_w': _L2_ffn_in['shared_gate_w'], 'L2_ffn_shared_up_w': _L2_ffn_in['shared_up_w'], 'L2_ffn_shared_down_w': _L2_ffn_in['shared_down_w'], 'L3_attn_proj': _L3_attn_in['proj'], 'L3_attn_w_qkv': _L3_attn_in['w_qkv'], 'L3_attn_w_out': _L3_attn_in['w_out'], 'L3_attn_b_out': _L3_attn_in['b_out'], 'L3_attn_gamma': _L3_attn_in['gamma'], 'L3_attn_beta': _L3_attn_in['beta'], 'L3_attn_w1': _L3_attn_in['w1'], 'L3_attn_b1': _L3_attn_in['b1'], 'L3_attn_w2': _L3_attn_in['w2'], 'L3_attn_b2': _L3_attn_in['b2'], 'L3_xattn_ln1_g': _L3_xattn_in['ln1_g'], 'L3_xattn_ln1_b': _L3_xattn_in['ln1_b'], 'L3_xattn_ln2_g': _L3_xattn_in['ln2_g'], 'L3_xattn_ln2_b': _L3_xattn_in['ln2_b'], 'L3_xattn_a1_wq': _L3_xattn_in['a1_wq'], 'L3_xattn_a1_wk': _L3_xattn_in['a1_wk'], 'L3_xattn_a1_wv': _L3_xattn_in['a1_wv'], 'L3_xattn_a1_li1_w': _L3_xattn_in['a1_li1_w'], 'L3_xattn_a1_li1_b': _L3_xattn_in['a1_li1_b'], 'L3_xattn_a1_lnx_g': _L3_xattn_in['a1_lnx_g'], 'L3_xattn_a1_lnx_b': _L3_xattn_in['a1_lnx_b'], 'L3_xattn_a1_lny_g': _L3_xattn_in['a1_lny_g'], 'L3_xattn_a1_lny_b': _L3_xattn_in['a1_lny_b'], 'L3_xattn_a1_ln3_g': _L3_xattn_in['a1_ln3_g'], 'L3_xattn_a1_ln3_b': _L3_xattn_in['a1_ln3_b'], 'L3_xattn_a1_li2_w': _L3_xattn_in['a1_li2_w'], 'L3_xattn_a1_li2_b': _L3_xattn_in['a1_li2_b'], 'L3_xattn_a1_li3_w': _L3_xattn_in['a1_li3_w'], 'L3_xattn_a1_li3_b': _L3_xattn_in['a1_li3_b'], 'L3_xattn_a2_wq': _L3_xattn_in['a2_wq'], 'L3_xattn_a2_wk': _L3_xattn_in['a2_wk'], 'L3_xattn_a2_wv': _L3_xattn_in['a2_wv'], 'L3_xattn_a2_li1_w': _L3_xattn_in['a2_li1_w'], 'L3_xattn_a2_li1_b': _L3_xattn_in['a2_li1_b'], 'L3_xattn_a2_lnx_g': _L3_xattn_in['a2_lnx_g'], 'L3_xattn_a2_lnx_b': _L3_xattn_in['a2_lnx_b'], 'L3_xattn_a2_lny_g': _L3_xattn_in['a2_lny_g'], 'L3_xattn_a2_lny_b': _L3_xattn_in['a2_lny_b'], 'L3_xattn_a2_ln3_g': _L3_xattn_in['a2_ln3_g'], 'L3_xattn_a2_ln3_b': _L3_xattn_in['a2_ln3_b'], 'L3_xattn_a2_li2_w': _L3_xattn_in['a2_li2_w'], 'L3_xattn_a2_li2_b': _L3_xattn_in['a2_li2_b'], 'L3_xattn_a2_li3_w': _L3_xattn_in['a2_li3_w'], 'L3_xattn_a2_li3_b': _L3_xattn_in['a2_li3_b'], 'L3_ffn_W_r': _L3_ffn_in['W_r'], 'L3_ffn_W_k': _L3_ffn_in['W_k'], 'L3_ffn_W_v': _L3_ffn_in['W_v'], 'L3_ffn_mu_r': _L3_ffn_in['mu_r'], 'L3_ffn_mu_k': _L3_ffn_in['mu_k']}

def reference(x, ctx_512, L0_attn_Wqkv_w, L0_attn_Wqkv_b, L0_attn_U, L0_attn_Wo_w, L0_xattn_Wq, L0_xattn_Wkv, L0_xattn_Wo, L0_ffn_w1, L0_ffn_w2, L0_ffn_w3, L0_ffn_new_w1, L0_ffn_new_w2, L0_ffn_new_w3, L0_ffn_gate_weight, L0_ffn_new_gate_weight, L0_ffn_gate_bias, L1_attn_W_dt, L1_attn_b_dt, L1_attn_W_B, L1_attn_W_C, L1_attn_D_param, L1_attn_A_log, L1_attn_gamma, L1_attn_beta, L1_xattn_Wq, L1_xattn_bq, L1_xattn_Wk, L1_xattn_bk, L1_xattn_Wv, L1_xattn_bv, L1_xattn_Wo, L1_xattn_bo, L1_ffn_g1, L1_ffn_g2, L1_ffn_wq, L1_ffn_wk, L1_ffn_wv, L1_ffn_wo, L1_ffn_router_w, L1_ffn_router_b, L1_ffn_w1, L1_ffn_w2, L1_ffn_w3, L2_attn_WQ, L2_attn_bQ, L2_attn_WK, L2_attn_bK, L2_attn_WV, L2_attn_bV, L2_attn_WO, L2_attn_bO, L2_attn_WQr, L2_attn_WKr, L2_xattn_Wq, L2_xattn_Wk, L2_xattn_Wv, L2_xattn_Wo, L2_xattn_bo, L2_ffn_router_weight, L2_ffn_router_bias, L2_ffn_gate_w, L2_ffn_up_w, L2_ffn_down_w, L2_ffn_shared_gate_w, L2_ffn_shared_up_w, L2_ffn_shared_down_w, L3_attn_proj, L3_attn_w_qkv, L3_attn_w_out, L3_attn_b_out, L3_attn_gamma, L3_attn_beta, L3_attn_w1, L3_attn_b1, L3_attn_w2, L3_attn_b2, L3_xattn_ln1_g, L3_xattn_ln1_b, L3_xattn_ln2_g, L3_xattn_ln2_b, L3_xattn_a1_wq, L3_xattn_a1_wk, L3_xattn_a1_wv, L3_xattn_a1_li1_w, L3_xattn_a1_li1_b, L3_xattn_a1_lnx_g, L3_xattn_a1_lnx_b, L3_xattn_a1_lny_g, L3_xattn_a1_lny_b, L3_xattn_a1_ln3_g, L3_xattn_a1_ln3_b, L3_xattn_a1_li2_w, L3_xattn_a1_li2_b, L3_xattn_a1_li3_w, L3_xattn_a1_li3_b, L3_xattn_a2_wq, L3_xattn_a2_wk, L3_xattn_a2_wv, L3_xattn_a2_li1_w, L3_xattn_a2_li1_b, L3_xattn_a2_lnx_g, L3_xattn_a2_lnx_b, L3_xattn_a2_lny_g, L3_xattn_a2_lny_b, L3_xattn_a2_ln3_g, L3_xattn_a2_ln3_b, L3_xattn_a2_li2_w, L3_xattn_a2_li2_b, L3_xattn_a2_li3_w, L3_xattn_a2_li3_b, L3_ffn_W_r, L3_ffn_W_k, L3_ffn_W_v, L3_ffn_mu_r, L3_ffn_mu_k):
    import jax
    import jax.numpy as jnp

    def _L0_attn_ref(x, Wqkv_w, Wqkv_b, U, Wo_w):
        import jax, jax.numpy as jnp
        import numpy as np
        import math
        H = 16

        def quant4(x):
            xs = jax.lax.stop_gradient(x)
            ma = jnp.maximum(jnp.max(jnp.abs(xs), axis=-1, keepdims=True), 1e-06)
            q = jnp.clip(jnp.round(xs / ma * 7.0), -8.0, 7.0)
            return x + jax.lax.stop_gradient(q * ma / 7.0 - xs)

        def ternary_weight(w):
            thresh = jax.lax.stop_gradient(0.05 * jnp.mean(jnp.abs(w)))
            sign = jnp.where(jnp.abs(w) < thresh, 0.0, jnp.sign(w))
            alpha = jnp.mean(jnp.abs(w), axis=1, keepdims=True)
            return sign * alpha + (w - jax.lax.stop_gradient(w))

        def rotary(t, n):
            half = t.shape[-1] // 2
            inv = 1.0 / 10000.0 ** (jnp.arange(half, dtype=t.dtype) / half)
            ang = jnp.arange(n, dtype=t.dtype)[:, None] * inv
            c, s = (jnp.cos(ang), jnp.sin(ang))
            t1, t2 = (t[..., ::2], t[..., 1::2])
            return jnp.concatenate([t1 * c - t2 * s, t1 * s + t2 * c], axis=-1)
        B, N, d = x.shape
        h = H
        dk = d // h
        proj = quant4(x) @ ternary_weight(Wqkv_w).T + Wqkv_b
        q = proj.reshape(B, N, h, dk).transpose(0, 2, 1, 3)
        k = proj.reshape(B, h, N, dk)
        v = proj.reshape(B, h, N, dk)
        q, k = (rotary(q, N), rotary(k, N))
        ql, kl = (q @ U, k @ U)
        att = jnp.einsum('bhnr,bhmr->bhnm', ql, kl) / math.sqrt(dk)
        y = jax.nn.softmax(att, axis=-1) @ v
        y = y.transpose(0, 2, 1, 3).reshape(B, N, d)
        return quant4(y) @ ternary_weight(Wo_w).T

    def _L0_xattn_ref(x, z, Wq, Wkv, Wo):
        import jax, jax.numpy as jnp
        import numpy as np
        DIM = 128
        LATENT_DIM = 64
        NUM_HEADS = 16
        HEAD_DIM = DIM // NUM_HEADS
        SCALE = HEAD_DIM ** (-0.5)
        B, xN, _ = x.shape
        _, zN, _ = z.shape
        Q = (x @ Wq.T).reshape(B, xN, NUM_HEADS, HEAD_DIM)
        KV = (z @ Wkv.T).reshape(B, zN, 2, NUM_HEADS, HEAD_DIM)
        K = KV[:, :, 0]
        V = KV[:, :, 1]
        attn = jnp.einsum('bqhd,bkhd->bhqk', Q, K) * SCALE
        attn = jax.nn.softmax(attn, axis=-1)
        O = jnp.einsum('bhqk,bkhd->bqhd', attn, V).reshape(B, xN, DIM)
        return O @ Wo.T

    def _L0_ffn_ref(x, w1, w2, w3, new_w1, new_w2, new_w3, gate_weight, new_gate_weight, gate_bias):
        import jax, jax.numpy as jnp
        import numpy as np
        TOP_K = 2
        ROUTE_SCALE = 1.0
        EPS = 1e-20
        bs, slen, dim = x.shape
        x_flat = x.reshape(-1, dim)
        ew1 = jnp.concatenate([w1, new_w1], axis=0)
        ew2 = jnp.concatenate([w2, new_w2], axis=0)
        ew3 = jnp.concatenate([w3, new_w3], axis=0)
        gate = jnp.concatenate([gate_weight, new_gate_weight], axis=0)
        e_orig = w1.shape[0]
        e_tot = gate.shape[0]
        bias = jnp.concatenate([jnp.zeros((e_orig,), x.dtype), gate_bias])
        scores = jax.nn.sigmoid((x_flat @ gate.T + bias).astype(jnp.float32))
        top_scores, selected = jax.lax.top_k(scores, TOP_K)
        top_scores = top_scores / (jnp.sum(top_scores, axis=-1, keepdims=True) + EPS)
        top_scores = top_scores * ROUTE_SCALE
        onehot = jax.nn.one_hot(selected, e_tot, dtype=jnp.float32)
        cw = jnp.einsum('tk,tke->te', top_scores, onehot)
        out = jnp.zeros_like(x_flat)
        for e in range(e_tot):
            h = jax.nn.silu(x_flat @ ew1[e].T) * (x_flat @ ew3[e].T)
            out = out + cw[:, e:e + 1] * (h @ ew2[e].T)
        return out.reshape(bs, slen, dim)

    def _L1_attn_ref(x, W_dt, b_dt, W_B, W_C, D_param, A_log, gamma, beta):
        import jax, jax.numpy as jnp
        import numpy as np
        Bsz, L, D, N = (2, 256, 128, 16)
        LN_EPS = 1e-05
        residual = x
        mu = jnp.mean(x, axis=-1, keepdims=True)
        var = jnp.var(x, axis=-1, keepdims=True)
        xn = (x - mu) * jax.lax.rsqrt(var + LN_EPS) * gamma + beta
        dt = jax.nn.softplus(xn @ W_dt.T + b_dt)
        A = -jnp.exp(A_log)
        B_in = xn @ W_B.T
        C_in = xn @ W_C.T
        A_bar = jnp.exp(dt[..., None] * A)
        Bx = dt[..., None] * B_in[:, :, None, :] * xn[..., None]

        def step(h, inputs):
            a_t, bx_t, c_t = inputs
            h = a_t * h + bx_t
            y_t = jnp.einsum('bn,bdn->bd', c_t, h)
            return (h, y_t)
        h0 = jnp.zeros((x.shape[0], D, N), x.dtype)
        _, ys = jax.lax.scan(step, h0, (jnp.transpose(A_bar, (1, 0, 2, 3)), jnp.transpose(Bx, (1, 0, 2, 3)), jnp.transpose(C_in, (1, 0, 2))))
        y = jnp.transpose(ys, (1, 0, 2)) + D_param * residual
        return y

    def _L1_xattn_ref(q, k, v, Wq, bq, Wk, bk, Wv, bv, Wo, bo):
        import jax, jax.numpy as jnp
        import numpy as np
        HEADS = 16
        D_MODEL = 128
        IMG_MODEL = 64
        D_K = D_MODEL // HEADS
        B, LQ, _ = q.shape
        LKV = k.shape[1]
        qh = (q @ Wq + bq).reshape(B, LQ, HEADS, D_K).transpose(0, 2, 1, 3)
        kh = (k @ Wk + bk).reshape(B, LKV, HEADS, D_K).transpose(0, 2, 1, 3)
        vh = (v @ Wv + bv).reshape(B, LKV, HEADS, D_K).transpose(0, 2, 1, 3)
        scale = 1.0 / np.sqrt(D_K)
        scores = jnp.einsum('bhqd,bhkd->bhqk', qh, kh) * scale
        attn = jax.nn.softmax(scores, axis=-1)
        out = jnp.einsum('bhqk,bhkd->bhqd', attn, vh)
        concat = out.transpose(0, 2, 1, 3).reshape(B, LQ, D_MODEL)
        return concat @ Wo + bo

    def _L1_ffn_ref(x, g1, g2, wq, wk, wv, wo, router_w, router_b, w1, w2, w3):
        import jax, jax.numpy as jnp
        import numpy as np
        D = 128
        HQ = 16
        HKV = 4
        G = HQ // HKV
        K = 64
        V = 64
        E = 8
        TOPK = 2
        HID = 256
        CAP_FRAC = 0.125
        EPS = 1e-06

        def _rmsnorm(x, g):
            return x * jax.lax.rsqrt(jnp.mean(x * x, axis=-1, keepdims=True) + EPS) * g

        def _rotary_tables(t, dim):
            thetas = 10000.0 ** (-np.arange(0, dim, 2, dtype=np.float32) / dim)
            ticks = np.outer(np.arange(t, dtype=np.float32), thetas)
            ticks = np.tile(ticks, (1, 2))[None, :, None, :]
            return (jnp.asarray(np.cos(ticks)), jnp.asarray(np.sin(ticks)))

        def _neg_half(x):
            x1, x2 = jnp.split(x, 2, axis=-1)
            return jnp.concatenate([-x2, x1], axis=-1)

        def _attention(x, wq, wk, wv, wo):
            b, t, _ = x.shape
            q = (x @ wq).reshape(b, t, HQ, K)
            k = (x @ wk).reshape(b, t, HKV, K)
            v = (x @ wv).reshape(b, t, HKV, V)
            cos, sin = _rotary_tables(t, K)
            q = q * cos + _neg_half(q) * sin
            k = k * cos + _neg_half(k) * sin
            qg = q.reshape(b, t, G, HKV, K)
            scores = jnp.einsum('btghk,bThk->bghtT', qg, k)
            mask = jnp.tril(jnp.ones((t, t), bool))
            scores = jnp.where(mask, scores, -jnp.inf) / np.float32(np.sqrt(K))
            p = jax.nn.softmax(scores, axis=-1)
            out = jnp.einsum('bghtT,bThv->btghv', p, v).reshape(b, t, HQ * V)
            return out @ wo

        def _moe(x, router_w, router_b, w1, w2, w3):
            b, t, d = x.shape
            n = b * t
            xf = x.reshape(n, d)
            logits = xf @ router_w + router_b
            vals, idx = jax.lax.top_k(logits, TOPK)
            scores = jax.nn.softmax(vals, axis=-1)
            cap = int(np.floor(n * CAP_FRAC))
            oh = jax.nn.one_hot(idx, E, dtype=jnp.float32)
            pos = jnp.cumsum(jnp.cumsum(oh, axis=0), axis=1).astype(jnp.int32)
            emask = oh * (pos < cap)
            tmask = jnp.sum(emask, axis=-1)
            assign = jnp.einsum('tke,e->tk', emask, jnp.arange(E, dtype=jnp.float32)).astype(jnp.int32)
            m = jnp.max(assign, axis=-1)

            def ff(w1e, w2e, w3e):
                h = jax.nn.gelu(xf @ w2e * (xf @ w1e), approximate=False)
                return h @ w3e
            y_all = jax.vmap(ff)(w1, w2, w3)
            y = y_all[m, jnp.arange(n)]
            slot = jnp.where(tmask[..., None] > 0, y[:, None, :], xf[:, None, :])
            out = jnp.einsum('tkD,tk->tD', slot, scores)
            return out.reshape(b, t, d)
        h = x + _attention(_rmsnorm(x, g1), wq, wk, wv, wo)
        return h + _moe(_rmsnorm(h, g2), router_w, router_b, w1, w2, w3)

    def _L2_attn_ref(x, WQ, bQ, WK, bK, WV, bV, WO, bO, WQr, WKr):
        import jax, jax.numpy as jnp
        import numpy as np
        import math
        D_MODEL, N_HEADS, RANK = (128, 16, 16)
        D_K = D_MODEL // N_HEADS
        BATCH, N = (2, 256)
        b, n, d = x.shape
        Q = (x @ WQ + bQ).reshape(b, n, N_HEADS, D_K)
        K = (x @ WK + bK).reshape(b, n, N_HEADS, D_K)
        V = (x @ WV + bV).reshape(b, n, N_HEADS, D_K)
        Qr = jnp.einsum('bnhd,dr->bnhr', Q, WQr)
        Kr = jnp.einsum('bnhd,dr->bnhr', K, WKr)
        scores = jnp.einsum('bnhr,bmhr->bnhm', Qr, Kr) / math.sqrt(RANK)
        A = jax.nn.softmax(scores, axis=-1)
        out = jnp.einsum('bnhm,bmhv->bnhv', A, V).reshape(b, n, d)
        return out @ WO + bO

    def _L2_xattn_ref(q, kv, Wq, Wk, Wv, Wo, bo):
        import jax, jax.numpy as jnp
        import numpy as np
        NUM_HEADS = 16
        HEAD_DIM = 64
        Q_DIM = 128
        KV_DIM = 64
        INNER = NUM_HEADS * HEAD_DIM
        B, N, _ = q.shape
        M = kv.shape[1]
        scale = HEAD_DIM ** (-0.5)
        qh = (q @ Wq).reshape(B, N, NUM_HEADS, HEAD_DIM).transpose(0, 2, 1, 3)
        kh = (kv @ Wk).reshape(B, M, NUM_HEADS, HEAD_DIM).transpose(0, 2, 1, 3)
        vh = (kv @ Wv).reshape(B, M, NUM_HEADS, HEAD_DIM).transpose(0, 2, 1, 3)
        scores = jnp.einsum('bhnd,bhmd->bhnm', qh, kh) * scale
        attn = jax.nn.softmax(scores, axis=-1)
        out = jnp.einsum('bhnm,bhmd->bhnd', attn, vh)
        out = out.transpose(0, 2, 1, 3).reshape(B, N, INNER)
        return out @ Wo + bo

    def _L2_ffn_ref(hidden_states, router_weight, router_bias, gate_w, up_w, down_w, shared_gate_w, shared_up_w, shared_down_w):
        import jax, jax.numpy as jnp
        import numpy as np
        from jax import lax
        B, S, H = (2, 128, 128)
        I = 64
        E = 32
        TOP_K = 4
        N_GROUP = 4
        TOPK_GROUP = 2
        SCALE = 2.5
        N_SHARED = 2
        SH_I = I * N_SHARED

        def _route(tokens, router_weight, router_bias):
            logits = tokens.astype(jnp.float32) @ router_weight.astype(jnp.float32).T
            scores = jax.nn.sigmoid(logits)
            sfc = scores + router_bias[None, :]
            T = tokens.shape[0]
            grp = sfc.reshape(T, N_GROUP, E // N_GROUP)
            group_scores = lax.top_k(grp, 2)[0].sum(-1)
            _, gidx = lax.top_k(group_scores, TOPK_GROUP)
            gmask = jax.nn.one_hot(gidx, N_GROUP, dtype=sfc.dtype).sum(1)
            smask = jnp.broadcast_to(gmask[:, :, None], (T, N_GROUP, E // N_GROUP)).reshape(T, E)
            tmp = jnp.where(smask > 0, sfc, 0.0)
            _, topk_idx = lax.top_k(tmp, TOP_K)
            topk_w = jnp.take_along_axis(scores, topk_idx, axis=1)
            topk_w = topk_w / (topk_w.sum(-1, keepdims=True) + 1e-20)
            topk_w = topk_w * SCALE
            return (topk_idx, topk_w)
        tokens = hidden_states.reshape(-1, H)
        topk_idx, topk_w = _route(tokens, router_weight, router_bias)
        gate_vals = jax.nn.silu(jnp.einsum('th,eih->tei', tokens, gate_w))
        up_vals = jnp.einsum('th,eih->tei', tokens, up_w)
        hidden_vals = gate_vals * up_vals
        expert_out = jnp.einsum('tei,ehi->teh', hidden_vals, down_w)
        sel = jnp.take_along_axis(expert_out, topk_idx[:, :, None], axis=1)
        mixed = (sel * topk_w[:, :, None].astype(sel.dtype)).sum(1)
        mixed = mixed.reshape(hidden_states.shape)
        sg = jax.nn.silu(jnp.einsum('bsh,ih->bsi', hidden_states, shared_gate_w))
        su = jnp.einsum('bsh,ih->bsi', hidden_states, shared_up_w)
        shared = jnp.einsum('bsi,hi->bsh', sg * su, shared_down_w)
        return mixed + shared

    def _L3_attn_ref(x, proj, w_qkv, w_out, b_out, gamma, beta, w1, b1, w2, b2):
        import jax, jax.numpy as jnp
        import numpy as np
        B, N, D = (4, 512, 128)
        H, F = (16, 32)
        HD = D // H
        EPS_ATTN = 1e-08
        EPS_LN = 1e-05

        def _layernorm(x, gamma, beta):
            mu = jnp.mean(x, axis=-1, keepdims=True)
            var = jnp.var(x, axis=-1, keepdims=True)
            return (x - mu) * jax.lax.rsqrt(var + EPS_LN) * gamma + beta
        residual = x
        b, n, d = x.shape
        qkv = x @ w_qkv.T
        q, k, v = jnp.split(qkv, 3, axis=-1)

        def to_heads(t):
            return t.reshape(b, n, H, HD).transpose(0, 2, 1, 3)
        q, k, v = (to_heads(q), to_heads(k), to_heads(v))
        q_f = jax.nn.elu(jnp.einsum('bhnd,hdf->bhnf', q, proj)) + 1.0
        k_f = jax.nn.elu(jnp.einsum('bhnd,hdf->bhnf', k, proj)) + 1.0
        kv = jnp.einsum('bhnf,bhnd->bhfd', k_f, v)
        attn = jnp.einsum('bhnf,bhfd->bhnd', q_f, kv)
        k_sum = jnp.sum(k_f, axis=2)
        z = 1.0 / (jnp.einsum('bhnf,bhf->bhn', q_f, k_sum) + EPS_ATTN)
        attn = attn * z[..., None]
        attn = attn.transpose(0, 2, 1, 3).reshape(b, n, d)
        x = residual + attn @ w_out.T + b_out
        x = _layernorm(x, gamma, beta)
        h = jax.nn.gelu(x @ w1.T + b1, approximate=False)
        x = x + h @ w2.T + b2
        x = _layernorm(x, gamma, beta)
        return x

    def _L3_xattn_ref(xx, ee, ln1_g, ln1_b, ln2_g, ln2_b, a1_wq, a1_wk, a1_wv, a1_li1_w, a1_li1_b, a1_lnx_g, a1_lnx_b, a1_lny_g, a1_lny_b, a1_ln3_g, a1_ln3_b, a1_li2_w, a1_li2_b, a1_li3_w, a1_li3_b, a2_wq, a2_wk, a2_wv, a2_li1_w, a2_li1_b, a2_lnx_g, a2_lnx_b, a2_lny_g, a2_lny_b, a2_ln3_g, a2_ln3_b, a2_li2_w, a2_li2_b, a2_li3_w, a2_li3_b, training):
        import jax, jax.numpy as jnp
        import numpy as np
        H, D, C1, C2, S, M, B, W = (16, 32, 128, 64, 256, 64, 2, 4)

        def _ln(x, g, b):
            m = jnp.mean(x, -1, keepdims=True)
            v = jnp.var(x, -1, keepdims=True)
            return (x - m) * jax.lax.rsqrt(v + 1e-05) * g + b

        def _mha(x, y, wq, wk, wv, li1_w, li1_b, lnx_g, lnx_b, lny_g, lny_b, ln3_g, ln3_b, li2_w, li2_b, li3_w, li3_b, causal):
            xn = _ln(x, lnx_g, lnx_b)
            yn = _ln(y, lny_g, lny_b)
            q = jnp.einsum('bsc,hcd->bhsd', xn, wq)
            k = jnp.einsum('btc,hcd->bhtd', yn, wk)
            v = jnp.einsum('btc,hcd->bhtd', yn, wv)
            a = jax.nn.softmax(jnp.einsum('bhsd,bhtd->bhst', q, k) * D ** (-0.5), axis=-1)
            if causal:
                s, t = (a.shape[-2], a.shape[-1])
                mask = (jnp.arange(t)[None, :] > jnp.arange(s)[:, None]).astype(a.dtype)
                a = a * mask
            o = jnp.einsum('bhst,bhtd->bhsd', a, v)
            o = o.transpose(0, 2, 1, 3).reshape(x.shape[0], x.shape[1], H * D)
            x_out = x + o @ li1_w + li1_b
            h = jax.nn.gelu(_ln(x_out, ln3_g, ln3_b) @ li2_w + li2_b, approximate=False)
            return x_out + h @ li3_w + li3_b
        x = _ln(xx, ln1_g, ln1_b)
        x = x + _mha(x, x, a1_wq, a1_wk, a1_wv, a1_li1_w, a1_li1_b, a1_lnx_g, a1_lnx_b, a1_lny_g, a1_lny_b, a1_ln3_g, a1_ln3_b, a1_li2_w, a1_li2_b, a1_li3_w, a1_li3_b, causal=True)
        x = _ln(x, ln2_g, ln2_b)
        return x + _mha(x, ee, a2_wq, a2_wk, a2_wv, a2_li1_w, a2_li1_b, a2_lnx_g, a2_lnx_b, a2_lny_g, a2_lny_b, a2_ln3_g, a2_ln3_b, a2_li2_w, a2_li2_b, a2_li3_w, a2_li3_b, causal=False)

    def _L3_ffn_ref(x, W_r, W_k, W_v, mu_r, mu_k):
        import jax, jax.numpy as jnp
        import numpy as np
        DIM = 128

        def _reference_tuple_inner(x, W_r, W_k, W_v, mu_r, mu_k):
            B, T, C = x.shape
            x_prev = jnp.concatenate([jnp.zeros((B, 1, C), x.dtype), x[:, :-1, :]], axis=1)
            xr = mu_r * x + (1.0 - mu_r) * x_prev
            xk = mu_k * x + (1.0 - mu_k) * x_prev
            r = jax.nn.sigmoid(jnp.einsum('btc,dc->btd', xr, W_r))
            k = jnp.einsum('btc,dc->btd', xk, W_k)
            k_act = jnp.square(jax.nn.relu(k))
            out = r * jnp.einsum('btc,dc->btd', k_act, W_v)
            new_state = x[:, -1, :]
            return (out, new_state)
        return _reference_tuple_inner(x, W_r, W_k, W_v, mu_r, mu_k)[0]
    x = _layernorm(x + _L0_attn_ref(x, L0_attn_Wqkv_w, L0_attn_Wqkv_b, L0_attn_U, L0_attn_Wo_w), axis=-1)
    x = _layernorm(x + _L0_xattn_ref(x, ctx_512, L0_xattn_Wq, L0_xattn_Wkv, L0_xattn_Wo), axis=-1)
    x = _layernorm(x + _L0_ffn_ref(x, L0_ffn_w1, L0_ffn_w2, L0_ffn_w3, L0_ffn_new_w1, L0_ffn_new_w2, L0_ffn_new_w3, L0_ffn_gate_weight, L0_ffn_new_gate_weight, L0_ffn_gate_bias), axis=-1)
    x = _layernorm(x + _L1_attn_ref(x, L1_attn_W_dt, L1_attn_b_dt, L1_attn_W_B, L1_attn_W_C, L1_attn_D_param, L1_attn_A_log, L1_attn_gamma, L1_attn_beta), axis=-1)
    x = _layernorm(x + _L1_xattn_ref(x, ctx_512, ctx_512, L1_xattn_Wq, L1_xattn_bq, L1_xattn_Wk, L1_xattn_bk, L1_xattn_Wv, L1_xattn_bv, L1_xattn_Wo, L1_xattn_bo), axis=-1)
    x = _layernorm(x + _L1_ffn_ref(x, L1_ffn_g1, L1_ffn_g2, L1_ffn_wq, L1_ffn_wk, L1_ffn_wv, L1_ffn_wo, L1_ffn_router_w, L1_ffn_router_b, L1_ffn_w1, L1_ffn_w2, L1_ffn_w3), axis=-1)
    x = _layernorm(x + _L2_attn_ref(x, L2_attn_WQ, L2_attn_bQ, L2_attn_WK, L2_attn_bK, L2_attn_WV, L2_attn_bV, L2_attn_WO, L2_attn_bO, L2_attn_WQr, L2_attn_WKr), axis=-1)
    x = _layernorm(x + _L2_xattn_ref(x, ctx_512, L2_xattn_Wq, L2_xattn_Wk, L2_xattn_Wv, L2_xattn_Wo, L2_xattn_bo), axis=-1)
    x = _layernorm(x + _L2_ffn_ref(x, L2_ffn_router_weight, L2_ffn_router_bias, L2_ffn_gate_w, L2_ffn_up_w, L2_ffn_down_w, L2_ffn_shared_gate_w, L2_ffn_shared_up_w, L2_ffn_shared_down_w), axis=-1)
    x = _layernorm(x + _L3_attn_ref(x, L3_attn_proj, L3_attn_w_qkv, L3_attn_w_out, L3_attn_b_out, L3_attn_gamma, L3_attn_beta, L3_attn_w1, L3_attn_b1, L3_attn_w2, L3_attn_b2), axis=-1)
    x = _layernorm(x + _L3_xattn_ref(x, ctx_512, L3_xattn_ln1_g, L3_xattn_ln1_b, L3_xattn_ln2_g, L3_xattn_ln2_b, L3_xattn_a1_wq, L3_xattn_a1_wk, L3_xattn_a1_wv, L3_xattn_a1_li1_w, L3_xattn_a1_li1_b, L3_xattn_a1_lnx_g, L3_xattn_a1_lnx_b, L3_xattn_a1_lny_g, L3_xattn_a1_lny_b, L3_xattn_a1_ln3_g, L3_xattn_a1_ln3_b, L3_xattn_a1_li2_w, L3_xattn_a1_li2_b, L3_xattn_a1_li3_w, L3_xattn_a1_li3_b, L3_xattn_a2_wq, L3_xattn_a2_wk, L3_xattn_a2_wv, L3_xattn_a2_li1_w, L3_xattn_a2_li1_b, L3_xattn_a2_lnx_g, L3_xattn_a2_lnx_b, L3_xattn_a2_lny_g, L3_xattn_a2_lny_b, L3_xattn_a2_ln3_g, L3_xattn_a2_ln3_b, L3_xattn_a2_li2_w, L3_xattn_a2_li2_b, L3_xattn_a2_li3_w, L3_xattn_a2_li3_b, 0), axis=-1)
    x = _layernorm(x + _L3_ffn_ref(x, L3_ffn_W_r, L3_ffn_W_k, L3_ffn_W_v, L3_ffn_mu_r, L3_ffn_mu_k), axis=-1)
    return x

_drawn_inputs = setup_inputs


def setup_inputs(seed=0):
    import zlib

    import numpy as np

    out = dict(_drawn_inputs(seed))
    spreads = {'L0_attn_Wqkv_b': (0.0, 0.1),
     'L0_ffn_new_w2': (0.0, 0.8),
     'L1_attn_b_dt': (0.0, 0.8),
     'L1_attn_D_param': (1.0, 0.2),
     'L1_attn_gamma': (1.0, 0.2),
     'L1_attn_beta': (0.0, 0.1),
     'L1_xattn_bq': (0.0, 0.356),
     'L1_xattn_bk': (0.0, 2.0),
     'L1_xattn_bv': (0.0, 0.1),
     'L1_xattn_bo': (0.0, 0.1),
     'L1_ffn_g1': (1.0, 0.6),
     'L1_ffn_g2': (1.0, 0.2),
     'L1_ffn_router_b': (0.0, 0.671),
     'L2_attn_bQ': (0.0, 0.8),
     'L2_attn_bK': (0.0, 2.0),
     'L2_attn_bV': (0.0, 0.1),
     'L2_attn_bO': (0.0, 0.1),
     'L2_ffn_router_bias': (0.0, 0.8),
     'L3_attn_b_out': (0.0, 0.1),
     'L3_attn_gamma': (1.0, 0.2),
     'L3_attn_beta': (0.0, 0.1),
     'L3_attn_b1': (0.0, 0.1),
     'L3_attn_b2': (0.0, 0.1),
     'L3_xattn_ln1_g': (1.0, 0.2),
     'L3_xattn_ln1_b': (0.0, 0.1),
     'L3_xattn_ln2_g': (1.0, 0.2),
     'L3_xattn_ln2_b': (0.0, 0.1),
     'L3_xattn_a1_li1_b': (0.0, 0.1),
     'L3_xattn_a1_lnx_g': (1.0, 0.6),
     'L3_xattn_a1_lnx_b': (0.0, 0.8),
     'L3_xattn_a1_lny_g': (1.0, 0.6),
     'L3_xattn_a1_lny_b': (0.0, 0.8),
     'L3_xattn_a1_ln3_g': (1.0, 0.6),
     'L3_xattn_a1_ln3_b': (0.0, 0.8),
     'L3_xattn_a1_li2_b': (0.0, 0.8),
     'L3_xattn_a1_li3_b': (0.0, 0.269),
     'L3_xattn_a2_li1_b': (0.0, 0.1),
     'L3_xattn_a2_lnx_g': (1.0, 0.6),
     'L3_xattn_a2_lnx_b': (0.0, 0.8),
     'L3_xattn_a2_lny_g': (1.0, 0.6),
     'L3_xattn_a2_lny_b': (0.0, 0.8),
     'L3_xattn_a2_ln3_g': (1.0, 0.6),
     'L3_xattn_a2_ln3_b': (0.0, 0.8),
     'L3_xattn_a2_li2_b': (0.0, 0.8),
     'L3_xattn_a2_li3_b': (0.0, 0.291)}
    factors = {'L0_ffn_w1': 8.0,
     'L0_ffn_w2': 8.0,
     'L0_ffn_w3': 8.0,
     'L0_ffn_new_w1': 6.205,
     'L0_ffn_new_w3': 6.378,
     'L0_ffn_gate_weight': 8.0,
     'L0_ffn_new_gate_weight': 8.0,
     'L1_ffn_wq': 8.0,
     'L1_ffn_wk': 8.0,
     'L1_ffn_router_w': 4.248,
     'L1_ffn_w1': 8.0,
     'L1_ffn_w2': 8.0,
     'L1_ffn_w3': 8.0,
     'L2_xattn_bo': 5.543,
     'L2_ffn_router_weight': 8.0,
     'L2_ffn_gate_w': 8.0,
     'L2_ffn_up_w': 8.0,
     'L2_ffn_down_w': 8.0,
     'L2_ffn_shared_gate_w': 8.0,
     'L2_ffn_shared_up_w': 8.0,
     'L2_ffn_shared_down_w': 8.0,
     'L3_attn_proj': 5.54,
     'L3_xattn_a1_wq': 8.0,
     'L3_xattn_a1_wk': 8.0,
     'L3_xattn_a1_wv': 3.289,
     'L3_xattn_a1_li1_w': 3.256,
     'L3_xattn_a1_li2_w': 2.98,
     'L3_xattn_a2_wq': 8.0,
     'L3_xattn_a2_wk': 8.0,
     'L3_xattn_a2_wv': 3.862,
     'L3_xattn_a2_li1_w': 4.132,
     'L3_xattn_a2_li2_w': 3.042,
     'L3_xattn_a2_li3_w': 2.95,
     'L3_ffn_mu_r': 8.0}
    for name, (base, spread) in spreads.items():
        noise = np.random.default_rng([zlib.crc32(name.encode()), seed]).standard_normal(out[name].shape)
        drawn = base * np.exp(spread * noise) if base else spread * noise
        out[name] = jnp.asarray(drawn.astype(out[name].dtype))
    for name, factor in factors.items():
        out[name] = (out[name] * factor).astype(out[name].dtype)
    return out
```

```python
from contextlib import ExitStack

import numpy as np
import concourse.bass as bass
from concourse import mybir
from concourse.alu_op_type import AluOpType as ALU

ACT = mybir.ActivationFunctionType
F32 = mybir.dt.float32
BF16 = mybir.dt.bfloat16
U32 = mybir.dt.uint32
AX_X = mybir.AxisListType.X

P = 128
B, S = 2, 512
TOK = B * S
NT = TOK // P
ST = S // P
HEADS = 16
SK = 77
CTX = 64
NEG = -1.0e30
ROUND = 1.5 * 2.0 ** 23


class Signal:

    def __init__(self, sem):
        self.sem, self.base, self.sent = sem, 0, 0

    def up(self):
        self.sent += 1
        return self.sem

    def at(self, n):
        return self.base + n


def width(pack):
    return sum(cols for _, _, cols in MATRICES[pack])


class Core:

    def __init__(self, nc, ctx):
        self.nc, self.ctx, self.counters = nc, ctx, {}

    def sb(self, name, shape, dt=F32):
        return self.ctx.enter_context(self.nc.sbuf_tensor(name, shape, dt))

    def ps(self, name, shape, dt=F32):
        return self.ctx.enter_context(self.nc.psum_tensor(name, shape, dt))

    def big1(self, a, n):
        return self.big[0][:, a:a + n]

    def big2(self, a, n):
        return self.big[1][:, a:a + n]

    def big3(self, a, n):
        return self.big[2][:, a:a + n]

    def m(self, name):
        return self.matrices[name]

    def row(self, name):
        i = row_names().index(name)
        return self.rows[:, i * P:(i + 1) * P]

    def col(self, name, n=1):
        at = 0
        for other, k in col_names():
            if other == name:
                return self.cols[:, at:at + n]
            at += k
        raise KeyError(name)

    def fetch(self, sp, pack):
        memory, at = self.memories[pack]
        n = width(pack)
        sp.dma_start(memory[:, at:at + n], self.dram[pack]).then_inc(self.loaded[pack], 16)

    def fetcher(self, *packs):
        def program(sp):
            for pack in packs:
                self.fetch(sp, pack)
        return program

    def await_loads(self, *packs):
        with self.nc.Block() as block:
            @block.sync
            def _(sp):
                for pack in packs:
                    sp.wait_ge(self.loaded[pack], 16)



def counter(c, name):
    if name not in c.counters:
        c.counters[name] = Signal(c.ctx.enter_context(c.nc.semaphore(name)))
    s = c.counters[name]
    s.base = s.sent
    return s


def seq(eng, step, ins):
    ins.then_inc(step.up(), 1)
    eng.wait_ge(step.sem, step.sent)



def row_names():
    return ["L0_attn_Wqkv_b", "L1_xattn_bv", "L1_xattn_bo", "L2_attn_bV", "L2_attn_bO",
            "L2_xattn_bo", "L3_attn_b_out", "L3_attn_gamma", "L3_attn_beta", "L3_attn_b2",
            "L3_xattn_ln1_g", "L3_xattn_ln1_b", "L3_xattn_ln2_g", "L3_xattn_ln2_b",
            "L3_xattn_a1_li1_b", "L3_xattn_a1_li3_b", "L3_xattn_a2_li1_b", "L3_xattn_a2_li3_b"]


def col_names():
    return [("L1_attn_gamma", 1), ("L1_attn_beta", 1), ("L1_attn_b_dt", 1), ("L1_attn_D_param", 1),
            ("L1_xattn_bq", 1), ("L1_xattn_bk", 1), ("L1_ffn_g1", 1), ("L1_ffn_g2", 1),
            ("L2_attn_bQ", 1), ("L2_attn_bK", 1), ("L3_attn_b1", 4),
            ("L3_xattn_a1_lnx_g", 1), ("L3_xattn_a1_lnx_b", 1), ("L3_xattn_a1_lny_g", 1),
            ("L3_xattn_a1_lny_b", 1), ("L3_xattn_a1_ln3_g", 1), ("L3_xattn_a1_ln3_b", 1),
            ("L3_xattn_a1_li2_b", 4), ("L3_xattn_a2_lnx_g", 1), ("L3_xattn_a2_lnx_b", 1),
            ("L3_xattn_a2_lny_g", 1), ("L3_xattn_a2_lny_b", 1), ("L3_xattn_a2_ln3_g", 1),
            ("L3_xattn_a2_ln3_b", 1), ("L3_xattn_a2_li2_b", 4), ("L3_ffn_mu_r", 1), ("L3_ffn_mu_k", 1)]


def chunks(n):
    return [(a, min(P, n - a)) for a in range(0, n, P)]


L0E, L0HID = 9, 352
L1E, L1HID = 8, 256
L2E, L2HID = 32, 64
MATRICES = {
    "first": [("L0_Wqkv", P, P), ("L0_Wo", P, P), ("L0_UT", 32, P), ("rope_q", P, 2 * ST * 4), ("rope_k", P, 2 * 64)],
    "early": [("L0x_WqT", P, P), ("L0x_WkvT", CTX, 2 * P), ("L0x_WoT", P, P), ("L0_gateT", P, L0E), ("gate_bias", P, L0E)],
    "moe0": [("w1T", P, L0E * L0HID), ("w3T", P, L0E * L0HID), ("w2T", P, L0E * 3 * P)],
    "const": [("ident", P, P), ("later", P, P), ("later_t", P, P), ("pick", 8, 4 * P), ("pick_id", 96, 32), ("pick_apart", P, P)],
    "mid": [("iota", P, 32), ("same_head", P, P), ("ctxT", CTX, B * SK), ("L1_WdtT", P, P), ("L1_WBT", P, 16), ("L1_WCT", P, 16), ("L1_A_log", P, 16),
            ("L1x_Wq", P, P), ("L1x_Wk", CTX, P), ("L1x_Wv", CTX, P), ("L1x_Wo", P, P),
            ("L1f_router", P, L1E), ("router_b", P, L1E),
            ("L2_WQ", P, P), ("L2_WK", P, P), ("L2_WV", P, P), ("L2_WO", P, P),
            ("L2_WQrT", 16, P), ("L2_WKrT", 16, P), ("L2_routerT", P, L2E), ("L2_bias", P, L2E)],
    "moe1": [("w1", P, L1E * L1HID), ("w2", P, L1E * L1HID), ("w3", P, L1E * 2 * P),
             ("wq", P, 1024), ("wk", P, 256), ("wv", P, 256), ("wo", P, 8 * P)],
    "turned": [("wqs", P, 1024), ("wks", P, 256), ("cos", P, S), ("sin", P, S)],
    "l2x": [("L2x_Wq", P, 1024), ("L2x_Wk", CTX, 1024), ("L2x_Wv", CTX, 1024), ("L2x_Wo", P, 8 * P)],
    "moe2": [("gateT", P, L2E * L2HID), ("upT", P, L2E * L2HID), ("downT", P, 16 * P),
             ("sgT", P, P), ("suT", P, P), ("sdT", P, P)],
    "l3": [("L3_wqkvT", P, 3 * P), ("L3_proj", P, 4 * P), ("L3_woutT", P, P), ("L3_w1T", P, 4 * P),
           ("L3_w2T", P, 4 * P), ("L3f_WrT", P, P), ("L3f_WkT", P, P), ("L3f_WvT", P, P),
           ("block_kv", P, 36)],
    "l3x": [(f"a{i}_{n}", r, c) for i in (1, 2) for n, r, c in
            (("wq", P, 512), ("wk", P if i == 1 else CTX, 512), ("wv", P if i == 1 else CTX, 512),
             ("li1", P, 4 * P), ("li2", P, 4 * P), ("li3", P, 4 * P))],
}



def matmul_stream(c, units, load=None):
    nc = c.nc
    product_ready, act_freed, dve_freed = counter(c, "product_ready"), counter(c, "act_freed"), counter(c, "dve_freed")
    dve_step = counter(c, "dve_step")
    freed = []
    count = {"act": 0, "dve": 0}
    for u in units:
        count[u[3]] += 1
        freed.append((u[3], count[u[3]]))

    def bank(u):
        return c.bank[u % 8][0:units[u][1], 0:units[u][2]]

    with nc.Block() as block:
        if load:
            block.sync(load)

        @block.tensor
        def _(pe):
            for u, (products, _, _, _, _) in enumerate(units):
                if u >= 8:
                    who, n = freed[u - 8]
                    s = act_freed if who == "act" else dve_freed
                    pe.wait_ge(s.sem, s.at(n))
                for k, (lhsT, rhs) in enumerate(products):
                    last = nc.tensor.matmul(bank(u), lhsT, rhs, start=(k == 0), stop=(k == len(products) - 1))
                last.then_inc(product_ready.up(), 1)

        @block.scalar
        def _(act):
            for u, unit in enumerate(units):
                if unit[3] == "act":
                    act.wait_ge(product_ready.sem, product_ready.at(u + 1))
                    unit[4](act, bank(u)).then_inc(act_freed.up(), 1)

        @block.vector
        def _(dve):
            for u, unit in enumerate(units):
                if unit[3] == "dve":
                    dve.wait_ge(product_ready.sem, product_ready.at(u + 1))
                    unit[4](dve, bank(u), dve_step).then_inc(dve_freed.up(), 1)


def act_copy(c, dst, bias=None, scale=1.0, func=None):
    def emit(act, bank):
        if bias is None and func is None and isinstance(scale, float):
            return c.nc.scalar.copy(dst, bank)
        return c.nc.scalar.activation(dst, bank, func or ACT.Identity, bias=0.0 if bias is None else bias, scale=scale)
    return emit


def dve_copy(c, dst, bias=None, row=None):
    def emit(dve, bank, step):
        if row is not None:
            return c.nc.vector.tensor_tensor(dst, bank, row, ALU.add)
        if bias is not None:
            return c.nc.vector.tensor_scalar(dst, bank, bias, None, ALU.add)
        return c.nc.vector.tensor_copy(dst, bank)
    return emit


def halves(c, products, rows, dst, bias=None, first="act"):
    other = "dve" if first == "act" else "act"
    out = []
    for half, who in ((0, first), (1, other)):
        d = dst[:, half * S:(half + 1) * S]
        emit = act_copy(c, d, bias=bias) if who == "act" else dve_copy(c, d, bias=bias)
        out.append((products(half), rows, S, who, emit))
    return out


def add_and_norm(c, add=None, bias=None, base=None, total=None, norm="ln", eps=1e-5, out=None, rows=None,
                 turned=(), load=None, store=None):
    nc = c.nc
    base = c.X if base is None else base
    total = base if total is None else total
    sum_ready, sum_used, stats_ready, rstd_ready = (counter(c, n) for n in ("sum_ready", "sum_used", "stats_ready", "rstd_ready"))
    norm_ready, turned_ready, turned_used, stored = (counter(c, n) for n in ("norm_ready", "turned_ready", "turned_used", "stored"))
    dve_step, pool_step = counter(c, "dve_step"), counter(c, "pool_step")
    stats, mv, rstd = c.stats, c.mv, c.rstd
    H = NT // 2

    with nc.Block() as block:
        if load:
            block.sync(load)

        @block.tensor
        def _(pe):
            if add:
                for t in range(NT):
                    last = add(pe, t, c.bank[t // H][:, t % H * P:(t % H + 1) * P])
                    if t % H == H - 1:
                        last.then_inc(sum_ready.up(), 1)
            if turned:
                for half in range(2):
                    pe.wait_ge(norm_ready.sem, norm_ready.at(half + 1))
                    for k in range(H):
                        last = nc.tensor.transpose(c.bank[2 + half][:, k * P:(k + 1) * P], out[:, half * H + k, :], c.ident[:])
                    last.then_inc(turned_ready.up(), 1)

        @block.vector
        def _(dve):
            for half in range(2):
                ts = slice(half * H, (half + 1) * H)
                if add:
                    dve.wait_ge(sum_ready.sem, sum_ready.at(half + 1))
                    psum = c.bank[half][:, :].rearrange("p (t f) -> p t f", t=H)
                    seq(dve, dve_step, nc.vector.tensor_tensor(total[:, ts, :], psum, base[:, ts, :], ALU.add))
                    if bias is not None:
                        seq(dve, dve_step, nc.vector.tensor_tensor(
                            total[:, ts, :], total[:, ts, :], bias.unsqueeze(1).broadcast_to([P, H, P]), ALU.add))
                if norm is None:
                    continue
                for k in range(half * H, (half + 1) * H):
                    last = nc.vector.bn_stats(stats[:, k, :], total[:, k, :])
                seq(dve, dve_step, last)
                for k in range(half * H, (half + 1) * H):
                    last = nc.vector.bn_aggr(mv[:, k, :], stats[:, k, :])
                seq(dve, dve_step, last)
                if norm == "rms":
                    seq(dve, dve_step, nc.vector.tensor_tensor(mv[:, ts, 0], mv[:, ts, 0], mv[:, ts, 0], ALU.mult))
                    seq(dve, dve_step, nc.vector.tensor_tensor(mv[:, ts, 1], mv[:, ts, 1], mv[:, ts, 0], ALU.add))
                nc.vector.tensor_scalar(mv[:, ts, 1], mv[:, ts, 1], eps, None, ALU.add).then_inc(stats_ready.up(), 1)
            if norm is None:
                return
            for half in range(2):
                ts = slice(half * H, (half + 1) * H)
                dve.wait_ge(rstd_ready.sem, rstd_ready.at(half + 1))
                for k in range(half * H, (half + 1) * H):
                    if norm == "rms":
                        last = nc.vector.tensor_scalar(out[:, k, :], total[:, k, :], rstd[:, k:k + 1], None, ALU.mult)
                    else:
                        last = nc.vector.tensor_scalar(out[:, k, :], total[:, k, :], mv[:, k, 0:1], rstd[:, k:k + 1],
                                                       ALU.subtract, ALU.mult)
                if rows:
                    g, b = (r.unsqueeze(1).broadcast_to([P, H, P]) for r in rows)
                    seq(dve, dve_step, last)
                    seq(dve, dve_step, nc.vector.tensor_tensor(out[:, ts, :], out[:, ts, :], g, ALU.mult))
                    last = nc.vector.tensor_tensor(out[:, ts, :], out[:, ts, :], b, ALU.add)
                last.then_inc(norm_ready.up(), 1)

        @block.gpsimd
        def _(pool):
            if norm is None:
                return
            for half in range(2):
                pool.wait_ge(stats_ready.sem, stats_ready.at(half + 1))
                nc.gpsimd.tensor_tensor(rstd[:, half * H:(half + 1) * H], mv[:, half * H:(half + 1) * H, 1],
                                        c.minus_half[:, 0:H], ALU.pow).then_inc(rstd_ready.up(), 1)

        @block.scalar
        def _(act):
            for half in range(2 if turned else 0):
                act.wait_ge(turned_ready.sem, turned_ready.at(half + 1))
                for dst, scale, b in turned:
                    d = dst[:, half * S:(half + 1) * S]
                    if scale is None:
                        nc.scalar.copy(d, c.bank[2 + half][:, :])
                    else:
                        nc.scalar.activation(d, c.bank[2 + half][:, :], ACT.Identity, bias=0.0 if b is None else b, scale=scale)
            if store is not None:
                for half in range(2):
                    act.wait_ge(norm_ready.sem, norm_ready.at(half + 1))
                    act.dma_start(store[:, half * H:(half + 1) * H, :], out[:, half * H:(half + 1) * H, :]).then_inc(c.stored, 16)
                act.wait_ge(c.stored, 32)


def turn(c, src, ntiles, cols, dst):
    nc = c.nc
    turned_ready, act_freed, dve_freed = counter(c, "turned_ready"), counter(c, "act_freed"), counter(c, "dve_freed")
    units = [(k, t) for k in range(cols // P) for t in range(0, ntiles, 4)]

    with nc.Block() as block:
        @block.tensor
        def _(pe):
            for u, (k, t) in enumerate(units):
                if u >= 8:
                    s = dve_freed if u % 2 else act_freed
                    pe.wait_ge(s.sem, s.at((u - 8) // 2 + 1))
                for i in range(4):
                    last = nc.tensor.transpose(c.bank[u % 8][:, i * P:(i + 1) * P], src[:, t + i, k * P:(k + 1) * P], c.ident[:])
                last.then_inc(turned_ready.up(), 1)

        @block.scalar
        def _(act):
            for u, (k, t) in enumerate(units):
                if u % 2 == 0:
                    act.wait_ge(turned_ready.sem, turned_ready.at(u + 1))
                    nc.scalar.copy(dst[:, k, t * P:(t + 4) * P], c.bank[u % 8][:, :]).then_inc(act_freed.up(), 1)

        @block.vector
        def _(dve):
            for u, (k, t) in enumerate(units):
                if u % 2:
                    dve.wait_ge(turned_ready.sem, turned_ready.at(u + 1))
                    nc.vector.tensor_copy(dst[:, k, t * P:(t + 4) * P], c.bank[u % 8][:, :]).then_inc(dve_freed.up(), 1)


def attention(c, key_tiles, dk, qop, kop, vop, scale, Y, mask=None, load=None):
    nc = c.nc
    G = 4
    W = 32 if dk == 8 else 64 if dk == 32 else P
    M = dk + 1
    HB = P // W
    NSC, NOV = (2, 2) if W == P else (3, 1)
    LAG = NSC - 1
    nkt = len(key_tiles)
    klen = sum(key_tiles)
    groups = [(b, h) for b in range(B) for h in range(0, HEADS, G)]
    steps = [(g, jb, i, jj) for g in range(len(groups)) for jb in range(G // HB) for i in range(nkt) for jj in range(HB)]
    per_group = G * nkt
    per_bank = HB * nkt
    packed = 4 * klen <= S
    tiles_of_unit = [list(range(ST))] if packed else [[t] for t in range(ST)]
    units = [(j, tl) for j in range(G) for tl in tiles_of_unit]
    assert len(units) == per_group
    SA, SC = c.bank[0:2], c.bank[2:2 + NSC]
    OV = c.bank[2 + NSC:2 + NSC + NOV]
    TR = c.bank[6]
    NB = c.bank_bf
    (raw_ready, max_ready, negmax_ready, negmax_turned, negmax_moved, score_ready, exp_ready, value_ready,
     out_moved, out_turned, out_normed, masked_ready, cleared, dve_step) = (counter(c, n) for n in (
         "raw_ready", "max_ready", "negmax_ready", "negmax_turned", "negmax_moved", "score_ready", "exp_ready",
         "value_ready", "out_moved", "out_turned", "out_normed", "masked_ready", "cleared", "dve_step"))
    E, OT, MX, RC = c.E, c.OT, c.MX, c.RC
    apart = dk == 32
    R = P if apart else 2 * G
    if apart:
        NM = c.NM.rearrange("p z t (j r) -> p z t r j", j=G)
        hi_of, lo_of = (lambda z: NM[:, z, :, 0, :]), (lambda z: NM[:, z, :, 1, :])
        pick_of = lambda j, z, ks, n0: (c.pick_apart[32 * j:32 * j + 32, 0:ks], c.NMT[32 * j:32 * j + 32, z, n0:S])
    else:
        hi_of, lo_of = (lambda z: c.NM[:, z, :, 0:G]), (lambda z: c.NM[:, z, :, G:2 * G])
        pick_of = lambda j, z, ks, n0: (c.pick[:, j, 0:ks], c.NMT[0:2 * G, z, n0:S])
    rows_of = M if W == P else P
    nbanks = len(steps) // per_bank

    def start(i):
        return i * P if mask == "causal" else 0

    def raw_scores(pe, g, u):
        n = g * per_group + u
        j, tl = units[u]
        b, h = groups[g][0], groups[g][1] + j
        if n >= 2:
            pe.wait_ge(max_ready.sem, max_ready.at(n - 1))
        for k, t in enumerate(tl):
            last_key = (t + 1) * P if mask == "causal" else klen
            q, kk = qop(b, h), kop(b, h)
            dst = SA[n % 2][:, k * klen:k * klen + last_key]
            for x in range(len(q)):
                last = nc.tensor.matmul(dst, q[x][:, t * P:(t + 1) * P], c.keys(kk[x], 0, last_key),
                                        start=(x == 0), stop=(x == len(q) - 1 and mask != "causal"))
            if mask == "causal":
                last = nc.tensor.matmul(dst, c.ident_bf[:], c.after_query[:, S - last_key:S], start=False, stop=True)
        last.then_inc(raw_ready.up(), 1)

    def turn_negmax(pe, g):
        pe.wait_ge(negmax_ready.sem, negmax_ready.at(g + 1))
        if g >= 1:
            pe.wait_ge(negmax_moved.sem, negmax_moved.at(g))
        for t in range(ST):
            last = nc.tensor.transpose(NB[0:R, t * P:(t + 1) * P], c.NM[:, g % 2, t, 0:R], c.ident_bf[:])
        last.then_inc(negmax_turned.up(), 1)

    def scores(pe, t):
        g, jb, i, jj = steps[t]
        b, j = groups[g][0], jb * HB + jj
        h, ks, n0 = groups[g][1] + j, key_tiles[i], start(i)
        if t >= NSC:
            pe.wait_ge(exp_ready.sem, exp_ready.at(t - NSC + 1))
        if t % per_group == 0:
            pe.wait_ge(negmax_moved.sem, negmax_moved.at(g + 1))
        dst = SC[t % NSC][0:ks, n0:S]
        q, kk = qop(b, h), kop(b, h)
        for x in range(len(q)):
            nc.tensor.matmul(dst, c.keys(kk[x], i * P, i * P + ks), q[x][:, n0:S], start=(x == 0), stop=False)
        last = nc.tensor.matmul(dst, *pick_of(j, g % 2, ks, n0), start=False, stop=(mask != "causal"))
        if mask == "causal":
            last = nc.tensor.matmul(dst, c.ident_bf[:], c.before_key[:, 0:S - n0], start=False, stop=True)
        last.then_inc(score_ready.up(), 1)

    def values(pe, t):
        g, jb, i, jj = steps[t]
        b, h, ks, n0 = groups[g][0], groups[g][1] + jb * HB + jj, key_tiles[i], start(i)
        n = t // per_bank
        pe.wait_ge(exp_ready.sem, exp_ready.at(t + 1))
        if t % per_bank == 0 and n >= NOV:
            pe.wait_ge(out_moved.sem, out_moved.at(n - NOV + 1))
        if t == 0:
            pe.wait_ge(cleared.sem, cleared.at(1))
        dst = OV[n % NOV][W * jj:W * jj + M, :]
        e = E[t % c.NE]
        if mask == "future":
            if i < nkt - 1:
                nc.tensor.matmul(dst, c.only_ones[:, 0:M], e[0:ks, 0:S], start=(i == 0), stop=False, skip_group_check=True)
            if i:
                nc.tensor.matmul(dst[:, 0:i * P], vop(b, h, i), e[0:ks, 0:i * P], start=False, stop=False, skip_group_check=True)
            pe.wait_ge(masked_ready.sem, masked_ready.at(t + 1))
            last = nc.tensor.matmul(dst[:, i * P:(i + 1) * P], vop(b, h, i), c.EM[t % c.NE], start=False,
                                    stop=False, skip_group_check=True)
            if i == nkt - 1:
                last = nc.tensor.matmul(dst, c.only_ones[:, 0:M], e[0:ks, 0:S], start=False, stop=True, skip_group_check=True)
        else:
            last = nc.tensor.matmul(dst[:, n0:S], vop(b, h, i), e[0:ks, n0:S], start=(i == 0), stop=(i == nkt - 1),
                                    skip_group_check=True)
        last.then_inc(value_ready.up(), 1)

    def turn_out(pe, n):
        pe.wait_ge(out_moved.sem, out_moved.at(n + 1))
        if n >= 1:
            pe.wait_ge(out_normed.sem, out_normed.at(n))
        for t in range(ST):
            last = nc.tensor.transpose(TR[:, t * rows_of:(t + 1) * rows_of], OT[0:rows_of, n % 2, t * P:(t + 1) * P],
                                       c.ident[0:rows_of, 0:rows_of])
        last.then_inc(out_turned.up(), 1)

    with nc.Block() as block:
        if load:
            block.sync(load)

        @block.tensor
        def _(pe):
            for u in range(per_group):
                raw_scores(pe, 0, u)
            turn_negmax(pe, 0)
            for t in range(len(steps) + LAG + 2):
                g, u = t // per_group, t % per_group
                if t < len(steps):
                    if u == 0 and g >= 1:
                        turn_negmax(pe, g)
                    scores(pe, t)
                    if g + 1 < len(groups):
                        raw_scores(pe, g + 1, u)
                if 0 <= t - LAG < len(steps):
                    values(pe, t - LAG)
                d = t - LAG - 2
                if d >= 0 and d % per_bank == per_bank - 1:
                    turn_out(pe, d // per_bank)

        def move_out(act, n):
            act.wait_ge(value_ready.sem, value_ready.at((n + 1) * per_bank))
            if n >= 2:
                act.wait_ge(out_turned.sem, out_turned.at(n - 1))
            nc.scalar.copy(OT[0:rows_of, n % 2, :], OV[n % NOV][0:rows_of, :]).then_inc(out_moved.up(), 1)

        @block.scalar
        def _(act):
            for t in range(len(steps) + LAG):
                if t < len(steps) and t % per_group == 0:
                    g = t // per_group
                    act.wait_ge(negmax_turned.sem, negmax_turned.at(g + 1))
                    nc.scalar.copy(c.NMT[0:R, g % 2, :], NB[0:R, :]).then_inc(negmax_moved.up(), 1)
                d = t - LAG - 1
                if d >= 0 and d % per_bank == per_bank - 1:
                    move_out(act, d // per_bank)
                if t >= len(steps):
                    continue
                g, jb, i, jj = steps[t]
                ks, n0 = key_tiles[i], start(i)
                act.wait_ge(score_ready.sem, score_ready.at(t + 1))
                if t >= c.NE:
                    act.wait_ge(value_ready.sem, value_ready.at(t - c.NE + 1))
                nc.scalar.activation(E[t % c.NE][0:ks, n0:S], SC[t % NSC][0:ks, n0:S], ACT.Exp,
                                     scale=scale).then_inc(exp_ready.up(), 1)
            move_out(act, nbanks - 1)

        @block.vector
        def _(dve):
            if W < P:
                nc.vector.memset(OV[0][:, :], 0.0).then_inc(cleared.up(), 1)
            else:
                nc.vector.memset(RC[:, 0, :, :], 0.0).then_inc(cleared.up(), 1)
            done = 0

            def reduce_max(g, u):
                j, tl = units[u]
                n = g * per_group + u
                dve.wait_ge(raw_ready.sem, raw_ready.at(n + 1))
                if len(tl) > 1:
                    src = SA[n % 2][:, 0:ST * klen].rearrange("p (t m) -> p t m", t=ST)
                    dst = MX[:, :, j]
                else:
                    last_key = (tl[0] + 1) * P if mask == "causal" else klen
                    src, dst = SA[n % 2][:, 0:last_key], MX[:, tl[0], j:j + 1]
                nc.vector.tensor_reduce(dst, src, AX_X, ALU.max).then_inc(max_ready.up(), 1)

            def negmax(g):
                dve.wait_ge(max_ready.sem, max_ready.at((g + 1) * per_group))
                if g >= 2:
                    dve.wait_ge(negmax_turned.sem, negmax_turned.at(g - 1))
                hi, lo = hi_of(g % 2), lo_of(g % 2)
                seq(dve, dve_step, nc.vector.tensor_scalar(hi, MX[:], -1.0, None, ALU.mult))
                nc.vector.scalar_tensor_tensor(out=lo, in0=MX[:], scalar=-1.0, in1=hi, op0=ALU.mult,
                                               op1=ALU.subtract).then_inc(negmax_ready.up(), 1)

            def norm_out(n):
                dve.wait_ge(out_turned.sem, out_turned.at(n + 1))
                b, h = groups[n * HB // G][0], groups[n * HB // G][1] + n * HB % G
                tr = TR[:, 0:ST * rows_of].rearrange("p (t r) -> p t r", t=ST)
                if W < P:
                    tr = tr.rearrange("p t (j w) -> p t j w", j=HB)
                else:
                    tr = tr.unsqueeze(2)
                seq(dve, dve_step, nc.vector.reciprocal(RC[:, n % 2, :, 0:HB], tr[:, :, :, dk]))
                dst = Y[:, b * ST:(b + 1) * ST, h * dk:(h + HB) * dk].rearrange("p t (j d) -> p t j d", j=HB)
                nc.vector.tensor_tensor(dst, tr[:, :, :, 0:dk], RC[:, n % 2, :, 0:HB].unsqueeze(3).broadcast_to([P, ST, HB, dk]),
                                        ALU.mult).then_inc(out_normed.up(), 1)

            for u in range(per_group):
                reduce_max(0, u)
            negmax(0)
            for t in range(len(steps) + LAG + 2):
                g, u = t // per_group, t % per_group
                if g + 1 < len(groups):
                    reduce_max(g + 1, u)
                    if u == per_group - 1:
                        negmax(g + 1)
                d = t - LAG - 2
                if d >= 0 and d % per_bank == per_bank - 1:
                    norm_out(d // per_bank)

        if mask == "future":
            @block.gpsimd
            def _(pool):
                for t, (g, jb, i, jj) in enumerate(steps):
                    pool.wait_ge(exp_ready.sem, exp_ready.at(t + 1))
                    if t >= c.NE:
                        pool.wait_ge(value_ready.sem, value_ready.at(t - c.NE + 1))
                    nc.gpsimd.tensor_tensor(c.EM[t % c.NE], E[t % c.NE][:, i * P:(i + 1) * P], c.key_later[:],
                                            ALU.mult).then_inc(masked_ready.up(), 1)


def split_heads(c, qT, kT, ktok):
    nc = c.nc
    parts_ready, parts_stored, heads_loaded, dve_step = (counter(c, n) for n in ("parts_ready", "parts_stored", "heads_loaded", "dve_step"))
    pool_step = counter(c, "pool_step")
    Q_PARTS, K_PARTS = (0, 0, 1, 1, 0, 2), (0, 1, 0, 1, 2, 0)
    qp, kp = c.q_parts, c.k_parts[:, :, 0:ktok]
    both = kT is not None

    def split(eng, e, step, src, parts, rest):
        seq(eng, step, e.tensor_copy(parts[:, 0, :], src))
        seq(eng, step, e.tensor_tensor(rest, src, parts[:, 0, :], ALU.subtract))
        seq(eng, step, e.tensor_copy(parts[:, 1, :], rest))
        seq(eng, step, e.tensor_tensor(rest, rest, parts[:, 1, :], ALU.subtract))
        return e.tensor_copy(parts[:, 2, :], rest)

    with nc.Block() as block:
        @block.vector
        def _(dve):
            split(dve, nc.vector, dve_step, qT, qp, c.rest_q).then_inc(parts_ready.up(), 1)
            if both and ktok > P * 2:
                split(dve, nc.vector, dve_step, kT, kp, c.rest_k[:, 0:ktok]).then_inc(parts_ready.up(), 1)

        @block.gpsimd
        def _(pool):
            if both and ktok <= P * 2:
                split(pool, nc.gpsimd, pool_step, kT, kp, c.rest_k[:, 0:ktok]).then_inc(parts_ready.up(), 1)

        @block.sync
        def _(sp):
            sp.wait_ge(parts_ready.sem, parts_ready.at(1 + both))
            sp.dma_start(c.q_dram, qp).then_inc(c.stored_parts, 16)
            if both:
                sp.dma_start(c.k_dram[:, :, 0:ktok], kp).then_inc(c.stored_parts, 16)
            c.nparts += 16 * (1 + both)
            sp.wait_ge(c.stored_parts, c.nparts)
            for s in range(6):
                sp.dma_start(c.QH[8 * s:8 * s + 8], c.q_dram[:, Q_PARTS[s], :].rearrange("(h d) t -> d h t", d=8)).then_inc(c.loaded_heads, 16)
                c.nheads += 16
                if both:
                  sp.dma_start(c.KH[8 * s:8 * s + 8, :, 0:ktok], c.k_dram[:, K_PARTS[s], 0:ktok].rearrange("(h d) t -> d h t", d=8)).then_inc(c.loaded_heads, 16)
                  c.nheads += 16
            sp.wait_ge(c.loaded_heads, c.nheads)


def stack_keys(c, src):
    nc, step = c.nc, counter(c, "dve_step")
    stacked_ready, turned_ready, act_freed, dve_freed = (counter(c, n) for n in ("stacked_ready", "turned_ready", "act_freed", "dve_freed"))
    stack = c.key_stack
    flat = src.rearrange("p x i d -> p (x i) d")
    rest = c.total[:].rearrange("p t (u d) -> p (t u) d", d=8)
    slot = lambda z: stack[:, :, z, :]
    KH = c.KH.rearrange("p h t -> p (h t)")

    with nc.Block() as block:
        @block.vector
        def _(dve):
            seq(dve, step, nc.vector.tensor_copy(slot(0), flat))
            nc.vector.tensor_copy(slot(2), slot(0))
            nc.vector.tensor_copy(slot(5), slot(0))
            seq(dve, step, nc.vector.tensor_tensor(rest, flat, slot(0), ALU.subtract))
            seq(dve, step, nc.vector.tensor_copy(slot(1), rest))
            nc.vector.tensor_copy(slot(3), slot(1))
            seq(dve, step, nc.vector.tensor_tensor(rest, rest, slot(1), ALU.subtract))
            nc.vector.tensor_copy(slot(4), rest).then_inc(stacked_ready.up(), 1)
            for u in range(1, B * HEADS, 2):
                dve.wait_ge(turned_ready.sem, turned_ready.at(u + 1))
                nc.vector.tensor_copy(KH[0:48, u * S:(u + 1) * S], c.banks_bf[u % 8][0:48, 0:S]).then_inc(dve_freed.up(), 1)

        @block.tensor
        def _(pe):
            pe.wait_ge(stacked_ready.sem, stacked_ready.at(1))
            for u in range(B * HEADS):
                if u >= 8:
                    s = dve_freed if u % 2 else act_freed
                    pe.wait_ge(s.sem, s.at((u - 8) // 2 + 1))
                for i in range(ST):
                    last = nc.tensor.transpose(c.banks_bf[u % 8][0:48, i * P:(i + 1) * P],
                                               stack[:, u * ST + i, :, :].rearrange("p z d -> p (z d)"), c.ident_bf[:])
                last.then_inc(turned_ready.up(), 1)

        @block.scalar
        def _(act):
            for u in range(0, B * HEADS, 2):
                act.wait_ge(turned_ready.sem, turned_ready.at(u + 1))
                nc.scalar.copy(KH[0:48, u * S:(u + 1) * S], c.banks_bf[u % 8][0:48, 0:S]).then_inc(act_freed.up(), 1)


def quantise(c, src, dst_bf, amax):
    nc, step = c.nc, counter(c, "dve_step")
    t1, r7 = c.total, c.rstd

    with nc.Block() as block:
        @block.vector
        def _(dve):
            seq(dve, step, nc.vector.tensor_reduce(amax, src, AX_X, ALU.max, apply_absolute_value=True))
            seq(dve, step, nc.vector.tensor_scalar(amax, amax, 1e-6, None, ALU.max))
            seq(dve, step, nc.vector.reciprocal(r7[:], amax))
            for t in range(NT):
                last = nc.vector.tensor_scalar(t1[:, t, :], src[:, t, :], r7[:, t:t + 1], 7.0, ALU.mult, ALU.mult)
            seq(dve, step, last)
            seq(dve, step, nc.vector.tensor_scalar(t1[:], t1[:], ROUND, ROUND - 8.0, ALU.add, ALU.max))
            seq(dve, step, nc.vector.tensor_scalar(dst_bf, t1[:], ROUND, 7.0, ALU.subtract, ALU.min))
            seq(dve, step, nc.vector.tensor_scalar(amax, amax, 1.0 / 7.0, None, ALU.mult))


def ternary(c, w, signT, alpha):
    nc, step = c.nc, counter(c, "dve_step")
    rows_ready, total_ready, sign_ready, sign_turned = (counter(c, n) for n in ("tern_rows", "tern_total", "tern_sign", "tern_turned"))
    row, thr, m1, m2 = c.small[:, 0:1], c.small[:, 1:3], c.tern[:, 0, :], c.tern[:, 1, :]
    diag = c.total[:, 0, :]

    with nc.Block() as block:
        @block.vector
        def _(dve):
            seq(dve, step, nc.vector.tensor_reduce(row, w, AX_X, ALU.add, apply_absolute_value=True))
            seq(dve, step, nc.vector.tensor_scalar(row, row, 1.0 / P, None, ALU.mult))
            nc.vector.tensor_scalar(diag, c.ident[:], row, None, ALU.mult).then_inc(rows_ready.up(), 1)
            dve.wait_ge(total_ready.sem, total_ready.at(1))
            nc.vector.tensor_copy(alpha, c.bank[1][:, 0:P])
            nc.vector.tensor_scalar(thr[:, 0:1], c.bank[0][:, 0:1], 0.05 / P, None, ALU.mult)
            seq(dve, step, nc.vector.tensor_scalar(thr[:, 1:2], c.bank[0][:, 0:1], -0.05 / P, None, ALU.mult))
            nc.vector.tensor_scalar(m1, w, thr[:, 0:1], None, ALU.is_ge)
            seq(dve, step, nc.vector.tensor_scalar(m2, w, thr[:, 1:2], None, ALU.is_le))
            nc.vector.tensor_tensor(m1, m1, m2, ALU.subtract).then_inc(sign_ready.up(), 1)
            dve.wait_ge(sign_turned.sem, sign_turned.at(1))
            nc.vector.tensor_copy(signT, c.bank_bf[:, 0:P])

        @block.tensor
        def _(pe):
            pe.wait_ge(rows_ready.sem, rows_ready.at(1))
            nc.tensor.matmul(c.bank[0][:, 0:1], c.ones[:], row, start=True, stop=True)
            nc.tensor.matmul(c.bank[1][:, 0:P], c.ones[:], diag, start=True, stop=True).then_inc(total_ready.up(), 1)
            pe.wait_ge(sign_ready.sem, sign_ready.at(1))
            nc.tensor.transpose(c.bank_bf[:, 0:P], m1, c.ident_bf[:]).then_inc(sign_turned.up(), 1)


def turn_quantised(c, q_bf, qT_bf):
    nc = c.nc
    turned_ready, act_freed = counter(c, "turned_ready"), counter(c, "act_freed")
    with nc.Block() as block:
        @block.tensor
        def _(pe):
            for half in range(2):
                if half:
                    pe.wait_ge(act_freed.sem, act_freed.at(1))
                for k in range(4):
                    last = nc.tensor.transpose(c.bank_bf[:, k * P:(k + 1) * P], q_bf[:, half * 4 + k, :], c.ident_bf[:])
                last.then_inc(turned_ready.up(), 1)

        @block.scalar
        def _(act):
            for half in range(2):
                act.wait_ge(turned_ready.sem, turned_ready.at(half + 1))
                nc.scalar.copy(qT_bf[:, half * S:(half + 1) * S], c.bank_bf[:, 0:S]).then_inc(act_freed.up(), 1)


def quantised_product(c, qT_bf, signT, amax, alpha, bias, dst):
    nc, step = c.nc, counter(c, "dve_step")
    product_ready = counter(c, "product_ready")
    with nc.Block() as block:
        @block.tensor
        def _(pe):
            for t in range(NT):
                nc.tensor.matmul(c.bank[t][:, 0:P], qT_bf[:, t * P:(t + 1) * P], signT,
                                 start=True, stop=True).then_inc(product_ready.up(), 1)

        @block.vector
        def _(dve):
            for t in range(NT):
                dve.wait_ge(product_ready.sem, product_ready.at(t + 1))
                last = nc.vector.scalar_tensor_tensor(out=dst[:, t, :], in0=c.bank[t][:, 0:P],
                                                      scalar=amax[:, t:t + 1], in1=alpha, op0=ALU.mult, op1=ALU.mult)
            if bias is not None:
                seq(dve, step, last)
                nc.vector.tensor_tensor(dst, dst, bias.unsqueeze(1).broadcast_to([P, NT, P]), ALU.add)


def attention_8(c, key_tiles, dst, scale, chunked=False):
    single = len(key_tiles) == 1

    def qop(b, h):
        return [c.QH[0:48, h, b * S:(b + 1) * S]]

    def kop(b, h):
        if chunked:
            x = (b * HEADS + h) * S
            return [c.KH[0:48].rearrange("p h t -> p (h t)")[:, x:x + S]]
        n = SK if single else S
        return [c.KH[0:48, h, b * n:(b + 1) * n]]

    def vop(b, h, i):
        if chunked:
            return c.VH[:, (b * HEADS + h) * 36 + i * 9:(b * HEADS + h) * 36 + i * 9 + 9]
        if single:
            return c.VH[0:SK, (b * HEADS + h) * 9:(b * HEADS + h) * 9 + 9]
        x = ((b * ST + i) * HEADS + h) * 9
        return c.VH[:, x:x + 9]

    attention(c, key_tiles, 8, qop, kop, vop, scale, dst)


def block_product(c, aT, bT, dst):
    nc = c.nc
    product_ready = counter(c, "product_ready")
    with nc.Block() as block:
        @block.tensor
        def _(pe):
            nc.tensor.matmul(c.bank[0][:, 0:P], aT, bT, start=True, stop=True).then_inc(product_ready.up(), 1)

        @block.vector
        def _(dve):
            dve.wait_ge(product_ready.sem, product_ready.at(1))
            nc.vector.tensor_tensor(dst, c.bank[0][:, 0:P], c.m("same_head"), ALU.mult)


def project_out(c, srcT, w, k=1):
    def add(pe, t, psum):
        for i in range(k):
            last = c.nc.tensor.matmul(psum, srcT[:, i, t * P:(t + 1) * P], w[:, i * P:(i + 1) * P],
                                      start=(i == 0), stop=(i == k - 1))
        return last
    return add


def turn_back(c, srcT):
    def add(pe, t, psum):
        return c.nc.tensor.transpose(psum, srcT[:, t * P:(t + 1) * P], c.ident[:])
    return add



def layer0_attention(c):
    nc = c.nc
    amax = c.amax
    proj = c.Y8
    ternary(c, c.m("L0_Wqkv"), c.signT[:, 0, :], c.alpha[:, 0, :])
    ternary(c, c.m("L0_Wo"), c.signT[:, 1, :], c.alpha[:, 1, :])
    block_product(c, c.m("L0_UT")[0:32], c.m("L0_UT")[0:32], c.headmat)
    quantise(c, c.X[:], c.q_bf[:], amax)
    turn_quantised(c, c.q_bf, c.qT_bf)
    quantised_product(c, c.qT_bf[:], c.signT[:, 0, :], amax, c.alpha[:, 0, :], c.row("L0_attn_Wqkv_b"), proj[:])

    step = counter(c, "dve_step")
    pool_step = counter(c, "pool_step")
    with nc.Block() as block:
        @block.vector
        def _(dve):
            p5 = proj.rearrange("p t (h i two) -> p t h i two", h=HEADS, two=2)
            for name, dst in (("q", c.XN), ("k", c.total)):
                d = dst[:].rearrange("p t (h z i) -> p t h z i", h=HEADS, z=2)
                tmp = c.rest2[:, 0:64].rearrange("p (h i) -> p h i", h=HEADS)
                for t in range(NT):
                    if name == "q":
                        tab = c.m("rope_q").rearrange("p (z t i) -> p z t i", z=2, t=ST)
                        cos, sin = (tab[:, z, t % ST, :].unsqueeze(1).broadcast_to([P, HEADS, 4]) for z in range(2))
                    else:
                        tab = c.m("rope_k").rearrange("p (z h i) -> p z h i", z=2, h=HEADS)
                        cos, sin = tab[:, 0], tab[:, 1]
                    t1, t2 = p5[:, t, :, :, 0], p5[:, t, :, :, 1]
                    a, b = c.rest2[:, 0:64].rearrange("p (h i) -> p h i", h=HEADS), c.rest2[:, 64:128].rearrange("p (h i) -> p h i", h=HEADS)
                    seq(dve, step, nc.vector.tensor_tensor(a, t2, sin, ALU.mult))
                    nc.vector.tensor_tensor(b, t1, cos, ALU.mult)
                    seq(dve, step, nc.vector.tensor_tensor(d[:, t, :, 1, :], t1, sin, ALU.mult))
                    seq(dve, step, nc.vector.tensor_tensor(d[:, t, :, 0, :], b, a, ALU.subtract))
                    seq(dve, step, nc.vector.tensor_tensor(a, t2, cos, ALU.mult))
                    seq(dve, step, nc.vector.tensor_tensor(d[:, t, :, 1, :], d[:, t, :, 1, :], a, ALU.add))

        @block.gpsimd
        def _(pool):
            v = c.VH[:, 0:B * HEADS * 36].rearrange("p (t bl i e) -> p t bl i e", t=NT, bl=4, i=4)
            seq(pool, pool_step, nc.gpsimd.memset(v[:, :, :, :, 8], 1.0))
            for bl in range(4):
                for cl in range(4):
                    src = proj[32 * bl:32 * bl + 32].rearrange("p t (i cl d) -> p t i cl d", i=4, cl=4)[:, :, :, cl, :]
                    seq(pool, pool_step, nc.gpsimd.tensor_copy(v[32 * cl:32 * cl + 32, :, bl, :, 0:8], src))

    keys = c.big1(2 * TOK, TOK).rearrange("p (t bl i d) -> p t bl i d", t=NT, bl=4, i=4)
    with nc.Block() as block:
        @block.vector
        def _(dve):
            for bl in range(4):
                for cl in range(4):
                    src = c.total[32 * bl:32 * bl + 32].rearrange("p t (i cl d) -> p t i cl d", i=4, cl=4)[:, :, :, cl, :]
                    nc.vector.tensor_copy(keys[32 * cl:32 * cl + 32, :, bl], src)

    turn(c, c.XN[:], NT, P, c.qk32[:, 0:1, :])
    qT = c.VH[:, B * HEADS * 36:B * HEADS * 36 + TOK]
    matmul_stream(c, halves(c, lambda half: [(c.headmat, c.qk32[:, 0, half * S:(half + 1) * S])], P, qT))
    stack_keys(c, keys.rearrange("p t bl i d -> p (t bl) i d"))
    split_heads(c, qT, None, 0)
    attention_8(c, [P] * ST, c.Y8, 8.0 ** -0.5, chunked=True)
    quantise(c, c.Y8, c.q_bf[:], amax)
    turn_quantised(c, c.q_bf, c.qT_bf)
    quantised_product(c, c.qT_bf[:], c.signT[:, 1, :], amax, c.alpha[:, 1, :], None, c.Y8)
    with nc.Block() as block:
        @block.vector
        def _(dve):
            nc.vector.tensor_tensor(c.total[:], c.X[:], c.Y8, ALU.add)
    add_and_norm(c, total=c.total, out=c.X, turned=[(c.XT, None, None)])


def cross_kv(c, wk, wv, bk=None, bv=None):
    ctxT = c.m("ctxT")[0:CTX]
    v = c.VH[0:SK, 0:B * HEADS * 9].rearrange("p (b h e) -> p b h e", b=B, e=9)

    def ones(act, bank):
        return None
    units = [([(wk, ctxT)], P, B * SK, "act", act_copy(c, c.ckT[:], bias=bk))]
    for b in range(B):
        if bv is None:
            emit = (lambda b: lambda dve, bank, step: c.nc.vector.tensor_copy(v[:, b, :, 0:8], bank.rearrange("p (h d) -> p h d", d=8)))(b)
        else:
            emit = (lambda b: lambda dve, bank, step: c.nc.vector.tensor_tensor(
                v[:, b, :, 0:8], bank.rearrange("p (h d) -> p h d", d=8), bv[0:SK].rearrange("p (h d) -> p h d", d=8), ALU.add))(b)
        units.append(([(ctxT[:, b * SK:(b + 1) * SK], wv)], SK, P, "dve", emit))
    return units, v[:, :, :, 8]


def fill(c, ap, value):
    with c.nc.Block() as block:
        @block.gpsimd
        def _(pool):
            c.nc.gpsimd.memset(ap, value)


def cross_attention_8(c, wq, wk, wv, wo, bq, bk, bv, bo):
    units, one = cross_kv(c, wk, wv, bk, bv)
    units += halves(c, lambda half: [(wq, c.XT[:, half * S:(half + 1) * S])], P, c.qT, bias=bq)
    fill(c, one, 1.0)
    matmul_stream(c, units)
    split_heads(c, c.qT[:], c.ckT[:], B * SK)
    attention_8(c, [SK], c.Y8, 8.0 ** -0.5)
    turn(c, c.Y8, NT, P, c.yT8)
    add_and_norm(c, add=project_out(c, c.yT8, wo), bias=bo, out=c.X, turned=[(c.XT, None, None)])


def moe(c, srcT, parts, cwT_parts, mix, outT, load=None):
    nc = c.nc
    gate_ready, gated, hidden_ready, hidden_used, acc_ready, dve_step, act_mid, act_step = (counter(c, n) for n in (
        "gate_ready", "gated", "hidden_ready", "hidden_used", "acc_ready", "dve_step", "act_mid", "act_step"))
    n = len(parts)
    steps = [(half, k) for half in range(2) for k in range(n)]
    G, U, CW, ACC = c.bank[0:2], c.bank[2:4], c.bank[4:6], c.bank[6]
    sg, hid = c.moe_sg, c.moe_h

    with nc.Block() as block:
        if load:
            block.sync(load)

        @block.tensor
        def _(pe):
            def up(s):
                half, k = steps[s]
                w1, w3, _, pick = parts[k]
                m = w1.shape[1]
                x = srcT[:, half * S:(half + 1) * S]
                if s >= 2:
                    pe.wait_ge(hidden_ready.sem, hidden_ready.at(s - 1))
                nc.tensor.matmul(G[s % 2][0:m, :], w1, x, start=True, stop=True).then_inc(gate_ready.up(), 1)
                last = nc.tensor.matmul(U[s % 2][0:m, :], w3, x, start=True, stop=True)
                if pick is not None:
                    last = nc.tensor.matmul(CW[s % 2][0:m, :], pick, cwT_parts[:, half * S:(half + 1) * S], start=True, stop=True)
                last.then_inc(gate_ready.up(), 1)

            def down(s):
                half, k = steps[s]
                w2 = parts[k][2]
                m = w2.shape[0]
                pe.wait_ge(hidden_ready.sem, hidden_ready.at(s + 1))
                if k == 0 and half:
                    pe.wait_ge(acc_ready.sem, acc_ready.at(1))
                last = nc.tensor.matmul(ACC[:, :], w2, hid[0:m, s % 2, :], start=(k == 0), stop=(k == n - 1))
                last.then_inc(hidden_used.up(), 1)

            for s in range(len(steps) + 1):
                if s < len(steps):
                    up(s)
                if s >= 1:
                    down(s - 1)

        @block.scalar
        def _(act):
            for s, (half, k) in enumerate(steps):
                m = parts[k][0].shape[1]
                act.wait_ge(gate_ready.sem, gate_ready.at(2 * s + 1))
                if s >= 2:
                    act.wait_ge(hidden_ready.sem, hidden_ready.at(s - 1))
                func = ACT.Silu if mix == "silu" else ACT.Copy
                nc.scalar.activation(sg[0:m, s % 2, :], G[s % 2][0:m, :], func).then_inc(gated.up(), 1)
                if mix == "gelu":
                    act.wait_ge(act_mid.sem, act_mid.at(s + 1))
                    nc.scalar.activation(sg[0:m, s % 2, :], sg[0:m, s % 2, :], ACT.Gelu).then_inc(gated.up(), 1)
                if k == 0 and half:
                    act.wait_ge(hidden_used.sem, hidden_used.at(n))
                    nc.scalar.copy(outT[:, 0:S], ACC[:, :]).then_inc(acc_ready.up(), 1)
            act.wait_ge(hidden_used.sem, hidden_used.at(2 * n))
            nc.scalar.copy(outT[:, S:2 * S], ACC[:, :])

        @block.vector
        def _(dve):
            for s, (half, k) in enumerate(steps):
                m = parts[k][0].shape[1]
                pick = parts[k][3]
                dve.wait_ge(gate_ready.sem, gate_ready.at(2 * s + 2))
                if s >= 2:
                    dve.wait_ge(hidden_used.sem, hidden_used.at(s - 1))
                if mix == "gelu":
                    dve.wait_ge(gated.sem, gated.at(2 * s + 1))
                    nc.vector.tensor_tensor(sg[0:m, s % 2, :], sg[0:m, s % 2, :], U[s % 2][0:m, :], ALU.mult).then_inc(act_mid.up(), 1)
                    dve.wait_ge(gated.sem, gated.at(2 * s + 2))
                    last = nc.vector.tensor_tensor(hid[0:m, s % 2, :], sg[0:m, s % 2, :], CW[s % 2][0:m, :], ALU.mult)
                else:
                    dve.wait_ge(gated.sem, gated.at(s + 1))
                    last = nc.vector.tensor_tensor(hid[0:m, s % 2, :], sg[0:m, s % 2, :], U[s % 2][0:m, :], ALU.mult)
                    if pick is not None:
                        seq(dve, dve_step, last)
                        last = nc.vector.tensor_tensor(hid[0:m, s % 2, :], hid[0:m, s % 2, :], CW[s % 2][0:m, :], ALU.mult)
                last.then_inc(hidden_ready.up(), 1)


def router_logits(c, srcT, w, E):
    nc = c.nc
    with nc.Block() as block:
        @block.tensor
        def _(pe):
            for t in range(NT):
                nc.tensor.matmul(c.bank[0][:, t * 32:t * 32 + E], srcT[:, t * P:(t + 1) * P], w, start=True, stop=True)


def turn_weights(c, cw, E):
    nc, step = c.nc, counter(c, "dve_step")
    cw_ready, cw_turned, act_freed = counter(c, "cw_ready"), counter(c, "cw_turned"), counter(c, "act_freed")
    parts = c.cw_parts
    with nc.Block() as block:
        @block.vector
        def _(dve):
            rest = c.cw_rest[:, :, 0:E]
            seq(dve, step, nc.vector.memset(parts[:], 0.0))
            seq(dve, step, nc.vector.tensor_copy(parts[:, :, 0:E], cw))
            seq(dve, step, nc.vector.tensor_tensor(rest, cw, parts[:, :, 0:E], ALU.subtract))
            seq(dve, step, nc.vector.tensor_copy(parts[:, :, 32:32 + E], rest))
            seq(dve, step, nc.vector.tensor_tensor(rest, rest, parts[:, :, 32:32 + E], ALU.subtract))
            nc.vector.tensor_copy(parts[:, :, 64:64 + E], rest).then_inc(cw_ready.up(), 1)

        @block.tensor
        def _(pe):
            pe.wait_ge(cw_ready.sem, cw_ready.at(1))
            for half in range(2):
                if half:
                    pe.wait_ge(act_freed.sem, act_freed.at(1))
                for k in range(4):
                    last = nc.tensor.transpose(c.bank_bf[0:96, k * P:(k + 1) * P], parts[:, half * 4 + k, :], c.ident_bf[:])
                last.then_inc(cw_turned.up(), 1)

        @block.scalar
        def _(act):
            for half in range(2):
                act.wait_ge(cw_turned.sem, cw_turned.at(half + 1))
                nc.scalar.copy(c.cwT[:, half * S:(half + 1) * S], c.bank_bf[0:96, 0:S]).then_inc(act_freed.up(), 1)


def top_indices(dve, c, step, values, E, dst):
    nc = c.nc
    for t in range(NT):
        last = nc.vector.max(c.top_v[:, t, :], values[:, t, 0:E])
    seq(dve, step, last)
    for t in range(NT):
        last = nc.vector.max_index(c.top_i[:, t, :], c.top_v[:, t, :], values[:, t, 0:E])
    seq(dve, step, last)
    seq(dve, step, nc.vector.tensor_copy(dst, c.top_i[:]))


def one_hot(c, E, index, dst):
    iota = c.m("iota")[:, 0:E].unsqueeze(1).broadcast_to([P, NT, E])
    return c.nc.vector.tensor_tensor(dst, iota, index.unsqueeze(2).broadcast_to([P, NT, E]), ALU.is_equal)


def layer0_moe(c):
    nc, step = c.nc, counter(c, "dve_step")
    E = L0E
    router_logits(c, c.XT[:], c.m("L0_gateT"), E)
    sc, sel, oh, top = c.rt[:, 0, :, 0:E], c.rt[:, 1, :, 0:E], c.rt[:, 2, :, 0:E], c.top_f
    biased, scored = counter(c, "biased"), counter(c, "scored")
    with nc.Block() as block:
        @block.vector
        def _(dve):
            lg = c.bank[0][:, 0:NT * 32].rearrange("p (t e) -> p t e", t=NT)[:, :, 0:E]
            nc.vector.tensor_tensor(sel, lg, c.m("gate_bias").unsqueeze(1).broadcast_to([P, NT, E]), ALU.add).then_inc(biased.up(), 1)
            dve.wait_ge(scored.sem, scored.at(1))
            top_indices(dve, c, step, c.rt[:, 0, :, :], E, top)
            seq(dve, step, one_hot(c, E, top[:, :, 0], sel))
            seq(dve, step, one_hot(c, E, top[:, :, 1], oh))
            seq(dve, step, nc.vector.tensor_tensor(sel, sel, oh, ALU.add))
            seq(dve, step, nc.vector.tensor_tensor(sel, sel, sc, ALU.mult))
            seq(dve, step, nc.vector.tensor_reduce(c.small8[:, 0, :], sel, AX_X, ALU.add))
            seq(dve, step, nc.vector.tensor_scalar(c.small8[:, 0, :], c.small8[:, 0, :], 1e-20, None, ALU.add))
            seq(dve, step, nc.vector.reciprocal(c.small8[:, 1, :], c.small8[:, 0, :]))
            seq(dve, step, nc.vector.tensor_tensor(sel, sel, c.small8[:, 1, :].unsqueeze(2).broadcast_to([P, NT, E]), ALU.mult))

        @block.scalar
        def _(act):
            act.wait_ge(biased.sem, biased.at(1))
            nc.scalar.activation(sc, sel, ACT.Sigmoid).then_inc(scored.up(), 1)
    turn_weights(c, sel, E)
    w1, w3, w2 = c.m("w1T"), c.m("w3T"), c.m("w2T")
    parts = []
    for e in range(E):
        for i, (a, m) in enumerate(chunks(L0HID)):
            col = e * L0HID + a
            parts.append((w1[:, col:col + m], w3[:, col:col + m], w2[0:m, (e * 3 + i) * P:(e * 3 + i + 1) * P],
                          c.pick_expert[:, e, 0:m]))
    moe(c, c.XT[:], parts, c.cwT, "silu", c.outT[:])
    add_and_norm(c, add=turn_back(c, c.outT), out=c.X, turned=[(c.XT, None, None)], load=c.fetcher("moe1", "turned"))



def layer1_scan(c):
    nc = c.nc
    N = 16
    xnT, dtT, uT = c.big1(0, TOK), c.big1(TOK, TOK), c.big1(2 * TOK, TOK)
    ex, mx = c.big1(3 * TOK, TOK), c.big1(4 * TOK, TOK)
    wb, wc = c.big1(5 * TOK, N * P).rearrange("p (n m) -> p n m", n=N), c.big3(0, N * P).rearrange("p (n m) -> p n m", n=N)
    a, bx, h, ch = (c.big3(2048 + 1024 * i, TOK).rearrange("p (z t) -> p z t", z=2) for i in range(4))
    yT = c.outT
    add_and_norm(c, out=c.XN, turned=[(xnT, c.col("L1_attn_gamma"), c.col("L1_attn_beta"))])
    step, act_step = counter(c, "dve_step"), counter(c, "act_step")
    matmul_stream(c, halves(c, lambda half: [(c.m("L1_WdtT"), xnT[:, half * S:(half + 1) * S])], P, dtT, bias=c.col("L1_attn_b_dt")))
    z_ready, soft_ready, dt_ready = counter(c, "z_ready"), counter(c, "soft_ready"), counter(c, "dt_ready")
    with nc.Block() as block:
        @block.vector
        def _(dve):
            seq(dve, step, nc.vector.tensor_scalar(ex, dtT, -1.0, None, ALU.mult))
            nc.vector.tensor_tensor(ex, ex, dtT, ALU.min).then_inc(z_ready.up(), 1)
            seq(dve, step, nc.vector.tensor_scalar(mx, dtT, 0.0, None, ALU.max))
            dve.wait_ge(soft_ready.sem, soft_ready.at(1))
            seq(dve, step, nc.vector.tensor_tensor(dtT, mx, ex, ALU.add))
            nc.vector.tensor_tensor(uT, dtT, xnT, ALU.mult)
            nc.vector.tensor_scalar(c.negA, c.negA, -1.0, None, ALU.mult).then_inc(dt_ready.up(), 1)

        @block.scalar
        def _(act):
            nc.scalar.activation(c.negA, c.m("L1_A_log"), ACT.Exp)
            act.wait_ge(z_ready.sem, z_ready.at(1))
            seq(act, act_step, nc.scalar.activation(ex, ex, ACT.Exp))
            nc.scalar.activation(ex, ex, ACT.Ln, bias=1.0).then_inc(soft_ready.up(), 1)

        @block.gpsimd
        def _(pool):
            nc.gpsimd.tensor_copy(wb, c.m("L1_WBT").unsqueeze(2).broadcast_to([P, N, P]))
            nc.gpsimd.tensor_copy(wc, c.m("L1_WCT").unsqueeze(2).broadcast_to([P, N, P]))

    BC, YS = c.bank[0:6], c.bank[6:8]
    in_ready, bx_ready, ch_ready, a_ready, sum_ready, decay_used = (counter(c, n) for n in ("in_ready", "bx_ready", "ch_ready", "a_ready", "sum_done", "decay_used"))
    steps = [(n, z) for n in range(N) for z in range(2)]
    with nc.Block() as block:
        @block.tensor
        def _(pe):
            def inputs(s):
                n, z = steps[s]
                x = xnT[:, z * S:(z + 1) * S]
                if s >= 3:
                    pe.wait_ge(ch_ready.sem, ch_ready.at(s - 2))
                nc.tensor.matmul(BC[2 * (s % 3)][:, :], wb[:, n, :], x, start=True, stop=True)
                nc.tensor.matmul(BC[2 * (s % 3) + 1][:, :], wc[:, n, :], x, start=True, stop=True).then_inc(in_ready.up(), 1)

            inputs(0)
            inputs(1)
            for s, (n, z) in enumerate(steps):
                if s + 2 < len(steps):
                    inputs(s + 2)
                pe.wait_ge(ch_ready.sem, ch_ready.at(s + 1))
                nc.tensor.matmul(YS[z][:, :], c.ident[:], ch[:, s % 2, :], start=(n == 0), stop=(n == N - 1)).then_inc(sum_ready.up(), 1)

        @block.scalar
        def _(act):
            for s, (n, z) in enumerate(steps):
                if s >= 2:
                    act.wait_ge(decay_used.sem, decay_used.at(s - 1))
                nc.scalar.activation(a[:, s % 2, :], dtT[:, z * S:(z + 1) * S], ACT.Exp, scale=c.negA[:, n:n + 1]).then_inc(a_ready.up(), 1)

        @block.vector
        def _(dve):
            for s, (n, z) in enumerate(steps):
                dve.wait_ge(in_ready.sem, in_ready.at(s + 1))
                seq(dve, step, nc.vector.tensor_tensor(bx[:, s % 2, :], uT[:, z * S:(z + 1) * S], BC[2 * (s % 3)][:, :], ALU.mult))
                dve.wait_ge(a_ready.sem, a_ready.at(s + 1))
                ins = nc.vector.tensor_tensor_scan(h[:, s % 2, :], a[:, s % 2, :], bx[:, s % 2, :], 0.0, ALU.mult, ALU.add)
                ins.then_inc(decay_used.up(), 1)
                dve.wait_ge(decay_used.sem, decay_used.at(s + 1))
                if s >= 2:
                    dve.wait_ge(sum_ready.sem, sum_ready.at(s - 1))
                nc.vector.tensor_tensor(ch[:, s % 2, :], h[:, s % 2, :], BC[2 * (s % 3) + 1][:, :], ALU.mult).then_inc(ch_ready.up(), 1)
            dve.wait_ge(sum_ready.sem, sum_ready.at(len(steps)))
            for z in range(2):
                nc.vector.scalar_tensor_tensor(out=yT[:, z * S:(z + 1) * S], in0=c.XT[:, z * S:(z + 1) * S],
                                               scalar=c.col("L1_attn_D_param"), in1=YS[z][:, :], op0=ALU.mult, op1=ALU.add)
    add_and_norm(c, add=turn_back(c, yT), out=c.X, turned=[(c.XT, None, None)])


def heads_natural(c, srcT, w, cols, V, width, tiles=NT):
    units = []
    for t in range(tiles):
        for a in range(0, cols, S):
            n = min(S, cols - a)
            who = "act" if t % 2 else "dve"
            dst = V[:, t, a // width:(a + n) // width, 0:width]
            if who == "act":
                emit = (lambda dst: lambda act, bank: c.nc.scalar.copy(dst, bank.rearrange("p (h d) -> p h d", d=width)))(dst)
            else:
                emit = (lambda dst: lambda dve, bank, step: c.nc.vector.tensor_copy(dst, bank.rearrange("p (h d) -> p h d", d=width)))(dst)
            units.append(([(srcT[:, t * P:(t + 1) * P], w[:, a:a + n])], P, n, who, emit))
    return units


def layer1_ffn(c):
    nc = c.nc
    nT = c.big2(2 * TOK, TOK)
    q = c.big1(0, 8 * TOK).rearrange("p (k t) -> p k t", k=8)
    k = c.big2(0, 2 * TOK).rearrange("p (k t) -> p k t", k=2)
    Y = c.big3(0, 8 * TOK).rearrange("p (t f) -> p t f", t=NT)
    V = c.VH[:, 0:NT * 4 * 65].rearrange("p (t h e) -> p t h e", t=NT, h=4)
    add_and_norm(c, norm="rms", eps=1e-6, out=c.XN, turned=[(nT, c.col("L1_ffn_g1"), None)])
    fill(c, V[:, :, :, 64], 1.0)
    matmul_stream(c, heads_natural(c, nT, c.m("wv"), 256, V, 64))

    plain_ready, rope_used, dve_step, pool_used = (counter(c, n) for n in ("plain_ready", "rope_used", "dve_step", "pool_used"))
    sin_ready = counter(c, "sin_ready")
    jobs = [(w, ws, dst, kk, half) for w, ws, dst, n in (("wq", "wqs", q, 8), ("wk", "wks", k, 2)) for kk in range(n) for half in range(2)]
    tmp = c.big2(3 * TOK, TOK).rearrange("p (z t) -> p z t", z=2)
    with nc.Block() as block:
        @block.tensor
        def _(pe):
            for s, (w, ws, dst, kk, half) in enumerate(jobs):
                if s >= 4:
                    pe.wait_ge(rope_used.sem, rope_used.at(s - 3))
                x = nT[:, half * S:(half + 1) * S]
                nc.tensor.matmul(c.bank[2 * (s % 4)][:, :], c.m(w)[:, kk * P:(kk + 1) * P], x, start=True, stop=True)
                nc.tensor.matmul(c.bank[2 * (s % 4) + 1][:, :], c.m(ws)[:, kk * P:(kk + 1) * P], x, start=True, stop=True).then_inc(plain_ready.up(), 1)

        @block.vector
        def _(dve):
            for s, (w, ws, dst, kk, half) in enumerate(jobs):
                d = dst[:, kk, half * S:(half + 1) * S]
                dve.wait_ge(plain_ready.sem, plain_ready.at(s + 1))
                nc.vector.tensor_tensor(d, c.bank[2 * (s % 4)][:, :], c.m("cos"), ALU.mult)
                if s >= 2:
                    dve.wait_ge(pool_used.sem, pool_used.at(s - 1))
                nc.vector.tensor_tensor(tmp[:, s % 2, :], c.bank[2 * (s % 4) + 1][:, :], c.m("sin"), ALU.mult).then_inc(rope_used.up(), 1)

        @block.gpsimd
        def _(pool):
            for s, (w, ws, dst, kk, half) in enumerate(jobs):
                d = dst[:, kk, half * S:(half + 1) * S]
                pool.wait_ge(rope_used.sem, rope_used.at(s + 1))
                nc.gpsimd.tensor_tensor(d, d, tmp[:, s % 2, :], ALU.add).then_inc(pool_used.up(), 1)

    def qop(b, h):
        return [q[64 * (h % 2):64 * (h % 2) + 64, h // 2, b * S:(b + 1) * S]]

    def kop(b, h):
        kv = h % 4
        return [k[64 * (kv % 2):64 * (kv % 2) + 64, kv // 2, b * S:(b + 1) * S]]

    attention(c, [P] * ST, 64, qop, kop, lambda b, h, i: V[:, b * ST + i, h % 4, :], 0.125, Y, mask="causal",
              load=c.fetcher("l2x"))
    yT = c.big1(0, 8 * TOK).rearrange("p (k t) -> p k t", k=8)
    turn(c, Y, NT, 1024, yT)
    hT = c.big2(0, TOK)
    c.rms_out = c.XN
    add_and_norm(c, add=project_out(c, yT, c.m("wo"), 8), total=c.total, norm="rms", eps=1e-6, out=c.XN,
                 turned=[(hT, c.col("L1_ffn_g2"), None)])
    router_logits(c, hT, c.m("L1f_router"), L1E)

    E = L1E
    step = counter(c, "dve_step")
    lg, oh1, oh2, cum, tmp1, tmp2 = (c.rt[:, i, :, 0:E] for i in range(6))
    top = c.top_f
    s_ = lambda i: c.small8[:, i, :]
    (top_done, weights_done, counted, carried) = (counter(c, n) for n in ("top_done", "weights_done", "counted", "carried"))
    with nc.Block() as block:
        @block.vector
        def _(dve):
            bank = c.bank[0][:, 0:NT * 32].rearrange("p (t e) -> p t e", t=NT)[:, :, 0:E]
            seq(dve, step, nc.vector.tensor_tensor(lg, bank, c.m("router_b").unsqueeze(1).broadcast_to([P, NT, E]), ALU.add))
            top_indices(dve, c, step, c.rt[:, 0, :, :], E, top)
            nc.vector.tensor_tensor(s_(0), c.top_v[:, :, 1], c.top_v[:, :, 0], ALU.subtract)
            nc.vector.tensor_copy(oh2, c.m("iota")[:, 0:E].unsqueeze(1).broadcast_to([P, NT, E]))
            seq(dve, step, one_hot(c, E, top[:, :, 0], oh1))
            oh = c.cw_rest[:, :, 0:2 * E]
            nc.vector.tensor_copy(oh[:, :, 0:E], oh1)
            one_hot(c, E, top[:, :, 1], oh[:, :, E:2 * E])
            seq(dve, step, one_hot(c, E, top[:, :, 1], oh2))
            nc.vector.tensor_copy(s_(7), s_(0)).then_inc(top_done.up(), 1)
            dve.wait_ge(counted.sem, counted.at(1))
            cnt = c.bank[1][:, 0:NT * 2 * E].rearrange("p (t e) -> p t e", t=NT)
            cap = float(TOK // 8)
            seq(dve, step, nc.vector.tensor_copy(tmp1, cnt[:, :, 0:E]))
            seq(dve, step, nc.vector.tensor_tensor(tmp2, cnt[:, :, E:2 * E], tmp1, ALU.add))
            seq(dve, step, nc.vector.tensor_scalar(tmp1, tmp1, cap, None, ALU.is_lt))
            seq(dve, step, nc.vector.tensor_scalar(tmp2, tmp2, cap, None, ALU.is_lt))
            seq(dve, step, nc.vector.tensor_tensor(tmp1, tmp1, oh1, ALU.mult))
            seq(dve, step, nc.vector.tensor_tensor(tmp2, tmp2, oh2, ALU.mult))
            nc.vector.tensor_reduce(s_(1), tmp1, AX_X, ALU.add)
            seq(dve, step, nc.vector.tensor_reduce(s_(2), tmp2, AX_X, ALU.add))
            seq(dve, step, nc.vector.tensor_tensor(s_(3), s_(1), top[:, :, 0], ALU.mult))
            seq(dve, step, nc.vector.tensor_tensor(s_(4), s_(2), top[:, :, 1], ALU.mult))
            seq(dve, step, nc.vector.tensor_tensor(s_(3), s_(3), s_(4), ALU.max))
            seq(dve, step, one_hot(c, E, s_(3), cum))
            dve.wait_ge(weights_done.sem, weights_done.at(1))
            seq(dve, step, nc.vector.tensor_scalar(s_(5), s_(7), 1.0, None, ALU.add))
            seq(dve, step, nc.vector.reciprocal(s_(5), s_(5)))
            seq(dve, step, nc.vector.tensor_tensor(s_(6), s_(7), s_(5), ALU.mult))
            seq(dve, step, nc.vector.tensor_tensor(s_(1), s_(1), s_(5), ALU.mult))
            seq(dve, step, nc.vector.tensor_tensor(s_(2), s_(2), s_(6), ALU.mult))
            seq(dve, step, nc.vector.tensor_tensor(s_(1), s_(1), s_(2), ALU.add))
            seq(dve, step, nc.vector.tensor_tensor(s_(5), s_(5), s_(6), ALU.add))
            seq(dve, step, nc.vector.tensor_tensor(s_(2), s_(5), s_(1), ALU.subtract))
            seq(dve, step, nc.vector.tensor_tensor(cum, cum, s_(1).unsqueeze(2).broadcast_to([P, NT, E]), ALU.mult))
            nc.vector.tensor_tensor(c.total[:], c.total[:], c.X[:], ALU.add)

        @block.scalar
        def _(act):
            act.wait_ge(top_done.sem, top_done.at(1))
            nc.scalar.activation(s_(7), s_(7), ACT.Exp).then_inc(weights_done.up(), 1)

        @block.tensor
        def _(pe):
            pe.wait_ge(top_done.sem, top_done.at(1))
            oh = c.cw_rest[:, :, 0:2 * E]
            for t in range(NT):
                for u in range(t + 1):
                    last = nc.tensor.matmul(c.bank[1][:, t * 2 * E:(t + 1) * 2 * E], c.up_to[:] if u == t else c.ones[:],
                                            oh[:, u, :], start=(u == 0), stop=(u == t))
            last.then_inc(counted.up(), 1)

    fill_pick(c, P)
    turn_weights(c, cum, E)
    parts = []
    for e in range(E):
        for i in range(2):
            col = e * L1HID + i * P
            parts.append((c.m("w2")[:, col:col + P], c.m("w1")[:, col:col + P], c.m("w3")[:, (e * 2 + i) * P:(e * 2 + i + 1) * P],
                          c.pick_expert[:, e, :]))
    moe(c, hT, parts, c.cwT, "gelu", c.outT[:])
    own_ready, own_moved = counter(c, "own_ready"), counter(c, "own_moved")
    hn = c.XN
    with nc.Block() as block:
        @block.tensor
        def _(pe):
            for half in range(2):
                for kk in range(4):
                    last = nc.tensor.transpose(c.bank[half][:, kk * P:(kk + 1) * P], hT[:, (half * 4 + kk) * P:(half * 4 + kk + 1) * P], c.ident[:])
                last.then_inc(own_ready.up(), 1)

        @block.vector
        def _(dve):
            for half in range(2):
                dve.wait_ge(own_ready.sem, own_ready.at(half + 1))
                for kk in range(4):
                    t = half * 4 + kk
                    nc.vector.scalar_tensor_tensor(out=c.total[:, t, :], in0=c.bank[half][:, kk * P:(kk + 1) * P],
                                                   scalar=s_(2)[:, t:t + 1], in1=c.total[:, t, :], op0=ALU.mult, op1=ALU.add)
    add_and_norm(c, add=turn_back(c, c.outT), base=c.total, out=c.X, turned=[(c.XT, None, None)], load=c.fetcher("moe2", "l3"))



def layer2_attention(c):
    nc = c.nc
    qf = c.big1(0, TOK)
    kf = c.big1(TOK, TOK)
    V = c.VH[:, 0:NT * HEADS * 9].rearrange("p (t h e) -> p t h e", t=NT, h=HEADS)
    block_product(c, c.m("L2_WQrT")[0:16], c.m("L2_WKrT")[0:16], c.headmat)
    fill(c, V[:, :, :, 8], 1.0)
    x = lambda half: c.XT[:, half * S:(half + 1) * S]
    units = halves(c, lambda half: [(c.m("L2_WQ"), x(half))], P, qf, bias=c.col("L2_attn_bQ"))
    units += halves(c, lambda half: [(c.m("L2_WK"), x(half))], P, kf, bias=c.col("L2_attn_bK"))
    bv = c.row("L2_attn_bV").rearrange("p (h d) -> p h d", d=8)
    for t in range(NT):
        emit = (lambda t: lambda dve, bank, step: nc.vector.tensor_tensor(V[:, t, :, 0:8], bank.rearrange("p (h d) -> p h d", d=8), bv, ALU.add))(t)
        units.append(([(c.XT[:, t * P:(t + 1) * P], c.m("L2_WV"))], P, P, "dve", emit))
    matmul_stream(c, units)
    matmul_stream(c, halves(c, lambda half: [(c.headmat, qf[:, half * S:(half + 1) * S])], P, c.qT))
    split_heads(c, c.qT[:], kf, TOK)
    attention_8(c, [P] * ST, c.Y8, 0.25)
    turn(c, c.Y8, NT, P, c.yT8)
    add_and_norm(c, add=project_out(c, c.yT8, c.m("L2_WO")), bias=c.row("L2_attn_bO"), out=c.X, turned=[(c.XT, None, None)])


def layer2_cross(c):
    q = c.big1(0, 8 * TOK).rearrange("p (k t) -> p k t", k=8)
    k = c.big2(0, 8 * B * SK).rearrange("p (k t) -> p k t", k=8)
    Y = c.big3(0, 8 * TOK).rearrange("p (t f) -> p t f", t=NT)
    V = c.VH[0:SK, 0:B * HEADS * 65].rearrange("p (b h e) -> p b h e", b=B, h=HEADS)
    ctxT = c.m("ctxT")[0:CTX]
    fill(c, V[:, :, :, 64], 1.0)
    units = []
    for kk in range(8):
        units += halves(c, (lambda kk: lambda half: [(c.m("L2x_Wq")[:, kk * P:(kk + 1) * P], c.XT[:, half * S:(half + 1) * S])])(kk), P, q[:, kk, :])
        units.append(([(c.m("L2x_Wk")[0:CTX, kk * P:(kk + 1) * P], ctxT)], P, B * SK, "dve" if kk % 2 else "act",
                      dve_copy(c, k[:, kk, :]) if kk % 2 else act_copy(c, k[:, kk, :])))
    for b in range(B):
        for a in range(0, 1024, S):
            emit = (lambda dst: lambda dve, bank, step: c.nc.vector.tensor_copy(dst, bank.rearrange("p (h d) -> p h d", d=64)))(V[:, b, a // 64:(a + S) // 64, 0:64])
            units.append(([(ctxT[:, b * SK:(b + 1) * SK], c.m("L2x_Wv")[0:CTX, a:a + S])], SK, S, "dve", emit))
    matmul_stream(c, units)
    attention(c, [SK], 64,
              lambda b, h: [q[64 * (h % 2):64 * (h % 2) + 64, h // 2, b * S:(b + 1) * S]],
              lambda b, h: [k[64 * (h % 2):64 * (h % 2) + 64, h // 2, b * SK:(b + 1) * SK]],
              lambda b, h, i: V[:, b, h, :], 0.125, Y)
    yT = c.big1(0, 8 * TOK).rearrange("p (k t) -> p k t", k=8)
    turn(c, Y, NT, 1024, yT)
    add_and_norm(c, add=project_out(c, yT, c.m("L2x_Wo"), 8), bias=c.row("L2_xattn_bo"), out=c.X, turned=[(c.XT, None, None)],
                 load=None)


def layer2_moe(c):
    nc, step = c.nc, counter(c, "dve_step")
    E, NG, PG = L2E, 4, 8
    router_logits(c, c.XT[:], c.m("L2_routerT"), E)
    sc, sfc, tmp, sel = (c.rt[:, i, :, :] for i in range(4))
    top = c.top_f
    gtop = c.big3(12 * 1024 // 4 * 1, 256).rearrange("p (t g e) -> p t g e", t=NT, g=NG)
    gs = c.big3(12 * 1024 // 4 + 256, 64).rearrange("p (t e) -> p t e", t=NT)
    gm = c.big3(12 * 1024 // 4 + 320, 64).rearrange("p (t e) -> p t e", t=NT)
    scored = counter(c, "scored")
    with nc.Block() as block:
        @block.scalar
        def _(act):
            lg = c.bank[0][:, 0:NT * 32].rearrange("p (t e) -> p t e", t=NT)
            nc.scalar.activation(sc, lg, ACT.Sigmoid).then_inc(scored.up(), 1)

        @block.vector
        def _(dve):
            seq(dve, step, nc.vector.memset(gs[:], -3.0e38))
            dve.wait_ge(scored.sem, scored.at(1))
            seq(dve, step, nc.vector.tensor_tensor(sfc, sc, c.m("L2_bias").unsqueeze(1).broadcast_to([P, NT, E]), ALU.add))
            for t in range(NT):
                for g in range(NG):
                    last = nc.vector.max(gtop[:, t, g, :], sfc[:, t, g * PG:(g + 1) * PG])
            seq(dve, step, last)
            seq(dve, step, nc.vector.tensor_tensor(gs[:, :, 0:NG], gtop[:, :, :, 0], gtop[:, :, :, 1], ALU.add))
            top_indices(dve, c, step, gs, 8, top)
            iota = c.m("iota")[:, 0:NG].unsqueeze(1).broadcast_to([P, NT, NG])
            seq(dve, step, nc.vector.tensor_tensor(gm[:, :, 0:NG], iota, top[:, :, 0].unsqueeze(2).broadcast_to([P, NT, NG]), ALU.is_equal))
            seq(dve, step, nc.vector.tensor_tensor(gm[:, :, NG:2 * NG], iota, top[:, :, 1].unsqueeze(2).broadcast_to([P, NT, NG]), ALU.is_equal))
            seq(dve, step, nc.vector.tensor_tensor(gm[:, :, 0:NG], gm[:, :, 0:NG], gm[:, :, NG:2 * NG], ALU.add))
            for t in range(NT):
                last = nc.vector.tensor_tensor(tmp[:, t, :].rearrange("p (g e) -> p g e", g=NG), sfc[:, t, :].rearrange("p (g e) -> p g e", g=NG),
                                               gm[:, t, 0:NG].unsqueeze(2).broadcast_to([P, NG, PG]), ALU.mult)
            seq(dve, step, last)
            top_indices(dve, c, step, tmp, E, top)
            seq(dve, step, one_hot(c, E, top[:, :, 0], sel))
            for i in range(1, 4):
                seq(dve, step, one_hot(c, E, top[:, :, i], tmp))
                seq(dve, step, nc.vector.tensor_tensor(sel, sel, tmp, ALU.add))
            seq(dve, step, nc.vector.tensor_tensor(sel, sel, sc, ALU.mult))
            seq(dve, step, nc.vector.tensor_reduce(c.small8[:, 0, :], sel, AX_X, ALU.add))
            seq(dve, step, nc.vector.tensor_scalar(c.small8[:, 0, :], c.small8[:, 0, :], 1e-20, None, ALU.add))
            seq(dve, step, nc.vector.reciprocal(c.small8[:, 1, :], c.small8[:, 0, :]))
            seq(dve, step, nc.vector.tensor_scalar(c.small8[:, 1, :], c.small8[:, 1, :], 2.5, None, ALU.mult))
            seq(dve, step, nc.vector.tensor_tensor(sel, sel, c.small8[:, 1, :].unsqueeze(2).broadcast_to([P, NT, E]), ALU.mult))
    turn_weights(c, sel, E)
    fill_pick(c, 64)
    pick = c.pick_expert.rearrange("p e m -> p (e m)")
    parts = [(c.m("sgT"), c.m("suT"), c.m("sdT"), None)]
    for i in range(E // 2):
        parts.append((c.m("gateT")[:, i * P:(i + 1) * P], c.m("upT")[:, i * P:(i + 1) * P], c.m("downT")[:, i * P:(i + 1) * P],
                      pick[:, i * P:(i + 1) * P]))
    moe(c, c.XT[:], parts, c.cwT, "silu", c.outT[:])
    add_and_norm(c, add=turn_back(c, c.outT), out=c.X, turned=[(c.XT, None, None)], load=c.fetcher("l3x"))


def fill_pick(c, width):
    n = c.pick_flat.shape[1] // width
    n = min(n, 32)
    c.pick_expert = c.pick_flat[:, 0:n * width].rearrange("p (e m) -> p e m", m=width)
    with c.nc.Block() as block:
        @block.gpsimd
        def _(pool):
            c.nc.gpsimd.tensor_copy(c.pick_expert, c.pick_id[:, 0:n].unsqueeze(2).broadcast_to([96, n, width]))



def feed_forward(c, srcT, w1, b1, w2, b2, base, total, **norm):
    h = c.big1(4 * TOK, 4 * TOK).rearrange("p (k t) -> p k t", k=4)
    units = []
    for k in range(4):
        for half in range(2):
            d = h[:, k, half * S:(half + 1) * S]
            units.append(([(w1[:, k * P:(k + 1) * P], srcT[:, half * S:(half + 1) * S])], P, S, "act",
                          act_copy(c, d, bias=b1[:, k:k + 1], func=ACT.Gelu)))
    matmul_stream(c, units)
    add_and_norm(c, add=project_out(c, h, w2, 4), bias=b2, base=base, total=total, **norm)


def layer3_attention(c):
    nc = c.nc
    step, act_step = counter(c, "dve_step"), counter(c, "act_step")
    qT, kT = c.big1(0, TOK), c.big1(TOK, TOK)
    qf = c.big3(0, 4 * TOK).rearrange("p (k t) -> p k t", k=4)
    kf = c.big3(4 * TOK, 4 * TOK).rearrange("p (t f) -> p t f", t=NT)
    V = c.VH[:, 0:NT * 4 * 33].rearrange("p (t h e) -> p t h e", t=NT, h=4)
    tmp = c.big2(0, 2 * TOK).rearrange("p (z t) -> p z t", z=4)
    kv = c.big2(2 * TOK, 4 * B * 36).rearrange("p (k b e) -> p k b e", k=4, b=B)
    w = c.m("L3_wqkvT")
    fill(c, V[:, :, :, 32], 1.0)
    units = halves(c, lambda half: [(w[:, 0:P], c.XT[:, half * S:(half + 1) * S])], P, qT)
    units += halves(c, lambda half: [(w[:, P:2 * P], c.XT[:, half * S:(half + 1) * S])], P, kT)
    units += heads_natural(c, c.XT, w[:, 2 * P:3 * P], P, V, 32)
    matmul_stream(c, units)

    z_ready, low_ready, e_ready, f_ready = (counter(c, n) for n in ("f_product", "low_ready", "e_ready", "f_ready"))
    proj = c.m("L3_proj")
    jobs = [("q", j, half) for j in range(4) for half in range(2)] + [("k", t, 0) for t in range(NT)]
    with nc.Block() as block:
        @block.tensor
        def _(pe):
            for s, (who, i, half) in enumerate(jobs):
                if s >= 4:
                    pe.wait_ge(f_ready.sem, f_ready.at(s - 3))
                if who == "q":
                    last = nc.tensor.matmul(c.bank[s % 4][:, :], proj[:, i * P:(i + 1) * P], qT[:, half * S:(half + 1) * S], start=True, stop=True)
                else:
                    last = nc.tensor.matmul(c.bank[s % 4][:, :], kT[:, i * P:(i + 1) * P], proj, start=True, stop=True)
                last.then_inc(z_ready.up(), 1)

        @block.vector
        def _(dve):
            def low(s):
                dve.wait_ge(z_ready.sem, z_ready.at(s + 1))
                nc.vector.tensor_scalar(tmp[:, s % 4, :], c.bank[s % 4][:, :], 0.0, None, ALU.min).then_inc(low_ready.up(), 1)
            low(0)
            for s, (who, i, half) in enumerate(jobs):
                if s + 1 < len(jobs):
                    low(s + 1)
                dve.wait_ge(e_ready.sem, e_ready.at(s + 1))
                d = qf[:, i, half * S:(half + 1) * S] if who == "q" else kf[:, i, :]
                nc.vector.scalar_tensor_tensor(out=d, in0=c.bank[s % 4][:, :], scalar=0.0, in1=tmp[:, s % 4, :], op0=ALU.max,
                                               op1=ALU.add).then_inc(f_ready.up(), 1)

        @block.scalar
        def _(act):
            for s in range(len(jobs)):
                act.wait_ge(low_ready.sem, low_ready.at(s + 1))
                nc.scalar.activation(tmp[:, s % 4, :], tmp[:, s % 4, :], ACT.Exp).then_inc(e_ready.up(), 1)

    def kv_emit(j, b):
        def emit(dve, bank, step):
            mask = c.m("block_kv")
            nc.vector.tensor_tensor(kv[:, j, b, 0:32], bank[:, 0:32], mask[:, 0:32], ALU.mult)
            return nc.vector.tensor_tensor(kv[:, j, b, 32:36], bank[:, 32:33].broadcast_to([P, 4]), mask[:, 32:36], ALU.mult)
        return emit
    matmul_stream(c, [([(kf[:, b * ST + t, j * P:(j + 1) * P], V[:, b * ST + t, j, :]) for t in range(ST)], P, 33, "dve", kv_emit(j, b))
                      for j in range(4) for b in range(B)])
    attn_ready, den_step = counter(c, "attn_ready"), counter(c, "dve_step")
    Y = c.Y8f.rearrange("p (t j h d) -> p t j h d", t=NT, j=4, h=4)
    rc = c.big2(3 * TOK - 256, 128).rearrange("p (t j h) -> p t j h", t=NT, j=4)
    with nc.Block() as block:
        @block.tensor
        def _(pe):
            for t in range(NT):
                for j in range(4):
                    last = nc.tensor.matmul(c.bank[t % 8][:, j * 36:(j + 1) * 36], qf[:, j, t * P:(t + 1) * P], kv[:, j, t // ST, :], start=True, stop=True)
                last.then_inc(attn_ready.up(), 1)

        @block.vector
        def _(dve):
            for t in range(NT):
                dve.wait_ge(attn_ready.sem, attn_ready.at(t + 1))
                a = c.bank[t % 8][:, 0:144].rearrange("p (j e) -> p j e", j=4)
                seq(dve, step, nc.vector.tensor_scalar(rc[:, t], a[:, :, 32:36], 1e-8, None, ALU.add))
                seq(dve, step, nc.vector.reciprocal(rc[:, t], rc[:, t]))
                nc.vector.tensor_tensor(Y[:, t], a[:, :, 0:32].rearrange("p j (h d) -> p j h d", h=4),
                                        rc[:, t].unsqueeze(3).broadcast_to([P, 4, 4, 8]), ALU.mult)
    turn(c, c.Y8, NT, P, c.yT8)
    rows = (c.row("L3_attn_gamma"), c.row("L3_attn_beta"))
    x1T = c.big3(0, TOK)
    add_and_norm(c, add=project_out(c, c.yT8, c.m("L3_woutT")), bias=c.row("L3_attn_b_out"), total=c.total, out=c.XN, rows=rows,
                 turned=[(x1T, None, None)])
    feed_forward(c, x1T, c.m("L3_w1T"), c.col("L3_attn_b1", 4), c.m("L3_w2T"), c.row("L3_attn_b2"), c.XN, c.total, out=c.XN, rows=rows)
    with nc.Block() as block:
        @block.vector
        def _(dve):
            nc.vector.tensor_tensor(c.X[:], c.X[:], c.XN[:], ALU.add)
    add_and_norm(c, out=c.X, turned=[(c.XT, None, None)])


def layer3_xattn(c):
    nc = c.nc
    x = c.x3
    L = "L3_xattn_"
    q = c.big1(0, 4 * TOK).rearrange("p (k t) -> p k t", k=4)
    k = c.big2(0, 4 * TOK).rearrange("p (k t) -> p k t", k=4)
    Y = c.big3(0, 4 * TOK).rearrange("p (t f) -> p t f", t=NT)
    xn, yn, x3T = c.big3(4 * TOK, TOK), c.big3(5 * TOK, TOK), c.big3(6 * TOK, TOK)

    for a in (1, 2):
        A = f"{L}a{a}_"
        src = c.X if a == 1 else c.total
        add_and_norm(c, base=src, total=src, out=x, rows=(c.row(f"{L}ln{a}_g"), c.row(f"{L}ln{a}_b")))
        turned = [(xn, c.col(A + "lnx_g"), c.col(A + "lnx_b"))]
        if a == 1:
            turned.append((yn, c.col(A + "lny_g"), c.col(A + "lny_b")))
        add_and_norm(c, base=x, total=x, out=c.XN, turned=turned)
        if a == 2:
            context_norm(c, A)
        units = []
        wq, wk, wv = c.m(f"a{a}_wq"), c.m(f"a{a}_wk"), c.m(f"a{a}_wv")
        for kk in range(4):
            units += halves(c, (lambda kk: lambda half: [(wq[:, kk * P:(kk + 1) * P], xn[:, half * S:(half + 1) * S])])(kk), P, q[:, kk, :])
            if a == 1:
                units += halves(c, (lambda kk: lambda half: [(wk[:, kk * P:(kk + 1) * P], yn[:, half * S:(half + 1) * S])])(kk), P, k[:, kk, :])
            else:
                units.append(([(wk[0:CTX, kk * P:(kk + 1) * P], c.ctxnT[:])], P, B * SK, "act", act_copy(c, k[:, kk, 0:B * SK])))
        if a == 1:
            V = c.VH[:, 0:NT * HEADS * 33].rearrange("p (t h e) -> p t h e", t=NT, h=HEADS)
            units += heads_natural(c, yn, wv, 512, V, 32)
            one = V[:, :, :, 32]
        else:
            V = c.VH[0:SK, 0:B * HEADS * 33].rearrange("p (t h e) -> p t h e", t=B, h=HEADS)
            for b in range(B):
                emit = (lambda dst: lambda dve, bank, step: nc.vector.tensor_copy(dst, bank.rearrange("p (h d) -> p h d", d=32)))(V[:, b, :, 0:32])
                units.append(([(c.ctxnT[:, b * SK:(b + 1) * SK], wv[0:CTX, :])], SK, S, "dve", emit))
            one = V[:, :, :, 32]
        fill(c, one, 0.0 if a == 1 else 1.0)
        matmul_stream(c, units)
        n = S if a == 1 else SK
        attention(c, [P] * ST if a == 1 else [SK], 32,
                  lambda b, h: [q[32 * (h % 4):32 * (h % 4) + 32, h // 4, b * S:(b + 1) * S]],
                  lambda b, h: [k[32 * (h % 4):32 * (h % 4) + 32, h // 4, b * n:(b + 1) * n]],
                  (lambda b, h, i: V[:, b * ST + i, h, :]) if a == 1 else (lambda b, h, i: V[:, b, h, :]),
                  32.0 ** -0.5, Y, mask="future" if a == 1 else None)
        yT = c.big1(0, 4 * TOK).rearrange("p (k t) -> p k t", k=4)
        turn(c, Y, NT, 512, yT)
        add_and_norm(c, add=project_out(c, yT, c.m(f"a{a}_li1"), 4), bias=c.row(A + "li1_b"), base=x, total=c.total, out=c.XN,
                     turned=[(x3T, c.col(A + "ln3_g"), c.col(A + "ln3_b"))])
        feed_forward(c, x3T, c.m(f"a{a}_li2"), c.col(A + "li2_b", 4), c.m(f"a{a}_li3"), c.row(A + "li3_b"), c.total, c.total, norm=None)
        with nc.Block() as block:
            @block.vector
            def _(dve):
                step = counter(c, "dve_step")
                seq(dve, step, nc.vector.tensor_tensor(c.total[:], c.total[:], x[:], ALU.add))
                if a == 2:
                    nc.vector.tensor_tensor(c.total[:], c.total[:], c.X[:], ALU.add)
    add_and_norm(c, base=c.total, total=c.total, out=c.X, turned=[(c.XT, None, None)])


def context_norm(c, A):
    nc = c.nc
    ctxT = c.m("ctxT")[0:CTX]
    mean_ready, sq_ready, var_ready, r_ready, step = (counter(c, n) for n in ("cm_ready", "csq_ready", "cvar_ready", "cr_ready", "dve_step"))
    n = B * SK
    d, sq, r = c.ctx_tmp[:, 0, :], c.ctx_tmp[:, 1, :], c.ctx_tmp[:, 2, :]
    with nc.Block() as block:
        @block.tensor
        def _(pe):
            nc.tensor.matmul(c.bank[0][0:CTX, 0:n], c.ones[0:CTX, 0:CTX], ctxT, start=True, stop=True).then_inc(mean_ready.up(), 1)
            pe.wait_ge(sq_ready.sem, sq_ready.at(1))
            nc.tensor.matmul(c.bank[1][0:CTX, 0:n], c.ones[0:CTX, 0:CTX], sq, start=True, stop=True).then_inc(var_ready.up(), 1)

        @block.vector
        def _(dve):
            dve.wait_ge(mean_ready.sem, mean_ready.at(1))
            seq(dve, step, nc.vector.scalar_tensor_tensor(out=d, in0=c.bank[0][0:CTX, 0:n], scalar=-1.0 / CTX, in1=ctxT, op0=ALU.mult, op1=ALU.add))
            nc.vector.tensor_tensor(sq, d, d, ALU.mult).then_inc(sq_ready.up(), 1)
            dve.wait_ge(var_ready.sem, var_ready.at(1))
            nc.vector.tensor_scalar(sq, c.bank[1][0:CTX, 0:n], 1.0 / CTX, 1e-5, ALU.mult, ALU.add).then_inc(sq_ready.up(), 1)
            dve.wait_ge(r_ready.sem, r_ready.at(1))
            seq(dve, step, nc.vector.tensor_tensor(d, d, r, ALU.mult))
            nc.vector.tensor_scalar(c.ctxnT[:], d, c.col(A + "lny_g")[0:CTX], c.col(A + "lny_b")[0:CTX], ALU.mult, ALU.add)

        @block.gpsimd
        def _(pool):
            pool.wait_ge(sq_ready.sem, sq_ready.at(2))
            nc.gpsimd.tensor_tensor(r, sq, c.minus_half[0:CTX, 0:1].broadcast_to([CTX, n]), ALU.pow).then_inc(r_ready.up(), 1)


def layer3_ffn(c, out_dram):
    nc, step = c.nc, counter(c, "dve_step")
    xp, xr, xk = c.big1(0, TOK), c.big1(TOK, TOK), c.big1(2 * TOK, TOK)
    r, k2 = c.big1(3 * TOK, TOK), c.big1(4 * TOK, TOK)
    one_minus = c.small[:, 4:6]
    with nc.Block() as block:
        @block.vector
        def _(dve):
            for b in range(B):
                nc.vector.memset(xp[:, b * S:b * S + 1], 0.0)
                last = nc.vector.tensor_copy(xp[:, b * S + 1:(b + 1) * S], c.XT[:, b * S:(b + 1) * S - 1])
            for i, n in enumerate(("L3_ffn_mu_r", "L3_ffn_mu_k")):
                last = nc.vector.tensor_scalar(one_minus[:, i:i + 1], c.col(n), -1.0, 1.0, ALU.mult, ALU.add)
            seq(dve, step, last)
            nc.vector.tensor_scalar(xr, xp, one_minus[:, 0:1], None, ALU.mult)
            seq(dve, step, nc.vector.tensor_scalar(xk, xp, one_minus[:, 1:2], None, ALU.mult))
            for n, d in (("L3_ffn_mu_r", xr), ("L3_ffn_mu_k", xk)):
                nc.vector.scalar_tensor_tensor(out=d, in0=c.XT[:], scalar=c.col(n), in1=d, op0=ALU.mult, op1=ALU.add)
    h = lambda ap, half: ap[:, half * S:(half + 1) * S]

    def square_relu(d):
        def emit(dve, bank, step):
            seq(dve, step, nc.vector.tensor_scalar(d, bank, 0.0, None, ALU.max))
            return nc.vector.tensor_tensor(d, d, d, ALU.mult)
        return emit
    units = []
    for half in range(2):
        units.append(([(c.m("L3f_WkT"), h(xk, half))], P, S, "dve", square_relu(h(k2, half))))
        units.append(([(c.m("L3f_WrT"), h(xr, half))], P, S, "act", act_copy(c, h(r, half), func=ACT.Sigmoid)))
    matmul_stream(c, units)

    def gate(half):
        return lambda dve, bank, step: nc.vector.tensor_tensor(h(c.outT, half), bank, h(r, half), ALU.mult)
    matmul_stream(c, [([(c.m("L3f_WvT"), h(k2, half))], P, S, "dve", gate(half)) for half in range(2)])
    add_and_norm(c, add=turn_back(c, c.outT), out=c.XN, store=out_dram)



def decoder(nc, dram, out_dram, q_dram, k_dram):
    with ExitStack() as ctx:
        c = Core(nc, ctx)
        c.dram, c.q_dram, c.k_dram = dram, q_dram, k_dram
        tiles = lambda t: t[:].rearrange("p (t f) -> p t f", t=NT)
        X, XT, XN, total = (c.sb(n, [P, TOK]) for n in ("x", "xT", "normed", "total"))
        c.X, c.XT, c.XN, c.total = tiles(X), XT, tiles(XN), tiles(total)
        c.rest_q, c.rest_k = XN[:], total[:]
        c.big = [c.sb("big1", [P, 8 * TOK]), c.sb("big2", [P, 4 * TOK]), c.sb("big3", [P, 8 * TOK])]
        c.VH = c.sb("v_heads", [P, NT * HEADS * 33])
        moe_w, late_w = c.sb("moe_weights", [P, max(width(p) for p in ("moe0", "moe1"))]), c.sb("late_weights", [P, 4 * TOK])
        mid_w = c.sb("mid_weights", [P, width("mid")])
        c.rows, c.cols = c.sb("rows", [P, P * len(row_names())]), c.sb("cols", [P, sum(n for _, n in col_names())])
        c.memories = {"const": (c.big[1], 0), "first": (late_w, width("turned")), "early": (late_w, width("turned") + width("first")), "moe0": (moe_w, 0),
                      "moe1": (moe_w, 0), "moe2": (moe_w, 0), "l3": (moe_w, width("moe2")), "mid": (mid_w, 0),
                      "turned": (late_w, 0), "l2x": (late_w, 0), "l3x": (moe_w, 0)}
        c.matrices = {}
        for pack, (memory, at) in c.memories.items():
            for name, rows, cols in MATRICES[pack]:
                c.matrices[name] = memory[0:rows, at:at + cols]
                at += cols
        c.loaded = {pack: ctx.enter_context(nc.semaphore(f"loaded_{pack}")) for pack in c.memories}
        vectors_loaded = ctx.enter_context(nc.semaphore("vectors_loaded"))
        x_loaded = ctx.enter_context(nc.semaphore("x_loaded"))
        c.stored = ctx.enter_context(nc.semaphore("out_stored"))
        c.stored_parts, c.loaded_heads = (ctx.enter_context(nc.semaphore(n)) for n in ("parts_in_dram", "heads_loaded_dma"))
        c.nparts = c.nheads = 0

        c.ident, c.key_later, c.up_to, c.ones = (c.sb(n, [P, P]) for n in ("ident", "key_later", "up_to", "ones"))
        c.ident_bf = c.sb("ident_bf", [P, P], BF16)
        c.before_key, c.after_query = (c.sb(n, [P, S], BF16) for n in ("before_key", "after_query"))
        pick = c.sb("pick", [8, 4 * P], BF16)
        c.pick = pick[:].rearrange("p (j m) -> p j m", j=4)
        c.pick_apart = c.sb("pick_apart", [P, P], BF16)
        c.pick_id = c.sb("pick_id", [96, 32], BF16)
        c.only_ones, c.minus_half = c.sb("only_ones", [P, 33]), c.sb("minus_half", [P, 8])

        c.NE = 3
        E, EM = c.sb("weights", [P, c.NE * S]), c.sb("masked_weights", [P, c.NE * P])
        c.E, c.EM = ([t[:, i * n:(i + 1) * n] for i in range(c.NE)] for t, n in ((E, S), (EM, P)))
        c.OT = c.sb("heads_out", [P, 2 * S])[:].rearrange("p (z t) -> p z t", z=2)
        c.MX = c.sb("maxima", [P, ST * 4])[:].rearrange("p (t j) -> p t j", t=ST)
        c.NM = c.sb("negmax", [P, 2 * ST * P], BF16)[:].rearrange("p (z t r) -> p z t r", z=2, t=ST)
        c.NMT = c.sb("negmaxT", [P, 2 * S], BF16)[:].rearrange("p (z t) -> p z t", z=2)
        c.RC = c.sb("reciprocals", [P, 2 * ST * 4])[:].rearrange("p (z t j) -> p z t j", z=2, t=ST)

        c.stats = c.sb("stats", [P, NT * 6])[:].rearrange("p (t s) -> p t s", t=NT)
        c.mv = c.sb("mean_var", [P, NT * 2])[:].rearrange("p (t s) -> p t s", t=NT)
        c.rstd, c.amax = c.sb("rstd", [P, NT]), c.sb("amax", [P, NT])[:]
        c.small, c.negA = c.sb("small", [P, 8]), c.sb("negA", [P, 16])[:]
        c.small8 = c.sb("small8", [P, 8 * NT])[:].rearrange("p (i t) -> p i t", i=8)
        c.ckT = c.sb("ctx_kT", [P, B * SK])
        bf = lambda ap: ap.bitcast(BF16)
        spare = width("turned") + width("first") + width("early")
        late = lambda a, n: late_w[:, spare + a:spare + a + n]
        c.signT = bf(late(0, P)).rearrange("p (z m) -> p z m", z=2)
        c.tern = bf(late(P, P)).rearrange("p (z m) -> p z m", z=2)
        c.alpha = late(2 * P, 2 * P).rearrange("p (z m) -> p z m", z=2)
        c.headmat = c.sb("headmat", [P, P])[:]

        c.Y8f, c.Y8 = c.big2(3 * TOK, TOK), c.big2(3 * TOK, TOK).rearrange("p (t f) -> p t f", t=NT)
        c.q_parts = bf(c.big2(0, 1536)).rearrange("p (z t) -> p z t", z=3)
        c.k_parts = bf(c.big2(1536, 1536)).rearrange("p (z t) -> p z t", z=3)
        c.rest2 = c.big2(0, P)
        c.qk32 = c.big1(0, 2 * TOK).rearrange("p (z t) -> p z t", z=2)
        c.QH, c.KH = (bf(x(0, 8 * TOK)).rearrange("p (h t) -> p h t", h=HEADS) for x in (c.big1, c.big3))
        c.qT, c.yT8 = c.big3(0, TOK), c.big1(0, TOK).rearrange("p (k t) -> p k t", k=1)
        c.q_bf, c.qT_bf = bf(c.big1(4 * TOK, TOK // 2)).rearrange("p (t f) -> p t f", t=NT), bf(c.big1(5 * TOK, TOK // 2))
        c.moe_sg, c.moe_h = (c.big1(i * TOK, TOK).rearrange("p (z t) -> p z t", z=2) for i in (0, 1))
        c.outT = c.big1(2 * TOK, TOK)
        c.cwT = bf(c.big3(0, TOK // 2))[0:96]
        c.cw_parts = bf(c.big3(512, 384)).rearrange("p (t r) -> p t r", t=NT)
        c.cw_rest = c.big3(1024, 256).rearrange("p (t e) -> p t e", t=NT)
        c.rt = c.big3(1280, 6 * 256).rearrange("p (i t e) -> p i t e", i=6, t=NT)
        c.top_v = c.big3(2816, 64).rearrange("p (t k) -> p t k", t=NT)
        c.top_i = c.big3(2880, 64).bitcast(U32).rearrange("p (t k) -> p t k", t=NT)
        c.top_f = c.big3(2944, 64).rearrange("p (t k) -> p t k", t=NT)
        c.pick_flat = bf(c.big3(4096, 1024))[0:96]
        c.x3 = c.big3(7 * TOK, TOK).rearrange("p (t f) -> p t f", t=NT)
        c.ctx_tmp = c.VH[0:CTX, 0:3 * B * SK].rearrange("p (z t) -> p z t", z=3)
        c.ctxnT = c.sb("ctx_normed", [CTX, B * SK])

        psum = c.ps("banks", [P, 8 * 512])
        c.bank = [psum[:, i * 512:(i + 1) * 512] for i in range(8)]
        c.banks_bf = [b[:, 0:256].bitcast(BF16) for b in c.bank]
        c.bank_bf = c.banks_bf[7]
        c.key_stack = bf(c.big2(0, 3 * TOK)).rearrange("p (u z d) -> p u z d", z=6, d=8)
        c.keys = lambda k, a, b: k[:, a:b]

        x_in = dram["x"].rearrange("(t p) f -> p t f", p=P)
        const_ready = counter(c, "const_ready")
        with nc.Block() as block:
            @block.sync
            def _(sp):
                sp.dma_start(c.X[:], x_in).then_inc(x_loaded, 16)
                for pack in ("const", "first"):
                    c.fetch(sp, pack)
                sp.dma_start(c.rows[:], dram["rows"].partition_broadcast(P)).then_inc(vectors_loaded, 16)
                sp.dma_start(c.cols[:], dram["cols"]).then_inc(vectors_loaded, 16)
                for pack in ("mid", "early", "moe0"):
                    c.fetch(sp, pack)
                sp.wait_ge(x_loaded, 16)
                sp.wait_ge(vectors_loaded, 32)
                for pack in ("first", "mid", "early"):
                    sp.wait_ge(c.loaded[pack], 16)

            @block.vector
            def _(dve):
                dve.wait_ge(c.loaded["const"], 16)
                nc.vector.tensor_copy(c.ident[:], c.m("ident"))
                nc.vector.tensor_copy(c.ident_bf[:], c.m("ident"))
                nc.vector.tensor_copy(c.key_later[:], c.m("later"))
                nc.vector.tensor_scalar(c.up_to[:], c.m("later"), -1.0, 1.0, ALU.mult, ALU.add)
                nc.vector.tensor_scalar(c.before_key[:, 0:P], c.m("later"), NEG, None, ALU.mult)
                nc.vector.tensor_scalar(c.after_query[:, S - P:S], c.m("later_t"), NEG, None, ALU.mult)
                nc.vector.tensor_copy(pick[:], c.m("pick"))
                nc.vector.tensor_copy(c.pick_id[:], c.m("pick_id"))
                nc.vector.tensor_copy(c.pick_apart[:], c.m("pick_apart"))

            @block.gpsimd
            def _(pool):
                nc.gpsimd.memset(c.ones[:], 1.0)
                nc.gpsimd.memset(c.before_key[:, P:S], 0.0)
                nc.gpsimd.memset(c.after_query[:, 0:S - P], 0.0)
                nc.gpsimd.memset(c.NM[:], 0.0)
                nc.gpsimd.memset(c.only_ones[:, 0:32], 0.0)
                nc.gpsimd.memset(c.only_ones[:, 32:33], 1.0)
                nc.gpsimd.memset(c.minus_half[:], -0.5)

        stages = [
            lambda: layer0_attention(c),
            lambda: cross_attention_8(c, c.m("L0x_WqT"), c.m("L0x_WkvT")[:, 0:P], c.m("L0x_WkvT")[:, P:2 * P], c.m("L0x_WoT"),
                                      None, None, None, None),
            lambda: (fill_pick(c, P), c.await_loads("moe0"), layer0_moe(c)),
            lambda: layer1_scan(c),
            lambda: cross_attention_8(c, c.m("L1x_Wq"), c.m("L1x_Wk"), c.m("L1x_Wv"), c.m("L1x_Wo"), c.col("L1_xattn_bq"),
                                      c.col("L1_xattn_bk"), c.row("L1_xattn_bv"), c.row("L1_xattn_bo")),
            lambda: (c.await_loads("moe1", "turned"), layer1_ffn(c)),
            lambda: layer2_attention(c),
            lambda: (c.await_loads("l2x"), layer2_cross(c)),
            lambda: (c.await_loads("moe2", "l3"), layer2_moe(c)),
            lambda: layer3_attention(c),
            lambda: (c.await_loads("l3x"), layer3_xattn(c)),
            lambda: layer3_ffn(c, out_dram),
        ]
        for stage in stages:
            stage()



def constants():
    p, f = np.arange(P)[:, None], np.arange(P)[None, :]
    pos = np.arange(S, dtype=np.float32)
    inv4 = (1.0 / 10000.0 ** (np.arange(4, dtype=np.float32) / np.float32(4))).astype(np.float32)
    tile_pos = pos.reshape(ST, P).T
    aq = tile_pos[:, :, None] * inv4
    ak = (16 * (np.arange(P) % 32)[:, None] + np.arange(16)[None, :]).astype(np.float32)[:, :, None] * inv4
    inv32 = (10000.0 ** (-np.arange(0, 64, 2, dtype=np.float32) / 64)).astype(np.float32)
    ticks = inv32[np.arange(P) % 32][:, None] * pos[None, :]
    sign = np.where(np.arange(P) % 64 < 32, -1.0, 1.0)[:, None]
    rows = np.arange(8)[:, None]
    block = np.zeros((P, 36))
    for h in range(4):
        block[32 * h:32 * h + 32, 8 * h:8 * h + 8] = 1.0
        block[32 * h:32 * h + 32, 32 + h] = 1.0
    out = {
        "ident": p == f, "later": p > f, "later_t": f > p,
        "pick": np.concatenate([np.repeat(rows % 4 == j, P, axis=1) for j in range(4)], axis=1),
        "pick_id": np.arange(96)[:, None] % 32 == np.arange(32)[None, :],
        "pick_apart": np.repeat(p % 32 < 2, P, axis=1),
        "same_head": p // 8 == f // 8,
        "iota": np.repeat(np.arange(32)[None, :], P, axis=0),
        "rope_q": np.concatenate([np.cos(aq).reshape(P, -1), np.sin(aq).reshape(P, -1)], axis=1),
        "rope_k": np.concatenate([np.cos(ak).reshape(P, -1), np.sin(ak).reshape(P, -1)], axis=1),
        "cos": np.cos(ticks), "sin": np.sin(ticks) * sign, "block_kv": block,
    }
    return {k: v.astype(np.float32) for k, v in out.items()}


def by_rows(w):
    k = w.shape[0] // P
    return w.reshape(k, P, -1).transpose(1, 0, 2).reshape(P, -1)


def lay_out(a):
    m = constants()
    every = lambda v: np.broadcast_to(v[None, :], (P, v.shape[0]))
    heads8 = lambda u: np.concatenate([u] * HEADS, axis=1)
    m["L0_Wqkv"], m["L0_Wo"] = a["L0_attn_Wqkv_w"], a["L0_attn_Wo_w"]
    m["L0_UT"] = heads8(a["L0_attn_U"].T)
    m["ctxT"] = a["ctx_512"].reshape(B * SK, CTX).T
    m["L0x_WqT"], m["L0x_WkvT"], m["L0x_WoT"] = a["L0_xattn_Wq"].T, a["L0_xattn_Wkv"].T, a["L0_xattn_Wo"].T
    m["L0_gateT"] = np.concatenate([a["L0_ffn_gate_weight"], a["L0_ffn_new_gate_weight"]]).T
    m["gate_bias"] = every(np.concatenate([np.zeros(8, np.float32), a["L0_ffn_gate_bias"]]))
    for n, new in (("w1", "new_w1"), ("w3", "new_w3")):
        w = np.concatenate([a[f"L0_ffn_{n}"], a[f"L0_ffn_{new}"]])
        m[n + "T"] = w.transpose(2, 0, 1).reshape(P, -1)
    w = np.concatenate([a["L0_ffn_w2"], a["L0_ffn_new_w2"]]).transpose(0, 2, 1)
    padded = np.zeros((L0E, 3 * P, P), np.float32)
    padded[:, 0:L0HID] = w
    m["w2T"] = padded.reshape(L0E, 3, P, P).transpose(2, 0, 1, 3).reshape(P, -1)
    m["L1_WdtT"], m["L1_WBT"], m["L1_WCT"], m["L1_A_log"] = a["L1_attn_W_dt"].T, a["L1_attn_W_B"].T, a["L1_attn_W_C"].T, a["L1_attn_A_log"]
    for n in ("Wq", "Wk", "Wv", "Wo"):
        m["L1x_" + n] = a["L1_xattn_" + n]
    m["L1f_router"], m["router_b"] = a["L1_ffn_router_w"], every(a["L1_ffn_router_b"])
    for n in ("WQ", "WK", "WV", "WO"):
        m["L2_" + n] = a["L2_attn_" + n]
    m["L2_WQrT"], m["L2_WKrT"] = heads8(a["L2_attn_WQr"].T), heads8(a["L2_attn_WKr"].T)
    m["L2_routerT"], m["L2_bias"] = a["L2_ffn_router_weight"].T, every(a["L2_ffn_router_bias"])
    m["w1"], m["w2"] = (a["L1_ffn_" + n].transpose(1, 0, 2).reshape(P, -1) for n in ("w1", "w2"))
    m["w3"] = by_rows(a["L1_ffn_w3"].reshape(L1E * L1HID, P))
    m["wq"], m["wk"], m["wv"], m["wo"] = a["L1_ffn_wq"], a["L1_ffn_wk"], a["L1_ffn_wv"], by_rows(a["L1_ffn_wo"])
    swap = lambda w: w.reshape(P, -1, 2, 32)[:, :, ::-1, :].reshape(P, -1)
    m["wqs"], m["wks"] = swap(a["L1_ffn_wq"]), swap(a["L1_ffn_wk"])
    m["L2x_Wq"], m["L2x_Wk"], m["L2x_Wv"], m["L2x_Wo"] = a["L2_xattn_Wq"], a["L2_xattn_Wk"], a["L2_xattn_Wv"], by_rows(a["L2_xattn_Wo"])
    m["gateT"], m["upT"] = (a["L2_ffn_" + n].transpose(2, 0, 1).reshape(P, -1) for n in ("gate_w", "up_w"))
    m["downT"] = by_rows(a["L2_ffn_down_w"].transpose(0, 2, 1).reshape(L2E * L2HID, P))
    m["sgT"], m["suT"], m["sdT"] = (a[f"L2_ffn_shared_{n}_w"].T for n in ("gate", "up", "down"))
    m["L3_wqkvT"] = a["L3_attn_w_qkv"].T
    proj = np.zeros((HEADS, 8, HEADS, 32), np.float32)
    for h in range(HEADS):
        proj[h, :, h, :] = a["L3_attn_proj"][h]
    m["L3_proj"] = proj.reshape(P, 4 * P)
    m["L3_woutT"], m["L3_w1T"], m["L3_w2T"] = a["L3_attn_w_out"].T, a["L3_attn_w1"].T, by_rows(a["L3_attn_w2"].T)
    m["L3f_WrT"], m["L3f_WkT"], m["L3f_WvT"] = a["L3_ffn_W_r"].T, a["L3_ffn_W_k"].T, a["L3_ffn_W_v"].T
    for i in (1, 2):
        x = f"L3_xattn_a{i}_"
        for n in ("wq", "wk", "wv"):
            w = a[x + n]
            m[f"a{i}_{n}"] = w.transpose(1, 0, 2).reshape(w.shape[1], -1)
        m[f"a{i}_li1"], m[f"a{i}_li2"], m[f"a{i}_li3"] = by_rows(a[x + "li1_w"]), a[x + "li2_w"], by_rows(a[x + "li3_w"])

    out = {"x": a["x"].reshape(TOK, P)}
    for pack, names in MATRICES.items():
        whole = np.zeros((P, width(pack)), np.float32)
        at = 0
        for name, rows, cols in names:
            whole[0:rows, at:at + cols] = m[name]
            at += cols
        out[pack] = whole
    out["rows"] = np.concatenate([a[n] for n in row_names()]).reshape(1, -1)
    cols = np.zeros((P, sum(n for _, n in col_names())), np.float32)
    at = 0
    for name, n in col_names():
        v = a[name]
        if v.shape[0] < P:
            cols[0:v.shape[0], at] = v
        else:
            cols[:, at:at + n] = v.reshape(n, P).T
        at += n
    out["cols"] = cols
    return out


def build(nc, arrays):
    dram = {name: nc.dram_tensor("in_" + name, v.shape, F32, kind="ExternalInput").ap() for name, v in arrays.items()}
    out = nc.dram_tensor("out", (TOK, P), F32, kind="ExternalOutput").ap()
    q_dram = nc.dram_tensor("q_parts", (P, 3, TOK), BF16, kind="Internal").ap()
    k_dram = nc.dram_tensor("k_parts", (P, 3, TOK), BF16, kind="Internal").ap()
    decoder(nc, dram, out.rearrange("(t p) f -> p t f", p=P), q_dram, k_dram)


def kernel(**inputs):
    import concourse.bacc as bacc
    from concourse.bass_utils import run_bass_kernel_spmd

    arrays = {k: np.ascontiguousarray(v) for k, v in lay_out({k: np.asarray(v) for k, v in inputs.items()}).items()}
    nc = bacc.Bacc("TRN2", target_bir_lowering=False, num_devices=1)
    build(nc, arrays)
    r = run_bass_kernel_spmd(nc, [{"in_" + k: v for k, v in arrays.items()}], core_ids=[0])
    return r.results[0]["out"].reshape(B, S, P)
```

```python
from contextlib import ExitStack

import numpy as np
import concourse.bass as bass
from concourse import mybir
from concourse.alu_op_type import AluOpType as ALU

ACT = mybir.ActivationFunctionType
F32 = mybir.dt.float32
BF16 = mybir.dt.bfloat16
U32 = mybir.dt.uint32
AX_X = mybir.AxisListType.X

P = 128
B, S = 2, 512
TOK = B * S
NT = TOK // P
ST = S // P
HEADS = 16
SK = 77
CTX = 64
NEG = -1.0e30
ROUND = 1.5 * 2.0 ** 23


class Signal:

    def __init__(self, sem):
        self.sem, self.base, self.sent = sem, 0, 0

    def up(self, n=1):
        self.sent += n
        return self.sem

    def at(self, n):
        return self.base + n


def width(pack):
    return sum(cols for _, _, cols in MATRICES[pack])


class Core:

    def __init__(self, nc, ctx):
        self.nc, self.ctx, self.counters = nc, ctx, {}

    def sb(self, name, shape, dt=F32):
        return self.ctx.enter_context(self.nc.sbuf_tensor(name, shape, dt))

    def ps(self, name, shape, dt=F32):
        return self.ctx.enter_context(self.nc.psum_tensor(name, shape, dt))

    def big1(self, a, n):
        return self.big[0][:, a:a + n]

    def big2(self, a, n):
        return self.big[1][:, a:a + n]

    def big3(self, a, n):
        return self.big[2][:, a:a + n]

    def m(self, name):
        return self.matrices[name]

    def row(self, name):
        i = row_names().index(name)
        return self.rows[:, i * P:(i + 1) * P]

    def col(self, name, n=1):
        at = 0
        for other, k in col_names():
            if other == name:
                return self.cols[:, at:at + n]
            at += k
        raise KeyError(name)

    def fetch(self, sp, pack):
        memory, at = self.memories[pack]
        n = width(pack)
        sp.dma_start(memory[:, at:at + n], self.dram[pack]).then_inc(self.loaded[pack], 16)

    def fetcher(self, *packs):
        def program(sp):
            for pack in packs:
                self.fetch(sp, pack)
        return program

    def await_loads(self, *packs):
        with self.nc.Block() as block:
            @block.sync
            def _(sp):
                for pack in packs:
                    sp.wait_ge(self.loaded[pack], 16)



def counter(c, name):
    if name not in c.counters:
        c.counters[name] = Signal(c.ctx.enter_context(c.nc.semaphore(name)))
    s = c.counters[name]
    s.base = s.sent
    return s


def seq(eng, step, ins):
    ins.then_inc(step.up(), 1)
    eng.wait_ge(step.sem, step.sent)



def row_names():
    return ["L0_attn_Wqkv_b", "L1_xattn_bv", "L1_xattn_bo", "L2_attn_bV", "L2_attn_bO",
            "L2_xattn_bo", "L3_attn_b_out", "L3_attn_gamma", "L3_attn_beta", "L3_attn_b2",
            "L3_xattn_ln1_g", "L3_xattn_ln1_b", "L3_xattn_ln2_g", "L3_xattn_ln2_b",
            "L3_xattn_a1_li1_b", "L3_xattn_a1_li3_b", "L3_xattn_a2_li1_b", "L3_xattn_a2_li3_b"]


def col_names():
    return [("L1_attn_gamma", 1), ("L1_attn_beta", 1), ("L1_attn_b_dt", 1), ("L1_attn_D_param", 1),
            ("L1_xattn_bq", 1), ("L1_xattn_bk", 1), ("L1_ffn_g1", 1), ("L1_ffn_g2", 1),
            ("L2_attn_bQ", 1), ("L2_attn_bK", 1), ("L3_attn_b1", 4),
            ("L3_xattn_a1_lnx_g", 1), ("L3_xattn_a1_lnx_b", 1), ("L3_xattn_a1_lny_g", 1),
            ("L3_xattn_a1_lny_b", 1), ("L3_xattn_a1_ln3_g", 1), ("L3_xattn_a1_ln3_b", 1),
            ("L3_xattn_a1_li2_b", 4), ("L3_xattn_a2_lnx_g", 1), ("L3_xattn_a2_lnx_b", 1),
            ("L3_xattn_a2_lny_g", 1), ("L3_xattn_a2_lny_b", 1), ("L3_xattn_a2_ln3_g", 1),
            ("L3_xattn_a2_ln3_b", 1), ("L3_xattn_a2_li2_b", 4), ("L3_ffn_mu_r", 1), ("L3_ffn_mu_k", 1)]


def chunks(n):
    return [(a, min(P, n - a)) for a in range(0, n, P)]


L0E, L0HID = 9, 352
L1E, L1HID = 8, 256
L2E, L2HID = 32, 64
MATRICES = {
    "first": [("L0_Wqkv", P, P), ("L0_Wo", P, P), ("L0_UT", 32, P), ("rope_q", P, 2 * ST * 4), ("rope_k", P, 2 * 64)],
    "early": [("L0x_WqT", P, P), ("L0x_WkvT", CTX, 2 * P), ("L0x_WoT", P, P), ("L0_gateT", P, L0E), ("gate_bias", P, L0E)],
    "moe0": [("w1T", P, L0E * L0HID), ("w3T", P, L0E * L0HID), ("w2T", P, L0E * 3 * P)],
    "const": [("ident", P, P), ("later", P, P), ("later_t", P, P), ("pick_id", 96, 32), ("pick", P, 4 * P)],
    "mid": [("iota", P, 32), ("same_head", P, P), ("ctxT", CTX, B * SK), ("L1_WdtT", P, P), ("L1_WBT", P, 16), ("L1_WCT", P, 16), ("L1_A_log", P, 16),
            ("L1x_Wq", P, P), ("L1x_Wk", CTX, P), ("L1x_Wv", CTX, P), ("L1x_Wo", P, P),
            ("L1f_router", P, L1E), ("router_b", P, L1E),
            ("L2_WQ", P, P), ("L2_WK", P, P), ("L2_WV", P, P), ("L2_WO", P, P),
            ("L2_WQrT", 16, P), ("L2_WKrT", 16, P), ("L2_routerT", P, L2E), ("L2_bias", P, L2E)],
    "moe1": [("w1", P, L1E * L1HID), ("w2", P, L1E * L1HID), ("w3", P, L1E * 2 * P),
             ("wq", P, 1024), ("wk", P, 256), ("wv", P, 256), ("wo", P, 8 * P)],
    "turned": [("wqs", P, 1024), ("wks", P, 256), ("cos", P, S), ("sin", P, S)],
    "l2x": [("L2x_Wq", P, 1024), ("L2x_Wk", CTX, 1024), ("L2x_Wv", CTX, 1024), ("L2x_Wo", P, 8 * P)],
    "moe2": [("gateT", P, L2E * L2HID), ("upT", P, L2E * L2HID), ("downT", P, 16 * P),
             ("sgT", P, P), ("suT", P, P), ("sdT", P, P)],
    "l3": [("L3_wqkvT", P, 3 * P), ("L3_proj", P, 4 * P), ("L3_woutT", P, P), ("L3_w1T", P, 4 * P),
           ("L3_w2T", P, 4 * P), ("L3f_WrT", P, P), ("L3f_WkT", P, P), ("L3f_WvT", P, P),
           ("block_kv", P, 36)],
    "l3x": [(f"a{i}_{n}", r, c) for i in (1, 2) for n, r, c in
            (("wq", P, 512), ("wk", P if i == 1 else CTX, 512), ("wv", P if i == 1 else CTX, 512),
             ("li1", P, 4 * P), ("li2", P, 4 * P), ("li3", P, 4 * P))],
}



def matmul_stream(c, units, load=None):
    nc = c.nc
    product_ready, act_freed, dve_freed = counter(c, "product_ready"), counter(c, "act_freed"), counter(c, "dve_freed")
    dve_step = counter(c, "dve_step")
    freed = []
    count = {"act": 0, "dve": 0}
    for u in units:
        count[u[3]] += 1
        freed.append((u[3], count[u[3]]))

    def bank(u):
        return c.bank[u % 8][0:units[u][1], 0:units[u][2]]

    with nc.Block() as block:
        if load:
            block.sync(load)

        @block.tensor
        def _(pe):
            for u, (products, _, _, _, _) in enumerate(units):
                if u >= 8:
                    who, n = freed[u - 8]
                    s = act_freed if who == "act" else dve_freed
                    pe.wait_ge(s.sem, s.at(n))
                for k, (lhsT, rhs) in enumerate(products):
                    last = nc.tensor.matmul(bank(u), lhsT, rhs, start=(k == 0), stop=(k == len(products) - 1))
                last.then_inc(product_ready.up(), 1)

        @block.scalar
        def _(act):
            for u, unit in enumerate(units):
                if unit[3] == "act":
                    act.wait_ge(product_ready.sem, product_ready.at(u + 1))
                    unit[4](act, bank(u)).then_inc(act_freed.up(), 1)

        @block.vector
        def _(dve):
            for u, unit in enumerate(units):
                if unit[3] == "dve":
                    dve.wait_ge(product_ready.sem, product_ready.at(u + 1))
                    unit[4](dve, bank(u), dve_step).then_inc(dve_freed.up(), 1)


def act_copy(c, dst, bias=None, scale=1.0, func=None):
    def emit(act, bank):
        if bias is None and func is None and isinstance(scale, float):
            return c.nc.scalar.copy(dst, bank)
        return c.nc.scalar.activation(dst, bank, func or ACT.Identity, bias=0.0 if bias is None else bias, scale=scale)
    return emit


def dve_copy(c, dst, bias=None, row=None):
    def emit(dve, bank, step):
        if row is not None:
            return c.nc.vector.tensor_tensor(dst, bank, row, ALU.add)
        if bias is not None:
            return c.nc.vector.tensor_scalar(dst, bank, bias, None, ALU.add)
        return c.nc.vector.tensor_copy(dst, bank)
    return emit


def halves(c, products, rows, dst, bias=None, first="act"):
    other = "dve" if first == "act" else "act"
    out = []
    for half, who in ((0, first), (1, other)):
        d = dst[:, half * S:(half + 1) * S]
        emit = act_copy(c, d, bias=bias) if who == "act" else dve_copy(c, d, bias=bias)
        out.append((products(half), rows, S, who, emit))
    return out


def add_and_norm(c, add=None, bias=None, base=None, total=None, norm="ln", eps=1e-5, out=None, rows=None,
                 turned=(), load=None, store=None):
    nc = c.nc
    base = c.X if base is None else base
    total = base if total is None else total
    sum_ready, sum_used, stats_ready, rstd_ready = (counter(c, n) for n in ("sum_ready", "sum_used", "stats_ready", "rstd_ready"))
    norm_ready, turned_ready, turned_used, stored = (counter(c, n) for n in ("norm_ready", "turned_ready", "turned_used", "stored"))
    dve_step, pool_step = counter(c, "dve_step"), counter(c, "pool_step")
    stats, mv, rstd = c.stats, c.mv, c.rstd
    H = NT // 2

    with nc.Block() as block:
        if load:
            block.sync(load)

        @block.tensor
        def _(pe):
            if add:
                for t in range(NT):
                    last = add(pe, t, c.bank[t // H][:, t % H * P:(t % H + 1) * P])
                    if t % H == H - 1:
                        last.then_inc(sum_ready.up(), 1)
            if turned:
                for half in range(2):
                    pe.wait_ge(norm_ready.sem, norm_ready.at(half + 1))
                    for k in range(H):
                        last = nc.tensor.transpose(c.bank[2 + half][:, k * P:(k + 1) * P], out[:, half * H + k, :], c.ident[:])
                    last.then_inc(turned_ready.up(), 1)

        @block.vector
        def _(dve):
            for half in range(2):
                ts = slice(half * H, (half + 1) * H)
                if add:
                    dve.wait_ge(sum_ready.sem, sum_ready.at(half + 1))
                    psum = c.bank[half][:, :].rearrange("p (t f) -> p t f", t=H)
                    seq(dve, dve_step, nc.vector.tensor_tensor(total[:, ts, :], psum, base[:, ts, :], ALU.add))
                    if bias is not None:
                        seq(dve, dve_step, nc.vector.tensor_tensor(
                            total[:, ts, :], total[:, ts, :], bias.unsqueeze(1).broadcast_to([P, H, P]), ALU.add))
                if norm is None:
                    continue
                for k in range(half * H, (half + 1) * H):
                    last = nc.vector.bn_stats(stats[:, k, :], total[:, k, :])
                seq(dve, dve_step, last)
                for k in range(half * H, (half + 1) * H):
                    last = nc.vector.bn_aggr(mv[:, k, :], stats[:, k, :])
                seq(dve, dve_step, last)
                if norm == "rms":
                    seq(dve, dve_step, nc.vector.tensor_tensor(mv[:, ts, 0], mv[:, ts, 0], mv[:, ts, 0], ALU.mult))
                    seq(dve, dve_step, nc.vector.tensor_tensor(mv[:, ts, 1], mv[:, ts, 1], mv[:, ts, 0], ALU.add))
                nc.vector.tensor_scalar(mv[:, ts, 1], mv[:, ts, 1], eps, None, ALU.add).then_inc(stats_ready.up(), 1)
            if norm is None:
                return
            for half in range(2):
                ts = slice(half * H, (half + 1) * H)
                dve.wait_ge(rstd_ready.sem, rstd_ready.at(half + 1))
                for k in range(half * H, (half + 1) * H):
                    if norm == "rms":
                        last = nc.vector.tensor_scalar(out[:, k, :], total[:, k, :], rstd[:, k:k + 1], None, ALU.mult)
                    else:
                        last = nc.vector.tensor_scalar(out[:, k, :], total[:, k, :], mv[:, k, 0:1], rstd[:, k:k + 1],
                                                       ALU.subtract, ALU.mult)
                if rows:
                    g, b = (r.unsqueeze(1).broadcast_to([P, H, P]) for r in rows)
                    seq(dve, dve_step, last)
                    seq(dve, dve_step, nc.vector.tensor_tensor(out[:, ts, :], out[:, ts, :], g, ALU.mult))
                    last = nc.vector.tensor_tensor(out[:, ts, :], out[:, ts, :], b, ALU.add)
                last.then_inc(norm_ready.up(), 1)

        @block.gpsimd
        def _(pool):
            if norm is None:
                return
            for half in range(2):
                pool.wait_ge(stats_ready.sem, stats_ready.at(half + 1))
                nc.gpsimd.tensor_tensor(rstd[:, half * H:(half + 1) * H], mv[:, half * H:(half + 1) * H, 1],
                                        c.minus_half[:, 0:H], ALU.pow).then_inc(rstd_ready.up(), 1)

        @block.scalar
        def _(act):
            for half in range(2 if turned else 0):
                act.wait_ge(turned_ready.sem, turned_ready.at(half + 1))
                for dst, scale, b in turned:
                    d = dst[:, half * S:(half + 1) * S]
                    if scale is None:
                        nc.scalar.copy(d, c.bank[2 + half][:, :])
                    else:
                        nc.scalar.activation(d, c.bank[2 + half][:, :], ACT.Identity, bias=0.0 if b is None else b, scale=scale)
            if store is not None:
                for half in range(2):
                    act.wait_ge(norm_ready.sem, norm_ready.at(half + 1))
                    act.dma_start(store[:, half * H:(half + 1) * H, :], out[:, half * H:(half + 1) * H, :]).then_inc(c.stored, 16)
                act.wait_ge(c.stored, 32)


def turn(c, src, ntiles, cols, dst):
    nc = c.nc
    turned_ready, act_freed, dve_freed = counter(c, "turned_ready"), counter(c, "act_freed"), counter(c, "dve_freed")
    units = [(k, t) for k in range(cols // P) for t in range(0, ntiles, 4)]

    with nc.Block() as block:
        @block.tensor
        def _(pe):
            for u, (k, t) in enumerate(units):
                if u >= 8:
                    s = dve_freed if u % 2 else act_freed
                    pe.wait_ge(s.sem, s.at((u - 8) // 2 + 1))
                for i in range(4):
                    last = nc.tensor.transpose(c.bank[u % 8][:, i * P:(i + 1) * P], src[:, t + i, k * P:(k + 1) * P], c.ident[:])
                last.then_inc(turned_ready.up(), 1)

        @block.scalar
        def _(act):
            for u, (k, t) in enumerate(units):
                if u % 2 == 0:
                    act.wait_ge(turned_ready.sem, turned_ready.at(u + 1))
                    nc.scalar.copy(dst[:, k, t * P:(t + 4) * P], c.bank[u % 8][:, :]).then_inc(act_freed.up(), 1)

        @block.vector
        def _(dve):
            for u, (k, t) in enumerate(units):
                if u % 2:
                    dve.wait_ge(turned_ready.sem, turned_ready.at(u + 1))
                    nc.vector.tensor_copy(dst[:, k, t * P:(t + 4) * P], c.bank[u % 8][:, :]).then_inc(dve_freed.up(), 1)


def attention(c, key_tiles, dk, operands, vop, scale, Y, mask=None, load=None, stacks=None):
    nc = c.nc
    G = 4
    turned = dk == 8
    HB = 2 if dk == 64 else 4
    W = P // HB
    M = dk + 1 if turned else dk
    nkt, klen = len(key_tiles), sum(key_tiles)
    groups = [(b, h) for b in range(B) for h in range(0, HEADS, G)]
    rounds = [(g, jb, i) for g in range(len(groups)) for jb in range(G // HB) for i in range(nkt)]
    per_group = G // HB * nkt
    pairs = HB // 2
    nbanks = len(rounds) // nkt
    packed = ST * klen <= S
    units = [(j, tl) for j in range(0, G, 2) for tl in ([list(range(ST))] if packed else [[t] for t in range(ST)])]
    U = len(units)
    per_round = U // per_group
    NU = U * len(groups)
    NEP = 4
    SA = c.banks[:, 0:2, :]
    SC = [c.banks[:, 2:4, :], c.banks[:, 4:6, :]]
    OV, DEN = c.bank[6], c.bank[7]
    NB = c.banks_bf[0]
    (raw_ready, max_ready, negmax_ready, negmax_turned, negmax_moved, score_ready, exp_ready, value_ready,
     out_moved, out_turned, out_normed, masked_ready, cleared, dve_step) = (counter(c, n) for n in (
         "raw_ready", "max_ready", "negmax_ready", "negmax_turned", "negmax_moved", "score_ready", "exp_ready",
         "value_ready", "out_moved", "out_turned", "out_normed", "masked_ready", "cleared", "dve_step"))
    E, EM, OT, MX, RC = c.E, c.EM, c.OT, c.MX, c.RC
    NM = c.NM.rearrange("p z t (j r) -> p z t j r", j=G)
    if stacks:
        operands = stacks.operands

    def start(i):
        return i * P if mask == "causal" else 0

    def last_key(t):
        return (t + 1) * P if mask == "causal" else klen

    def raw_scores(pe, n):
        g, (j0, tl) = n // U, units[n % U]
        if n >= 1:
            pe.wait_ge(max_ready.sem, max_ready.at(n))
        if n >= U and n % U == 0:
            pe.wait_ge(negmax_moved.sem, negmax_moved.at(n // U))
        if stacks and n % U == 0:
            pe.wait_ge(*stacks.first_loaded(g))
        for k, t in enumerate(tl):
            for x in range(2):
                b, h = groups[g][0], groups[g][1] + j0 + x
                dst = SA[:, x, k * klen:k * klen + last_key(t)]
                products = operands(b, h)[:1] if stacks else operands(b, h)
                for m, (q, keys) in enumerate(products):
                    last = nc.tensor.matmul(dst, q[:, t * P:(t + 1) * P], keys[:, 0:last_key(t)],
                                            start=(m == 0), stop=(mask != "causal" and m == len(products) - 1))
            if mask == "causal":
                for x in range(2):
                    last = nc.tensor.matmul(SA[:, x, 0:last_key(t)], c.ident_bf[:], c.after_query[:, S - last_key(t):S],
                                            start=False, stop=True)
        last.then_inc(raw_ready.up(), 1)

    def turn_negmax(pe, g):
        pe.wait_ge(negmax_ready.sem, negmax_ready.at(g + 1))
        for t in range(ST):
            last = nc.tensor.transpose(NB[:, t * P:(t + 1) * P], c.NM[:, g % 2, t, :], c.ident_bf[:])
        last.then_inc(negmax_turned.up(), 1)

    def scores(pe, r):
        g, jb, i = rounds[r]
        b, ks, n0 = groups[g][0], key_tiles[i], start(i)
        heads = [(jb * HB + x, groups[g][1] + jb * HB + x) for x in range(HB)]
        if r % per_group == 0:
            pe.wait_ge(negmax_moved.sem, negmax_moved.at(g + 1))
            if stacks:
                pe.wait_ge(*stacks.second_loaded(g))
        dst = []
        for x in range(HB):
            pair = r * pairs + x // 2
            if x % 2 == 0 and pair >= 2:
                pe.wait_ge(exp_ready.sem, exp_ready.at(pair - 1))
            dst.append(SC[pair % 2][0:ks, x % 2, n0:S])
        for x, (j, h) in enumerate(heads):
            for m, (q, keys) in enumerate(operands(b, h)):
                nc.tensor.matmul(dst[x], keys[:, i * P:i * P + ks], q[:, n0:S], start=(m == 0), stop=False)
        for x, (j, h) in enumerate(heads):
            last = nc.tensor.matmul(dst[x], c.pick[:, j, 0:ks], c.NMT[:, g % 2, n0:S], start=False, stop=(mask != "causal"))
            if mask != "causal" and x % 2:
                last.then_inc(score_ready.up(), 1)
        if mask == "causal":
            for x in range(HB):
                last = nc.tensor.matmul(dst[x], c.ident_bf[:], c.before_key[:, 0:S - n0], start=False, stop=True)
                if x % 2:
                    last.then_inc(score_ready.up(), 1)

    def values(pe, r):
        g, jb, i = rounds[r]
        b, ks, n0, n = groups[g][0], key_tiles[i], start(i), r // nkt
        pe.wait_ge(exp_ready.sem, exp_ready.at((r + 1) * pairs))
        if i == 0 and n:
            pe.wait_ge(out_moved.sem, out_moved.at(n))
        if r == 0 and turned:
            pe.wait_ge(cleared.sem, cleared.at(1))
        heads = [(W * x, groups[g][1] + jb * HB + x, E[(r * pairs + x // 2) % NEP][:, x % 2, :],
                  EM[(r * pairs + x // 2) % NEP][:, x % 2, :]) for x in range(HB)]
        first, end = i == 0, i == nkt - 1
        if mask == "future":
            if first:
                nc.tensor.matmul(OV[:, :], c.zeros_bf[:], c.after_query[:, :], start=True, stop=False, skip_group_check=True)
            else:
                for row, h, e, _ in heads:
                    nc.tensor.matmul(OV[row:row + M, 0:i * P], vop(b, h, i), e[0:ks, 0:i * P], start=False, stop=False,
                                     skip_group_check=True)
        else:
            for row, h, e, _ in heads:
                last = nc.tensor.matmul(OV[row:row + M, n0:S], vop(b, h, i), e[0:ks, n0:S], start=first, stop=end)
        if not turned:
            for row, h, e, _ in heads:
                last = nc.tensor.matmul(DEN[row:row + W, n0:S], c.ones[0:ks, 0:W], e[0:ks, n0:S], start=first, stop=end)
        if mask == "future":
            pe.wait_ge(masked_ready.sem, masked_ready.at((r + 1) * pairs))
            for row, h, e, em in heads:
                last = nc.tensor.matmul(OV[row:row + M, i * P:(i + 1) * P], vop(b, h, i), em, start=False, stop=False,
                                        skip_group_check=True)
            if end:
                last = nc.tensor.matmul(OV[:, :], c.zeros_bf[:], c.after_query[:, :], start=False, stop=True, skip_group_check=True)
        last.then_inc(value_ready.up(), 1)

    def turn_out(pe, n):
        pe.wait_ge(out_moved.sem, out_moved.at(n + 1))
        if n >= 1:
            pe.wait_ge(out_normed.sem, out_normed.at(n))
        for t in range(ST):
            last = nc.tensor.transpose(DEN[:, t * P:(t + 1) * P], OT[:, n % 2, t * P:(t + 1) * P], c.ident[:])
        last.then_inc(out_turned.up(), 1)

    def reduce_max(dve, n):
        j0, tl = units[n % U]
        dve.wait_ge(raw_ready.sem, raw_ready.at(n + 1))
        if packed:
            src = SA[:, :, 0:ST * klen].rearrange("p x (t m) -> p x t m", t=ST)
            dst = MX[:, j0:j0 + 2, :]
        else:
            src, dst = SA[:, :, 0:last_key(tl[0])], MX[:, j0:j0 + 2, tl[0]]
        nc.vector.tensor_reduce(dst, src, AX_X, ALU.max).then_inc(max_ready.up(), 1)

    def negmax(dve, g):
        dve.wait_ge(max_ready.sem, max_ready.at((g + 1) * U))
        if g >= 2:
            dve.wait_ge(negmax_turned.sem, negmax_turned.at(g - 1))
        m = MX.rearrange("p j t -> p t j")
        hi, lo = NM[:, g % 2, :, :, 0], NM[:, g % 2, :, :, 1]
        seq(dve, dve_step, nc.vector.tensor_scalar(hi, m, -1.0, None, ALU.mult))
        last = nc.vector.scalar_tensor_tensor(out=lo, in0=m, scalar=-1.0, in1=hi, op0=ALU.mult, op1=ALU.subtract)
        last.then_inc(negmax_ready.up(), 1)

    def norm_turned(dve, n):
        dve.wait_ge(out_turned.sem, out_turned.at(n + 1))
        b, h = groups[n][0], groups[n][1]
        tr = DEN[:, :].rearrange("p (t j w) -> p t j w", t=ST, j=HB)
        seq(dve, dve_step, nc.vector.reciprocal(RC[:, n % 2], tr[:, :, :, dk]))
        dst = Y[:, b * ST:(b + 1) * ST, h * dk:(h + HB) * dk].rearrange("p t (j d) -> p t j d", j=HB)
        nc.vector.tensor_tensor(dst, tr[:, :, :, 0:dk], RC[:, n % 2].unsqueeze(3).broadcast_to([P, ST, HB, dk]),
                                ALU.mult).then_inc(out_normed.up(), 1)

    def norm_in_place(dve, n):
        dve.wait_ge(value_ready.sem, value_ready.at((n + 1) * nkt))
        g, jb, _ = rounds[n * nkt]
        b, h = groups[g][0], groups[g][1] + jb * HB
        seq(dve, dve_step, nc.vector.reciprocal(OT[:, 0, :], DEN[:, :]))
        nc.vector.tensor_tensor(Y[:, h // HB, b * S:(b + 1) * S], OV[:, :], OT[:, 0, :], ALU.mult).then_inc(out_moved.up(), 1)

    def move_out(act, n):
        act.wait_ge(value_ready.sem, value_ready.at((n + 1) * nkt))
        if n >= 2:
            act.wait_ge(out_turned.sem, out_turned.at(n - 1))
        nc.scalar.copy(OT[:, n % 2, :], OV[:, :]).then_inc(out_moved.up(), 1)

    def ended(r):
        return r // nkt if 0 <= r < len(rounds) and r % nkt == nkt - 1 else None

    def move_negmax(dve, g):
        dve.wait_ge(negmax_turned.sem, negmax_turned.at(g + 1))
        nc.vector.tensor_copy(c.NMT[:, g % 2, :], NB).then_inc(negmax_moved.up(), 1)

    def ahead(r):
        first = (r + per_group + 1) * per_round
        return list(range(first, min(first + per_round, NU)))

    def next_group(r):
        return r // per_group + 1 if r % per_group == per_group - 1 and r + 1 < R else None

    R = len(rounds)
    with nc.Block() as block:
        if load:
            block.sync(load)
        if stacks:
            @block.sync
            def _(sp):
                sp.wait_ge(c.stored_parts, c.nparts)
                for g in range(2):
                    stacks.load_first(sp, g, groups[g])
                    stacks.load_second(sp, g, groups[g])
                stacks.load_first(sp, 2, groups[2])
                for g in range(2, len(groups)):
                    sp.wait_ge(score_ready.sem, score_ready.at((g - 1) * per_group * pairs))
                    stacks.load_second(sp, g, groups[g])
                    if g + 1 < len(groups):
                        stacks.load_first(sp, g + 1, groups[g + 1])

        @block.tensor
        def _(pe):
            for n in range(U):
                raw_scores(pe, n)
            turn_negmax(pe, 0)
            for n in range(U, min(U + per_round, NU)):
                raw_scores(pe, n)
            for r in range(R + 3):
                if r < R:
                    scores(pe, r)
                if next_group(r) is not None:
                    turn_negmax(pe, next_group(r))
                    if 0 <= r - 1 < R:
                        values(pe, r - 1)
                for n in ahead(r)[:1]:
                    raw_scores(pe, n)
                if turned and ended(r - 3) is not None:
                    turn_out(pe, ended(r - 3))
                if next_group(r) is None and 0 <= r - 1 < R:
                    values(pe, r - 1)
                for n in ahead(r)[1:]:
                    raw_scores(pe, n)

        @block.scalar
        def _(act):
            for r in range(R + 3):
                if turned and ended(r - 2) is not None:
                    move_out(act, ended(r - 2))
                if r >= R:
                    continue
                ks, n0 = key_tiles[rounds[r][2]], start(rounds[r][2])
                for m in range(pairs):
                    pair = r * pairs + m
                    act.wait_ge(score_ready.sem, score_ready.at(pair + 1))
                    if pair >= NEP:
                        act.wait_ge(value_ready.sem, value_ready.at((pair - NEP) // pairs + 1))
                    nc.scalar.activation(E[pair % NEP][0:ks, :, n0:S], SC[pair % 2][0:ks, :, n0:S], ACT.Exp,
                                         scale=scale).then_inc(exp_ready.up(), 1)

        @block.vector
        def _(dve):
            if turned:
                nc.vector.memset(OV[:, :], 0.0).then_inc(cleared.up(), 1)
            for n in range(U):
                reduce_max(dve, n)
            negmax(dve, 0)
            move_negmax(dve, 0)
            for n in range(U, min(U + per_round, NU)):
                reduce_max(dve, n)
            for r in range(R + 3):
                if next_group(r) is not None:
                    negmax(dve, next_group(r))
                    move_negmax(dve, next_group(r))
                if next_group(r) is None:
                    for n in ahead(r)[:1]:
                        reduce_max(dve, n)
                if not turned and ended(r - 2) is not None:
                    norm_in_place(dve, ended(r - 2))
                if next_group(r) is not None:
                    for n in ahead(r)[:1]:
                        reduce_max(dve, n)
                for n in ahead(r)[1:]:
                    reduce_max(dve, n)
                if turned and ended(r - 3) is not None:
                    norm_turned(dve, ended(r - 3))

        if mask == "future":
            @block.gpsimd
            def _(pool):
                later = c.key_later[:].unsqueeze(1).broadcast_to([P, 2, P])
                for pair in range(R * pairs):
                    i = rounds[pair // pairs][2]
                    pool.wait_ge(exp_ready.sem, exp_ready.at(pair + 1))
                    if pair >= NEP:
                        pool.wait_ge(value_ready.sem, value_ready.at((pair - NEP) // pairs + 1))
                    nc.gpsimd.tensor_tensor(EM[pair % NEP], E[pair % NEP][:, :, i * P:(i + 1) * P], later,
                                            ALU.mult).then_inc(masked_ready.up(), 1)


Q_PARTS, K_PARTS = (0, 0, 1, 1, 0, 2), (0, 1, 0, 1, 2, 0)


class HeadStacks:

    def __init__(self, c, keys):
        self.c, self.keys = c, keys
        self.first = [counter(c, f"first_stack_{z}") for z in range(3)]
        self.second = [counter(c, f"second_stack_{z}") for z in range(2)]
        slot = lambda a: a.bitcast(BF16).rearrange("p (o j t) -> p o j t", o=2, j=4)
        self.first_slot = [slot(c.big1(2 * z * TOK, 2 * TOK)) for z in range(3)]
        self.second_slot = [slot(c.big1(6 * TOK, 2 * TOK)), slot(c.big3(4 * TOK, 2 * TOK))]
        self.slots = {}

    def load(self, sp, slot, loaded, products, group):
        b, h = group
        n = self.keys
        for s, product in enumerate(products):
            rows = slice(32 * s, 32 * s + 32)
            for o, (dram, part, size) in enumerate(((self.c.q_wide, Q_PARTS[product], S), (self.c.k_wide, K_PARTS[product], n))):
                src = dram[:, part, h // 4, b * size:(b + 1) * size].rearrange("(j d) t -> d j t", d=32)
                sp.dma_start(slot[rows, o, :, 0:size], src).then_inc(loaded.up(16), 16)

    def load_first(self, sp, g, group):
        self.load(sp, self.first_slot[g % 3], self.first[g % 3], (0, 1, 2), group)

    def load_second(self, sp, g, group):
        self.load(sp, self.second_slot[g % 2], self.second[g % 2], (3, 4, 5), group)

    def first_loaded(self, g):
        s = self.first[g % 3]
        return s.sem, s.at(96 * (g // 3 + 1))

    def second_loaded(self, g):
        s = self.second[g % 2]
        return s.sem, s.at(96 * (g // 2 + 1))

    def operands(self, b, h):
        g = (b * HEADS + h) // 4
        slots = self.first_slot[g % 3], self.second_slot[g % 2]
        return [(slot[0:96, 0, h % 4, :], slot[0:96, 1, h % 4, 0:self.keys]) for slot in slots]


def project_split(c, units):
    nc = c.nc
    product_ready, high_ready, rest_ready, mid_ready, low_ready = (
        counter(c, n) for n in ("product_ready", "high_ready", "rest_ready", "mid_ready", "low_ready"))
    SLOT = 3 * S // 2
    room = [c.big1(u * SLOT, SLOT) for u in range(10)] + [c.big2(u * SLOT, SLOT) for u in range(5)] + [c.big3(0, SLOT)]
    parts = [r.bitcast(BF16).rearrange("p (z t) -> p z t", z=3) for r in room]
    rest = [c.big3(TOK + z * S, S) for z in range(3)]
    with nc.Block() as block:
        @block.tensor
        def _(pe):
            for u, (lhsT, rhs, n, _) in enumerate(units):
                if u >= 8:
                    pe.wait_ge(rest_ready.sem, rest_ready.at(u - 7))
                nc.tensor.matmul(c.bank[u % 8][:, 0:n], lhsT, rhs, start=True, stop=True).then_inc(product_ready.up(), 1)

        @block.scalar
        def _(act):
            for u in range(len(units) + 1):
                if u < len(units):
                    n = units[u][2]
                    act.wait_ge(product_ready.sem, product_ready.at(u + 1))
                    nc.scalar.copy(parts[u][:, 0, 0:n], c.bank[u % 8][:, 0:n]).then_inc(high_ready.up(), 1)
                if u >= 1:
                    n = units[u - 1][2]
                    act.wait_ge(rest_ready.sem, rest_ready.at(u))
                    nc.scalar.copy(parts[u - 1][:, 1, 0:n], rest[(u - 1) % 3][:, 0:n]).then_inc(mid_ready.up(), 1)

        @block.vector
        def _(dve):
            for u, (_, _, n, _) in enumerate(units):
                dve.wait_ge(high_ready.sem, high_ready.at(u + 1))
                if u >= 3:
                    dve.wait_ge(low_ready.sem, low_ready.at(u - 2))
                nc.vector.tensor_tensor(rest[u % 3][:, 0:n], c.bank[u % 8][:, 0:n], parts[u][:, 0, 0:n],
                                        ALU.subtract).then_inc(rest_ready.up(), 1)

        @block.gpsimd
        def _(pool):
            for u, (_, _, n, _) in enumerate(units):
                pool.wait_ge(mid_ready.sem, mid_ready.at(u + 1))
                nc.gpsimd.tensor_tensor(parts[u][:, 2, 0:n], rest[u % 3][:, 0:n], parts[u][:, 1, 0:n],
                                        ALU.subtract).then_inc(low_ready.up(), 1)

        @block.sync
        def _(sp):
            for u, (_, _, n, dst) in enumerate(units):
                sp.wait_ge(low_ready.sem, low_ready.at(u + 1))
                sp.dma_start(dst, parts[u][:, :, 0:n]).then_inc(c.stored_parts, 16)
                c.nparts += 16


def split_heads(c, qT, kT, ktok):
    nc = c.nc
    parts_ready, parts_stored, heads_loaded, dve_step = (counter(c, n) for n in ("parts_ready", "parts_stored", "heads_loaded", "dve_step"))
    pool_step, zeros_ready = counter(c, "pool_step"), counter(c, "zeros_ready")
    qp, kp = c.q_parts, c.k_parts[:, :, 0:ktok]
    both = kT is not None

    def split(eng, e, step, src, parts, rest):
        seq(eng, step, e.tensor_copy(parts[:, 0, :], src))
        seq(eng, step, e.tensor_tensor(rest, src, parts[:, 0, :], ALU.subtract))
        seq(eng, step, e.tensor_copy(parts[:, 1, :], rest))
        seq(eng, step, e.tensor_tensor(rest, rest, parts[:, 1, :], ALU.subtract))
        return e.tensor_copy(parts[:, 2, :], rest)

    with nc.Block() as block:
        @block.vector
        def _(dve):
            split(dve, nc.vector, dve_step, qT, qp, c.rest_q).then_inc(parts_ready.up(), 1)
            if both and ktok > P * 2:
                split(dve, nc.vector, dve_step, kT, kp, c.rest_k[:, 0:ktok]).then_inc(parts_ready.up(), 1)
            nc.vector.memset(c.big1(0, 2 * TOK)[0:96], 0.0).then_inc(zeros_ready.up(), 1)

        @block.gpsimd
        def _(pool):
            if both and ktok <= P * 2:
                split(pool, nc.gpsimd, pool_step, kT, kp, c.rest_k[:, 0:ktok]).then_inc(parts_ready.up(), 1)
            nc.gpsimd.memset(c.big1(2 * TOK, 6 * TOK)[0:96], 0.0).then_inc(zeros_ready.up(), 1)

        @block.sync
        def _(sp):
            sp.wait_ge(parts_ready.sem, parts_ready.at(1 + both))
            sp.dma_start(c.q_dram, qp).then_inc(c.stored_parts, 16)
            if both:
                sp.dma_start(c.k_dram[:, :, 0:ktok], kp).then_inc(c.stored_parts, 16)
            c.nparts += 16 * (1 + both)
            sp.wait_ge(c.stored_parts, c.nparts)
            sp.wait_ge(zeros_ready.sem, zeros_ready.at(2))
            for s in range(6):
                for x in range(2):
                    rows = slice(48 * x + 8 * s, 48 * x + 8 * s + 8)
                    sp.dma_start(c.QH[rows, :, x, :], c.q_dram[:, Q_PARTS[s], :].rearrange(
                        "(h x d) t -> x d h t", x=2, d=8)[x]).then_inc(c.loaded_heads, 16)
                    c.nheads += 16
                    if both:
                        sp.dma_start(c.KH[rows].rearrange("p (h t) -> p h t", t=TOK)[:, :, 0:ktok], c.k_dram[:, K_PARTS[s], 0:ktok].rearrange(
                            "(h x d) t -> x d h t", x=2, d=8)[x]).then_inc(c.loaded_heads, 16)
                        c.nheads += 16
            sp.wait_ge(c.loaded_heads, c.nheads)


def stack_keys(c, src):
    nc, step = c.nc, counter(c, "dve_step")
    stacked_ready, turned_ready, act_freed, dve_freed = (counter(c, n) for n in ("stacked_ready", "turned_ready", "act_freed", "dve_freed"))
    stack = c.key_stack.rearrange("p (u i x) z d -> p u x i z d", i=ST, x=2)
    tile_of = lambda u, i: c.key_stack[:, (u * ST + i) * 2:(u * ST + i) * 2 + 2].rearrange("p x z d -> p (x z d)")
    flat = src.rearrange("p (u x) i d -> p u x i d", x=2)
    rest = c.total[:].rearrange("p t (v i d) -> p (t v) i d", i=ST, d=8).rearrange("p (u x) i d -> p u x i d", x=2)
    slot = lambda z: stack[:, :, :, :, z, :]
    place = lambda u: c.KH[0:96, u * S:(u + 1) * S]
    turned = lambda u: c.banks_bf[u % 8][0:96, :]

    with nc.Block() as block:
        @block.vector
        def _(dve):
            for x in range(2):
                one = lambda ap: ap[:, :, x]
                seq(dve, step, nc.vector.tensor_copy(one(slot(0)), one(flat)))
                nc.vector.tensor_copy(one(slot(2)), one(slot(0)))
                nc.vector.tensor_copy(one(slot(5)), one(slot(0)))
                seq(dve, step, nc.vector.tensor_tensor(one(rest), one(flat), one(slot(0)), ALU.subtract))
                seq(dve, step, nc.vector.tensor_copy(one(slot(1)), one(rest)))
                nc.vector.tensor_copy(one(slot(3)), one(slot(1)))
                seq(dve, step, nc.vector.tensor_tensor(one(rest), one(rest), one(slot(1)), ALU.subtract))
                last = nc.vector.tensor_copy(one(slot(4)), one(rest))
            last.then_inc(stacked_ready.up(), 1)
            for u in range(1, B * HEADS // 2, 2):
                dve.wait_ge(turned_ready.sem, turned_ready.at(u + 1))
                nc.vector.tensor_copy(place(u), turned(u)).then_inc(dve_freed.up(), 1)

        @block.tensor
        def _(pe):
            pe.wait_ge(stacked_ready.sem, stacked_ready.at(1))
            for u in range(B * HEADS // 2):
                if u >= 8:
                    s = dve_freed if u % 2 else act_freed
                    pe.wait_ge(s.sem, s.at((u - 8) // 2 + 1))
                for i in range(ST):
                    last = nc.tensor.transpose(turned(u)[:, i * P:(i + 1) * P], tile_of(u, i), c.ident_bf[:])
                last.then_inc(turned_ready.up(), 1)

        @block.scalar
        def _(act):
            for u in range(0, B * HEADS // 2, 2):
                act.wait_ge(turned_ready.sem, turned_ready.at(u + 1))
                nc.scalar.copy(place(u), turned(u)).then_inc(act_freed.up(), 1)


def quantise(c, src, dst_bf, amax):
    nc, step = c.nc, counter(c, "dve_step")
    t1, r7 = c.total, c.rstd

    with nc.Block() as block:
        @block.vector
        def _(dve):
            seq(dve, step, nc.vector.tensor_reduce(amax, src, AX_X, ALU.max, apply_absolute_value=True))
            seq(dve, step, nc.vector.tensor_scalar(amax, amax, 1e-6, None, ALU.max))
            seq(dve, step, nc.vector.reciprocal(r7[:], amax))
            for t in range(NT):
                last = nc.vector.tensor_scalar(t1[:, t, :], src[:, t, :], r7[:, t:t + 1], 7.0, ALU.mult, ALU.mult)
            seq(dve, step, last)
            seq(dve, step, nc.vector.tensor_scalar(t1[:], t1[:], ROUND, ROUND - 8.0, ALU.add, ALU.max))
            seq(dve, step, nc.vector.tensor_scalar(dst_bf, t1[:], ROUND, 7.0, ALU.subtract, ALU.min))
            seq(dve, step, nc.vector.tensor_scalar(amax, amax, 1.0 / 7.0, None, ALU.mult))


def ternary(c, w, signT, alpha):
    nc, step = c.nc, counter(c, "dve_step")
    rows_ready, total_ready, sign_ready, sign_turned = (counter(c, n) for n in ("tern_rows", "tern_total", "tern_sign", "tern_turned"))
    row, thr, m1, m2 = c.small[:, 0:1], c.small[:, 1:3], c.tern[:, 0, :], c.tern[:, 1, :]
    diag = c.total[:, 0, :]

    with nc.Block() as block:
        @block.vector
        def _(dve):
            seq(dve, step, nc.vector.tensor_reduce(row, w, AX_X, ALU.add, apply_absolute_value=True))
            seq(dve, step, nc.vector.tensor_scalar(row, row, 1.0 / P, None, ALU.mult))
            nc.vector.tensor_scalar(diag, c.ident[:], row, None, ALU.mult).then_inc(rows_ready.up(), 1)
            dve.wait_ge(total_ready.sem, total_ready.at(1))
            nc.vector.tensor_copy(alpha, c.bank[1][:, 0:P])
            nc.vector.tensor_scalar(thr[:, 0:1], c.bank[0][:, 0:1], 0.05 / P, None, ALU.mult)
            seq(dve, step, nc.vector.tensor_scalar(thr[:, 1:2], c.bank[0][:, 0:1], -0.05 / P, None, ALU.mult))
            nc.vector.tensor_scalar(m1, w, thr[:, 0:1], None, ALU.is_ge)
            seq(dve, step, nc.vector.tensor_scalar(m2, w, thr[:, 1:2], None, ALU.is_le))
            nc.vector.tensor_tensor(m1, m1, m2, ALU.subtract).then_inc(sign_ready.up(), 1)
            dve.wait_ge(sign_turned.sem, sign_turned.at(1))
            nc.vector.tensor_copy(signT, c.bank_bf[:, 0:P])

        @block.tensor
        def _(pe):
            pe.wait_ge(rows_ready.sem, rows_ready.at(1))
            nc.tensor.matmul(c.bank[0][:, 0:1], c.ones[:], row, start=True, stop=True)
            nc.tensor.matmul(c.bank[1][:, 0:P], c.ones[:], diag, start=True, stop=True).then_inc(total_ready.up(), 1)
            pe.wait_ge(sign_ready.sem, sign_ready.at(1))
            nc.tensor.transpose(c.bank_bf[:, 0:P], m1, c.ident_bf[:]).then_inc(sign_turned.up(), 1)


def turn_quantised(c, q_bf, qT_bf):
    nc = c.nc
    turned_ready, act_freed = counter(c, "turned_ready"), counter(c, "act_freed")
    with nc.Block() as block:
        @block.tensor
        def _(pe):
            for half in range(2):
                if half:
                    pe.wait_ge(act_freed.sem, act_freed.at(1))
                for k in range(4):
                    last = nc.tensor.transpose(c.bank_bf[:, k * P:(k + 1) * P], q_bf[:, half * 4 + k, :], c.ident_bf[:])
                last.then_inc(turned_ready.up(), 1)

        @block.scalar
        def _(act):
            for half in range(2):
                act.wait_ge(turned_ready.sem, turned_ready.at(half + 1))
                nc.scalar.copy(qT_bf[:, half * S:(half + 1) * S], c.bank_bf[:, 0:S]).then_inc(act_freed.up(), 1)


def quantised_product(c, qT_bf, signT, amax, alpha, bias, dst):
    nc, step = c.nc, counter(c, "dve_step")
    product_ready = counter(c, "product_ready")
    with nc.Block() as block:
        @block.tensor
        def _(pe):
            for t in range(NT):
                nc.tensor.matmul(c.bank[t][:, 0:P], qT_bf[:, t * P:(t + 1) * P], signT,
                                 start=True, stop=True).then_inc(product_ready.up(), 1)

        @block.vector
        def _(dve):
            for t in range(NT):
                dve.wait_ge(product_ready.sem, product_ready.at(t + 1))
                last = nc.vector.scalar_tensor_tensor(out=dst[:, t, :], in0=c.bank[t][:, 0:P],
                                                      scalar=amax[:, t:t + 1], in1=alpha, op0=ALU.mult, op1=ALU.mult)
            if bias is not None:
                seq(dve, step, last)
                nc.vector.tensor_tensor(dst, dst, bias.unsqueeze(1).broadcast_to([P, NT, P]), ALU.add)


def attention_8(c, key_tiles, dst, scale, chunked=False):
    single = len(key_tiles) == 1

    def operands(b, h):
        if chunked:
            keys = c.KH[0:96, (b * HEADS + h) // 2 * S:(b * HEADS + h) // 2 * S + S]
        else:
            n = SK if single else S
            keys = c.KH[0:96, h // 2 * TOK + b * n:h // 2 * TOK + (b + 1) * n]
        return [(c.QH[0:96, h // 2, h % 2, b * S:(b + 1) * S], keys)]

    def vop(b, h, i):
        if chunked:
            return c.VH[:, (b * HEADS + h) * 36 + i * 9:(b * HEADS + h) * 36 + i * 9 + 9]
        if single:
            return c.VH[0:SK, (b * HEADS + h) * 9:(b * HEADS + h) * 9 + 9]
        x = ((b * ST + i) * HEADS + h) * 9
        return c.VH[:, x:x + 9]

    attention(c, key_tiles, 8, operands, vop, scale, dst)


def block_product(c, aT, bT, dst):
    nc = c.nc
    product_ready = counter(c, "product_ready")
    with nc.Block() as block:
        @block.tensor
        def _(pe):
            nc.tensor.matmul(c.bank[0][:, 0:P], aT, bT, start=True, stop=True).then_inc(product_ready.up(), 1)

        @block.vector
        def _(dve):
            dve.wait_ge(product_ready.sem, product_ready.at(1))
            nc.vector.tensor_tensor(dst, c.bank[0][:, 0:P], c.m("same_head"), ALU.mult)


def project_out(c, srcT, w, k=1):
    def add(pe, t, psum):
        for i in range(k):
            last = c.nc.tensor.matmul(psum, srcT[:, i, t * P:(t + 1) * P], w[:, i * P:(i + 1) * P],
                                      start=(i == 0), stop=(i == k - 1))
        return last
    return add


def turn_back(c, srcT):
    def add(pe, t, psum):
        return c.nc.tensor.transpose(psum, srcT[:, t * P:(t + 1) * P], c.ident[:])
    return add



def layer0_attention(c):
    nc = c.nc
    amax = c.amax
    proj = c.Y8
    ternary(c, c.m("L0_Wqkv"), c.signT[:, 0, :], c.alpha[:, 0, :])
    ternary(c, c.m("L0_Wo"), c.signT[:, 1, :], c.alpha[:, 1, :])
    block_product(c, c.m("L0_UT")[0:32], c.m("L0_UT")[0:32], c.headmat)
    quantise(c, c.X[:], c.q_bf[:], amax)
    turn_quantised(c, c.q_bf, c.qT_bf)
    quantised_product(c, c.qT_bf[:], c.signT[:, 0, :], amax, c.alpha[:, 0, :], c.row("L0_attn_Wqkv_b"), proj[:])

    step = counter(c, "dve_step")
    pool_step = counter(c, "pool_step")
    with nc.Block() as block:
        @block.vector
        def _(dve):
            p5 = proj.rearrange("p t (h i two) -> p t h i two", h=HEADS, two=2)
            for name, dst in (("q", c.XN), ("k", c.total)):
                d = dst[:].rearrange("p t (h z i) -> p t h z i", h=HEADS, z=2)
                tmp = c.rest2[:, 0:64].rearrange("p (h i) -> p h i", h=HEADS)
                for t in range(NT):
                    if name == "q":
                        tab = c.m("rope_q").rearrange("p (z t i) -> p z t i", z=2, t=ST)
                        cos, sin = (tab[:, z, t % ST, :].unsqueeze(1).broadcast_to([P, HEADS, 4]) for z in range(2))
                    else:
                        tab = c.m("rope_k").rearrange("p (z h i) -> p z h i", z=2, h=HEADS)
                        cos, sin = tab[:, 0], tab[:, 1]
                    t1, t2 = p5[:, t, :, :, 0], p5[:, t, :, :, 1]
                    a, b = c.rest2[:, 0:64].rearrange("p (h i) -> p h i", h=HEADS), c.rest2[:, 64:128].rearrange("p (h i) -> p h i", h=HEADS)
                    seq(dve, step, nc.vector.tensor_tensor(a, t2, sin, ALU.mult))
                    nc.vector.tensor_tensor(b, t1, cos, ALU.mult)
                    seq(dve, step, nc.vector.tensor_tensor(d[:, t, :, 1, :], t1, sin, ALU.mult))
                    seq(dve, step, nc.vector.tensor_tensor(d[:, t, :, 0, :], b, a, ALU.subtract))
                    seq(dve, step, nc.vector.tensor_tensor(a, t2, cos, ALU.mult))
                    seq(dve, step, nc.vector.tensor_tensor(d[:, t, :, 1, :], d[:, t, :, 1, :], a, ALU.add))

        @block.gpsimd
        def _(pool):
            v = c.VH[:, 0:B * HEADS * 36].rearrange("p (t bl i e) -> p t bl i e", t=NT, bl=4, i=4)
            seq(pool, pool_step, nc.gpsimd.memset(v[:, :, :, :, 8], 1.0))
            for bl in range(4):
                for cl in range(4):
                    src = proj[32 * bl:32 * bl + 32].rearrange("p t (i cl d) -> p t i cl d", i=4, cl=4)[:, :, :, cl, :]
                    seq(pool, pool_step, nc.gpsimd.tensor_copy(v[32 * cl:32 * cl + 32, :, bl, :, 0:8], src))

    keys = c.big1(2 * TOK, TOK).rearrange("p (t bl i d) -> p t bl i d", t=NT, bl=4, i=4)
    with nc.Block() as block:
        @block.vector
        def _(dve):
            for bl in range(4):
                for cl in range(4):
                    src = c.total[32 * bl:32 * bl + 32].rearrange("p t (i cl d) -> p t i cl d", i=4, cl=4)[:, :, :, cl, :]
                    nc.vector.tensor_copy(keys[32 * cl:32 * cl + 32, :, bl], src)

    turn(c, c.XN[:], NT, P, c.qk32[:, 0:1, :])
    qT = c.VH[:, B * HEADS * 36:B * HEADS * 36 + TOK]
    matmul_stream(c, halves(c, lambda half: [(c.headmat, c.qk32[:, 0, half * S:(half + 1) * S])], P, qT))
    stack_keys(c, keys.rearrange("p t bl i d -> p (t bl) i d"))
    split_heads(c, qT, None, 0)
    attention_8(c, [P] * ST, c.Y8, 8.0 ** -0.5, chunked=True)
    quantise(c, c.Y8, c.q_bf[:], amax)
    turn_quantised(c, c.q_bf, c.qT_bf)
    quantised_product(c, c.qT_bf[:], c.signT[:, 1, :], amax, c.alpha[:, 1, :], None, c.Y8)
    with nc.Block() as block:
        @block.vector
        def _(dve):
            nc.vector.tensor_tensor(c.total[:], c.X[:], c.Y8, ALU.add)
    add_and_norm(c, total=c.total, out=c.X, turned=[(c.XT, None, None)])


def cross_kv(c, wk, wv, bk=None, bv=None):
    ctxT = c.m("ctxT")[0:CTX]
    v = c.VH[0:SK, 0:B * HEADS * 9].rearrange("p (b h e) -> p b h e", b=B, e=9)

    def ones(act, bank):
        return None
    units = [([(wk, ctxT)], P, B * SK, "act", act_copy(c, c.ckT[:], bias=bk))]
    for b in range(B):
        if bv is None:
            emit = (lambda b: lambda dve, bank, step: c.nc.vector.tensor_copy(v[:, b, :, 0:8], bank.rearrange("p (h d) -> p h d", d=8)))(b)
        else:
            emit = (lambda b: lambda dve, bank, step: c.nc.vector.tensor_tensor(
                v[:, b, :, 0:8], bank.rearrange("p (h d) -> p h d", d=8), bv[0:SK].rearrange("p (h d) -> p h d", d=8), ALU.add))(b)
        units.append(([(ctxT[:, b * SK:(b + 1) * SK], wv)], SK, P, "dve", emit))
    return units, v[:, :, :, 8]


def fill(c, ap, value):
    with c.nc.Block() as block:
        @block.gpsimd
        def _(pool):
            c.nc.gpsimd.memset(ap, value)


def cross_attention_8(c, wq, wk, wv, wo, bq, bk, bv, bo):
    units, one = cross_kv(c, wk, wv, bk, bv)
    units += halves(c, lambda half: [(wq, c.XT[:, half * S:(half + 1) * S])], P, c.qT, bias=bq)
    fill(c, one, 1.0)
    matmul_stream(c, units)
    split_heads(c, c.qT[:], c.ckT[:], B * SK)
    attention_8(c, [SK], c.Y8, 8.0 ** -0.5)
    turn(c, c.Y8, NT, P, c.yT8)
    add_and_norm(c, add=project_out(c, c.yT8, wo), bias=bo, out=c.X, turned=[(c.XT, None, None)])


def moe(c, srcT, parts, cwT_parts, mix, outT, load=None):
    nc = c.nc
    gate_ready, gated, hidden_ready, hidden_used, acc_ready, dve_step, act_mid, act_step = (counter(c, n) for n in (
        "gate_ready", "gated", "hidden_ready", "hidden_used", "acc_ready", "dve_step", "act_mid", "act_step"))
    n = len(parts)
    steps = [(half, k) for half in range(2) for k in range(n)]
    G, U, CW, ACC = c.bank[0:2], c.bank[2:4], c.bank[4:6], c.bank[6]
    sg, hid = c.moe_sg, c.moe_h

    with nc.Block() as block:
        if load:
            block.sync(load)

        @block.tensor
        def _(pe):
            def up(s):
                half, k = steps[s]
                w1, w3, _, pick = parts[k]
                m = w1.shape[1]
                x = srcT[:, half * S:(half + 1) * S]
                if s >= 2:
                    pe.wait_ge(hidden_ready.sem, hidden_ready.at(s - 1))
                nc.tensor.matmul(G[s % 2][0:m, :], w1, x, start=True, stop=True).then_inc(gate_ready.up(), 1)
                last = nc.tensor.matmul(U[s % 2][0:m, :], w3, x, start=True, stop=True)
                if pick is not None:
                    last = nc.tensor.matmul(CW[s % 2][0:m, :], pick, cwT_parts[:, half * S:(half + 1) * S], start=True, stop=True)
                last.then_inc(gate_ready.up(), 1)

            def down(s):
                half, k = steps[s]
                w2 = parts[k][2]
                m = w2.shape[0]
                pe.wait_ge(hidden_ready.sem, hidden_ready.at(s + 1))
                if k == 0 and half:
                    pe.wait_ge(acc_ready.sem, acc_ready.at(1))
                last = nc.tensor.matmul(ACC[:, :], w2, hid[0:m, s % 2, :], start=(k == 0), stop=(k == n - 1))
                last.then_inc(hidden_used.up(), 1)

            for s in range(len(steps) + 1):
                if s < len(steps):
                    up(s)
                if s >= 1:
                    down(s - 1)

        @block.scalar
        def _(act):
            for s, (half, k) in enumerate(steps):
                m = parts[k][0].shape[1]
                act.wait_ge(gate_ready.sem, gate_ready.at(2 * s + 1))
                if s >= 2:
                    act.wait_ge(hidden_ready.sem, hidden_ready.at(s - 1))
                func = ACT.Silu if mix == "silu" else ACT.Copy
                nc.scalar.activation(sg[0:m, s % 2, :], G[s % 2][0:m, :], func).then_inc(gated.up(), 1)
                if mix == "gelu":
                    act.wait_ge(act_mid.sem, act_mid.at(s + 1))
                    nc.scalar.activation(sg[0:m, s % 2, :], sg[0:m, s % 2, :], ACT.Gelu).then_inc(gated.up(), 1)
                if k == 0 and half:
                    act.wait_ge(hidden_used.sem, hidden_used.at(n))
                    nc.scalar.copy(outT[:, 0:S], ACC[:, :]).then_inc(acc_ready.up(), 1)
            act.wait_ge(hidden_used.sem, hidden_used.at(2 * n))
            nc.scalar.copy(outT[:, S:2 * S], ACC[:, :])

        @block.vector
        def _(dve):
            for s, (half, k) in enumerate(steps):
                m = parts[k][0].shape[1]
                pick = parts[k][3]
                dve.wait_ge(gate_ready.sem, gate_ready.at(2 * s + 2))
                if s >= 2:
                    dve.wait_ge(hidden_used.sem, hidden_used.at(s - 1))
                if mix == "gelu":
                    dve.wait_ge(gated.sem, gated.at(2 * s + 1))
                    nc.vector.tensor_tensor(sg[0:m, s % 2, :], sg[0:m, s % 2, :], U[s % 2][0:m, :], ALU.mult).then_inc(act_mid.up(), 1)
                    dve.wait_ge(gated.sem, gated.at(2 * s + 2))
                    last = nc.vector.tensor_tensor(hid[0:m, s % 2, :], sg[0:m, s % 2, :], CW[s % 2][0:m, :], ALU.mult)
                else:
                    dve.wait_ge(gated.sem, gated.at(s + 1))
                    last = nc.vector.tensor_tensor(hid[0:m, s % 2, :], sg[0:m, s % 2, :], U[s % 2][0:m, :], ALU.mult)
                    if pick is not None:
                        seq(dve, dve_step, last)
                        last = nc.vector.tensor_tensor(hid[0:m, s % 2, :], hid[0:m, s % 2, :], CW[s % 2][0:m, :], ALU.mult)
                last.then_inc(hidden_ready.up(), 1)


def router_logits(c, srcT, w, E):
    nc = c.nc
    with nc.Block() as block:
        @block.tensor
        def _(pe):
            for t in range(NT):
                nc.tensor.matmul(c.bank[0][:, t * 32:t * 32 + E], srcT[:, t * P:(t + 1) * P], w, start=True, stop=True)


def turn_weights(c, cw, E):
    nc, step = c.nc, counter(c, "dve_step")
    cw_ready, cw_turned, act_freed = counter(c, "cw_ready"), counter(c, "cw_turned"), counter(c, "act_freed")
    parts = c.cw_parts
    with nc.Block() as block:
        @block.vector
        def _(dve):
            rest = c.cw_rest[:, :, 0:E]
            seq(dve, step, nc.vector.memset(parts[:], 0.0))
            seq(dve, step, nc.vector.tensor_copy(parts[:, :, 0:E], cw))
            seq(dve, step, nc.vector.tensor_tensor(rest, cw, parts[:, :, 0:E], ALU.subtract))
            seq(dve, step, nc.vector.tensor_copy(parts[:, :, 32:32 + E], rest))
            seq(dve, step, nc.vector.tensor_tensor(rest, rest, parts[:, :, 32:32 + E], ALU.subtract))
            nc.vector.tensor_copy(parts[:, :, 64:64 + E], rest).then_inc(cw_ready.up(), 1)

        @block.tensor
        def _(pe):
            pe.wait_ge(cw_ready.sem, cw_ready.at(1))
            for half in range(2):
                if half:
                    pe.wait_ge(act_freed.sem, act_freed.at(1))
                for k in range(4):
                    last = nc.tensor.transpose(c.bank_bf[0:96, k * P:(k + 1) * P], parts[:, half * 4 + k, :], c.ident_bf[:])
                last.then_inc(cw_turned.up(), 1)

        @block.scalar
        def _(act):
            for half in range(2):
                act.wait_ge(cw_turned.sem, cw_turned.at(half + 1))
                nc.scalar.copy(c.cwT[:, half * S:(half + 1) * S], c.bank_bf[0:96, 0:S]).then_inc(act_freed.up(), 1)


def top_indices(dve, c, step, values, E, dst):
    nc = c.nc
    for t in range(NT):
        last = nc.vector.max(c.top_v[:, t, :], values[:, t, 0:E])
    seq(dve, step, last)
    for t in range(NT):
        last = nc.vector.max_index(c.top_i[:, t, :], c.top_v[:, t, :], values[:, t, 0:E])
    seq(dve, step, last)
    seq(dve, step, nc.vector.tensor_copy(dst, c.top_i[:]))


def one_hot(c, E, index, dst):
    iota = c.m("iota")[:, 0:E].unsqueeze(1).broadcast_to([P, NT, E])
    return c.nc.vector.tensor_tensor(dst, iota, index.unsqueeze(2).broadcast_to([P, NT, E]), ALU.is_equal)


def layer0_moe(c):
    nc, step = c.nc, counter(c, "dve_step")
    E = L0E
    router_logits(c, c.XT[:], c.m("L0_gateT"), E)
    sc, sel, oh, top = c.rt[:, 0, :, 0:E], c.rt[:, 1, :, 0:E], c.rt[:, 2, :, 0:E], c.top_f
    biased, scored = counter(c, "biased"), counter(c, "scored")
    with nc.Block() as block:
        @block.vector
        def _(dve):
            lg = c.bank[0][:, 0:NT * 32].rearrange("p (t e) -> p t e", t=NT)[:, :, 0:E]
            nc.vector.tensor_tensor(sel, lg, c.m("gate_bias").unsqueeze(1).broadcast_to([P, NT, E]), ALU.add).then_inc(biased.up(), 1)
            dve.wait_ge(scored.sem, scored.at(1))
            top_indices(dve, c, step, c.rt[:, 0, :, :], E, top)
            seq(dve, step, one_hot(c, E, top[:, :, 0], sel))
            seq(dve, step, one_hot(c, E, top[:, :, 1], oh))
            seq(dve, step, nc.vector.tensor_tensor(sel, sel, oh, ALU.add))
            seq(dve, step, nc.vector.tensor_tensor(sel, sel, sc, ALU.mult))
            seq(dve, step, nc.vector.tensor_reduce(c.small8[:, 0, :], sel, AX_X, ALU.add))
            seq(dve, step, nc.vector.tensor_scalar(c.small8[:, 0, :], c.small8[:, 0, :], 1e-20, None, ALU.add))
            seq(dve, step, nc.vector.reciprocal(c.small8[:, 1, :], c.small8[:, 0, :]))
            seq(dve, step, nc.vector.tensor_tensor(sel, sel, c.small8[:, 1, :].unsqueeze(2).broadcast_to([P, NT, E]), ALU.mult))

        @block.scalar
        def _(act):
            act.wait_ge(biased.sem, biased.at(1))
            nc.scalar.activation(sc, sel, ACT.Sigmoid).then_inc(scored.up(), 1)
    turn_weights(c, sel, E)
    w1, w3, w2 = c.m("w1T"), c.m("w3T"), c.m("w2T")
    parts = []
    for e in range(E):
        for i, (a, m) in enumerate(chunks(L0HID)):
            col = e * L0HID + a
            parts.append((w1[:, col:col + m], w3[:, col:col + m], w2[0:m, (e * 3 + i) * P:(e * 3 + i + 1) * P],
                          c.pick_expert[:, e, 0:m]))
    moe(c, c.XT[:], parts, c.cwT, "silu", c.outT[:])
    add_and_norm(c, add=turn_back(c, c.outT), out=c.X, turned=[(c.XT, None, None)], load=c.fetcher("moe1", "turned"))



def layer1_scan(c):
    nc = c.nc
    N = 16
    xnT, dtT, uT = c.big1(0, TOK), c.big1(TOK, TOK), c.big1(2 * TOK, TOK)
    ex, mx = c.big1(3 * TOK, TOK), c.big1(4 * TOK, TOK)
    wb, wc = c.big1(5 * TOK, N * P).rearrange("p (n m) -> p n m", n=N), c.big3(0, N * P).rearrange("p (n m) -> p n m", n=N)
    a, bx, h, ch = (c.big3(2048 + 1024 * i, TOK).rearrange("p (z t) -> p z t", z=2) for i in range(4))
    yT = c.outT
    add_and_norm(c, out=c.XN, turned=[(xnT, c.col("L1_attn_gamma"), c.col("L1_attn_beta"))])
    step, act_step = counter(c, "dve_step"), counter(c, "act_step")
    matmul_stream(c, halves(c, lambda half: [(c.m("L1_WdtT"), xnT[:, half * S:(half + 1) * S])], P, dtT, bias=c.col("L1_attn_b_dt")))
    z_ready, soft_ready, dt_ready = counter(c, "z_ready"), counter(c, "soft_ready"), counter(c, "dt_ready")
    with nc.Block() as block:
        @block.vector
        def _(dve):
            seq(dve, step, nc.vector.tensor_scalar(ex, dtT, -1.0, None, ALU.mult))
            nc.vector.tensor_tensor(ex, ex, dtT, ALU.min).then_inc(z_ready.up(), 1)
            seq(dve, step, nc.vector.tensor_scalar(mx, dtT, 0.0, None, ALU.max))
            dve.wait_ge(soft_ready.sem, soft_ready.at(1))
            seq(dve, step, nc.vector.tensor_tensor(dtT, mx, ex, ALU.add))
            nc.vector.tensor_tensor(uT, dtT, xnT, ALU.mult)
            nc.vector.tensor_scalar(c.negA, c.negA, -1.0, None, ALU.mult).then_inc(dt_ready.up(), 1)

        @block.scalar
        def _(act):
            nc.scalar.activation(c.negA, c.m("L1_A_log"), ACT.Exp)
            act.wait_ge(z_ready.sem, z_ready.at(1))
            seq(act, act_step, nc.scalar.activation(ex, ex, ACT.Exp))
            nc.scalar.activation(ex, ex, ACT.Ln, bias=1.0).then_inc(soft_ready.up(), 1)

        @block.gpsimd
        def _(pool):
            nc.gpsimd.tensor_copy(wb, c.m("L1_WBT").unsqueeze(2).broadcast_to([P, N, P]))
            nc.gpsimd.tensor_copy(wc, c.m("L1_WCT").unsqueeze(2).broadcast_to([P, N, P]))

    BC, YS = c.bank[0:6], c.bank[6:8]
    in_ready, bx_ready, ch_ready, a_ready, sum_ready, decay_used = (counter(c, n) for n in ("in_ready", "bx_ready", "ch_ready", "a_ready", "sum_done", "decay_used"))
    steps = [(n, z) for n in range(N) for z in range(2)]
    with nc.Block() as block:
        @block.tensor
        def _(pe):
            def inputs(s):
                n, z = steps[s]
                x = xnT[:, z * S:(z + 1) * S]
                if s >= 3:
                    pe.wait_ge(ch_ready.sem, ch_ready.at(s - 2))
                nc.tensor.matmul(BC[2 * (s % 3)][:, :], wb[:, n, :], x, start=True, stop=True)
                nc.tensor.matmul(BC[2 * (s % 3) + 1][:, :], wc[:, n, :], x, start=True, stop=True).then_inc(in_ready.up(), 1)

            inputs(0)
            inputs(1)
            for s, (n, z) in enumerate(steps):
                if s + 2 < len(steps):
                    inputs(s + 2)
                pe.wait_ge(ch_ready.sem, ch_ready.at(s + 1))
                nc.tensor.matmul(YS[z][:, :], c.ident[:], ch[:, s % 2, :], start=(n == 0), stop=(n == N - 1)).then_inc(sum_ready.up(), 1)

        @block.scalar
        def _(act):
            for s, (n, z) in enumerate(steps):
                if s >= 2:
                    act.wait_ge(decay_used.sem, decay_used.at(s - 1))
                nc.scalar.activation(a[:, s % 2, :], dtT[:, z * S:(z + 1) * S], ACT.Exp, scale=c.negA[:, n:n + 1]).then_inc(a_ready.up(), 1)

        @block.vector
        def _(dve):
            for s, (n, z) in enumerate(steps):
                dve.wait_ge(in_ready.sem, in_ready.at(s + 1))
                seq(dve, step, nc.vector.tensor_tensor(bx[:, s % 2, :], uT[:, z * S:(z + 1) * S], BC[2 * (s % 3)][:, :], ALU.mult))
                dve.wait_ge(a_ready.sem, a_ready.at(s + 1))
                ins = nc.vector.tensor_tensor_scan(h[:, s % 2, :], a[:, s % 2, :], bx[:, s % 2, :], 0.0, ALU.mult, ALU.add)
                ins.then_inc(decay_used.up(), 1)
                dve.wait_ge(decay_used.sem, decay_used.at(s + 1))
                if s >= 2:
                    dve.wait_ge(sum_ready.sem, sum_ready.at(s - 1))
                nc.vector.tensor_tensor(ch[:, s % 2, :], h[:, s % 2, :], BC[2 * (s % 3) + 1][:, :], ALU.mult).then_inc(ch_ready.up(), 1)
            dve.wait_ge(sum_ready.sem, sum_ready.at(len(steps)))
            for z in range(2):
                nc.vector.scalar_tensor_tensor(out=yT[:, z * S:(z + 1) * S], in0=c.XT[:, z * S:(z + 1) * S],
                                               scalar=c.col("L1_attn_D_param"), in1=YS[z][:, :], op0=ALU.mult, op1=ALU.add)
    add_and_norm(c, add=turn_back(c, yT), out=c.X, turned=[(c.XT, None, None)])


def heads_natural(c, srcT, w, cols, V, width, tiles=NT):
    units = []
    for t in range(tiles):
        for a in range(0, cols, S):
            n = min(S, cols - a)
            who = "act" if t % 2 else "dve"
            dst = V[:, t, a // width:(a + n) // width, 0:width]
            if who == "act":
                emit = (lambda dst: lambda act, bank: c.nc.scalar.copy(dst, bank.rearrange("p (h d) -> p h d", d=width)))(dst)
            else:
                emit = (lambda dst: lambda dve, bank, step: c.nc.vector.tensor_copy(dst, bank.rearrange("p (h d) -> p h d", d=width)))(dst)
            units.append(([(srcT[:, t * P:(t + 1) * P], w[:, a:a + n])], P, n, who, emit))
    return units


def layer1_ffn(c):
    nc = c.nc
    nT = c.big2(2 * TOK, TOK)
    q = c.big1(0, 8 * TOK).rearrange("p (k t) -> p k t", k=8)
    k = c.big2(0, 2 * TOK).rearrange("p (k t) -> p k t", k=2)
    V = c.VH[:, 0:NT * 4 * 64].rearrange("p (t h e) -> p t h e", t=NT, h=4)
    add_and_norm(c, norm="rms", eps=1e-6, out=c.XN, turned=[(nT, c.col("L1_ffn_g1"), None)])
    matmul_stream(c, heads_natural(c, nT, c.m("wv"), 256, V, 64))

    plain_ready, rope_used, dve_step, pool_used = (counter(c, n) for n in ("plain_ready", "rope_used", "dve_step", "pool_used"))
    sin_ready = counter(c, "sin_ready")
    jobs = [(w, ws, dst, kk, half) for w, ws, dst, n in (("wq", "wqs", q, 8), ("wk", "wks", k, 2)) for kk in range(n) for half in range(2)]
    tmp = c.big2(3 * TOK, TOK).rearrange("p (z t) -> p z t", z=2)
    with nc.Block() as block:
        @block.tensor
        def _(pe):
            for s, (w, ws, dst, kk, half) in enumerate(jobs):
                if s >= 4:
                    pe.wait_ge(rope_used.sem, rope_used.at(s - 3))
                x = nT[:, half * S:(half + 1) * S]
                nc.tensor.matmul(c.bank[2 * (s % 4)][:, :], c.m(w)[:, kk * P:(kk + 1) * P], x, start=True, stop=True)
                nc.tensor.matmul(c.bank[2 * (s % 4) + 1][:, :], c.m(ws)[:, kk * P:(kk + 1) * P], x, start=True, stop=True).then_inc(plain_ready.up(), 1)

        @block.vector
        def _(dve):
            for s, (w, ws, dst, kk, half) in enumerate(jobs):
                d = dst[:, kk, half * S:(half + 1) * S]
                dve.wait_ge(plain_ready.sem, plain_ready.at(s + 1))
                nc.vector.tensor_tensor(d, c.bank[2 * (s % 4)][:, :], c.m("cos"), ALU.mult)
                if s >= 2:
                    dve.wait_ge(pool_used.sem, pool_used.at(s - 1))
                nc.vector.tensor_tensor(tmp[:, s % 2, :], c.bank[2 * (s % 4) + 1][:, :], c.m("sin"), ALU.mult).then_inc(rope_used.up(), 1)

        @block.gpsimd
        def _(pool):
            for s, (w, ws, dst, kk, half) in enumerate(jobs):
                d = dst[:, kk, half * S:(half + 1) * S]
                pool.wait_ge(rope_used.sem, rope_used.at(s + 1))
                nc.gpsimd.tensor_tensor(d, d, tmp[:, s % 2, :], ALU.add).then_inc(pool_used.up(), 1)

    def qop(b, h):
        return q[64 * (h % 2):64 * (h % 2) + 64, h // 2, b * S:(b + 1) * S]

    def kop(b, h):
        kv = h % 4
        return k[64 * (kv % 2):64 * (kv % 2) + 64, kv // 2, b * S:(b + 1) * S]

    attention(c, [P] * ST, 64, lambda b, h: [(qop(b, h), kop(b, h))], lambda b, h, i: V[:, b * ST + i, h % 4, 0:64], 0.125, q, mask="causal",
              load=c.fetcher("l2x"))
    yT = q
    hT = c.big2(0, TOK)
    c.rms_out = c.XN
    add_and_norm(c, add=project_out(c, yT, c.m("wo"), 8), total=c.total, norm="rms", eps=1e-6, out=c.XN,
                 turned=[(hT, c.col("L1_ffn_g2"), None)])
    router_logits(c, hT, c.m("L1f_router"), L1E)

    E = L1E
    step = counter(c, "dve_step")
    lg, oh1, oh2, cum, tmp1, tmp2 = (c.rt[:, i, :, 0:E] for i in range(6))
    top = c.top_f
    s_ = lambda i: c.small8[:, i, :]
    (top_done, weights_done, counted, carried) = (counter(c, n) for n in ("top_done", "weights_done", "counted", "carried"))
    with nc.Block() as block:
        @block.vector
        def _(dve):
            bank = c.bank[0][:, 0:NT * 32].rearrange("p (t e) -> p t e", t=NT)[:, :, 0:E]
            seq(dve, step, nc.vector.tensor_tensor(lg, bank, c.m("router_b").unsqueeze(1).broadcast_to([P, NT, E]), ALU.add))
            top_indices(dve, c, step, c.rt[:, 0, :, :], E, top)
            nc.vector.tensor_tensor(s_(0), c.top_v[:, :, 1], c.top_v[:, :, 0], ALU.subtract)
            nc.vector.tensor_copy(oh2, c.m("iota")[:, 0:E].unsqueeze(1).broadcast_to([P, NT, E]))
            seq(dve, step, one_hot(c, E, top[:, :, 0], oh1))
            oh = c.cw_rest[:, :, 0:2 * E]
            nc.vector.tensor_copy(oh[:, :, 0:E], oh1)
            one_hot(c, E, top[:, :, 1], oh[:, :, E:2 * E])
            seq(dve, step, one_hot(c, E, top[:, :, 1], oh2))
            nc.vector.tensor_copy(s_(7), s_(0)).then_inc(top_done.up(), 1)
            dve.wait_ge(counted.sem, counted.at(1))
            cnt = c.bank[1][:, 0:NT * 2 * E].rearrange("p (t e) -> p t e", t=NT)
            cap = float(TOK // 8)
            seq(dve, step, nc.vector.tensor_copy(tmp1, cnt[:, :, 0:E]))
            seq(dve, step, nc.vector.tensor_tensor(tmp2, cnt[:, :, E:2 * E], tmp1, ALU.add))
            seq(dve, step, nc.vector.tensor_scalar(tmp1, tmp1, cap, None, ALU.is_lt))
            seq(dve, step, nc.vector.tensor_scalar(tmp2, tmp2, cap, None, ALU.is_lt))
            seq(dve, step, nc.vector.tensor_tensor(tmp1, tmp1, oh1, ALU.mult))
            seq(dve, step, nc.vector.tensor_tensor(tmp2, tmp2, oh2, ALU.mult))
            nc.vector.tensor_reduce(s_(1), tmp1, AX_X, ALU.add)
            seq(dve, step, nc.vector.tensor_reduce(s_(2), tmp2, AX_X, ALU.add))
            seq(dve, step, nc.vector.tensor_tensor(s_(3), s_(1), top[:, :, 0], ALU.mult))
            seq(dve, step, nc.vector.tensor_tensor(s_(4), s_(2), top[:, :, 1], ALU.mult))
            seq(dve, step, nc.vector.tensor_tensor(s_(3), s_(3), s_(4), ALU.max))
            seq(dve, step, one_hot(c, E, s_(3), cum))
            dve.wait_ge(weights_done.sem, weights_done.at(1))
            seq(dve, step, nc.vector.tensor_scalar(s_(5), s_(7), 1.0, None, ALU.add))
            seq(dve, step, nc.vector.reciprocal(s_(5), s_(5)))
            seq(dve, step, nc.vector.tensor_tensor(s_(6), s_(7), s_(5), ALU.mult))
            seq(dve, step, nc.vector.tensor_tensor(s_(1), s_(1), s_(5), ALU.mult))
            seq(dve, step, nc.vector.tensor_tensor(s_(2), s_(2), s_(6), ALU.mult))
            seq(dve, step, nc.vector.tensor_tensor(s_(1), s_(1), s_(2), ALU.add))
            seq(dve, step, nc.vector.tensor_tensor(s_(5), s_(5), s_(6), ALU.add))
            seq(dve, step, nc.vector.tensor_tensor(s_(2), s_(5), s_(1), ALU.subtract))
            seq(dve, step, nc.vector.tensor_tensor(cum, cum, s_(1).unsqueeze(2).broadcast_to([P, NT, E]), ALU.mult))
            nc.vector.tensor_tensor(c.total[:], c.total[:], c.X[:], ALU.add)

        @block.scalar
        def _(act):
            act.wait_ge(top_done.sem, top_done.at(1))
            nc.scalar.activation(s_(7), s_(7), ACT.Exp).then_inc(weights_done.up(), 1)

        @block.tensor
        def _(pe):
            pe.wait_ge(top_done.sem, top_done.at(1))
            oh = c.cw_rest[:, :, 0:2 * E]
            for t in range(NT):
                for u in range(t + 1):
                    last = nc.tensor.matmul(c.bank[1][:, t * 2 * E:(t + 1) * 2 * E], c.up_to[:] if u == t else c.ones[:],
                                            oh[:, u, :], start=(u == 0), stop=(u == t))
            last.then_inc(counted.up(), 1)

    fill_pick(c, P)
    turn_weights(c, cum, E)
    parts = []
    for e in range(E):
        for i in range(2):
            col = e * L1HID + i * P
            parts.append((c.m("w2")[:, col:col + P], c.m("w1")[:, col:col + P], c.m("w3")[:, (e * 2 + i) * P:(e * 2 + i + 1) * P],
                          c.pick_expert[:, e, :]))
    moe(c, hT, parts, c.cwT, "gelu", c.outT[:])
    own_ready, own_moved = counter(c, "own_ready"), counter(c, "own_moved")
    hn = c.XN
    with nc.Block() as block:
        @block.tensor
        def _(pe):
            for half in range(2):
                for kk in range(4):
                    last = nc.tensor.transpose(c.bank[half][:, kk * P:(kk + 1) * P], hT[:, (half * 4 + kk) * P:(half * 4 + kk + 1) * P], c.ident[:])
                last.then_inc(own_ready.up(), 1)

        @block.vector
        def _(dve):
            for half in range(2):
                dve.wait_ge(own_ready.sem, own_ready.at(half + 1))
                for kk in range(4):
                    t = half * 4 + kk
                    nc.vector.scalar_tensor_tensor(out=c.total[:, t, :], in0=c.bank[half][:, kk * P:(kk + 1) * P],
                                                   scalar=s_(2)[:, t:t + 1], in1=c.total[:, t, :], op0=ALU.mult, op1=ALU.add)
    add_and_norm(c, add=turn_back(c, c.outT), base=c.total, out=c.X, turned=[(c.XT, None, None)], load=c.fetcher("moe2", "l3"))



def layer2_attention(c):
    nc = c.nc
    qf = c.big1(0, TOK)
    kf = c.big1(TOK, TOK)
    V = c.VH[:, 0:NT * HEADS * 9].rearrange("p (t h e) -> p t h e", t=NT, h=HEADS)
    block_product(c, c.m("L2_WQrT")[0:16], c.m("L2_WKrT")[0:16], c.headmat)
    fill(c, V[:, :, :, 8], 1.0)
    x = lambda half: c.XT[:, half * S:(half + 1) * S]
    units = halves(c, lambda half: [(c.m("L2_WQ"), x(half))], P, qf, bias=c.col("L2_attn_bQ"))
    units += halves(c, lambda half: [(c.m("L2_WK"), x(half))], P, kf, bias=c.col("L2_attn_bK"))
    bv = c.row("L2_attn_bV").rearrange("p (h d) -> p h d", d=8)
    for t in range(NT):
        emit = (lambda t: lambda dve, bank, step: nc.vector.tensor_tensor(V[:, t, :, 0:8], bank.rearrange("p (h d) -> p h d", d=8), bv, ALU.add))(t)
        units.append(([(c.XT[:, t * P:(t + 1) * P], c.m("L2_WV"))], P, P, "dve", emit))
    matmul_stream(c, units)
    matmul_stream(c, halves(c, lambda half: [(c.headmat, qf[:, half * S:(half + 1) * S])], P, c.qT))
    split_heads(c, c.qT[:], kf, TOK)
    attention_8(c, [P] * ST, c.Y8, 0.25)
    turn(c, c.Y8, NT, P, c.yT8)
    add_and_norm(c, add=project_out(c, c.yT8, c.m("L2_WO")), bias=c.row("L2_attn_bO"), out=c.X, turned=[(c.XT, None, None)])


def layer2_cross(c):
    q = c.big1(0, 8 * TOK).rearrange("p (k t) -> p k t", k=8)
    k = c.big2(0, 8 * B * SK).rearrange("p (k t) -> p k t", k=8)
    V = c.VH[0:SK, 0:B * HEADS * 64].rearrange("p (b h e) -> p b h e", b=B, h=HEADS)
    ctxT = c.m("ctxT")[0:CTX]
    units = []
    for kk in range(8):
        units += halves(c, (lambda kk: lambda half: [(c.m("L2x_Wq")[:, kk * P:(kk + 1) * P], c.XT[:, half * S:(half + 1) * S])])(kk), P, q[:, kk, :])
        units.append(([(c.m("L2x_Wk")[0:CTX, kk * P:(kk + 1) * P], ctxT)], P, B * SK, "dve" if kk % 2 else "act",
                      dve_copy(c, k[:, kk, :]) if kk % 2 else act_copy(c, k[:, kk, :])))
    for b in range(B):
        for a in range(0, 1024, S):
            emit = (lambda dst: lambda dve, bank, step: c.nc.vector.tensor_copy(dst, bank.rearrange("p (h d) -> p h d", d=64)))(V[:, b, a // 64:(a + S) // 64, 0:64])
            units.append(([(ctxT[:, b * SK:(b + 1) * SK], c.m("L2x_Wv")[0:CTX, a:a + S])], SK, S, "dve", emit))
    matmul_stream(c, units)
    attention(c, [SK], 64,
              lambda b, h: [(q[64 * (h % 2):64 * (h % 2) + 64, h // 2, b * S:(b + 1) * S],
                             k[64 * (h % 2):64 * (h % 2) + 64, h // 2, b * SK:(b + 1) * SK])],
              lambda b, h, i: V[:, b, h, 0:64], 0.125, q)
    add_and_norm(c, add=project_out(c, q, c.m("L2x_Wo"), 8), bias=c.row("L2_xattn_bo"), out=c.X, turned=[(c.XT, None, None)],
                 load=None)


def layer2_moe(c):
    nc, step = c.nc, counter(c, "dve_step")
    E, NG, PG = L2E, 4, 8
    router_logits(c, c.XT[:], c.m("L2_routerT"), E)
    sc, sfc, tmp, sel = (c.rt[:, i, :, :] for i in range(4))
    top = c.top_f
    gtop = c.big3(12 * 1024 // 4 * 1, 256).rearrange("p (t g e) -> p t g e", t=NT, g=NG)
    gs = c.big3(12 * 1024 // 4 + 256, 64).rearrange("p (t e) -> p t e", t=NT)
    gm = c.big3(12 * 1024 // 4 + 320, 64).rearrange("p (t e) -> p t e", t=NT)
    scored = counter(c, "scored")
    with nc.Block() as block:
        @block.scalar
        def _(act):
            lg = c.bank[0][:, 0:NT * 32].rearrange("p (t e) -> p t e", t=NT)
            nc.scalar.activation(sc, lg, ACT.Sigmoid).then_inc(scored.up(), 1)

        @block.vector
        def _(dve):
            seq(dve, step, nc.vector.memset(gs[:], -3.0e38))
            dve.wait_ge(scored.sem, scored.at(1))
            seq(dve, step, nc.vector.tensor_tensor(sfc, sc, c.m("L2_bias").unsqueeze(1).broadcast_to([P, NT, E]), ALU.add))
            for t in range(NT):
                for g in range(NG):
                    last = nc.vector.max(gtop[:, t, g, :], sfc[:, t, g * PG:(g + 1) * PG])
            seq(dve, step, last)
            seq(dve, step, nc.vector.tensor_tensor(gs[:, :, 0:NG], gtop[:, :, :, 0], gtop[:, :, :, 1], ALU.add))
            top_indices(dve, c, step, gs, 8, top)
            iota = c.m("iota")[:, 0:NG].unsqueeze(1).broadcast_to([P, NT, NG])
            seq(dve, step, nc.vector.tensor_tensor(gm[:, :, 0:NG], iota, top[:, :, 0].unsqueeze(2).broadcast_to([P, NT, NG]), ALU.is_equal))
            seq(dve, step, nc.vector.tensor_tensor(gm[:, :, NG:2 * NG], iota, top[:, :, 1].unsqueeze(2).broadcast_to([P, NT, NG]), ALU.is_equal))
            seq(dve, step, nc.vector.tensor_tensor(gm[:, :, 0:NG], gm[:, :, 0:NG], gm[:, :, NG:2 * NG], ALU.add))
            for t in range(NT):
                last = nc.vector.tensor_tensor(tmp[:, t, :].rearrange("p (g e) -> p g e", g=NG), sfc[:, t, :].rearrange("p (g e) -> p g e", g=NG),
                                               gm[:, t, 0:NG].unsqueeze(2).broadcast_to([P, NG, PG]), ALU.mult)
            seq(dve, step, last)
            top_indices(dve, c, step, tmp, E, top)
            seq(dve, step, one_hot(c, E, top[:, :, 0], sel))
            for i in range(1, 4):
                seq(dve, step, one_hot(c, E, top[:, :, i], tmp))
                seq(dve, step, nc.vector.tensor_tensor(sel, sel, tmp, ALU.add))
            seq(dve, step, nc.vector.tensor_tensor(sel, sel, sc, ALU.mult))
            seq(dve, step, nc.vector.tensor_reduce(c.small8[:, 0, :], sel, AX_X, ALU.add))
            seq(dve, step, nc.vector.tensor_scalar(c.small8[:, 0, :], c.small8[:, 0, :], 1e-20, None, ALU.add))
            seq(dve, step, nc.vector.reciprocal(c.small8[:, 1, :], c.small8[:, 0, :]))
            seq(dve, step, nc.vector.tensor_scalar(c.small8[:, 1, :], c.small8[:, 1, :], 2.5, None, ALU.mult))
            seq(dve, step, nc.vector.tensor_tensor(sel, sel, c.small8[:, 1, :].unsqueeze(2).broadcast_to([P, NT, E]), ALU.mult))
    turn_weights(c, sel, E)
    fill_pick(c, 64)
    pick = c.pick_expert.rearrange("p e m -> p (e m)")
    parts = [(c.m("sgT"), c.m("suT"), c.m("sdT"), None)]
    for i in range(E // 2):
        parts.append((c.m("gateT")[:, i * P:(i + 1) * P], c.m("upT")[:, i * P:(i + 1) * P], c.m("downT")[:, i * P:(i + 1) * P],
                      pick[:, i * P:(i + 1) * P]))
    moe(c, c.XT[:], parts, c.cwT, "silu", c.outT[:])
    add_and_norm(c, add=turn_back(c, c.outT), out=c.X, turned=[(c.XT, None, None)], load=c.fetcher("l3x"))


def fill_pick(c, width):
    n = c.pick_flat.shape[1] // width
    n = min(n, 32)
    c.pick_expert = c.pick_flat[:, 0:n * width].rearrange("p (e m) -> p e m", m=width)
    with c.nc.Block() as block:
        @block.gpsimd
        def _(pool):
            c.nc.gpsimd.tensor_copy(c.pick_expert, c.pick_id[:, 0:n].unsqueeze(2).broadcast_to([96, n, width]))



def feed_forward(c, srcT, w1, b1, w2, b2, base, total, **norm):
    h = c.big1(4 * TOK, 4 * TOK).rearrange("p (k t) -> p k t", k=4)
    units = []
    for k in range(4):
        for half in range(2):
            d = h[:, k, half * S:(half + 1) * S]
            units.append(([(w1[:, k * P:(k + 1) * P], srcT[:, half * S:(half + 1) * S])], P, S, "act",
                          act_copy(c, d, bias=b1[:, k:k + 1], func=ACT.Gelu)))
    matmul_stream(c, units)
    add_and_norm(c, add=project_out(c, h, w2, 4), bias=b2, base=base, total=total, **norm)


def layer3_attention(c):
    nc = c.nc
    step, act_step = counter(c, "dve_step"), counter(c, "act_step")
    qT, kT = c.big1(0, TOK), c.big1(TOK, TOK)
    qf = c.big3(0, 4 * TOK).rearrange("p (k t) -> p k t", k=4)
    kf = c.big3(4 * TOK, 4 * TOK).rearrange("p (t f) -> p t f", t=NT)
    V = c.VH[:, 0:NT * 4 * 33].rearrange("p (t h e) -> p t h e", t=NT, h=4)
    tmp = c.big2(0, 2 * TOK).rearrange("p (z t) -> p z t", z=4)
    kv = c.big2(2 * TOK, 4 * B * 36).rearrange("p (k b e) -> p k b e", k=4, b=B)
    w = c.m("L3_wqkvT")
    fill(c, V[:, :, :, 32], 1.0)
    units = halves(c, lambda half: [(w[:, 0:P], c.XT[:, half * S:(half + 1) * S])], P, qT)
    units += halves(c, lambda half: [(w[:, P:2 * P], c.XT[:, half * S:(half + 1) * S])], P, kT)
    units += heads_natural(c, c.XT, w[:, 2 * P:3 * P], P, V, 32)
    matmul_stream(c, units)

    z_ready, low_ready, e_ready, f_ready = (counter(c, n) for n in ("f_product", "low_ready", "e_ready", "f_ready"))
    proj = c.m("L3_proj")
    jobs = [("q", j, half) for j in range(4) for half in range(2)] + [("k", t, 0) for t in range(NT)]
    with nc.Block() as block:
        @block.tensor
        def _(pe):
            for s, (who, i, half) in enumerate(jobs):
                if s >= 4:
                    pe.wait_ge(f_ready.sem, f_ready.at(s - 3))
                if who == "q":
                    last = nc.tensor.matmul(c.bank[s % 4][:, :], proj[:, i * P:(i + 1) * P], qT[:, half * S:(half + 1) * S], start=True, stop=True)
                else:
                    last = nc.tensor.matmul(c.bank[s % 4][:, :], kT[:, i * P:(i + 1) * P], proj, start=True, stop=True)
                last.then_inc(z_ready.up(), 1)

        @block.vector
        def _(dve):
            def low(s):
                dve.wait_ge(z_ready.sem, z_ready.at(s + 1))
                nc.vector.tensor_scalar(tmp[:, s % 4, :], c.bank[s % 4][:, :], 0.0, None, ALU.min).then_inc(low_ready.up(), 1)
            low(0)
            for s, (who, i, half) in enumerate(jobs):
                if s + 1 < len(jobs):
                    low(s + 1)
                dve.wait_ge(e_ready.sem, e_ready.at(s + 1))
                d = qf[:, i, half * S:(half + 1) * S] if who == "q" else kf[:, i, :]
                nc.vector.scalar_tensor_tensor(out=d, in0=c.bank[s % 4][:, :], scalar=0.0, in1=tmp[:, s % 4, :], op0=ALU.max,
                                               op1=ALU.add).then_inc(f_ready.up(), 1)

        @block.scalar
        def _(act):
            for s in range(len(jobs)):
                act.wait_ge(low_ready.sem, low_ready.at(s + 1))
                nc.scalar.activation(tmp[:, s % 4, :], tmp[:, s % 4, :], ACT.Exp).then_inc(e_ready.up(), 1)

    def kv_emit(j, b):
        def emit(dve, bank, step):
            mask = c.m("block_kv")
            nc.vector.tensor_tensor(kv[:, j, b, 0:32], bank[:, 0:32], mask[:, 0:32], ALU.mult)
            return nc.vector.tensor_tensor(kv[:, j, b, 32:36], bank[:, 32:33].broadcast_to([P, 4]), mask[:, 32:36], ALU.mult)
        return emit
    matmul_stream(c, [([(kf[:, b * ST + t, j * P:(j + 1) * P], V[:, b * ST + t, j, :]) for t in range(ST)], P, 33, "dve", kv_emit(j, b))
                      for j in range(4) for b in range(B)])
    attn_ready, den_step = counter(c, "attn_ready"), counter(c, "dve_step")
    Y = c.Y8f.rearrange("p (t j h d) -> p t j h d", t=NT, j=4, h=4)
    rc = c.big2(3 * TOK - 256, 128).rearrange("p (t j h) -> p t j h", t=NT, j=4)
    with nc.Block() as block:
        @block.tensor
        def _(pe):
            for t in range(NT):
                for j in range(4):
                    last = nc.tensor.matmul(c.bank[t % 8][:, j * 36:(j + 1) * 36], qf[:, j, t * P:(t + 1) * P], kv[:, j, t // ST, :], start=True, stop=True)
                last.then_inc(attn_ready.up(), 1)

        @block.vector
        def _(dve):
            for t in range(NT):
                dve.wait_ge(attn_ready.sem, attn_ready.at(t + 1))
                a = c.bank[t % 8][:, 0:144].rearrange("p (j e) -> p j e", j=4)
                seq(dve, step, nc.vector.tensor_scalar(rc[:, t], a[:, :, 32:36], 1e-8, None, ALU.add))
                seq(dve, step, nc.vector.reciprocal(rc[:, t], rc[:, t]))
                nc.vector.tensor_tensor(Y[:, t], a[:, :, 0:32].rearrange("p j (h d) -> p j h d", h=4),
                                        rc[:, t].unsqueeze(3).broadcast_to([P, 4, 4, 8]), ALU.mult)
    turn(c, c.Y8, NT, P, c.yT8)
    rows = (c.row("L3_attn_gamma"), c.row("L3_attn_beta"))
    x1T = c.big3(0, TOK)
    add_and_norm(c, add=project_out(c, c.yT8, c.m("L3_woutT")), bias=c.row("L3_attn_b_out"), total=c.total, out=c.XN, rows=rows,
                 turned=[(x1T, None, None)])
    feed_forward(c, x1T, c.m("L3_w1T"), c.col("L3_attn_b1", 4), c.m("L3_w2T"), c.row("L3_attn_b2"), c.XN, c.total, out=c.XN, rows=rows)
    with nc.Block() as block:
        @block.vector
        def _(dve):
            nc.vector.tensor_tensor(c.X[:], c.X[:], c.XN[:], ALU.add)
    add_and_norm(c, out=c.X, turned=[(c.XT, None, None)])


def layer3_xattn(c):
    nc = c.nc
    x = c.x3
    L = "L3_xattn_"
    y = c.big2(0, 4 * TOK).rearrange("p (k t) -> p k t", k=4)
    xn, yn, x3T = c.big3(4 * TOK, TOK), c.big3(5 * TOK, TOK), c.big3(6 * TOK, TOK)

    for a in (1, 2):
        A = f"{L}a{a}_"
        src = c.X if a == 1 else c.total
        add_and_norm(c, base=src, total=src, out=x, rows=(c.row(f"{L}ln{a}_g"), c.row(f"{L}ln{a}_b")))
        turned = [(xn, c.col(A + "lnx_g"), c.col(A + "lnx_b"))]
        if a == 1:
            turned.append((yn, c.col(A + "lny_g"), c.col(A + "lny_b")))
        add_and_norm(c, base=x, total=x, out=c.XN, turned=turned)
        if a == 2:
            context_norm(c, A)
        units = []
        wq, wk, wv = c.m(f"a{a}_wq"), c.m(f"a{a}_wk"), c.m(f"a{a}_wv")
        split = []
        for kk in range(4):
            cols = slice(kk * P, (kk + 1) * P)
            for b in range(B):
                rows = slice(b * S, (b + 1) * S)
                split.append((wq[:, cols], xn[:, rows], S, c.q_wide[:, :, kk, rows]))
                if a == 1:
                    split.append((wk[:, cols], yn[:, rows], S, c.k_wide[:, :, kk, rows]))
            if a == 2:
                split.append((wk[0:CTX, cols], c.ctxnT[:], B * SK, c.k_wide[:, :, kk, 0:B * SK]))
        project_split(c, split)
        if a == 1:
            V = c.VH[:, 0:NT * HEADS * 32].rearrange("p (t h e) -> p t h e", t=NT, h=HEADS)
            units += heads_natural(c, yn, wv, 512, V, 32)
        else:
            V = c.VH[0:SK, 0:B * HEADS * 32].rearrange("p (t h e) -> p t h e", t=B, h=HEADS)
            for b in range(B):
                emit = (lambda dst: lambda dve, bank, step: nc.vector.tensor_copy(dst, bank.rearrange("p (h d) -> p h d", d=32)))(V[:, b, :, 0:32])
                units.append(([(c.ctxnT[:, b * SK:(b + 1) * SK], wv[0:CTX, :])], SK, S, "dve", emit))
        matmul_stream(c, units)
        attention(c, [P] * ST if a == 1 else [SK], 32, None,
                  (lambda b, h, i: V[:, b * ST + i, h, :]) if a == 1 else (lambda b, h, i: V[:, b, h, :]),
                  32.0 ** -0.5, y, mask="future" if a == 1 else None, stacks=HeadStacks(c, S if a == 1 else SK))
        add_and_norm(c, add=project_out(c, y, c.m(f"a{a}_li1"), 4), bias=c.row(A + "li1_b"), base=x, total=c.total, out=c.XN,
                     turned=[(x3T, c.col(A + "ln3_g"), c.col(A + "ln3_b"))])
        feed_forward(c, x3T, c.m(f"a{a}_li2"), c.col(A + "li2_b", 4), c.m(f"a{a}_li3"), c.row(A + "li3_b"), c.total, c.total, norm=None)
        with nc.Block() as block:
            @block.vector
            def _(dve):
                step = counter(c, "dve_step")
                seq(dve, step, nc.vector.tensor_tensor(c.total[:], c.total[:], x[:], ALU.add))
                if a == 2:
                    nc.vector.tensor_tensor(c.total[:], c.total[:], c.X[:], ALU.add)
    add_and_norm(c, base=c.total, total=c.total, out=c.X, turned=[(c.XT, None, None)])


def context_norm(c, A):
    nc = c.nc
    ctxT = c.m("ctxT")[0:CTX]
    mean_ready, sq_ready, var_ready, r_ready, step = (counter(c, n) for n in ("cm_ready", "csq_ready", "cvar_ready", "cr_ready", "dve_step"))
    n = B * SK
    d, sq, r = c.ctx_tmp[:, 0, :], c.ctx_tmp[:, 1, :], c.ctx_tmp[:, 2, :]
    with nc.Block() as block:
        @block.tensor
        def _(pe):
            nc.tensor.matmul(c.bank[0][0:CTX, 0:n], c.ones[0:CTX, 0:CTX], ctxT, start=True, stop=True).then_inc(mean_ready.up(), 1)
            pe.wait_ge(sq_ready.sem, sq_ready.at(1))
            nc.tensor.matmul(c.bank[1][0:CTX, 0:n], c.ones[0:CTX, 0:CTX], sq, start=True, stop=True).then_inc(var_ready.up(), 1)

        @block.vector
        def _(dve):
            dve.wait_ge(mean_ready.sem, mean_ready.at(1))
            seq(dve, step, nc.vector.scalar_tensor_tensor(out=d, in0=c.bank[0][0:CTX, 0:n], scalar=-1.0 / CTX, in1=ctxT, op0=ALU.mult, op1=ALU.add))
            nc.vector.tensor_tensor(sq, d, d, ALU.mult).then_inc(sq_ready.up(), 1)
            dve.wait_ge(var_ready.sem, var_ready.at(1))
            nc.vector.tensor_scalar(sq, c.bank[1][0:CTX, 0:n], 1.0 / CTX, 1e-5, ALU.mult, ALU.add).then_inc(sq_ready.up(), 1)
            dve.wait_ge(r_ready.sem, r_ready.at(1))
            seq(dve, step, nc.vector.tensor_tensor(d, d, r, ALU.mult))
            nc.vector.tensor_scalar(c.ctxnT[:], d, c.col(A + "lny_g")[0:CTX], c.col(A + "lny_b")[0:CTX], ALU.mult, ALU.add)

        @block.gpsimd
        def _(pool):
            pool.wait_ge(sq_ready.sem, sq_ready.at(2))
            nc.gpsimd.tensor_tensor(r, sq, c.minus_half[0:CTX, 0:1].broadcast_to([CTX, n]), ALU.pow).then_inc(r_ready.up(), 1)


def layer3_ffn(c, out_dram):
    nc, step = c.nc, counter(c, "dve_step")
    xp, xr, xk = c.big1(0, TOK), c.big1(TOK, TOK), c.big1(2 * TOK, TOK)
    r, k2 = c.big1(3 * TOK, TOK), c.big1(4 * TOK, TOK)
    one_minus = c.small[:, 4:6]
    with nc.Block() as block:
        @block.vector
        def _(dve):
            for b in range(B):
                nc.vector.memset(xp[:, b * S:b * S + 1], 0.0)
                last = nc.vector.tensor_copy(xp[:, b * S + 1:(b + 1) * S], c.XT[:, b * S:(b + 1) * S - 1])
            for i, n in enumerate(("L3_ffn_mu_r", "L3_ffn_mu_k")):
                last = nc.vector.tensor_scalar(one_minus[:, i:i + 1], c.col(n), -1.0, 1.0, ALU.mult, ALU.add)
            seq(dve, step, last)
            nc.vector.tensor_scalar(xr, xp, one_minus[:, 0:1], None, ALU.mult)
            seq(dve, step, nc.vector.tensor_scalar(xk, xp, one_minus[:, 1:2], None, ALU.mult))
            for n, d in (("L3_ffn_mu_r", xr), ("L3_ffn_mu_k", xk)):
                nc.vector.scalar_tensor_tensor(out=d, in0=c.XT[:], scalar=c.col(n), in1=d, op0=ALU.mult, op1=ALU.add)
    h = lambda ap, half: ap[:, half * S:(half + 1) * S]

    def square_relu(d):
        def emit(dve, bank, step):
            seq(dve, step, nc.vector.tensor_scalar(d, bank, 0.0, None, ALU.max))
            return nc.vector.tensor_tensor(d, d, d, ALU.mult)
        return emit
    units = []
    for half in range(2):
        units.append(([(c.m("L3f_WkT"), h(xk, half))], P, S, "dve", square_relu(h(k2, half))))
        units.append(([(c.m("L3f_WrT"), h(xr, half))], P, S, "act", act_copy(c, h(r, half), func=ACT.Sigmoid)))
    matmul_stream(c, units)

    def gate(half):
        return lambda dve, bank, step: nc.vector.tensor_tensor(h(c.outT, half), bank, h(r, half), ALU.mult)
    matmul_stream(c, [([(c.m("L3f_WvT"), h(k2, half))], P, S, "dve", gate(half)) for half in range(2)])
    add_and_norm(c, add=turn_back(c, c.outT), out=c.XN, store=out_dram)



def decoder(nc, dram, out_dram, q_dram, k_dram, q_wide, k_wide):
    with ExitStack() as ctx:
        c = Core(nc, ctx)
        c.dram, c.q_dram, c.k_dram, c.q_wide, c.k_wide = dram, q_dram, k_dram, q_wide, k_wide
        tiles = lambda t: t[:].rearrange("p (t f) -> p t f", t=NT)
        X, XT, XN, total = (c.sb(n, [P, TOK]) for n in ("x", "xT", "normed", "total"))
        c.X, c.XT, c.XN, c.total = tiles(X), XT, tiles(XN), tiles(total)
        c.rest_q, c.rest_k = XN[:], total[:]
        c.big = [c.sb("big1", [P, 8 * TOK]), c.sb("big2", [P, 4 * TOK]), c.sb("big3", [P, 8 * TOK])]
        c.VH = c.sb("v_heads", [P, NT * HEADS * 33])
        moe_w, late_w = c.sb("moe_weights", [P, max(width(p) for p in ("moe0", "moe1"))]), c.sb("late_weights", [P, 4 * TOK])
        mid_w = c.sb("mid_weights", [P, width("mid")])
        c.rows, c.cols = c.sb("rows", [P, P * len(row_names())]), c.sb("cols", [P, sum(n for _, n in col_names())])
        c.memories = {"const": (c.big[1], 0), "first": (late_w, width("turned")), "early": (late_w, width("turned") + width("first")), "moe0": (moe_w, 0),
                      "moe1": (moe_w, 0), "moe2": (moe_w, 0), "l3": (moe_w, width("moe2")), "mid": (mid_w, 0),
                      "turned": (late_w, 0), "l2x": (late_w, 0), "l3x": (moe_w, 0)}
        c.matrices = {}
        for pack, (memory, at) in c.memories.items():
            for name, rows, cols in MATRICES[pack]:
                c.matrices[name] = memory[0:rows, at:at + cols]
                at += cols
        c.loaded = {pack: ctx.enter_context(nc.semaphore(f"loaded_{pack}")) for pack in c.memories}
        vectors_loaded = ctx.enter_context(nc.semaphore("vectors_loaded"))
        x_loaded = ctx.enter_context(nc.semaphore("x_loaded"))
        c.stored = ctx.enter_context(nc.semaphore("out_stored"))
        c.stored_parts, c.loaded_heads = (ctx.enter_context(nc.semaphore(n)) for n in ("parts_in_dram", "heads_loaded_dma"))
        c.nparts = c.nheads = 0

        c.ident, c.key_later, c.up_to, c.ones = (c.sb(n, [P, P]) for n in ("ident", "key_later", "up_to", "ones"))
        c.ident_bf = c.sb("ident_bf", [P, P], BF16)
        c.before_key, c.after_query = (c.sb(n, [P, S], BF16) for n in ("before_key", "after_query"))
        pick = c.sb("pick", [P, 4 * P], BF16)
        c.pick = pick[:].rearrange("p (j m) -> p j m", j=4)
        c.zeros_bf = c.sb("zeros_bf", [P, P], BF16)
        c.pick_id = c.sb("pick_id", [96, 32], BF16)
        c.minus_half = c.sb("minus_half", [P, 8])

        E, EM = c.big3(0, 4 * TOK), c.sb("masked_weights", [P, 8 * P])
        c.E = [E[:, i * TOK:(i + 1) * TOK].rearrange("p (x t) -> p x t", x=2) for i in range(4)]
        c.EM = [EM[:, i * 2 * P:(i + 1) * 2 * P].rearrange("p (x t) -> p x t", x=2) for i in range(4)]
        c.OT = c.sb("heads_out", [P, 2 * S])[:].rearrange("p (z t) -> p z t", z=2)
        c.MX = c.sb("maxima", [P, ST * 4])[:].rearrange("p (j t) -> p j t", t=ST)
        c.NM = c.sb("negmax", [P, 2 * ST * P], BF16)[:].rearrange("p (z t r) -> p z t r", z=2, t=ST)
        c.NMT = c.sb("negmaxT", [P, 2 * S], BF16)[:].rearrange("p (z t) -> p z t", z=2)
        c.RC = c.sb("reciprocals", [P, 2 * ST * 4])[:].rearrange("p (z t j) -> p z t j", z=2, t=ST)

        c.stats = c.sb("stats", [P, NT * 6])[:].rearrange("p (t s) -> p t s", t=NT)
        c.mv = c.sb("mean_var", [P, NT * 2])[:].rearrange("p (t s) -> p t s", t=NT)
        c.rstd, c.amax = c.sb("rstd", [P, NT]), c.sb("amax", [P, NT])[:]
        c.small, c.negA = c.sb("small", [P, 8]), c.sb("negA", [P, 16])[:]
        c.small8 = c.sb("small8", [P, 8 * NT])[:].rearrange("p (i t) -> p i t", i=8)
        c.ckT = c.sb("ctx_kT", [P, B * SK])
        bf = lambda ap: ap.bitcast(BF16)
        spare = width("turned") + width("first") + width("early")
        late = lambda a, n: late_w[:, spare + a:spare + a + n]
        c.signT = bf(late(0, P)).rearrange("p (z m) -> p z m", z=2)
        c.tern = bf(late(P, P)).rearrange("p (z m) -> p z m", z=2)
        c.alpha = late(2 * P, 2 * P).rearrange("p (z m) -> p z m", z=2)
        c.headmat = c.sb("headmat", [P, P])[:]

        c.Y8f, c.Y8 = c.big2(3 * TOK, TOK), c.big2(3 * TOK, TOK).rearrange("p (t f) -> p t f", t=NT)
        c.q_parts = bf(c.big2(0, 1536)).rearrange("p (z t) -> p z t", z=3)
        c.k_parts = bf(c.big2(1536, 1536)).rearrange("p (z t) -> p z t", z=3)
        c.rest2 = c.big2(0, P)
        c.qk32 = c.big1(0, 2 * TOK).rearrange("p (z t) -> p z t", z=2)
        c.QH = bf(c.big1(0, 8 * TOK)).rearrange("p (h x t) -> p h x t", h=HEADS // 2, x=2)
        c.KH = bf(c.big3(4 * TOK, 4 * TOK))
        c.qT, c.yT8 = c.big3(0, TOK), c.big1(0, TOK).rearrange("p (k t) -> p k t", k=1)
        c.q_bf, c.qT_bf = bf(c.big1(4 * TOK, TOK // 2)).rearrange("p (t f) -> p t f", t=NT), bf(c.big1(5 * TOK, TOK // 2))
        c.moe_sg, c.moe_h = (c.big1(i * TOK, TOK).rearrange("p (z t) -> p z t", z=2) for i in (0, 1))
        c.outT = c.big1(2 * TOK, TOK)
        c.cwT = bf(c.big3(0, TOK // 2))[0:96]
        c.cw_parts = bf(c.big3(512, 384)).rearrange("p (t r) -> p t r", t=NT)
        c.cw_rest = c.big3(1024, 256).rearrange("p (t e) -> p t e", t=NT)
        c.rt = c.big3(1280, 6 * 256).rearrange("p (i t e) -> p i t e", i=6, t=NT)
        c.top_v = c.big3(2816, 64).rearrange("p (t k) -> p t k", t=NT)
        c.top_i = c.big3(2880, 64).bitcast(U32).rearrange("p (t k) -> p t k", t=NT)
        c.top_f = c.big3(2944, 64).rearrange("p (t k) -> p t k", t=NT)
        c.pick_flat = bf(c.big3(4096, 1024))[0:96]
        c.x3 = c.big3(7 * TOK, TOK).rearrange("p (t f) -> p t f", t=NT)
        c.ctx_tmp = c.VH[0:CTX, 0:3 * B * SK].rearrange("p (z t) -> p z t", z=3)
        c.ctxnT = c.sb("ctx_normed", [CTX, B * SK])

        psum = c.ps("banks", [P, 8 * 512])
        c.banks = psum[:].rearrange("p (i t) -> p i t", i=8)
        c.bank = [psum[:, i * 512:(i + 1) * 512] for i in range(8)]
        c.banks_bf = [b[:, 0:256].bitcast(BF16) for b in c.bank]
        c.bank_bf = c.banks_bf[7]
        c.key_stack = bf(c.big2(0, 3 * TOK)).rearrange("p (u z d) -> p u z d", z=6, d=8)

        x_in = dram["x"].rearrange("(t p) f -> p t f", p=P)
        const_ready = counter(c, "const_ready")
        with nc.Block() as block:
            @block.sync
            def _(sp):
                sp.dma_start(c.X[:], x_in).then_inc(x_loaded, 16)
                for pack in ("const", "first"):
                    c.fetch(sp, pack)
                sp.dma_start(c.rows[:], dram["rows"].partition_broadcast(P)).then_inc(vectors_loaded, 16)
                sp.dma_start(c.cols[:], dram["cols"]).then_inc(vectors_loaded, 16)
                for pack in ("mid", "early", "moe0"):
                    c.fetch(sp, pack)
                sp.wait_ge(x_loaded, 16)
                sp.wait_ge(vectors_loaded, 32)
                for pack in ("first", "mid", "early"):
                    sp.wait_ge(c.loaded[pack], 16)

            @block.vector
            def _(dve):
                dve.wait_ge(c.loaded["const"], 16)
                nc.vector.tensor_copy(c.ident[:], c.m("ident"))
                nc.vector.tensor_copy(c.ident_bf[:], c.m("ident"))
                nc.vector.tensor_copy(c.key_later[:], c.m("later"))
                nc.vector.tensor_scalar(c.up_to[:], c.m("later"), -1.0, 1.0, ALU.mult, ALU.add)
                nc.vector.tensor_scalar(c.before_key[:, 0:P], c.m("later"), NEG, None, ALU.mult)
                nc.vector.tensor_scalar(c.after_query[:, S - P:S], c.m("later_t"), NEG, None, ALU.mult)
                nc.vector.tensor_copy(pick[:], c.m("pick"))
                nc.vector.tensor_copy(c.pick_id[:], c.m("pick_id"))

            @block.gpsimd
            def _(pool):
                nc.gpsimd.memset(c.ones[:], 1.0)
                nc.gpsimd.memset(c.before_key[:, P:S], 0.0)
                nc.gpsimd.memset(c.after_query[:, 0:S - P], 0.0)
                nc.gpsimd.memset(c.NM[:], 0.0)
                nc.gpsimd.memset(c.zeros_bf[:], 0.0)
                nc.gpsimd.memset(c.minus_half[:], -0.5)

        stages = [
            lambda: layer0_attention(c),
            lambda: cross_attention_8(c, c.m("L0x_WqT"), c.m("L0x_WkvT")[:, 0:P], c.m("L0x_WkvT")[:, P:2 * P], c.m("L0x_WoT"),
                                      None, None, None, None),
            lambda: (fill_pick(c, P), c.await_loads("moe0"), layer0_moe(c)),
            lambda: layer1_scan(c),
            lambda: cross_attention_8(c, c.m("L1x_Wq"), c.m("L1x_Wk"), c.m("L1x_Wv"), c.m("L1x_Wo"), c.col("L1_xattn_bq"),
                                      c.col("L1_xattn_bk"), c.row("L1_xattn_bv"), c.row("L1_xattn_bo")),
            lambda: (c.await_loads("moe1", "turned"), layer1_ffn(c)),
            lambda: layer2_attention(c),
            lambda: (c.await_loads("l2x"), layer2_cross(c)),
            lambda: (c.await_loads("moe2", "l3"), layer2_moe(c)),
            lambda: layer3_attention(c),
            lambda: (c.await_loads("l3x"), layer3_xattn(c)),
            lambda: layer3_ffn(c, out_dram),
        ]
        for stage in stages:
            stage()



def constants():
    p, f = np.arange(P)[:, None], np.arange(P)[None, :]
    pos = np.arange(S, dtype=np.float32)
    inv4 = (1.0 / 10000.0 ** (np.arange(4, dtype=np.float32) / np.float32(4))).astype(np.float32)
    tile_pos = pos.reshape(ST, P).T
    aq = tile_pos[:, :, None] * inv4
    ak = (16 * (np.arange(P) % 32)[:, None] + np.arange(16)[None, :]).astype(np.float32)[:, :, None] * inv4
    inv32 = (10000.0 ** (-np.arange(0, 64, 2, dtype=np.float32) / 64)).astype(np.float32)
    ticks = inv32[np.arange(P) % 32][:, None] * pos[None, :]
    sign = np.where(np.arange(P) % 64 < 32, -1.0, 1.0)[:, None]
    block = np.zeros((P, 36))
    for h in range(4):
        block[32 * h:32 * h + 32, 8 * h:8 * h + 8] = 1.0
        block[32 * h:32 * h + 32, 32 + h] = 1.0
    out = {
        "ident": p == f, "later": p > f, "later_t": f > p,
        "pick": np.concatenate([np.repeat(p // 2 == 16 * j, P, axis=1) for j in range(4)], axis=1),
        "pick_id": np.arange(96)[:, None] % 32 == np.arange(32)[None, :],
        "same_head": p // 8 == f // 8,
        "iota": np.repeat(np.arange(32)[None, :], P, axis=0),
        "rope_q": np.concatenate([np.cos(aq).reshape(P, -1), np.sin(aq).reshape(P, -1)], axis=1),
        "rope_k": np.concatenate([np.cos(ak).reshape(P, -1), np.sin(ak).reshape(P, -1)], axis=1),
        "cos": np.cos(ticks), "sin": np.sin(ticks) * sign, "block_kv": block,
    }
    return {k: v.astype(np.float32) for k, v in out.items()}


def by_rows(w):
    k = w.shape[0] // P
    return w.reshape(k, P, -1).transpose(1, 0, 2).reshape(P, -1)


def lay_out(a):
    m = constants()
    every = lambda v: np.broadcast_to(v[None, :], (P, v.shape[0]))
    heads8 = lambda u: np.concatenate([u] * HEADS, axis=1)
    m["L0_Wqkv"], m["L0_Wo"] = a["L0_attn_Wqkv_w"], a["L0_attn_Wo_w"]
    m["L0_UT"] = heads8(a["L0_attn_U"].T)
    m["ctxT"] = a["ctx_512"].reshape(B * SK, CTX).T
    m["L0x_WqT"], m["L0x_WkvT"], m["L0x_WoT"] = a["L0_xattn_Wq"].T, a["L0_xattn_Wkv"].T, a["L0_xattn_Wo"].T
    m["L0_gateT"] = np.concatenate([a["L0_ffn_gate_weight"], a["L0_ffn_new_gate_weight"]]).T
    m["gate_bias"] = every(np.concatenate([np.zeros(8, np.float32), a["L0_ffn_gate_bias"]]))
    for n, new in (("w1", "new_w1"), ("w3", "new_w3")):
        w = np.concatenate([a[f"L0_ffn_{n}"], a[f"L0_ffn_{new}"]])
        m[n + "T"] = w.transpose(2, 0, 1).reshape(P, -1)
    w = np.concatenate([a["L0_ffn_w2"], a["L0_ffn_new_w2"]]).transpose(0, 2, 1)
    padded = np.zeros((L0E, 3 * P, P), np.float32)
    padded[:, 0:L0HID] = w
    m["w2T"] = padded.reshape(L0E, 3, P, P).transpose(2, 0, 1, 3).reshape(P, -1)
    m["L1_WdtT"], m["L1_WBT"], m["L1_WCT"], m["L1_A_log"] = a["L1_attn_W_dt"].T, a["L1_attn_W_B"].T, a["L1_attn_W_C"].T, a["L1_attn_A_log"]
    for n in ("Wq", "Wk", "Wv", "Wo"):
        m["L1x_" + n] = a["L1_xattn_" + n]
    m["L1f_router"], m["router_b"] = a["L1_ffn_router_w"], every(a["L1_ffn_router_b"])
    for n in ("WQ", "WK", "WV", "WO"):
        m["L2_" + n] = a["L2_attn_" + n]
    m["L2_WQrT"], m["L2_WKrT"] = heads8(a["L2_attn_WQr"].T), heads8(a["L2_attn_WKr"].T)
    m["L2_routerT"], m["L2_bias"] = a["L2_ffn_router_weight"].T, every(a["L2_ffn_router_bias"])
    m["w1"], m["w2"] = (a["L1_ffn_" + n].transpose(1, 0, 2).reshape(P, -1) for n in ("w1", "w2"))
    m["w3"] = by_rows(a["L1_ffn_w3"].reshape(L1E * L1HID, P))
    m["wq"], m["wk"], m["wv"], m["wo"] = a["L1_ffn_wq"], a["L1_ffn_wk"], a["L1_ffn_wv"], by_rows(a["L1_ffn_wo"])
    swap = lambda w: w.reshape(P, -1, 2, 32)[:, :, ::-1, :].reshape(P, -1)
    m["wqs"], m["wks"] = swap(a["L1_ffn_wq"]), swap(a["L1_ffn_wk"])
    m["L2x_Wq"], m["L2x_Wk"], m["L2x_Wv"], m["L2x_Wo"] = a["L2_xattn_Wq"], a["L2_xattn_Wk"], a["L2_xattn_Wv"], by_rows(a["L2_xattn_Wo"])
    m["gateT"], m["upT"] = (a["L2_ffn_" + n].transpose(2, 0, 1).reshape(P, -1) for n in ("gate_w", "up_w"))
    m["downT"] = by_rows(a["L2_ffn_down_w"].transpose(0, 2, 1).reshape(L2E * L2HID, P))
    m["sgT"], m["suT"], m["sdT"] = (a[f"L2_ffn_shared_{n}_w"].T for n in ("gate", "up", "down"))
    m["L3_wqkvT"] = a["L3_attn_w_qkv"].T
    proj = np.zeros((HEADS, 8, HEADS, 32), np.float32)
    for h in range(HEADS):
        proj[h, :, h, :] = a["L3_attn_proj"][h]
    m["L3_proj"] = proj.reshape(P, 4 * P)
    m["L3_woutT"], m["L3_w1T"], m["L3_w2T"] = a["L3_attn_w_out"].T, a["L3_attn_w1"].T, by_rows(a["L3_attn_w2"].T)
    m["L3f_WrT"], m["L3f_WkT"], m["L3f_WvT"] = a["L3_ffn_W_r"].T, a["L3_ffn_W_k"].T, a["L3_ffn_W_v"].T
    for i in (1, 2):
        x = f"L3_xattn_a{i}_"
        for n in ("wq", "wk", "wv"):
            w = a[x + n]
            m[f"a{i}_{n}"] = w.transpose(1, 0, 2).reshape(w.shape[1], -1)
        m[f"a{i}_li1"], m[f"a{i}_li2"], m[f"a{i}_li3"] = by_rows(a[x + "li1_w"]), a[x + "li2_w"], by_rows(a[x + "li3_w"])

    out = {"x": a["x"].reshape(TOK, P)}
    for pack, names in MATRICES.items():
        whole = np.zeros((P, width(pack)), np.float32)
        at = 0
        for name, rows, cols in names:
            whole[0:rows, at:at + cols] = m[name]
            at += cols
        out[pack] = whole
    out["rows"] = np.concatenate([a[n] for n in row_names()]).reshape(1, -1)
    cols = np.zeros((P, sum(n for _, n in col_names())), np.float32)
    at = 0
    for name, n in col_names():
        v = a[name]
        if v.shape[0] < P:
            cols[0:v.shape[0], at] = v
        else:
            cols[:, at:at + n] = v.reshape(n, P).T
        at += n
    out["cols"] = cols
    return out


def build(nc, arrays):
    dram = {name: nc.dram_tensor("in_" + name, v.shape, F32, kind="ExternalInput").ap() for name, v in arrays.items()}
    out = nc.dram_tensor("out", (TOK, P), F32, kind="ExternalOutput").ap()
    q_dram = nc.dram_tensor("q_parts", (P, 3, TOK), BF16, kind="Internal").ap()
    k_dram = nc.dram_tensor("k_parts", (P, 3, TOK), BF16, kind="Internal").ap()
    q_wide, k_wide = (nc.dram_tensor(n, (P, 3, 4, TOK), BF16, kind="Internal").ap() for n in ("q_wide", "k_wide"))
    decoder(nc, dram, out.rearrange("(t p) f -> p t f", p=P), q_dram, k_dram, q_wide, k_wide)


def kernel(**inputs):
    import concourse.bacc as bacc
    from concourse.bass_utils import run_bass_kernel_spmd

    arrays = {k: np.ascontiguousarray(v) for k, v in lay_out({k: np.asarray(v) for k, v in inputs.items()}).items()}
    nc = bacc.Bacc("TRN2", target_bir_lowering=False, num_devices=1)
    build(nc, arrays)
    r = run_bass_kernel_spmd(nc, [{"in_" + k: v for k, v in arrays.items()}], core_ids=[0])
    return r.results[0]["out"].reshape(B, S, P)
```

```python
from contextlib import ExitStack

import numpy as np
import concourse.bass as bass
from concourse import mybir
from concourse.alu_op_type import AluOpType as ALU

ACT = mybir.ActivationFunctionType
F32 = mybir.dt.float32
BF16 = mybir.dt.bfloat16
U32 = mybir.dt.uint32
AX_X = mybir.AxisListType.X

P = 128
B, S = 2, 512
TOK = B * S
NT = TOK // P
ST = S // P
HEADS = 16
SK = 77
CTX = 64
NEG = -1.0e30
ROUND = 1.5 * 2.0 ** 23


class Signal:

    def __init__(self, sem):
        self.sem, self.base, self.sent = sem, 0, 0

    def up(self, n=1):
        self.sent += n
        return self.sem

    def at(self, n):
        return self.base + n


def width(pack):
    return sum(cols for _, _, cols in MATRICES[pack])


class Core:

    def __init__(self, nc, ctx):
        self.nc, self.ctx, self.counters = nc, ctx, {}

    def sb(self, name, shape, dt=F32):
        return self.ctx.enter_context(self.nc.sbuf_tensor(name, shape, dt))

    def ps(self, name, shape, dt=F32):
        return self.ctx.enter_context(self.nc.psum_tensor(name, shape, dt))

    def big1(self, a, n):
        return self.big[0][:, a:a + n]

    def big2(self, a, n):
        return self.big[1][:, a:a + n]

    def big3(self, a, n):
        return self.big[2][:, a:a + n]

    def m(self, name):
        return self.matrices[name]

    def row(self, name):
        i = row_names().index(name)
        return self.rows[:, i * P:(i + 1) * P]

    def col(self, name, n=1):
        at = 0
        for other, k in col_names():
            if other == name:
                return self.cols[:, at:at + n]
            at += k
        raise KeyError(name)

    def fetch(self, sp, pack):
        memory, at = self.memories[pack]
        n = width(pack)
        sp.dma_start(memory[:, at:at + n], self.dram[pack]).then_inc(self.loaded[pack], 16)

    def fetcher(self, *packs):
        def program(sp):
            for pack in packs:
                self.fetch(sp, pack)
        return program

    def await_loads(self, *packs):
        with self.nc.Block() as block:
            @block.sync
            def _(sp):
                for pack in packs:
                    sp.wait_ge(self.loaded[pack], 16)



def counter(c, name):
    if name not in c.counters:
        c.counters[name] = Signal(c.ctx.enter_context(c.nc.semaphore(name)))
    s = c.counters[name]
    s.base = s.sent
    return s


def seq(eng, step, ins):
    ins.then_inc(step.up(), 1)
    eng.wait_ge(step.sem, step.sent)



def row_names():
    return ["L0_attn_Wqkv_b", "L1_xattn_bv", "L1_xattn_bo", "L2_attn_bV", "L2_attn_bO",
            "L2_xattn_bo", "L3_attn_b_out", "L3_attn_gamma", "L3_attn_beta", "L3_attn_b2",
            "L3_xattn_ln1_g", "L3_xattn_ln1_b", "L3_xattn_ln2_g", "L3_xattn_ln2_b",
            "L3_xattn_a1_li1_b", "L3_xattn_a1_li3_b", "L3_xattn_a2_li1_b", "L3_xattn_a2_li3_b"]


def col_names():
    return [("L1_attn_gamma", 1), ("L1_attn_beta", 1), ("L1_attn_b_dt", 1), ("L1_attn_D_param", 1),
            ("L1_xattn_bq", 1), ("L1_xattn_bk", 1), ("L1_ffn_g1", 1), ("L1_ffn_g2", 1),
            ("L2_attn_bQ", 1), ("L2_attn_bK", 1), ("L3_attn_b1", 4),
            ("L3_xattn_a1_lnx_g", 1), ("L3_xattn_a1_lnx_b", 1), ("L3_xattn_a1_lny_g", 1),
            ("L3_xattn_a1_lny_b", 1), ("L3_xattn_a1_ln3_g", 1), ("L3_xattn_a1_ln3_b", 1),
            ("L3_xattn_a1_li2_b", 4), ("L3_xattn_a2_lnx_g", 1), ("L3_xattn_a2_lnx_b", 1),
            ("L3_xattn_a2_lny_g", 1), ("L3_xattn_a2_lny_b", 1), ("L3_xattn_a2_ln3_g", 1),
            ("L3_xattn_a2_ln3_b", 1), ("L3_xattn_a2_li2_b", 4), ("L3_ffn_mu_r", 1), ("L3_ffn_mu_k", 1)]


def chunks(n):
    return [(a, min(P, n - a)) for a in range(0, n, P)]


L0E, L0HID = 9, 352
L1E, L1HID = 8, 256
L2E, L2HID = 32, 64
MATRICES = {
    "first": [("L0_Wqkv", P, P), ("L0_Wo", P, P), ("L0_UT", 32, P), ("rope_q", P, 2 * ST * 4), ("rope_k", P, 2 * 64)],
    "early": [("L0x_WqT", P, P), ("L0x_WkvT", CTX, 2 * P), ("L0x_WoT", P, P), ("L0_gateT", P, L0E), ("gate_bias", P, L0E)],
    "moe0": [("w1T", P, L0E * L0HID), ("w3T", P, L0E * L0HID), ("w2T", P, L0E * 3 * P)],
    "const": [("ident", P, P), ("later", P, P), ("later_t", P, P), ("pick_id", 96, 32), ("pick", P, 4 * P)],
    "mid": [("iota", P, 32), ("same_head", P, P), ("ctxT", CTX, B * SK), ("L1_WdtT", P, P), ("L1_WBT", P, 16), ("L1_WCT", P, 16), ("L1_A_log", P, 16),
            ("L1x_Wq", P, P), ("L1x_Wk", CTX, P), ("L1x_Wv", CTX, P), ("L1x_Wo", P, P),
            ("L1f_router", P, L1E), ("router_b", P, L1E),
            ("L2_WQ", P, P), ("L2_WK", P, P), ("L2_WV", P, P), ("L2_WO", P, P),
            ("L2_WQrT", 16, P), ("L2_WKrT", 16, P), ("L2_routerT", P, L2E), ("L2_bias", P, L2E)],
    "moe1": [("w1", P, L1E * L1HID), ("w2", P, L1E * L1HID), ("w3", P, L1E * 2 * P),
             ("wq", P, 1024), ("wk", P, 256), ("wv", P, 256), ("wo", P, 8 * P)],
    "turned": [("wqs", P, 1024), ("wks", P, 256), ("cos", P, S), ("sin", P, S)],
    "l2x": [("L2x_Wq", P, 1024), ("L2x_Wk", CTX, 1024), ("L2x_Wv", CTX, 1024), ("L2x_Wo", P, 8 * P)],
    "moe2": [("gateT", P, L2E * L2HID), ("upT", P, L2E * L2HID), ("downT", P, 16 * P),
             ("sgT", P, P), ("suT", P, P), ("sdT", P, P)],
    "l3": [("L3_wqkvT", P, 3 * P), ("L3_proj", P, 4 * P), ("L3_woutT", P, P), ("L3_w1T", P, 4 * P),
           ("L3_w2T", P, 4 * P), ("L3f_WrT", P, P), ("L3f_WkT", P, P), ("L3f_WvT", P, P),
           ("block_kv", P, 36)],
    "l3x": [(f"a{i}_{n}", r, c) for i in (1, 2) for n, r, c in
            (("wq", P, 512), ("wk", P if i == 1 else CTX, 512), ("wv", P if i == 1 else CTX, 512),
             ("li1", P, 4 * P), ("li2", P, 4 * P), ("li3", P, 4 * P))],
}



def matmul_stream(c, units, load=None):
    nc = c.nc
    product_ready, act_freed, dve_freed = counter(c, "product_ready"), counter(c, "act_freed"), counter(c, "dve_freed")
    dve_step = counter(c, "dve_step")
    freed = []
    count = {"act": 0, "dve": 0}
    for u in units:
        count[u[3]] += 1
        freed.append((u[3], count[u[3]]))

    def bank(u):
        return c.bank[u % 8][0:units[u][1], 0:units[u][2]]

    with nc.Block() as block:
        if load:
            block.sync(load)

        @block.tensor
        def _(pe):
            for u, (products, _, _, _, _) in enumerate(units):
                if u >= 8:
                    who, n = freed[u - 8]
                    s = act_freed if who == "act" else dve_freed
                    pe.wait_ge(s.sem, s.at(n))
                for k, (lhsT, rhs) in enumerate(products):
                    last = nc.tensor.matmul(bank(u), lhsT, rhs, start=(k == 0), stop=(k == len(products) - 1))
                last.then_inc(product_ready.up(), 1)

        @block.scalar
        def _(act):
            for u, unit in enumerate(units):
                if unit[3] == "act":
                    act.wait_ge(product_ready.sem, product_ready.at(u + 1))
                    unit[4](act, bank(u)).then_inc(act_freed.up(), 1)

        @block.vector
        def _(dve):
            for u, unit in enumerate(units):
                if unit[3] == "dve":
                    dve.wait_ge(product_ready.sem, product_ready.at(u + 1))
                    unit[4](dve, bank(u), dve_step).then_inc(dve_freed.up(), 1)


def act_copy(c, dst, bias=None, scale=1.0, func=None):
    def emit(act, bank):
        if bias is None and func is None and isinstance(scale, float):
            return c.nc.scalar.copy(dst, bank)
        return c.nc.scalar.activation(dst, bank, func or ACT.Identity, bias=0.0 if bias is None else bias, scale=scale)
    return emit


def dve_copy(c, dst, bias=None, row=None):
    def emit(dve, bank, step):
        if row is not None:
            return c.nc.vector.tensor_tensor(dst, bank, row, ALU.add)
        if bias is not None:
            return c.nc.vector.tensor_scalar(dst, bank, bias, None, ALU.add)
        return c.nc.vector.tensor_copy(dst, bank)
    return emit


def halves(c, products, rows, dst, bias=None, first="act"):
    other = "dve" if first == "act" else "act"
    out = []
    for half, who in ((0, first), (1, other)):
        d = dst[:, half * S:(half + 1) * S]
        emit = act_copy(c, d, bias=bias) if who == "act" else dve_copy(c, d, bias=bias)
        out.append((products(half), rows, S, who, emit))
    return out


def add_and_norm(c, add=None, bias=None, base=None, total=None, norm="ln", eps=1e-5, out=None, rows=None,
                 turned=(), load=None, store=None):
    nc = c.nc
    base = c.X if base is None else base
    total = base if total is None else total
    sum_ready, stats_ready, rstd_ready, norm_ready, turned_ready = (counter(c, n) for n in (
        "sum_ready", "stats_ready", "rstd_ready", "norm_ready", "turned_ready"))
    dve_step = counter(c, "dve_step")
    stats, mv, rstd = c.stats, c.mv, c.rstd
    H = NT // 2

    with nc.Block() as block:
        if load:
            block.sync(load)

        @block.tensor
        def _(pe):
            if add:
                for t in range(NT):
                    last = add(pe, t, c.bank[t // H][:, t % H * P:(t % H + 1) * P])
                    if t % H == H - 1:
                        last.then_inc(sum_ready.up(), 1)
            if turned:
                for half in range(2):
                    pe.wait_ge(norm_ready.sem, norm_ready.at(half + 1))
                    for k in range(H):
                        last = nc.tensor.transpose(c.bank[2 + half][:, k * P:(k + 1) * P], out[:, half * H + k, :], c.ident[:])
                    last.then_inc(turned_ready.up(), 1)

        @block.vector
        def _(dve):
            for half in range(2):
                ts = slice(half * H, (half + 1) * H)
                if add:
                    dve.wait_ge(sum_ready.sem, sum_ready.at(half + 1))
                    psum = c.bank[half][:, :].rearrange("p (t f) -> p t f", t=H)
                    seq(dve, dve_step, nc.vector.tensor_tensor(total[:, ts, :], psum, base[:, ts, :], ALU.add))
                    if bias is not None:
                        seq(dve, dve_step, nc.vector.tensor_tensor(
                            total[:, ts, :], total[:, ts, :], bias.unsqueeze(1).broadcast_to([P, H, P]), ALU.add))
                if norm is None:
                    continue
                for k in range(half * H, (half + 1) * H):
                    last = nc.vector.bn_stats(stats[:, k, :], total[:, k, :])
                seq(dve, dve_step, last)
                for k in range(half * H, (half + 1) * H):
                    last = nc.vector.bn_aggr(mv[:, k, :], stats[:, k, :])
                seq(dve, dve_step, last)
                if norm == "rms":
                    seq(dve, dve_step, nc.vector.tensor_tensor(mv[:, ts, 0], mv[:, ts, 0], mv[:, ts, 0], ALU.mult))
                    seq(dve, dve_step, nc.vector.tensor_tensor(mv[:, ts, 1], mv[:, ts, 1], mv[:, ts, 0], ALU.add))
                nc.vector.tensor_scalar(mv[:, ts, 1], mv[:, ts, 1], eps, None, ALU.add).then_inc(stats_ready.up(), 1)
            if norm is None:
                return
            for half in range(2):
                ts = slice(half * H, (half + 1) * H)
                dve.wait_ge(rstd_ready.sem, rstd_ready.at(half + 1))
                for k in range(half * H, (half + 1) * H):
                    if norm == "rms":
                        last = nc.vector.tensor_scalar(out[:, k, :], total[:, k, :], rstd[:, k:k + 1], None, ALU.mult)
                    else:
                        last = nc.vector.tensor_scalar(out[:, k, :], total[:, k, :], mv[:, k, 0:1], rstd[:, k:k + 1],
                                                       ALU.subtract, ALU.mult)
                if rows:
                    g, b = (r.unsqueeze(1).broadcast_to([P, H, P]) for r in rows)
                    seq(dve, dve_step, last)
                    seq(dve, dve_step, nc.vector.tensor_tensor(out[:, ts, :], out[:, ts, :], g, ALU.mult))
                    last = nc.vector.tensor_tensor(out[:, ts, :], out[:, ts, :], b, ALU.add)
                last.then_inc(norm_ready.up(), 1)

        @block.gpsimd
        def _(pool):
            if norm is None:
                return
            for half in range(2):
                pool.wait_ge(stats_ready.sem, stats_ready.at(half + 1))
                nc.gpsimd.tensor_tensor(rstd[:, half * H:(half + 1) * H], mv[:, half * H:(half + 1) * H, 1],
                                        c.minus_half[:, 0:H], ALU.pow).then_inc(rstd_ready.up(), 1)

        @block.scalar
        def _(act):
            for half in range(2 if turned else 0):
                act.wait_ge(turned_ready.sem, turned_ready.at(half + 1))
                for dst, scale, b in turned:
                    d = dst[:, half * S:(half + 1) * S]
                    if scale is None:
                        nc.scalar.copy(d, c.bank[2 + half][:, :])
                    else:
                        nc.scalar.activation(d, c.bank[2 + half][:, :], ACT.Identity, bias=0.0 if b is None else b, scale=scale)
            if store is not None:
                for half in range(2):
                    act.wait_ge(norm_ready.sem, norm_ready.at(half + 1))
                    act.dma_start(store[:, half * H:(half + 1) * H, :], out[:, half * H:(half + 1) * H, :]).then_inc(c.stored, 16)
                act.wait_ge(c.stored, 32)


def turn(c, src, ntiles, cols, dst):
    nc = c.nc
    turned_ready, act_freed, dve_freed = counter(c, "turned_ready"), counter(c, "act_freed"), counter(c, "dve_freed")
    units = [(k, t) for k in range(cols // P) for t in range(0, ntiles, 4)]

    with nc.Block() as block:
        @block.tensor
        def _(pe):
            for u, (k, t) in enumerate(units):
                if u >= 8:
                    s = dve_freed if u % 2 else act_freed
                    pe.wait_ge(s.sem, s.at((u - 8) // 2 + 1))
                for i in range(4):
                    last = nc.tensor.transpose(c.bank[u % 8][:, i * P:(i + 1) * P], src[:, t + i, k * P:(k + 1) * P], c.ident[:])
                last.then_inc(turned_ready.up(), 1)

        @block.scalar
        def _(act):
            for u, (k, t) in enumerate(units):
                if u % 2 == 0:
                    act.wait_ge(turned_ready.sem, turned_ready.at(u + 1))
                    nc.scalar.copy(dst[:, k, t * P:(t + 4) * P], c.bank[u % 8][:, :]).then_inc(act_freed.up(), 1)

        @block.vector
        def _(dve):
            for u, (k, t) in enumerate(units):
                if u % 2:
                    dve.wait_ge(turned_ready.sem, turned_ready.at(u + 1))
                    nc.vector.tensor_copy(dst[:, k, t * P:(t + 4) * P], c.bank[u % 8][:, :]).then_inc(dve_freed.up(), 1)


def attention(c, key_tiles, dk, operands, vop, scale, Y, mask=None, load=None, loaded=None, stacks=None):
    nc = c.nc
    G = 2 if dk == 64 else 4
    turned = dk == 8
    HB = 2 if dk == 64 else 4
    W = P // HB
    M = dk + 1 if turned else dk
    nkt, klen = len(key_tiles), sum(key_tiles)
    groups = [(b, h) for b in range(B) for h in range(0, HEADS, G)]
    rounds = [(g, jb, i) for g in range(len(groups)) for jb in range(G // HB) for i in range(nkt)]
    per_group = G // HB * nkt
    pairs = HB // 2
    nbanks = len(rounds) // nkt
    packed = ST * klen <= S
    units = [(j, tl) for tl in ([list(range(ST))] if packed else [[t] for t in range(ST)]) for j in range(G)]
    U = len(units)
    per_round = U // per_group
    NU = U * len(groups)
    NEP = 4
    SA = c.banks[:, 0:2, :]
    SC = [c.banks[:, 2:4, :], c.banks[:, 4:6, :]]
    OV, DEN = c.bank[6], c.bank[7]
    folded = stacks.folded if stacks else True
    NB = c.banks.rearrange("p i t -> p (i t)")[:, 0:S * 2].bitcast(BF16).rearrange("p (j t) -> p j t", t=S)
    (raw_ready, max_ready, negmax_ready, negmax_turned, negmax_moved, score_ready, exp_ready, value_ready,
     out_moved, out_turned, out_normed, masked_ready, cleared, dve_step) = (counter(c, n) for n in (
         "raw_ready", "max_ready", "negmax_ready", "negmax_turned", "negmax_moved", "score_ready", "exp_ready",
         "value_ready", "out_moved", "out_turned", "out_normed", "masked_ready", "cleared", "dve_step"))
    ones_ready = counter(c, "ones_ready")
    E, EM, OT, MX, RC = c.E, c.EM, c.OT, c.MX[:, 0:G], c.RC
    NM = c.NM.rearrange("p z t (j r) -> p z t j r", j=4)[:, :, :, 0:G]
    if stacks:
        operands = stacks.operands

    def start(i):
        return i * P if mask == "causal" else 0

    def last_key(t):
        return (t + 1) * P if mask == "causal" else klen

    def raw_scores(pe, n):
        g, (j, tl) = n // U, units[n % U]
        if n >= 2:
            pe.wait_ge(max_ready.sem, max_ready.at(n - 1))
        if n >= U and n % U == 0:
            pe.wait_ge(negmax_moved.sem, negmax_moved.at(n // U))
        if loaded and n % (NU // B) == 0:
            pe.wait_ge(loaded[n // (NU // B)].sem, loaded[n // (NU // B)].sent)
        if stacks and n == 0 and stacks.resident:
            pe.wait_ge(*stacks.keys_loaded())
        if stacks and n % U == 0:
            pe.wait_ge(*stacks.first_loaded(g))
        for k, t in enumerate(tl):
            b, h = groups[g][0], groups[g][1] + j
            dst = SA[:, n % 2, k * klen:k * klen + last_key(t)]
            products = stacks.leading(b, h) if stacks else operands(b, h)
            for m, (q, keys) in enumerate(products):
                last = nc.tensor.matmul(dst, q[:, t * P:(t + 1) * P], keys[:, 0:last_key(t)],
                                        start=(m == 0), stop=(mask != "causal" and m == len(products) - 1))
            if mask == "causal":
                last = nc.tensor.matmul(dst, c.ident_bf[:], c.after_query[:, S - last_key(t):S], start=False, stop=True)
        last.then_inc(raw_ready.up(), 1)

    def turn_negmax(pe, g):
        pe.wait_ge(negmax_ready.sem, negmax_ready.at(g + 1))
        for t in range(ST):
            to = slice(t * P, (t + 1) * P)
            if folded:
                for j in range(G):
                    last = nc.tensor.transpose(NB[96:98, j, to], c.NM[:, g % 2, t, 32 * j:32 * j + 2], c.ident_bf[:])
            else:
                last = nc.tensor.transpose(NB[:, 0, to], c.NM[:, g % 2, t, :], c.ident_bf[:])
        last.then_inc(negmax_turned.up(), 1)

    def scores(pe, r, between):
        g, jb, i = rounds[r]
        b, ks, n0 = groups[g][0], key_tiles[i], start(i)
        heads = [(jb * HB + x, groups[g][1] + jb * HB + x) for x in range(HB)]
        if r % per_group == 0:
            pe.wait_ge(negmax_moved.sem, negmax_moved.at(g + 1))
            if stacks:
                pe.wait_ge(*stacks.second_loaded(g))
        dst = []
        for x in range(HB):
            pair = r * pairs + x // 2
            if x % 2 == 0 and pair >= 2:
                pe.wait_ge(exp_ready.sem, exp_ready.at(pair - 1))
            dst.append(SC[pair % 2][0:ks, x % 2, n0:S])
        for x, (j, h) in enumerate(heads):
            products = operands(b, h, folded) if folded else operands(b, h)
            for m, (q, keys) in enumerate(products):
                stop = folded and m == len(products) - 1
                last = nc.tensor.matmul(dst[x], keys[:, i * P:i * P + ks], q[:, n0:S], start=(m == 0), stop=stop)
            if folded and x % 2:
                last.then_inc(score_ready.up(), 1)
                for n in between if x == 1 else ():
                    raw_scores(pe, n)
        if folded:
            return
        for x, (j, h) in enumerate(heads):
            last = nc.tensor.matmul(dst[x], c.pick[:, j, 0:ks], c.NMT[:, g % 2, n0:S], start=False, stop=(mask != "causal"))
            if mask != "causal" and x % 2:
                last.then_inc(score_ready.up(), 1)
        if mask == "causal":
            for x in range(HB):
                last = nc.tensor.matmul(dst[x], c.ident_bf[:], c.before_key[:, 0:S - n0], start=False, stop=True)
                if x % 2:
                    last.then_inc(score_ready.up(), 1)

    def values(pe, r):
        g, jb, i = rounds[r]
        b, ks, n0, n = groups[g][0], key_tiles[i], start(i), r // nkt
        pe.wait_ge(exp_ready.sem, exp_ready.at((r + 1) * pairs))
        if i == 0 and n:
            pe.wait_ge(out_moved.sem, out_moved.at(n))
        if r == 0 and turned:
            pe.wait_ge(cleared.sem, cleared.at(1))
        heads = [(W * x, groups[g][1] + jb * HB + x, E[(r * pairs + x // 2) % NEP][:, x % 2, :],
                  EM[(r * pairs + x // 2) % NEP][:, x % 2, :]) for x in range(HB)]
        first, end = i == 0, i == nkt - 1
        if mask == "future":
            if first:
                nc.tensor.matmul(OV[:, :], c.zeros_bf[:], c.after_query[:, :], start=True, stop=False, skip_group_check=True)
            else:
                for row, h, e, _ in heads:
                    nc.tensor.matmul(OV[row:row + M, 0:i * P], vop(b, h, i), e[0:ks, 0:i * P], start=False, stop=False,
                                     skip_group_check=True)
        else:
            for row, h, e, _ in heads:
                last = nc.tensor.matmul(OV[row:row + M, n0:S], vop(b, h, i), e[0:ks, n0:S], start=first, stop=end)
        if not turned:
            for row, h, e, _ in heads:
                last = nc.tensor.matmul(DEN[row:row + W, n0:S], c.ones[0:ks, 0:W], e[0:ks, n0:S], start=first, stop=end)
        if mask == "future":
            pe.wait_ge(masked_ready.sem, masked_ready.at((r + 1) * pairs))
            for row, h, e, em in heads:
                last = nc.tensor.matmul(OV[row:row + M, i * P:(i + 1) * P], vop(b, h, i), em, start=False, stop=False,
                                        skip_group_check=True)
            if end:
                last = nc.tensor.matmul(OV[:, :], c.zeros_bf[:], c.after_query[:, :], start=False, stop=True, skip_group_check=True)
        last.then_inc(value_ready.up(), 1)

    def turn_out(pe, n):
        pe.wait_ge(out_moved.sem, out_moved.at(n + 1))
        if n >= 1:
            pe.wait_ge(out_normed.sem, out_normed.at(n))
        for t in range(ST):
            last = nc.tensor.transpose(DEN[:, t * P:(t + 1) * P], OT[:, n % 2, t * P:(t + 1) * P], c.ident[:])
        last.then_inc(out_turned.up(), 1)

    def reduce_max(dve, n):
        j, tl = units[n % U]
        dve.wait_ge(raw_ready.sem, raw_ready.at(n + 1))
        if packed:
            src, dst = SA[:, n % 2, 0:ST * klen].rearrange("p (t m) -> p t m", t=ST), MX[:, j, :]
        else:
            src, dst = SA[:, n % 2, 0:last_key(tl[0])], MX[:, j, tl[0]:tl[0] + 1]
        nc.vector.tensor_reduce(dst, src, AX_X, ALU.max).then_inc(max_ready.up(), 1)

    def negmax(dve, g):
        dve.wait_ge(max_ready.sem, max_ready.at((g + 1) * U))
        if g >= 2:
            dve.wait_ge(negmax_turned.sem, negmax_turned.at(g - 1))
        m = MX.rearrange("p j t -> p t j")
        hi, lo = NM[:, g % 2, :, :, 0], NM[:, g % 2, :, :, 1]
        seq(dve, dve_step, nc.vector.tensor_scalar(hi, m, -1.0, None, ALU.mult))
        last = nc.vector.scalar_tensor_tensor(out=lo, in0=m, scalar=-1.0, in1=hi, op0=ALU.mult, op1=ALU.subtract)
        last.then_inc(negmax_ready.up(), 1)

    def norm_turned(dve, n):
        dve.wait_ge(out_turned.sem, out_turned.at(n + 1))
        b, h = groups[n][0], groups[n][1]
        tr = DEN[:, :].rearrange("p (t j w) -> p t j w", t=ST, j=HB)
        seq(dve, dve_step, nc.vector.reciprocal(RC[:, n % 2], tr[:, :, :, dk]))
        dst = Y[:, b * ST:(b + 1) * ST, h * dk:(h + HB) * dk].rearrange("p t (j d) -> p t j d", j=HB)
        nc.vector.tensor_tensor(dst, tr[:, :, :, 0:dk], RC[:, n % 2].unsqueeze(3).broadcast_to([P, ST, HB, dk]),
                                ALU.mult).then_inc(out_normed.up(), 1)

    def place(n):
        g, jb, _ = rounds[n * nkt]
        return Y[:, (groups[g][1] + jb * HB) // HB, groups[g][0] * S:(groups[g][0] + 1) * S]

    def norm_in_place(dve, r):
        n = (r - 2 - nkt + 1) // nkt
        if r < nkt + 1 or n >= nbanks:
            return
        dve.wait_ge(out_moved.sem, out_moved.at(n + 1))
        part = S // nkt
        at = (r - nkt - 1) % nkt * part
        last = nc.vector.reciprocal(OT[:, n % 2, at:at + part], OT[:, n % 2, at:at + part])
        if at + part == S:
            seq(dve, dve_step, last)
            nc.vector.tensor_tensor(place(n), place(n), OT[:, n % 2, :], ALU.mult).then_inc(out_normed.up(), 1)

    def move_out(act, n):
        act.wait_ge(value_ready.sem, value_ready.at((n + 1) * nkt))
        if turned:
            if n >= 2:
                act.wait_ge(out_turned.sem, out_turned.at(n - 1))
            nc.scalar.copy(OT[:, n % 2, :], OV[:, :]).then_inc(out_moved.up(), 1)
        else:
            if n >= 2:
                act.wait_ge(out_normed.sem, out_normed.at(n - 1))
            nc.scalar.copy(place(n), OV[:, :])
            nc.scalar.copy(OT[:, n % 2, :], DEN[:, :]).then_inc(out_moved.up(), 1)

    def ended(r):
        return r // nkt if 0 <= r < len(rounds) and r % nkt == nkt - 1 else None

    def move_negmax(dve, g):
        dve.wait_ge(negmax_turned.sem, negmax_turned.at(g + 1))
        if folded:
            nc.vector.tensor_copy(negmax_rows(g), NB[96:98]).then_inc(negmax_moved.up(), 1)
        else:
            nc.vector.tensor_copy(c.NMT[:, g % 2, :], NB[:, 0, :]).then_inc(negmax_moved.up(), 1)

    def negmax_rows(g):
        return stacks.negmax_rows(g) if stacks else c.QH[96:98].rearrange("p h x t -> p (h x) t")[
            :, groups[g][1]:groups[g][1] + G, groups[g][0] * S:(groups[g][0] + 1) * S]

    def ahead(r):
        first = (r + per_group + 1) * per_round
        return list(range(first, min(first + per_round, NU)))

    def next_group(r):
        return r // per_group + 1 if r % per_group == per_group - 1 and r + 1 < R else None

    R = len(rounds)

    def mask_weights(pool):
        if mask != "future":
            return
        later = c.key_later[:].unsqueeze(1).broadcast_to([P, 2, P])
        for pair in range(R * pairs):
            i = rounds[pair // pairs][2]
            pool.wait_ge(exp_ready.sem, exp_ready.at(pair + 1))
            if pair >= NEP:
                pool.wait_ge(value_ready.sem, value_ready.at((pair - NEP) // pairs + 1))
            nc.gpsimd.tensor_tensor(EM[pair % NEP], E[pair % NEP][:, :, i * P:(i + 1) * P], later,
                                    ALU.mult).then_inc(masked_ready.up(), 1)

    with nc.Block() as block:
        if load:
            block.sync(load)
        if stacks:
            @block.sync
            def _(sp):
                sp.wait_ge(c.stored_parts, c.nparts)
                if stacks.resident:
                    stacks.load_keys(sp)
                for g in range(2):
                    stacks.load_first(sp, g, groups[g])
                    stacks.load_second(sp, g, groups[g])
                stacks.load_first(sp, 2, groups[2])
                for g in range(2, len(groups)):
                    sp.wait_ge(score_ready.sem, score_ready.at((g - 1) * per_group * pairs))
                    stacks.load_second(sp, g, groups[g])
                    if g + 1 < len(groups):
                        stacks.load_first(sp, g + 1, groups[g + 1])

        if stacks and folded:
            @block.gpsimd
            def _(pool):
                pool.wait_ge(c.stored_parts, c.nparts)
                for slot in stacks.k_last:
                    last = nc.gpsimd.memset(slot[96:98, 0], 1.0)
                last.then_inc(ones_ready.up(), 1)
                mask_weights(pool)

        @block.tensor
        def _(pe):
            if stacks and folded:
                pe.wait_ge(ones_ready.sem, ones_ready.at(1))
            for n in range(U):
                raw_scores(pe, n)
            turn_negmax(pe, 0)
            for n in range(U, min(U + per_round, NU)):
                raw_scores(pe, n)
            for r in range(R + 3):
                soon = ahead(r)
                split = per_round // 4 if folded and pairs == 2 and next_group(r) is None else 0
                if r < R:
                    scores(pe, r, soon[:split])
                if next_group(r) is not None:
                    turn_negmax(pe, next_group(r))
                    if 0 <= r - 1 < R:
                        values(pe, r - 1)
                for n in soon[split:per_round // 2]:
                    raw_scores(pe, n)
                if turned and ended(r - 3) is not None:
                    turn_out(pe, ended(r - 3))
                if next_group(r) is None and 0 <= r - 1 < R:
                    values(pe, r - 1)
                for n in soon[per_round // 2:]:
                    raw_scores(pe, n)

        @block.scalar
        def _(act):
            for r in range(R + 3):
                if ended(r - 2) is not None:
                    move_out(act, ended(r - 2))
                if r >= R:
                    continue
                ks, n0 = key_tiles[rounds[r][2]], start(rounds[r][2])
                for m in range(pairs):
                    pair = r * pairs + m
                    act.wait_ge(score_ready.sem, score_ready.at(pair + 1))
                    if pair >= NEP:
                        act.wait_ge(value_ready.sem, value_ready.at((pair - NEP) // pairs + 1))
                    nc.scalar.activation(E[pair % NEP][0:ks, :, n0:S], SC[pair % 2][0:ks, :, n0:S], ACT.Exp,
                                         scale=scale).then_inc(exp_ready.up(), 1)

        @block.vector
        def _(dve):
            if turned:
                nc.vector.memset(OV[:, :], 0.0).then_inc(cleared.up(), 1)
            for n in range(U):
                reduce_max(dve, n)
            negmax(dve, 0)
            move_negmax(dve, 0)
            for n in range(U, min(U + per_round, NU)):
                reduce_max(dve, n)
            for r in range(R + 3 + nkt):
                if next_group(r) is not None:
                    negmax(dve, next_group(r))
                    move_negmax(dve, next_group(r))
                if not turned and (nkt == 1 or dk == 64):
                    norm_in_place(dve, r)
                for n in ahead(r):
                    reduce_max(dve, n)
                if not turned and nkt > 1 and dk != 64:
                    norm_in_place(dve, r)
                if turned and ended(r - 3) is not None:
                    norm_turned(dve, ended(r - 3))


Q_PARTS, K_PARTS = (0, 0, 1, 1, 0, 2), (0, 1, 0, 1, 2, 0)


class HeadStacks:

    def __init__(self, c, dk, keys, resident=0, kv=lambda h: h):
        self.c, self.dk, self.keys, self.resident, self.kv = c, dk, keys, resident, kv
        self.folded = not resident
        self.G = P // dk
        self.per = 3 if dk == 32 else 2
        self.stacks = [tuple(range(a, a + self.per)) for a in range(0, 6, self.per)]
        n = self.leads = len(self.stacks) - 1
        self.first = [counter(c, f"first_stacks_{z}") for z in range(3)]
        self.second = [counter(c, f"last_stack_{z}") for z in range(2)]
        self.all_keys = counter(c, "all_keys")
        view = lambda a, k, heads: a.bitcast(BF16).rearrange("p (k j t) -> p k j t", k=k, j=heads)
        if resident:
            size = resident * B * keys // 2
            self.k_stacks = [view(c.big2(0, n * size), n, resident), view(c.VH[:, 2176:2176 + size], 1, resident)]
            self.q_first = [view(c.big3((4 + z) * TOK, TOK), n, self.G) for z in range(3)]
            self.q_last = [view(c.big3(7 * TOK + z * S, S), 1, self.G) for z in range(2)]
        else:
            both = [view(c.big1(2 * z * TOK, 2 * TOK), 2, self.G) for z in range(4)] + [view(c.big3(4 * TOK, 2 * TOK), 2, self.G)]
            self.q_first, self.k_first = ([v[:, o:o + 1] for v in both[0:3]] for o in range(2))
            self.q_last, self.k_last = ([v[:, o:o + 1] for v in both[3:5]] for o in range(2))

    def load(self, sp, slot, dram, parts, size, stacks, loaded, b, h):
        for k, products in enumerate(stacks):
            for s, product in enumerate(products):
                src = dram[:, parts[product], h // self.G, b * size:(b + 1) * size].rearrange("(j d) t -> d j t", d=self.dk)
                sp.dma_start(slot[s * self.dk:(s + 1) * self.dk, k, :, 0:size], src).then_inc(loaded.up(16), 16)

    def load_first(self, sp, g, group):
        z, stacks = g % 3, self.stacks[:-1]
        self.load(sp, self.q_first[z], self.c.q_wide, Q_PARTS, S, stacks, self.first[z], *group)
        if not self.resident:
            self.load(sp, self.k_first[z], self.c.k_wide, K_PARTS, self.keys, stacks, self.first[z], *group)

    def load_second(self, sp, g, group):
        z, stacks = g % 2, self.stacks[-1:]
        self.load(sp, self.q_last[z], self.c.q_wide, Q_PARTS, S, stacks, self.second[z], *group)
        if not self.resident:
            self.load(sp, self.k_last[z], self.c.k_wide, K_PARTS, self.keys, stacks, self.second[z], *group)

    def load_keys(self, sp):
        n = B * self.keys
        for k, products in enumerate(self.stacks):
            dst = self.k_stacks[0][:, k] if k < self.leads else self.k_stacks[1][:, 0]
            for s, product in enumerate(products):
                for x in range(self.G):
                    src = self.c.k_wide[:, K_PARTS[product], 0:self.resident // self.G, 0:n].rearrange("(x d) k t -> x d k t", x=self.G)[x]
                    sp.dma_start(dst[s * self.dk:(s + 1) * self.dk].rearrange("p (k x) t -> p x k t", x=self.G)[:, x], src).then_inc(
                        self.all_keys.up(16), 16)

    def keys_loaded(self):
        return self.all_keys.sem, self.all_keys.at(16 * 6 * self.G)

    def first_loaded(self, g):
        s = self.first[g % 3]
        return s.sem, s.at(16 * self.per * self.leads * (1 if self.resident else 2) * (g // 3 + 1))

    def second_loaded(self, g):
        s = self.second[g % 2]
        return s.sem, s.at(16 * self.per * (1 if self.resident else 2) * (g // 2 + 1))

    def negmax_rows(self, g):
        return self.q_last[g % 2][96:98, 0]

    def operands(self, b, h, folded=False):
        g, j = (b * HEADS + h) // self.G, h % self.G
        out = []
        for k in range(self.leads + 1):
            lead = k < self.leads
            R = self.per * self.dk + (2 if folded and not lead else 0)
            q = self.q_first[g % 3][0:R, k, j] if lead else self.q_last[g % 2][0:R, 0, j]
            if self.resident:
                keys = (self.k_stacks[0][:, k] if lead else self.k_stacks[1][:, 0])[0:R, self.kv(h), b * self.keys:(b + 1) * self.keys]
            else:
                keys = (self.k_first[g % 3][0:R, k, j] if lead else self.k_last[g % 2][0:R, 0, j])[:, 0:self.keys]
            out.append((q, keys))
        return out

    def leading(self, b, h):
        return self.operands(b, h)[:-1]


def project_split(c, units, spans):
    nc = c.nc
    product_ready, high_ready, rest_ready, mid_ready, low_ready = (
        counter(c, n) for n in ("product_ready", "high_ready", "rest_ready", "mid_ready", "low_ready"))
    rest = [spans[0][:, z * S:(z + 1) * S] for z in range(3)]
    spans, at, parts = [spans[0][:, 3 * S:]] + spans[1:], 0, []
    for _, _, n, _ in units:
        if at + 3 * n // 2 > spans[0].shape[1]:
            spans, at = spans[1:], 0
        parts.append(spans[0][:, at:at + 3 * n // 2].bitcast(BF16).rearrange("p (z t) -> p z t", z=3))
        at += 3 * n // 2
    with nc.Block() as block:
        @block.tensor
        def _(pe):
            for u, (lhsT, rhs, n, _) in enumerate(units):
                if u >= 8:
                    pe.wait_ge(rest_ready.sem, rest_ready.at(u - 7))
                nc.tensor.matmul(c.bank[u % 8][:, 0:n], lhsT, rhs, start=True, stop=True).then_inc(product_ready.up(), 1)

        @block.scalar
        def _(act):
            for u in range(len(units) + 1):
                if u < len(units):
                    n = units[u][2]
                    act.wait_ge(product_ready.sem, product_ready.at(u + 1))
                    nc.scalar.copy(parts[u][:, 0, 0:n], c.bank[u % 8][:, 0:n]).then_inc(high_ready.up(), 1)
                if u >= 1:
                    n = units[u - 1][2]
                    act.wait_ge(rest_ready.sem, rest_ready.at(u))
                    nc.scalar.copy(parts[u - 1][:, 1, 0:n], rest[(u - 1) % 3][:, 0:n]).then_inc(mid_ready.up(), 1)

        @block.vector
        def _(dve):
            for u, (_, _, n, _) in enumerate(units):
                dve.wait_ge(high_ready.sem, high_ready.at(u + 1))
                if u >= 3:
                    dve.wait_ge(low_ready.sem, low_ready.at(u - 2))
                nc.vector.tensor_tensor(rest[u % 3][:, 0:n], c.bank[u % 8][:, 0:n], parts[u][:, 0, 0:n],
                                        ALU.subtract).then_inc(rest_ready.up(), 1)

        @block.gpsimd
        def _(pool):
            for u, (_, _, n, _) in enumerate(units):
                pool.wait_ge(mid_ready.sem, mid_ready.at(u + 1))
                nc.gpsimd.tensor_tensor(parts[u][:, 2, 0:n], rest[u % 3][:, 0:n], parts[u][:, 1, 0:n],
                                        ALU.subtract).then_inc(low_ready.up(), 1)

        @block.sync
        def _(sp):
            for u, (_, _, n, dst) in enumerate(units):
                sp.wait_ge(low_ready.sem, low_ready.at(u + 1))
                sp.dma_start(dst, parts[u][:, :, 0:n]).then_inc(c.stored_parts, 16)
                c.nparts += 16


def split_heads(c, qT, kT, n):
    nc = c.nc
    parts_ready, zeros_ready, dve_step = (counter(c, name) for name in ("parts_ready", "zeros_ready", "dve_step"))
    c.parts_stored = [counter(c, f"parts_stored_{b}") for b in range(B)]
    c.heads_loaded = [counter(c, f"heads_loaded_{b}") for b in range(B)]
    zeroed = c.big1(0, 8 * TOK)[0:96].rearrange("p (h t) -> p h t", h=HEADS)

    def split(dve, src, parts, rest):
        seq(dve, dve_step, nc.vector.tensor_copy(parts[:, 0, :], src))
        seq(dve, dve_step, nc.vector.tensor_tensor(rest, src, parts[:, 0, :], ALU.subtract))
        seq(dve, dve_step, nc.vector.tensor_copy(parts[:, 1, :], rest))
        nc.vector.tensor_tensor(parts[:, 2, :], rest, parts[:, 1, :], ALU.subtract).then_inc(parts_ready.up(), 1)

    def store(sp, b):
        sp.wait_ge(parts_ready.sem, parts_ready.at((b + 1) * (1 if kT is None else 2)))
        q = c.q_parts[:, :, b * S:(b + 1) * S]
        for a, copies in ((0, 3), (1, 2), (2, 1)):
            at = (0, 3, 5)[a]
            src = q[:, a:a + 1, :].broadcast_to([P, copies, S])
            sp.dma_start(c.q_dram[:, at:at + copies, b * S:(b + 1) * S], src).then_inc(c.parts_stored[b].up(16), 16)
            if kT is not None:
                sp.dma_start(c.k_dram[:, at:at + copies, b * n:(b + 1) * n], c.k_parts[:, 0:copies, b * n:(b + 1) * n]).then_inc(
                    c.parts_stored[b].up(16), 16)

    def load_heads(sp, b):
        sp.wait_ge(c.parts_stored[b].sem, c.parts_stored[b].sent)
        stacks = lambda dram, a, m: dram[:, :, a:a + m].rearrange("(h x d) s t -> x (d s) h t", x=2, d=8)
        for x in range(2):
            rows = slice(48 * x, 48 * x + 48)
            sp.dma_start(c.QH[rows, :, x, b * S:(b + 1) * S], stacks(c.q_dram, b * S, S)[x]).then_inc(c.heads_loaded[b].up(16), 16)
            if kT is not None:
                to = c.KH.rearrange("p (h t) -> p h t", t=TOK)[rows, :, b * n:(b + 1) * n]
                sp.dma_start(to, stacks(c.k_dram, b * n, n)[x]).then_inc(c.heads_loaded[b].up(16), 16)

    with nc.Block() as block:
        @block.vector
        def _(dve):
            for b in range(B):
                split(dve, qT[:, b * S:(b + 1) * S], c.q_parts[:, :, b * S:(b + 1) * S], c.rest_q[:, b * S:(b + 1) * S])
                if kT is not None:
                    split(dve, kT[:, b * n:(b + 1) * n], c.k_parts[:, :, b * n:(b + 1) * n], c.rest_k[:, b * n:(b + 1) * n])

        @block.gpsimd
        def _(pool):
            for b in range(B):
                nc.gpsimd.memset(zeroed[:, :, b * S // 2:(b + 1) * S // 2], 0.0).then_inc(zeros_ready.up(), 1)

        @block.scalar
        def _(act):
            keys = c.KH[96:98] if kT is None or n == S else c.KH[96:98].rearrange("p (h t) -> p h t", t=TOK)[:, :, 0:B * n]
            ones = c.ones[96:98, 0:1] if len(keys.shape) == 2 else c.ones[96:98, 0:1].unsqueeze(2)
            nc.scalar.copy(keys, ones.broadcast_to(list(keys.shape)))

        @block.sync
        def _(sp):
            store(sp, 0)
            sp.wait_ge(zeros_ready.sem, zeros_ready.at(1))
            load_heads(sp, 0)
            store(sp, 1)
            sp.wait_ge(zeros_ready.sem, zeros_ready.at(2))

    return lambda sp: load_heads(sp, 1)


def stack_keys(c, src):
    nc, step = c.nc, counter(c, "dve_step")
    stacked_ready, turned_ready, act_freed, dve_freed = (counter(c, n) for n in ("stacked_ready", "turned_ready", "act_freed", "dve_freed"))
    stack = c.key_stack.rearrange("p (u i x) d z -> p u x i d z", i=ST, x=2)
    tile_of = lambda u, i: c.key_stack[:, (u * ST + i) * 2:(u * ST + i) * 2 + 2].rearrange("p x d z -> p (x d z)")
    flat = src.rearrange("p (u x) i d -> p u x i d", x=2)
    rest = c.total[:].rearrange("p t (v i d) -> p (t v) i d", i=ST, d=8).rearrange("p (u x) i d -> p u x i d", x=2)
    slot = lambda z: stack[:, :, :, :, :, z]
    place = lambda u: c.KH[0:96, u * S:(u + 1) * S]
    turned = lambda u: c.banks_bf[u % 8][0:96, :]

    with nc.Block() as block:
        @block.vector
        def _(dve):
            for x in range(2):
                one = lambda ap: ap[:, :, x]
                seq(dve, step, nc.vector.tensor_copy(one(slot(0)), one(flat)))
                nc.vector.tensor_copy(one(slot(3)), one(slot(0)))
                nc.vector.tensor_copy(one(slot(5)), one(slot(0)))
                seq(dve, step, nc.vector.tensor_tensor(one(rest), one(flat), one(slot(0)), ALU.subtract))
                seq(dve, step, nc.vector.tensor_copy(one(slot(1)), one(rest)))
                nc.vector.tensor_copy(one(slot(4)), one(slot(1)))
                seq(dve, step, nc.vector.tensor_tensor(one(rest), one(rest), one(slot(1)), ALU.subtract))
                last = nc.vector.tensor_copy(one(slot(2)), one(rest))
            last.then_inc(stacked_ready.up(), 1)
            for u in range(1, B * HEADS // 2, 2):
                dve.wait_ge(turned_ready.sem, turned_ready.at(u + 1))
                nc.vector.tensor_copy(place(u), turned(u)).then_inc(dve_freed.up(), 1)

        @block.tensor
        def _(pe):
            pe.wait_ge(stacked_ready.sem, stacked_ready.at(1))
            for u in range(B * HEADS // 2):
                if u >= 8:
                    s = dve_freed if u % 2 else act_freed
                    pe.wait_ge(s.sem, s.at((u - 8) // 2 + 1))
                for i in range(ST):
                    last = nc.tensor.transpose(turned(u)[:, i * P:(i + 1) * P], tile_of(u, i), c.ident_bf[:])
                last.then_inc(turned_ready.up(), 1)

        @block.scalar
        def _(act):
            for u in range(0, B * HEADS // 2, 2):
                act.wait_ge(turned_ready.sem, turned_ready.at(u + 1))
                nc.scalar.copy(place(u), turned(u)).then_inc(act_freed.up(), 1)


def quantise(c, src, dst_bf, amax):
    nc, step = c.nc, counter(c, "dve_step")
    t1, r7 = c.total, c.rstd

    with nc.Block() as block:
        @block.vector
        def _(dve):
            seq(dve, step, nc.vector.tensor_reduce(amax, src, AX_X, ALU.max, apply_absolute_value=True))
            seq(dve, step, nc.vector.tensor_scalar(amax, amax, 1e-6, None, ALU.max))
            seq(dve, step, nc.vector.reciprocal(r7[:], amax))
            for t in range(NT):
                last = nc.vector.tensor_scalar(t1[:, t, :], src[:, t, :], r7[:, t:t + 1], 7.0, ALU.mult, ALU.mult)
            seq(dve, step, last)
            seq(dve, step, nc.vector.tensor_scalar(t1[:], t1[:], ROUND, ROUND - 8.0, ALU.add, ALU.max))
            seq(dve, step, nc.vector.tensor_scalar(dst_bf, t1[:], ROUND, 7.0, ALU.subtract, ALU.min))
            seq(dve, step, nc.vector.tensor_scalar(amax, amax, 1.0 / 7.0, None, ALU.mult))


def ternary(c, w, signT, alpha):
    nc, step = c.nc, counter(c, "dve_step")
    rows_ready, total_ready, sign_ready, sign_turned = (counter(c, n) for n in ("tern_rows", "tern_total", "tern_sign", "tern_turned"))
    row, thr, m1, m2 = c.small[:, 0:1], c.small[:, 1:3], c.tern[:, 0, :], c.tern[:, 1, :]
    diag = c.total[:, 0, :]

    with nc.Block() as block:
        @block.vector
        def _(dve):
            seq(dve, step, nc.vector.tensor_reduce(row, w, AX_X, ALU.add, apply_absolute_value=True))
            seq(dve, step, nc.vector.tensor_scalar(row, row, 1.0 / P, None, ALU.mult))
            nc.vector.tensor_scalar(diag, c.ident[:], row, None, ALU.mult).then_inc(rows_ready.up(), 1)
            dve.wait_ge(total_ready.sem, total_ready.at(1))
            nc.vector.tensor_copy(alpha, c.bank[1][:, 0:P])
            nc.vector.tensor_scalar(thr[:, 0:1], c.bank[0][:, 0:1], 0.05 / P, None, ALU.mult)
            seq(dve, step, nc.vector.tensor_scalar(thr[:, 1:2], c.bank[0][:, 0:1], -0.05 / P, None, ALU.mult))
            nc.vector.tensor_scalar(m1, w, thr[:, 0:1], None, ALU.is_ge)
            seq(dve, step, nc.vector.tensor_scalar(m2, w, thr[:, 1:2], None, ALU.is_le))
            nc.vector.tensor_tensor(m1, m1, m2, ALU.subtract).then_inc(sign_ready.up(), 1)
            dve.wait_ge(sign_turned.sem, sign_turned.at(1))
            nc.vector.tensor_copy(signT, c.bank_bf[:, 0:P])

        @block.tensor
        def _(pe):
            pe.wait_ge(rows_ready.sem, rows_ready.at(1))
            nc.tensor.matmul(c.bank[0][:, 0:1], c.ones[:], row, start=True, stop=True)
            nc.tensor.matmul(c.bank[1][:, 0:P], c.ones[:], diag, start=True, stop=True).then_inc(total_ready.up(), 1)
            pe.wait_ge(sign_ready.sem, sign_ready.at(1))
            nc.tensor.transpose(c.bank_bf[:, 0:P], m1, c.ident_bf[:]).then_inc(sign_turned.up(), 1)


def turn_quantised(c, q_bf, qT_bf):
    nc = c.nc
    turned_ready, act_freed = counter(c, "turned_ready"), counter(c, "act_freed")
    with nc.Block() as block:
        @block.tensor
        def _(pe):
            for half in range(2):
                if half:
                    pe.wait_ge(act_freed.sem, act_freed.at(1))
                for k in range(4):
                    last = nc.tensor.transpose(c.bank_bf[:, k * P:(k + 1) * P], q_bf[:, half * 4 + k, :], c.ident_bf[:])
                last.then_inc(turned_ready.up(), 1)

        @block.scalar
        def _(act):
            for half in range(2):
                act.wait_ge(turned_ready.sem, turned_ready.at(half + 1))
                nc.scalar.copy(qT_bf[:, half * S:(half + 1) * S], c.bank_bf[:, 0:S]).then_inc(act_freed.up(), 1)


def quantised_product(c, qT_bf, signT, amax, alpha, bias, dst):
    nc, step = c.nc, counter(c, "dve_step")
    product_ready = counter(c, "product_ready")
    with nc.Block() as block:
        @block.tensor
        def _(pe):
            for t in range(NT):
                nc.tensor.matmul(c.bank[t][:, 0:P], qT_bf[:, t * P:(t + 1) * P], signT,
                                 start=True, stop=True).then_inc(product_ready.up(), 1)

        @block.vector
        def _(dve):
            for t in range(NT):
                dve.wait_ge(product_ready.sem, product_ready.at(t + 1))
                last = nc.vector.scalar_tensor_tensor(out=dst[:, t, :], in0=c.bank[t][:, 0:P],
                                                      scalar=amax[:, t:t + 1], in1=alpha, op0=ALU.mult, op1=ALU.mult)
            if bias is not None:
                seq(dve, step, last)
                nc.vector.tensor_tensor(dst, dst, bias.unsqueeze(1).broadcast_to([P, NT, P]), ALU.add)


def attention_8(c, key_tiles, dst, scale, load, chunked=False):
    single = len(key_tiles) == 1

    def operands(b, h, folded=False):
        R = 98 if folded else 96
        if chunked:
            keys = c.KH[0:R, (b * HEADS + h) // 2 * S:(b * HEADS + h) // 2 * S + S]
        else:
            n = SK if single else S
            keys = c.KH[0:R, h // 2 * TOK + b * n:h // 2 * TOK + (b + 1) * n]
        return [(c.QH[0:R, h // 2, h % 2, b * S:(b + 1) * S], keys)]

    def vop(b, h, i):
        if chunked:
            return c.VH[:, (b * HEADS + h) * 36 + i * 9:(b * HEADS + h) * 36 + i * 9 + 9]
        if single:
            return c.VH[0:SK, (b * HEADS + h) * 9:(b * HEADS + h) * 9 + 9]
        x = ((b * ST + i) * HEADS + h) * 9
        return c.VH[:, x:x + 9]

    attention(c, key_tiles, 8, operands, vop, scale, dst, load=load, loaded=c.heads_loaded)


def block_product(c, aT, bT, dst):
    nc = c.nc
    product_ready = counter(c, "product_ready")
    with nc.Block() as block:
        @block.tensor
        def _(pe):
            nc.tensor.matmul(c.bank[0][:, 0:P], aT, bT, start=True, stop=True).then_inc(product_ready.up(), 1)

        @block.vector
        def _(dve):
            dve.wait_ge(product_ready.sem, product_ready.at(1))
            nc.vector.tensor_tensor(dst, c.bank[0][:, 0:P], c.m("same_head"), ALU.mult)


def project_out(c, srcT, w, k=1):
    def add(pe, t, psum):
        for i in range(k):
            last = c.nc.tensor.matmul(psum, srcT[:, i, t * P:(t + 1) * P], w[:, i * P:(i + 1) * P],
                                      start=(i == 0), stop=(i == k - 1))
        return last
    return add


def turn_back(c, srcT):
    def add(pe, t, psum):
        return c.nc.tensor.transpose(psum, srcT[:, t * P:(t + 1) * P], c.ident[:])
    return add



def layer0_attention(c):
    nc = c.nc
    amax = c.amax
    proj = c.Y8
    ternary(c, c.m("L0_Wqkv"), c.signT[:, 0, :], c.alpha[:, 0, :])
    ternary(c, c.m("L0_Wo"), c.signT[:, 1, :], c.alpha[:, 1, :])
    block_product(c, c.m("L0_UT")[0:32], c.m("L0_UT")[0:32], c.headmat)
    quantise(c, c.X[:], c.q_bf[:], amax)
    turn_quantised(c, c.q_bf, c.qT_bf)
    quantised_product(c, c.qT_bf[:], c.signT[:, 0, :], amax, c.alpha[:, 0, :], c.row("L0_attn_Wqkv_b"), proj[:])

    step = counter(c, "dve_step")
    pool_step = counter(c, "pool_step")
    with nc.Block() as block:
        @block.vector
        def _(dve):
            p5 = proj.rearrange("p t (h i two) -> p t h i two", h=HEADS, two=2)
            tab_q = c.m("rope_q").rearrange("p (z t i) -> p z t i", z=2, t=ST)
            tab_k = c.m("rope_k").rearrange("p (z h) -> p z h", z=2)
            spread = lambda tab: tab.unsqueeze(2).broadcast_to([P, ST, HEADS, 4])
            jobs = [(c.XN, slice(b * ST, (b + 1) * ST), [spread(tab_q[:, z]) for z in range(2)]) for b in range(B)]
            jobs.append((c.total, slice(0, NT), [tab_k[:, z].unsqueeze(1).broadcast_to([P, NT, HEADS * 4]) for z in range(2)]))
            for dst, ts, (cos, sin) in jobs:
                n = ts.stop - ts.start
                if n == NT:
                    view = lambda ap: ap.rearrange("p t h i -> p t (h i)")
                else:
                    view = lambda ap: ap
                out = dst[:, ts].rearrange("p t (h z i) -> p t h z i", h=HEADS, z=2)
                t1, t2 = (view(p5[:, ts, :, :, k]) for k in range(2))
                room = [c.big2(k * S, n * HEADS * 4).rearrange("p (t h i) -> p t h i", h=HEADS, i=4) for k in range(4)]
                for k, (x, y) in enumerate(((t1, cos), (t2, sin), (t1, sin), (t2, cos))):
                    last = nc.vector.tensor_tensor(view(room[k]), x, y, ALU.mult)
                seq(dve, step, last)
                nc.vector.tensor_tensor(out[:, :, :, 0, :], room[0], room[1], ALU.subtract)
                seq(dve, step, nc.vector.tensor_tensor(out[:, :, :, 1, :], room[2], room[3], ALU.add))

        def cut_values(copy, chunks_of):
            for bl in chunks_of:
                for cl in range(4):
                    src = proj[32 * bl:32 * bl + 32].rearrange("p t (i cl d) -> p t i cl d", i=4, cl=4)[:, :, :, cl, :]
                    copy(values[32 * cl:32 * cl + 32, :, bl, :, 0:8], src)

        values = c.VH[:, 0:B * HEADS * 36].rearrange("p (t bl i e) -> p t bl i e", t=NT, bl=4, i=4)

        @block.gpsimd
        def _(pool):
            seq(pool, pool_step, nc.gpsimd.memset(values[:, :, :, :, 8], 1.0))
            cut_values(lambda dst, src: seq(pool, pool_step, nc.gpsimd.tensor_copy(dst, src)), (0, 1))

        @block.scalar
        def _(act):
            cut_values(nc.scalar.copy, (2, 3))

    keys = c.big1(2 * TOK, TOK).rearrange("p (t bl i d) -> p t bl i d", t=NT, bl=4, i=4)
    with nc.Block() as block:
        @block.vector
        def _(dve):
            for bl in range(4):
                for cl in range(4):
                    src = c.total[32 * bl:32 * bl + 32].rearrange("p t (i cl d) -> p t i cl d", i=4, cl=4)[:, :, :, cl, :]
                    nc.vector.tensor_copy(keys[32 * cl:32 * cl + 32, :, bl], src)

    turn(c, c.XN[:], NT, P, c.qk32[:, 0:1, :])
    qT = c.VH[:, B * HEADS * 36:B * HEADS * 36 + TOK]
    matmul_stream(c, halves(c, lambda half: [(c.headmat, c.qk32[:, 0, half * S:(half + 1) * S])], P, qT))
    stack_keys(c, keys.rearrange("p t bl i d -> p (t bl) i d"))
    rest_of_heads = split_heads(c, qT, None, 0)
    attention_8(c, [P] * ST, c.Y8, 8.0 ** -0.5, rest_of_heads, chunked=True)
    quantise(c, c.Y8, c.q_bf[:], amax)
    turn_quantised(c, c.q_bf, c.qT_bf)
    quantised_product(c, c.qT_bf[:], c.signT[:, 1, :], amax, c.alpha[:, 1, :], None, c.Y8)
    with nc.Block() as block:
        @block.vector
        def _(dve):
            nc.vector.tensor_tensor(c.total[:], c.X[:], c.Y8, ALU.add)
    add_and_norm(c, total=c.total, out=c.X, turned=[(c.XT, None, None)])


def cross_kv(c, wk, wv, bk=None, bv=None):
    ctxT = c.m("ctxT")[0:CTX]
    v = c.VH[0:SK, 0:B * HEADS * 9].rearrange("p (b h e) -> p b h e", b=B, e=9)

    def ones(act, bank):
        return None
    units = [([(wk, ctxT)], P, B * SK, "act", act_copy(c, c.ckT[:], bias=bk))]
    for b in range(B):
        if bv is None:
            emit = (lambda b: lambda dve, bank, step: c.nc.vector.tensor_copy(v[:, b, :, 0:8], bank.rearrange("p (h d) -> p h d", d=8)))(b)
        else:
            emit = (lambda b: lambda dve, bank, step: c.nc.vector.tensor_tensor(
                v[:, b, :, 0:8], bank.rearrange("p (h d) -> p h d", d=8), bv[0:SK].rearrange("p (h d) -> p h d", d=8), ALU.add))(b)
        units.append(([(ctxT[:, b * SK:(b + 1) * SK], wv)], SK, P, "dve", emit))
    return units, v[:, :, :, 8]


def fill(c, ap, value):
    with c.nc.Block() as block:
        @block.gpsimd
        def _(pool):
            c.nc.gpsimd.memset(ap, value)


def cross_attention_8(c, wq, wk, wv, wo, bq, bk, bv, bo):
    units, one = cross_kv(c, wk, wv, bk, bv)
    units += halves(c, lambda half: [(wq, c.XT[:, half * S:(half + 1) * S])], P, c.qT, bias=bq)
    fill(c, one, 1.0)
    matmul_stream(c, units)
    rest_of_heads = split_heads(c, c.qT[:], c.ckT[:], SK)
    attention_8(c, [SK], c.Y8, 8.0 ** -0.5, rest_of_heads)
    turn(c, c.Y8, NT, P, c.yT8)
    add_and_norm(c, add=project_out(c, c.yT8, wo), bias=bo, out=c.X, turned=[(c.XT, None, None)])


def moe(c, srcT, parts, cwT_parts, mix, outT, load=None):
    nc = c.nc
    gate_ready, gated, hidden_ready, hidden_used, acc_ready, dve_step, act_mid = (counter(c, n) for n in (
        "gate_ready", "gated", "hidden_ready", "hidden_used", "acc_ready", "dve_step", "act_mid"))
    n = len(parts)
    steps = [(half, k) for half in range(2) for k in range(n)]
    G, U, CW, ACC = c.bank[0:2], c.bank[2:4], c.bank[4:6], c.bank[6]
    sg, hid = c.moe_sg, c.moe_h

    with nc.Block() as block:
        if load:
            block.sync(load)

        @block.tensor
        def _(pe):
            def up(s):
                half, k = steps[s]
                w1, w3, _, pick = parts[k]
                m = w1.shape[1]
                x = srcT[:, half * S:(half + 1) * S]
                if s >= 2:
                    pe.wait_ge(hidden_ready.sem, hidden_ready.at(s - 1))
                nc.tensor.matmul(G[s % 2][0:m, :], w1, x, start=True, stop=True).then_inc(gate_ready.up(), 1)
                last = nc.tensor.matmul(U[s % 2][0:m, :], w3, x, start=True, stop=True)
                if pick is not None:
                    last = nc.tensor.matmul(CW[s % 2][0:m, :], pick, cwT_parts[:, half * S:(half + 1) * S], start=True, stop=True)
                last.then_inc(gate_ready.up(), 1)

            def down(s):
                half, k = steps[s]
                w2 = parts[k][2]
                m = w2.shape[0]
                pe.wait_ge(hidden_ready.sem, hidden_ready.at(s + 1))
                if k == 0 and half:
                    pe.wait_ge(acc_ready.sem, acc_ready.at(1))
                last = nc.tensor.matmul(ACC[:, :], w2, hid[0:m, s % 2, :], start=(k == 0), stop=(k == n - 1))
                last.then_inc(hidden_used.up(), 1)

            for s in range(len(steps) + 1):
                if s < len(steps):
                    up(s)
                if s >= 1:
                    down(s - 1)

        @block.scalar
        def _(act):
            for s, (half, k) in enumerate(steps):
                m = parts[k][0].shape[1]
                act.wait_ge(gate_ready.sem, gate_ready.at(2 * s + 1))
                if s >= 2:
                    act.wait_ge(hidden_ready.sem, hidden_ready.at(s - 1))
                func = ACT.Silu if mix == "silu" else ACT.Copy
                nc.scalar.activation(sg[0:m, s % 2, :], G[s % 2][0:m, :], func).then_inc(gated.up(), 1)
                if mix == "gelu":
                    act.wait_ge(act_mid.sem, act_mid.at(s + 1))
                    nc.scalar.activation(sg[0:m, s % 2, :], sg[0:m, s % 2, :], ACT.Gelu).then_inc(gated.up(), 1)
                if k == 0 and half:
                    act.wait_ge(hidden_used.sem, hidden_used.at(n))
                    nc.scalar.copy(outT[:, 0:S], ACC[:, :]).then_inc(acc_ready.up(), 1)
            act.wait_ge(hidden_used.sem, hidden_used.at(2 * n))
            nc.scalar.copy(outT[:, S:2 * S], ACC[:, :])

        @block.vector
        def _(dve):
            for s, (half, k) in enumerate(steps):
                m = parts[k][0].shape[1]
                pick = parts[k][3]
                dve.wait_ge(gate_ready.sem, gate_ready.at(2 * s + 2))
                if s >= 2:
                    dve.wait_ge(hidden_used.sem, hidden_used.at(s - 1))
                if mix == "gelu":
                    dve.wait_ge(gated.sem, gated.at(2 * s + 1))
                    nc.vector.tensor_tensor(sg[0:m, s % 2, :], sg[0:m, s % 2, :], U[s % 2][0:m, :], ALU.mult).then_inc(act_mid.up(), 1)
                    dve.wait_ge(gated.sem, gated.at(2 * s + 2))
                    last = nc.vector.tensor_tensor(hid[0:m, s % 2, :], sg[0:m, s % 2, :], CW[s % 2][0:m, :], ALU.mult)
                else:
                    dve.wait_ge(gated.sem, gated.at(s + 1))
                    last = nc.vector.tensor_tensor(hid[0:m, s % 2, :], sg[0:m, s % 2, :], U[s % 2][0:m, :], ALU.mult)
                    if pick is not None:
                        seq(dve, dve_step, last)
                        last = nc.vector.tensor_tensor(hid[0:m, s % 2, :], hid[0:m, s % 2, :], CW[s % 2][0:m, :], ALU.mult)
                last.then_inc(hidden_ready.up(), 1)


def router_logits(c, srcT, w, E):
    nc = c.nc
    with nc.Block() as block:
        @block.tensor
        def _(pe):
            for t in range(NT):
                nc.tensor.matmul(c.bank[0][:, t * 32:t * 32 + E], srcT[:, t * P:(t + 1) * P], w, start=True, stop=True)


def turn_weights(c, cw, E):
    nc, step = c.nc, counter(c, "dve_step")
    cw_ready, cw_turned, act_freed = counter(c, "cw_ready"), counter(c, "cw_turned"), counter(c, "act_freed")
    parts = c.cw_parts
    with nc.Block() as block:
        @block.vector
        def _(dve):
            rest = c.cw_rest[:, :, 0:E]
            seq(dve, step, nc.vector.memset(parts[:], 0.0))
            seq(dve, step, nc.vector.tensor_copy(parts[:, :, 0:E], cw))
            seq(dve, step, nc.vector.tensor_tensor(rest, cw, parts[:, :, 0:E], ALU.subtract))
            seq(dve, step, nc.vector.tensor_copy(parts[:, :, 32:32 + E], rest))
            seq(dve, step, nc.vector.tensor_tensor(rest, rest, parts[:, :, 32:32 + E], ALU.subtract))
            nc.vector.tensor_copy(parts[:, :, 64:64 + E], rest).then_inc(cw_ready.up(), 1)

        @block.tensor
        def _(pe):
            pe.wait_ge(cw_ready.sem, cw_ready.at(1))
            for half in range(2):
                if half:
                    pe.wait_ge(act_freed.sem, act_freed.at(1))
                for k in range(4):
                    last = nc.tensor.transpose(c.bank_bf[0:96, k * P:(k + 1) * P], parts[:, half * 4 + k, :], c.ident_bf[:])
                last.then_inc(cw_turned.up(), 1)

        @block.scalar
        def _(act):
            for half in range(2):
                act.wait_ge(cw_turned.sem, cw_turned.at(half + 1))
                nc.scalar.copy(c.cwT[:, half * S:(half + 1) * S], c.bank_bf[0:96, 0:S]).then_inc(act_freed.up(), 1)


def top_indices(dve, c, step, values, E, dst):
    nc = c.nc
    for t in range(NT):
        last = nc.vector.max(c.top_v[:, t, :], values[:, t, 0:E])
    seq(dve, step, last)
    for t in range(NT):
        last = nc.vector.max_index(c.top_i[:, t, :], c.top_v[:, t, :], values[:, t, 0:E])
    seq(dve, step, last)
    seq(dve, step, nc.vector.tensor_copy(dst, c.top_i[:]))


def one_hot(c, E, index, dst):
    iota = c.m("iota")[:, 0:E].unsqueeze(1).broadcast_to([P, NT, E])
    return c.nc.vector.tensor_tensor(dst, iota, index.unsqueeze(2).broadcast_to([P, NT, E]), ALU.is_equal)


def layer0_moe(c):
    nc, step = c.nc, counter(c, "dve_step")
    E = L0E
    router_logits(c, c.XT[:], c.m("L0_gateT"), E)
    sc, sel, oh, top = c.rt[:, 0, :, 0:E], c.rt[:, 1, :, 0:E], c.rt[:, 2, :, 0:E], c.top_f
    biased, scored = counter(c, "biased"), counter(c, "scored")
    with nc.Block() as block:
        @block.vector
        def _(dve):
            lg = c.bank[0][:, 0:NT * 32].rearrange("p (t e) -> p t e", t=NT)[:, :, 0:E]
            nc.vector.tensor_tensor(sel, lg, c.m("gate_bias").unsqueeze(1).broadcast_to([P, NT, E]), ALU.add).then_inc(biased.up(), 1)
            dve.wait_ge(scored.sem, scored.at(1))
            top_indices(dve, c, step, c.rt[:, 0, :, :], E, top)
            seq(dve, step, one_hot(c, E, top[:, :, 0], sel))
            seq(dve, step, one_hot(c, E, top[:, :, 1], oh))
            seq(dve, step, nc.vector.tensor_tensor(sel, sel, oh, ALU.add))
            seq(dve, step, nc.vector.tensor_tensor(sel, sel, sc, ALU.mult))
            seq(dve, step, nc.vector.tensor_reduce(c.small8[:, 0, :], sel, AX_X, ALU.add))
            seq(dve, step, nc.vector.tensor_scalar(c.small8[:, 0, :], c.small8[:, 0, :], 1e-20, None, ALU.add))
            seq(dve, step, nc.vector.reciprocal(c.small8[:, 1, :], c.small8[:, 0, :]))
            seq(dve, step, nc.vector.tensor_tensor(sel, sel, c.small8[:, 1, :].unsqueeze(2).broadcast_to([P, NT, E]), ALU.mult))

        @block.scalar
        def _(act):
            act.wait_ge(biased.sem, biased.at(1))
            nc.scalar.activation(sc, sel, ACT.Sigmoid).then_inc(scored.up(), 1)
    turn_weights(c, sel, E)
    w1, w3, w2 = c.m("w1T"), c.m("w3T"), c.m("w2T")
    parts = []
    for e in range(E):
        for i, (a, m) in enumerate(chunks(L0HID)):
            col = e * L0HID + a
            parts.append((w1[:, col:col + m], w3[:, col:col + m], w2[0:m, (e * 3 + i) * P:(e * 3 + i + 1) * P],
                          c.pick_expert[:, e, 0:m]))
    moe(c, c.XT[:], parts, c.cwT, "silu", c.outT[:])
    add_and_norm(c, add=turn_back(c, c.outT), out=c.X, turned=[(c.XT, None, None)], load=c.fetcher("moe1", "turned"))



def layer1_scan(c):
    nc = c.nc
    N = 16
    xnT, dtT, uT = c.big1(0, TOK), c.big1(TOK, TOK), c.big1(2 * TOK, TOK)
    ex, mx = c.big1(3 * TOK, TOK), c.big1(4 * TOK, TOK)
    weights = c.big1(5 * TOK, 96).rearrange("p (k n) -> p k n", k=3)
    bc, mid = (c.big1(6 * TOK + i * S, S)[0:96].bitcast(BF16) for i in range(2))
    rest = c.big1(7 * TOK, TOK)[0:96]
    pick = c.big3(0, N * P)[0:96].bitcast(BF16).rearrange("p (n m) -> p n m", n=2 * N)
    a, bx, h, ch = (c.big3(2048 + 1024 * i, TOK).rearrange("p (z t) -> p z t", z=2) for i in range(4))
    yT = c.outT
    add_and_norm(c, out=c.XN, turned=[(xnT, c.col("L1_attn_gamma"), c.col("L1_attn_beta"))])
    step, act_step = counter(c, "dve_step"), counter(c, "act_step")
    matmul_stream(c, halves(c, lambda half: [(c.m("L1_WdtT"), xnT[:, half * S:(half + 1) * S])], P, dtT, bias=c.col("L1_attn_b_dt")))
    z_ready, soft_ready, dt_ready, weights_ready, bc_ready = (counter(c, n) for n in (
        "z_ready", "soft_ready", "dt_ready", "weights_ready", "bc_ready"))
    with nc.Block() as block:
        @block.vector
        def _(dve):
            seq(dve, step, nc.vector.tensor_scalar(ex, dtT, -1.0, None, ALU.mult))
            nc.vector.tensor_tensor(ex, ex, dtT, ALU.min).then_inc(z_ready.up(), 1)
            seq(dve, step, nc.vector.tensor_scalar(mx, dtT, 0.0, None, ALU.max))
            dve.wait_ge(soft_ready.sem, soft_ready.at(1))
            seq(dve, step, nc.vector.tensor_tensor(dtT, mx, ex, ALU.add))
            nc.vector.tensor_tensor(uT, dtT, xnT, ALU.mult)
            nc.vector.tensor_scalar(c.negA, c.negA, -1.0, None, ALU.mult).then_inc(dt_ready.up(), 1)
            dve.wait_ge(bc_ready.sem, bc_ready.at(1))
            tokens = [slice(z * S, (z + 1) * S) for z in range(2)]
            for z in range(2):
                last = nc.vector.tensor_copy(bc[:, tokens[z]], c.bank[z][0:96, :])
            seq(dve, step, last)
            for z in range(2):
                last = nc.vector.tensor_tensor(rest[:, tokens[z]], c.bank[z][0:96, :], bc[:, tokens[z]], ALU.subtract)
            seq(dve, step, last)
            nc.vector.tensor_copy(bc[32:64, :], rest[32:64, :])
            seq(dve, step, nc.vector.tensor_copy(mid[64:96, :], rest[64:96, :]))
            nc.vector.tensor_tensor(bc[64:96, :], rest[64:96, :], mid[64:96, :], ALU.subtract)

        @block.tensor
        def _(pe):
            pe.wait_ge(weights_ready.sem, weights_ready.at(1))
            for z in range(2):
                last = nc.tensor.matmul(c.bank[z][0:96, :], weights.rearrange("p k n -> p (k n)"), xnT[:, z * S:(z + 1) * S], start=True, stop=True)
            last.then_inc(bc_ready.up(), 1)

        @block.scalar
        def _(act):
            nc.scalar.activation(c.negA, c.m("L1_A_log"), ACT.Exp)
            act.wait_ge(z_ready.sem, z_ready.at(1))
            seq(act, act_step, nc.scalar.activation(ex, ex, ACT.Exp))
            nc.scalar.activation(ex, ex, ACT.Ln, bias=1.0).then_inc(soft_ready.up(), 1)
            nc.scalar.copy(pick[:, N // 2:, :], c.pick_id[:, N // 2:].unsqueeze(2).broadcast_to([96, 3 * N // 2, P]))

        @block.gpsimd
        def _(pool):
            nc.gpsimd.tensor_copy(weights[:, :, 0:N], c.m("L1_WBT").unsqueeze(1).broadcast_to([P, 3, N]))
            nc.gpsimd.tensor_copy(weights[:, :, N:2 * N], c.m("L1_WCT").unsqueeze(1).broadcast_to([P, 3, N])).then_inc(weights_ready.up(), 1)
            nc.gpsimd.tensor_copy(pick[:, 0:N // 2, :], c.pick_id[:, 0:N // 2].unsqueeze(2).broadcast_to([96, N // 2, P]))

    BC, YS = c.bank[0:6], c.bank[6:8]
    in_ready, ch_ready, a_ready, sum_ready, decay_used = (counter(c, n) for n in ("in_ready", "ch_ready", "a_ready", "sum_done", "decay_used"))
    driven = counter(c, "driven")
    steps = [(n, z) for n in range(N) for z in range(2)]
    with nc.Block() as block:
        @block.tensor
        def _(pe):
            def inputs(s):
                n, z = steps[s]
                x = bc[:, z * S:(z + 1) * S]
                if s >= 3:
                    pe.wait_ge(ch_ready.sem, ch_ready.at(s - 2))
                nc.tensor.matmul(BC[2 * (s % 3)][:, :], pick[:, n, :], x, start=True, stop=True)
                nc.tensor.matmul(BC[2 * (s % 3) + 1][:, :], pick[:, N + n, :], x, start=True, stop=True).then_inc(in_ready.up(), 1)

            inputs(0)
            inputs(1)
            for s, (n, z) in enumerate(steps):
                if s + 2 < len(steps):
                    inputs(s + 2)
                pe.wait_ge(ch_ready.sem, ch_ready.at(s + 1))
                nc.tensor.matmul(YS[z][:, :], c.ident[:], ch[:, s % 2, :], start=(n == 0), stop=(n == N - 1)).then_inc(sum_ready.up(), 1)

        @block.scalar
        def _(act):
            for s, (n, z) in enumerate(steps):
                if s >= 2:
                    act.wait_ge(decay_used.sem, decay_used.at(s - 1))
                nc.scalar.activation(a[:, s % 2, :], dtT[:, z * S:(z + 1) * S], ACT.Exp, scale=c.negA[:, n:n + 1]).then_inc(a_ready.up(), 1)

        @block.vector
        def _(dve):
            def drive(s):
                _, z = steps[s]
                dve.wait_ge(in_ready.sem, in_ready.at(s + 1))
                nc.vector.tensor_tensor(bx[:, s % 2, :], uT[:, z * S:(z + 1) * S], BC[2 * (s % 3)][:, :], ALU.mult).then_inc(driven.up(), 1)

            drive(0)
            for s in range(len(steps)):
                dve.wait_ge(driven.sem, driven.at(s + 1))
                dve.wait_ge(a_ready.sem, a_ready.at(s + 1))
                nc.vector.tensor_tensor_scan(h[:, s % 2, :], a[:, s % 2, :], bx[:, s % 2, :], 0.0, ALU.mult, ALU.add).then_inc(decay_used.up(), 1)
                if s + 1 < len(steps):
                    drive(s + 1)
                dve.wait_ge(decay_used.sem, decay_used.at(s + 1))
                if s >= 2:
                    dve.wait_ge(sum_ready.sem, sum_ready.at(s - 1))
                nc.vector.tensor_tensor(ch[:, s % 2, :], h[:, s % 2, :], BC[2 * (s % 3) + 1][:, :], ALU.mult).then_inc(ch_ready.up(), 1)
            dve.wait_ge(sum_ready.sem, sum_ready.at(len(steps)))
            for z in range(2):
                nc.vector.scalar_tensor_tensor(out=yT[:, z * S:(z + 1) * S], in0=c.XT[:, z * S:(z + 1) * S],
                                               scalar=c.col("L1_attn_D_param"), in1=YS[z][:, :], op0=ALU.mult, op1=ALU.add)
    add_and_norm(c, add=turn_back(c, yT), out=c.X, turned=[(c.XT, None, None)])


def heads_natural(c, srcT, w, cols, V, width, tiles=NT):
    units = []
    for t in range(tiles):
        for a in range(0, cols, S):
            n = min(S, cols - a)
            who = "act" if t % 2 else "dve"
            dst = V[:, t, a // width:(a + n) // width, 0:width]
            if who == "act":
                emit = (lambda dst: lambda act, bank: c.nc.scalar.copy(dst, bank.rearrange("p (h d) -> p h d", d=width)))(dst)
            else:
                emit = (lambda dst: lambda dve, bank, step: c.nc.vector.tensor_copy(dst, bank.rearrange("p (h d) -> p h d", d=width)))(dst)
            units.append(([(srcT[:, t * P:(t + 1) * P], w[:, a:a + n])], P, n, who, emit))
    return units


def layer1_ffn(c):
    nc = c.nc
    nT = c.big2(2 * TOK, TOK)
    y = c.big1(0, 8 * TOK).rearrange("p (k t) -> p k t", k=8)
    V = c.VH[:, 0:NT * 4 * 64].rearrange("p (t h e) -> p t h e", t=NT, h=4)
    add_and_norm(c, norm="rms", eps=1e-6, out=c.XN, turned=[(nT, c.col("L1_ffn_g1"), None)])
    matmul_stream(c, heads_natural(c, nT, c.m("wv"), 256, V, 64))

    product_ready, terms_ready, sum_ready, high_ready, rest_ready, mid_ready, low_ready = (counter(c, n) for n in (
        "product_ready", "terms_ready", "sum_ready", "high_ready", "rest_ready", "mid_ready", "low_ready"))
    jobs = [(w, ws, dram, kk, b) for w, ws, dram, n in (("wk", "wks", c.k_wide, 2), ("wq", "wqs", c.q_wide, 8))
            for kk in range(n) for b in range(B)]
    tmp = c.big2(3 * TOK, TOK).rearrange("p (z t) -> p z t", z=2)
    total = c.big2(0, 4 * S).rearrange("p (z t) -> p z t", z=4)
    size = 3 * S // 2
    parts = [m(u * size, size).bitcast(BF16).rearrange("p (z t) -> p z t", z=3) for m in (c.big1, c.big3) for u in range(10)]
    J = len(jobs)
    with nc.Block() as block:
        @block.tensor
        def _(pe):
            for s, (w, ws, _, kk, b) in enumerate(jobs):
                if s >= 4:
                    pe.wait_ge(terms_ready.sem, terms_ready.at(s - 3))
                x = nT[:, b * S:(b + 1) * S]
                nc.tensor.matmul(c.bank[2 * (s % 4)][:, :], c.m(w)[:, kk * P:(kk + 1) * P], x, start=True, stop=True)
                nc.tensor.matmul(c.bank[2 * (s % 4) + 1][:, :], c.m(ws)[:, kk * P:(kk + 1) * P], x, start=True, stop=True).then_inc(
                    product_ready.up(), 1)

        @block.vector
        def _(dve):
            for s in range(J + 1):
                if s < J:
                    dve.wait_ge(product_ready.sem, product_ready.at(s + 1))
                    if s >= 4:
                        dve.wait_ge(low_ready.sem, low_ready.at(s - 3))
                    nc.vector.tensor_tensor(total[:, s % 4, :], c.bank[2 * (s % 4)][:, :], c.m("cos"), ALU.mult)
                    if s >= 2:
                        dve.wait_ge(sum_ready.sem, sum_ready.at(s - 1))
                    nc.vector.tensor_tensor(tmp[:, s % 2, :], c.bank[2 * (s % 4) + 1][:, :], c.m("sin"), ALU.mult).then_inc(terms_ready.up(), 1)
                if s >= 1:
                    v = s - 1
                    dve.wait_ge(high_ready.sem, high_ready.at(v + 1))
                    nc.vector.tensor_tensor(total[:, v % 4, :], total[:, v % 4, :], parts[v][:, 0, :], ALU.subtract).then_inc(rest_ready.up(), 1)

        @block.gpsimd
        def _(pool):
            for s in range(J + 2):
                if s < J:
                    pool.wait_ge(terms_ready.sem, terms_ready.at(s + 1))
                    nc.gpsimd.tensor_tensor(total[:, s % 4, :], total[:, s % 4, :], tmp[:, s % 2, :], ALU.add).then_inc(sum_ready.up(), 1)
                if s >= 2:
                    v = s - 2
                    pool.wait_ge(mid_ready.sem, mid_ready.at(v + 1))
                    nc.gpsimd.tensor_tensor(parts[v][:, 2, :], total[:, v % 4, :], parts[v][:, 1, :], ALU.subtract).then_inc(low_ready.up(), 1)

        @block.scalar
        def _(act):
            for s in range(J + 1):
                if s < J:
                    act.wait_ge(sum_ready.sem, sum_ready.at(s + 1))
                    nc.scalar.copy(parts[s][:, 0, :], total[:, s % 4, :]).then_inc(high_ready.up(), 1)
                if s >= 1:
                    act.wait_ge(rest_ready.sem, rest_ready.at(s))
                    nc.scalar.copy(parts[s - 1][:, 1, :], total[:, (s - 1) % 4, :]).then_inc(mid_ready.up(), 1)

        @block.sync
        def _(sp):
            for s, (_, _, dram, kk, b) in enumerate(jobs):
                sp.wait_ge(low_ready.sem, low_ready.at(s + 1))
                sp.dma_start(dram[:, :, kk, b * S:(b + 1) * S], parts[s]).then_inc(c.stored_parts, 16)
                c.nparts += 16
            c.fetch(sp, "l2x")

    attention(c, [P] * ST, 64, None, lambda b, h, i: V[:, b * ST + i, h % 4, 0:64], 0.125, y, mask="causal",
              stacks=HeadStacks(c, 64, S, resident=4, kv=lambda h: h % 4))
    yT = y
    hT = c.big2(0, TOK)
    add_and_norm(c, add=project_out(c, yT, c.m("wo"), 8), total=c.total, norm="rms", eps=1e-6, out=c.XN,
                 turned=[(hT, c.col("L1_ffn_g2"), None)])
    router_logits(c, hT, c.m("L1f_router"), L1E)

    E = L1E
    step = counter(c, "dve_step")
    lg, oh1, oh2, cum, tmp1, tmp2 = (c.rt[:, i, :, 0:E] for i in range(6))
    top = c.top_f
    s_ = lambda i: c.small8[:, i, :]
    top_done, weights_done, counted = (counter(c, n) for n in ("top_done", "weights_done", "counted"))
    with nc.Block() as block:
        @block.vector
        def _(dve):
            bank = c.bank[0][:, 0:NT * 32].rearrange("p (t e) -> p t e", t=NT)[:, :, 0:E]
            seq(dve, step, nc.vector.tensor_tensor(lg, bank, c.m("router_b").unsqueeze(1).broadcast_to([P, NT, E]), ALU.add))
            top_indices(dve, c, step, c.rt[:, 0, :, :], E, top)
            nc.vector.tensor_tensor(s_(0), c.top_v[:, :, 1], c.top_v[:, :, 0], ALU.subtract)
            nc.vector.tensor_copy(oh2, c.m("iota")[:, 0:E].unsqueeze(1).broadcast_to([P, NT, E]))
            seq(dve, step, one_hot(c, E, top[:, :, 0], oh1))
            oh = c.cw_rest[:, :, 0:2 * E]
            nc.vector.tensor_copy(oh[:, :, 0:E], oh1)
            one_hot(c, E, top[:, :, 1], oh[:, :, E:2 * E])
            seq(dve, step, one_hot(c, E, top[:, :, 1], oh2))
            nc.vector.tensor_copy(s_(7), s_(0)).then_inc(top_done.up(), 1)
            dve.wait_ge(counted.sem, counted.at(1))
            cnt = c.bank[1][:, 0:NT * 2 * E].rearrange("p (t e) -> p t e", t=NT)
            cap = float(TOK // 8)
            seq(dve, step, nc.vector.tensor_copy(tmp1, cnt[:, :, 0:E]))
            seq(dve, step, nc.vector.tensor_tensor(tmp2, cnt[:, :, E:2 * E], tmp1, ALU.add))
            seq(dve, step, nc.vector.tensor_scalar(tmp1, tmp1, cap, None, ALU.is_lt))
            seq(dve, step, nc.vector.tensor_scalar(tmp2, tmp2, cap, None, ALU.is_lt))
            seq(dve, step, nc.vector.tensor_tensor(tmp1, tmp1, oh1, ALU.mult))
            seq(dve, step, nc.vector.tensor_tensor(tmp2, tmp2, oh2, ALU.mult))
            nc.vector.tensor_reduce(s_(1), tmp1, AX_X, ALU.add)
            seq(dve, step, nc.vector.tensor_reduce(s_(2), tmp2, AX_X, ALU.add))
            seq(dve, step, nc.vector.tensor_tensor(s_(3), s_(1), top[:, :, 0], ALU.mult))
            seq(dve, step, nc.vector.tensor_tensor(s_(4), s_(2), top[:, :, 1], ALU.mult))
            seq(dve, step, nc.vector.tensor_tensor(s_(3), s_(3), s_(4), ALU.max))
            seq(dve, step, one_hot(c, E, s_(3), cum))
            dve.wait_ge(weights_done.sem, weights_done.at(1))
            seq(dve, step, nc.vector.tensor_scalar(s_(5), s_(7), 1.0, None, ALU.add))
            seq(dve, step, nc.vector.reciprocal(s_(5), s_(5)))
            seq(dve, step, nc.vector.tensor_tensor(s_(6), s_(7), s_(5), ALU.mult))
            seq(dve, step, nc.vector.tensor_tensor(s_(1), s_(1), s_(5), ALU.mult))
            seq(dve, step, nc.vector.tensor_tensor(s_(2), s_(2), s_(6), ALU.mult))
            seq(dve, step, nc.vector.tensor_tensor(s_(1), s_(1), s_(2), ALU.add))
            seq(dve, step, nc.vector.tensor_tensor(s_(5), s_(5), s_(6), ALU.add))
            seq(dve, step, nc.vector.tensor_tensor(s_(2), s_(5), s_(1), ALU.subtract))
            seq(dve, step, nc.vector.tensor_tensor(cum, cum, s_(1).unsqueeze(2).broadcast_to([P, NT, E]), ALU.mult))
            nc.vector.tensor_tensor(c.total[:], c.total[:], c.X[:], ALU.add)

        @block.scalar
        def _(act):
            act.wait_ge(top_done.sem, top_done.at(1))
            nc.scalar.activation(s_(7), s_(7), ACT.Exp).then_inc(weights_done.up(), 1)

        @block.tensor
        def _(pe):
            pe.wait_ge(top_done.sem, top_done.at(1))
            oh = c.cw_rest[:, :, 0:2 * E]
            for t in range(NT):
                last = nc.tensor.matmul(c.bank[1][:, t * 2 * E:NT * 2 * E], c.ones[:], oh[:, 0:NT - t, :], start=(t == 0), stop=False)
            last = nc.tensor.matmul(c.bank[1][:, 0:NT * 2 * E], c.minus_later[:], oh, start=False, stop=True)
            last.then_inc(counted.up(), 1)

    fill_pick(c, P)
    turn_weights(c, cum, E)
    parts = []
    for e in range(E):
        for i in range(2):
            col = e * L1HID + i * P
            parts.append((c.m("w2")[:, col:col + P], c.m("w1")[:, col:col + P], c.m("w3")[:, (e * 2 + i) * P:(e * 2 + i + 1) * P],
                          c.pick_expert[:, e, :]))
    moe(c, hT, parts, c.cwT, "gelu", c.outT[:])
    own_ready = counter(c, "own_ready")
    with nc.Block() as block:
        @block.tensor
        def _(pe):
            for half in range(2):
                for kk in range(4):
                    last = nc.tensor.transpose(c.bank[half][:, kk * P:(kk + 1) * P], hT[:, (half * 4 + kk) * P:(half * 4 + kk + 1) * P], c.ident[:])
                last.then_inc(own_ready.up(), 1)

        @block.vector
        def _(dve):
            for half in range(2):
                dve.wait_ge(own_ready.sem, own_ready.at(half + 1))
                for kk in range(4):
                    t = half * 4 + kk
                    nc.vector.scalar_tensor_tensor(out=c.total[:, t, :], in0=c.bank[half][:, kk * P:(kk + 1) * P],
                                                   scalar=s_(2)[:, t:t + 1], in1=c.total[:, t, :], op0=ALU.mult, op1=ALU.add)
    add_and_norm(c, add=turn_back(c, c.outT), base=c.total, out=c.X, turned=[(c.XT, None, None)], load=c.fetcher("moe2", "l3"))



def layer2_attention(c):
    nc = c.nc
    qf = c.big1(0, TOK)
    kf = c.big3(TOK, TOK)
    V = c.VH[:, 0:NT * HEADS * 9].rearrange("p (t h e) -> p t h e", t=NT, h=HEADS)
    block_product(c, c.m("L2_WQrT")[0:16], c.m("L2_WKrT")[0:16], c.headmat)
    fill(c, V[:, :, :, 8], 1.0)
    x = lambda half: c.XT[:, half * S:(half + 1) * S]
    units = halves(c, lambda half: [(c.m("L2_WQ"), x(half))], P, qf, bias=c.col("L2_attn_bQ"))
    units += halves(c, lambda half: [(c.m("L2_WK"), x(half))], P, kf, bias=c.col("L2_attn_bK"))
    bv = c.row("L2_attn_bV").rearrange("p (h d) -> p h d", d=8)
    for t in range(NT):
        emit = (lambda t: lambda dve, bank, step: nc.vector.tensor_tensor(V[:, t, :, 0:8], bank.rearrange("p (h d) -> p h d", d=8), bv, ALU.add))(t)
        units.append(([(c.XT[:, t * P:(t + 1) * P], c.m("L2_WV"))], P, P, "dve", emit))
    matmul_stream(c, units)
    matmul_stream(c, halves(c, lambda half: [(c.headmat, qf[:, half * S:(half + 1) * S])], P, c.qT))
    rest_of_heads = split_heads(c, c.qT[:], kf, S)
    attention_8(c, [P] * ST, c.Y8, 0.25, rest_of_heads)
    turn(c, c.Y8, NT, P, c.yT8)
    add_and_norm(c, add=project_out(c, c.yT8, c.m("L2_WO")), bias=c.row("L2_attn_bO"), out=c.X, turned=[(c.XT, None, None)])


def layer2_cross(c):
    y = c.big1(0, 8 * TOK).rearrange("p (k t) -> p k t", k=8)
    V = c.VH[0:SK, 0:B * HEADS * 64].rearrange("p (b h e) -> p b h e", b=B, h=HEADS)
    ctxT = c.m("ctxT")[0:CTX]
    split = []
    for kk in range(8):
        cols = slice(kk * P, (kk + 1) * P)
        split.append((c.m("L2x_Wk")[0:CTX, cols], ctxT, B * SK, c.k_wide[:, :, kk, 0:B * SK]))
    for kk in range(8):
        cols = slice(kk * P, (kk + 1) * P)
        for b in range(B):
            split.append((c.m("L2x_Wq")[:, cols], c.XT[:, b * S:(b + 1) * S], S, c.q_wide[:, :, kk, b * S:(b + 1) * S]))
    project_split(c, split, [c.big3(0, 8 * TOK), c.big1(0, 8 * TOK), c.big2(0, 4 * TOK)])
    units = []
    for b in range(B):
        for a in range(0, 1024, S):
            emit = (lambda dst: lambda dve, bank, step: c.nc.vector.tensor_copy(dst, bank.rearrange("p (h d) -> p h d", d=64)))(V[:, b, a // 64:(a + S) // 64, 0:64])
            units.append(([(ctxT[:, b * SK:(b + 1) * SK], c.m("L2x_Wv")[0:CTX, a:a + S])], SK, S, "dve", emit))
    matmul_stream(c, units)
    attention(c, [SK], 64, None, lambda b, h, i: V[:, b, h, 0:64], 0.125, y, stacks=HeadStacks(c, 64, SK, resident=HEADS))
    add_and_norm(c, add=project_out(c, y, c.m("L2x_Wo"), 8), bias=c.row("L2_xattn_bo"), out=c.X, turned=[(c.XT, None, None)])


def layer2_moe(c):
    nc, step = c.nc, counter(c, "dve_step")
    E, NG, PG = L2E, 4, 8
    router_logits(c, c.XT[:], c.m("L2_routerT"), E)
    sc, sfc, tmp, sel = (c.rt[:, i, :, :] for i in range(4))
    top = c.top_f
    gtop = c.big3(12 * 1024 // 4 * 1, 256).rearrange("p (t g e) -> p t g e", t=NT, g=NG)
    gs = c.big3(12 * 1024 // 4 + 256, 64).rearrange("p (t e) -> p t e", t=NT)
    gm = c.big3(12 * 1024 // 4 + 320, 64).rearrange("p (t e) -> p t e", t=NT)
    scored = counter(c, "scored")
    with nc.Block() as block:
        @block.scalar
        def _(act):
            lg = c.bank[0][:, 0:NT * 32].rearrange("p (t e) -> p t e", t=NT)
            nc.scalar.activation(sc, lg, ACT.Sigmoid).then_inc(scored.up(), 1)

        @block.vector
        def _(dve):
            seq(dve, step, nc.vector.memset(gs[:], -3.0e38))
            dve.wait_ge(scored.sem, scored.at(1))
            seq(dve, step, nc.vector.tensor_tensor(sfc, sc, c.m("L2_bias").unsqueeze(1).broadcast_to([P, NT, E]), ALU.add))
            for t in range(NT):
                for g in range(NG):
                    last = nc.vector.max(gtop[:, t, g, :], sfc[:, t, g * PG:(g + 1) * PG])
            seq(dve, step, last)
            seq(dve, step, nc.vector.tensor_tensor(gs[:, :, 0:NG], gtop[:, :, :, 0], gtop[:, :, :, 1], ALU.add))
            top_indices(dve, c, step, gs, 8, top)
            iota = c.m("iota")[:, 0:NG].unsqueeze(1).broadcast_to([P, NT, NG])
            seq(dve, step, nc.vector.tensor_tensor(gm[:, :, 0:NG], iota, top[:, :, 0].unsqueeze(2).broadcast_to([P, NT, NG]), ALU.is_equal))
            seq(dve, step, nc.vector.tensor_tensor(gm[:, :, NG:2 * NG], iota, top[:, :, 1].unsqueeze(2).broadcast_to([P, NT, NG]), ALU.is_equal))
            seq(dve, step, nc.vector.tensor_tensor(gm[:, :, 0:NG], gm[:, :, 0:NG], gm[:, :, NG:2 * NG], ALU.add))
            for t in range(NT):
                last = nc.vector.tensor_tensor(tmp[:, t, :].rearrange("p (g e) -> p g e", g=NG), sfc[:, t, :].rearrange("p (g e) -> p g e", g=NG),
                                               gm[:, t, 0:NG].unsqueeze(2).broadcast_to([P, NG, PG]), ALU.mult)
            seq(dve, step, last)
            top_indices(dve, c, step, tmp, E, top)
            seq(dve, step, one_hot(c, E, top[:, :, 0], sel))
            for i in range(1, 4):
                seq(dve, step, one_hot(c, E, top[:, :, i], tmp))
                seq(dve, step, nc.vector.tensor_tensor(sel, sel, tmp, ALU.add))
            seq(dve, step, nc.vector.tensor_tensor(sel, sel, sc, ALU.mult))
            seq(dve, step, nc.vector.tensor_reduce(c.small8[:, 0, :], sel, AX_X, ALU.add))
            seq(dve, step, nc.vector.tensor_scalar(c.small8[:, 0, :], c.small8[:, 0, :], 1e-20, None, ALU.add))
            seq(dve, step, nc.vector.reciprocal(c.small8[:, 1, :], c.small8[:, 0, :]))
            seq(dve, step, nc.vector.tensor_scalar(c.small8[:, 1, :], c.small8[:, 1, :], 2.5, None, ALU.mult))
            seq(dve, step, nc.vector.tensor_tensor(sel, sel, c.small8[:, 1, :].unsqueeze(2).broadcast_to([P, NT, E]), ALU.mult))
    turn_weights(c, sel, E)
    fill_pick(c, 64)
    pick = c.pick_expert.rearrange("p e m -> p (e m)")
    parts = [(c.m("sgT"), c.m("suT"), c.m("sdT"), None)]
    for i in range(E // 2):
        parts.append((c.m("gateT")[:, i * P:(i + 1) * P], c.m("upT")[:, i * P:(i + 1) * P], c.m("downT")[:, i * P:(i + 1) * P],
                      pick[:, i * P:(i + 1) * P]))
    moe(c, c.XT[:], parts, c.cwT, "silu", c.outT[:])
    add_and_norm(c, add=turn_back(c, c.outT), out=c.X, turned=[(c.XT, None, None)], load=c.fetcher("l3x"))


def fill_pick(c, width):
    n = c.pick_flat.shape[1] // width
    n = min(n, 32)
    c.pick_expert = c.pick_flat[:, 0:n * width].rearrange("p (e m) -> p e m", m=width)
    with c.nc.Block() as block:
        @block.vector
        def _(dve):
            c.nc.vector.tensor_copy(c.pick_expert, c.pick_id[:, 0:n].unsqueeze(2).broadcast_to([96, n, width]))



def feed_forward(c, srcT, w1, b1, w2, b2, base, total, **norm):
    h = c.big1(4 * TOK, 4 * TOK).rearrange("p (k t) -> p k t", k=4)
    units = []
    for k in range(4):
        for half in range(2):
            d = h[:, k, half * S:(half + 1) * S]
            units.append(([(w1[:, k * P:(k + 1) * P], srcT[:, half * S:(half + 1) * S])], P, S, "act",
                          act_copy(c, d, bias=b1[:, k:k + 1], func=ACT.Gelu)))
    matmul_stream(c, units)
    add_and_norm(c, add=project_out(c, h, w2, 4), bias=b2, base=base, total=total, **norm)


def layer3_attention(c):
    nc = c.nc
    step = counter(c, "dve_step")
    qT, kT = c.big1(0, TOK), c.big1(TOK, TOK)
    qf = c.big3(0, 4 * TOK).rearrange("p (k t) -> p k t", k=4)
    kf = c.big3(4 * TOK, 4 * TOK).rearrange("p (t f) -> p t f", t=NT)
    V = c.VH[:, 0:NT * 4 * 33].rearrange("p (t h e) -> p t h e", t=NT, h=4)
    tmp = c.big2(0, 2 * TOK).rearrange("p (z t) -> p z t", z=4)
    kv = c.big2(2 * TOK, 4 * B * 36).rearrange("p (k b e) -> p k b e", k=4, b=B)
    w = c.m("L3_wqkvT")
    fill(c, V[:, :, :, 32], 1.0)
    units = halves(c, lambda half: [(w[:, 0:P], c.XT[:, half * S:(half + 1) * S])], P, qT)
    units += halves(c, lambda half: [(w[:, P:2 * P], c.XT[:, half * S:(half + 1) * S])], P, kT)
    units += heads_natural(c, c.XT, w[:, 2 * P:3 * P], P, V, 32)
    matmul_stream(c, units)

    z_ready, low_ready, e_ready, f_ready = (counter(c, n) for n in ("f_product", "low_ready", "e_ready", "f_ready"))
    proj = c.m("L3_proj")
    jobs = [("q", j, half) for j in range(4) for half in range(2)] + [("k", t, 0) for t in range(NT)]
    with nc.Block() as block:
        @block.tensor
        def _(pe):
            for s, (who, i, half) in enumerate(jobs):
                if s >= 4:
                    pe.wait_ge(f_ready.sem, f_ready.at(s - 3))
                if who == "q":
                    last = nc.tensor.matmul(c.bank[s % 4][:, :], proj[:, i * P:(i + 1) * P], qT[:, half * S:(half + 1) * S], start=True, stop=True)
                else:
                    last = nc.tensor.matmul(c.bank[s % 4][:, :], kT[:, i * P:(i + 1) * P], proj, start=True, stop=True)
                last.then_inc(z_ready.up(), 1)

        @block.vector
        def _(dve):
            def low(s):
                dve.wait_ge(z_ready.sem, z_ready.at(s + 1))
                nc.vector.tensor_scalar(tmp[:, s % 4, :], c.bank[s % 4][:, :], 0.0, None, ALU.min).then_inc(low_ready.up(), 1)
            low(0)
            for s, (who, i, half) in enumerate(jobs):
                if s + 1 < len(jobs):
                    low(s + 1)
                dve.wait_ge(e_ready.sem, e_ready.at(s + 1))
                d = qf[:, i, half * S:(half + 1) * S] if who == "q" else kf[:, i, :]
                nc.vector.scalar_tensor_tensor(out=d, in0=c.bank[s % 4][:, :], scalar=0.0, in1=tmp[:, s % 4, :], op0=ALU.max,
                                               op1=ALU.add).then_inc(f_ready.up(), 1)

        @block.scalar
        def _(act):
            for s in range(len(jobs)):
                act.wait_ge(low_ready.sem, low_ready.at(s + 1))
                nc.scalar.activation(tmp[:, s % 4, :], tmp[:, s % 4, :], ACT.Exp).then_inc(e_ready.up(), 1)

    def kv_emit(j, b):
        def emit(dve, bank, step):
            mask = c.m("block_kv")
            nc.vector.tensor_tensor(kv[:, j, b, 0:32], bank[:, 0:32], mask[:, 0:32], ALU.mult)
            return nc.vector.tensor_tensor(kv[:, j, b, 32:36], bank[:, 32:33].broadcast_to([P, 4]), mask[:, 32:36], ALU.mult)
        return emit
    matmul_stream(c, [([(kf[:, b * ST + t, j * P:(j + 1) * P], V[:, b * ST + t, j, :]) for t in range(ST)], P, 33, "dve", kv_emit(j, b))
                      for j in range(4) for b in range(B)])
    attn_ready = counter(c, "attn_ready")
    Y = c.Y8f.rearrange("p (t j h d) -> p t j h d", t=NT, j=4, h=4)
    rc = c.big2(3 * TOK - 256, 128).rearrange("p (t j h) -> p t j h", t=NT, j=4)
    with nc.Block() as block:
        @block.tensor
        def _(pe):
            for t in range(NT):
                for j in range(4):
                    last = nc.tensor.matmul(c.bank[t % 8][:, j * 36:(j + 1) * 36], qf[:, j, t * P:(t + 1) * P], kv[:, j, t // ST, :], start=True, stop=True)
                last.then_inc(attn_ready.up(), 1)

        @block.vector
        def _(dve):
            for t in range(NT):
                dve.wait_ge(attn_ready.sem, attn_ready.at(t + 1))
                a = c.bank[t % 8][:, 0:144].rearrange("p (j e) -> p j e", j=4)
                seq(dve, step, nc.vector.tensor_scalar(rc[:, t], a[:, :, 32:36], 1e-8, None, ALU.add))
                seq(dve, step, nc.vector.reciprocal(rc[:, t], rc[:, t]))
                nc.vector.tensor_tensor(Y[:, t], a[:, :, 0:32].rearrange("p j (h d) -> p j h d", h=4),
                                        rc[:, t].unsqueeze(3).broadcast_to([P, 4, 4, 8]), ALU.mult)
    turn(c, c.Y8, NT, P, c.yT8)
    rows = (c.row("L3_attn_gamma"), c.row("L3_attn_beta"))
    x1T = c.big3(0, TOK)
    add_and_norm(c, add=project_out(c, c.yT8, c.m("L3_woutT")), bias=c.row("L3_attn_b_out"), total=c.total, out=c.XN, rows=rows,
                 turned=[(x1T, None, None)])
    feed_forward(c, x1T, c.m("L3_w1T"), c.col("L3_attn_b1", 4), c.m("L3_w2T"), c.row("L3_attn_b2"), c.XN, c.total, out=c.XN, rows=rows)
    with nc.Block() as block:
        @block.vector
        def _(dve):
            nc.vector.tensor_tensor(c.X[:], c.X[:], c.XN[:], ALU.add)
    add_and_norm(c, out=c.X, turned=[(c.XT, None, None)])


def layer3_xattn(c):
    nc = c.nc
    x = c.x3
    L = "L3_xattn_"
    y = c.big2(0, 4 * TOK).rearrange("p (k t) -> p k t", k=4)
    xn, yn, x3T = c.big3(4 * TOK, TOK), c.big3(5 * TOK, TOK), c.big3(6 * TOK, TOK)

    for a in (1, 2):
        A = f"{L}a{a}_"
        src = c.X if a == 1 else c.total
        add_and_norm(c, base=src, total=src, out=x, rows=(c.row(f"{L}ln{a}_g"), c.row(f"{L}ln{a}_b")))
        turned = [(xn, c.col(A + "lnx_g"), c.col(A + "lnx_b"))]
        if a == 1:
            turned.append((yn, c.col(A + "lny_g"), c.col(A + "lny_b")))
        add_and_norm(c, base=x, total=x, out=c.XN, turned=turned)
        if a == 2:
            context_norm(c, A)
        units = []
        wq, wk, wv = c.m(f"a{a}_wq"), c.m(f"a{a}_wk"), c.m(f"a{a}_wv")
        split = []
        for kk in range(4):
            cols = slice(kk * P, (kk + 1) * P)
            for b in range(B):
                rows = slice(b * S, (b + 1) * S)
                split.append((wq[:, cols], xn[:, rows], S, c.q_wide[:, :, kk, rows]))
                if a == 1:
                    split.append((wk[:, cols], yn[:, rows], S, c.k_wide[:, :, kk, rows]))
            if a == 2:
                split.append((wk[0:CTX, cols], c.ctxnT[:], B * SK, c.k_wide[:, :, kk, 0:B * SK]))
        project_split(c, split, [c.big3(0, 3 * TOK), c.big1(0, 8 * TOK), c.big2(0, 4 * TOK)])
        if a == 1:
            V = c.VH[:, 0:NT * HEADS * 32].rearrange("p (t h e) -> p t h e", t=NT, h=HEADS)
            units += heads_natural(c, yn, wv, 512, V, 32)
        else:
            V = c.VH[0:SK, 0:B * HEADS * 32].rearrange("p (t h e) -> p t h e", t=B, h=HEADS)
            for b in range(B):
                emit = (lambda dst: lambda dve, bank, step: nc.vector.tensor_copy(dst, bank.rearrange("p (h d) -> p h d", d=32)))(V[:, b, :, 0:32])
                units.append(([(c.ctxnT[:, b * SK:(b + 1) * SK], wv[0:CTX, :])], SK, S, "dve", emit))
        matmul_stream(c, units)
        attention(c, [P] * ST if a == 1 else [SK], 32, None,
                  (lambda b, h, i: V[:, b * ST + i, h, :]) if a == 1 else (lambda b, h, i: V[:, b, h, :]),
                  32.0 ** -0.5, y, mask="future" if a == 1 else None, stacks=HeadStacks(c, 32, S if a == 1 else SK))
        add_and_norm(c, add=project_out(c, y, c.m(f"a{a}_li1"), 4), bias=c.row(A + "li1_b"), base=x, total=c.total, out=c.XN,
                     turned=[(x3T, c.col(A + "ln3_g"), c.col(A + "ln3_b"))])
        feed_forward(c, x3T, c.m(f"a{a}_li2"), c.col(A + "li2_b", 4), c.m(f"a{a}_li3"), c.row(A + "li3_b"), c.total, c.total, norm=None)
        with nc.Block() as block:
            @block.vector
            def _(dve):
                step = counter(c, "dve_step")
                seq(dve, step, nc.vector.tensor_tensor(c.total[:], c.total[:], x[:], ALU.add))
                if a == 2:
                    nc.vector.tensor_tensor(c.total[:], c.total[:], c.X[:], ALU.add)
    add_and_norm(c, base=c.total, total=c.total, out=c.X, turned=[(c.XT, None, None)])


def context_norm(c, A):
    nc = c.nc
    ctxT = c.m("ctxT")[0:CTX]
    mean_ready, sq_ready, var_ready, r_ready, diag_ready, spread_ready, step = (counter(c, n) for n in (
        "cm_ready", "csq_ready", "cvar_ready", "cr_ready", "cdiag_ready", "cspread_ready", "dve_step"))
    n = B * SK
    d, sq = c.ctx_tmp[0:CTX, 0, :], c.ctx_tmp[0:CTX, 1, :]
    diag, r = c.ctx_tmp[0:SK, 2, :], c.small[0:SK, 0:B]
    with nc.Block() as block:
        @block.tensor
        def _(pe):
            nc.tensor.matmul(c.bank[0][0:CTX, 0:n], c.ones[0:CTX, 0:CTX], ctxT, start=True, stop=True).then_inc(mean_ready.up(), 1)
            pe.wait_ge(sq_ready.sem, sq_ready.at(1))
            for b in range(B):
                last = nc.tensor.matmul(c.bank[1][0:SK, b:b + 1], sq[:, b * SK:(b + 1) * SK], c.ones[0:CTX, 0:1], start=True, stop=True)
            last.then_inc(var_ready.up(), 1)
            pe.wait_ge(diag_ready.sem, diag_ready.at(1))
            for b in range(B):
                last = nc.tensor.matmul(c.bank[2][0:CTX, b * SK:(b + 1) * SK], c.ones[0:SK, 0:CTX], diag[:, b * SK:(b + 1) * SK],
                                        start=True, stop=True)
            last.then_inc(spread_ready.up(), 1)

        @block.vector
        def _(dve):
            dve.wait_ge(mean_ready.sem, mean_ready.at(1))
            seq(dve, step, nc.vector.scalar_tensor_tensor(out=d, in0=c.bank[0][0:CTX, 0:n], scalar=-1.0 / CTX, in1=ctxT, op0=ALU.mult, op1=ALU.add))
            nc.vector.tensor_tensor(sq, d, d, ALU.mult).then_inc(sq_ready.up(), 1)
            dve.wait_ge(var_ready.sem, var_ready.at(1))
            nc.vector.tensor_scalar(r, c.bank[1][0:SK, 0:B], 1.0 / CTX, 1e-5, ALU.mult, ALU.add).then_inc(sq_ready.up(), 1)
            dve.wait_ge(r_ready.sem, r_ready.at(1))
            for b in range(B):
                last = nc.vector.tensor_scalar(diag[:, b * SK:(b + 1) * SK], c.ident[0:SK, 0:SK], r[:, b:b + 1], None, ALU.mult)
            last.then_inc(diag_ready.up(), 1)
            dve.wait_ge(spread_ready.sem, spread_ready.at(1))
            seq(dve, step, nc.vector.tensor_tensor(d, d, c.bank[2][0:CTX, 0:n], ALU.mult))
            nc.vector.tensor_scalar(c.ctxnT[:], d, c.col(A + "lny_g")[0:CTX], c.col(A + "lny_b")[0:CTX], ALU.mult, ALU.add)

        @block.gpsimd
        def _(pool):
            pool.wait_ge(sq_ready.sem, sq_ready.at(2))
            nc.gpsimd.tensor_tensor(r, r, c.minus_half[0:SK, 0:B], ALU.pow).then_inc(r_ready.up(), 1)


def layer3_ffn(c, out_dram):
    nc, step = c.nc, counter(c, "dve_step")
    xp, xr, xk = c.big1(0, TOK), c.big1(TOK, TOK), c.big1(2 * TOK, TOK)
    r, k2 = c.big1(3 * TOK, TOK), c.big1(4 * TOK, TOK)
    one_minus = c.small[:, 4:6]
    with nc.Block() as block:
        @block.vector
        def _(dve):
            for b in range(B):
                nc.vector.memset(xp[:, b * S:b * S + 1], 0.0)
                last = nc.vector.tensor_copy(xp[:, b * S + 1:(b + 1) * S], c.XT[:, b * S:(b + 1) * S - 1])
            for i, n in enumerate(("L3_ffn_mu_r", "L3_ffn_mu_k")):
                last = nc.vector.tensor_scalar(one_minus[:, i:i + 1], c.col(n), -1.0, 1.0, ALU.mult, ALU.add)
            seq(dve, step, last)
            nc.vector.tensor_scalar(xr, xp, one_minus[:, 0:1], None, ALU.mult)
            seq(dve, step, nc.vector.tensor_scalar(xk, xp, one_minus[:, 1:2], None, ALU.mult))
            for n, d in (("L3_ffn_mu_r", xr), ("L3_ffn_mu_k", xk)):
                nc.vector.scalar_tensor_tensor(out=d, in0=c.XT[:], scalar=c.col(n), in1=d, op0=ALU.mult, op1=ALU.add)
    h = lambda ap, half: ap[:, half * S:(half + 1) * S]

    def square_relu(d):
        def emit(dve, bank, step):
            seq(dve, step, nc.vector.tensor_scalar(d, bank, 0.0, None, ALU.max))
            return nc.vector.tensor_tensor(d, d, d, ALU.mult)
        return emit
    units = []
    for half in range(2):
        units.append(([(c.m("L3f_WkT"), h(xk, half))], P, S, "dve", square_relu(h(k2, half))))
        units.append(([(c.m("L3f_WrT"), h(xr, half))], P, S, "act", act_copy(c, h(r, half), func=ACT.Sigmoid)))
    matmul_stream(c, units)

    def gate(half):
        return lambda dve, bank, step: nc.vector.tensor_tensor(h(c.outT, half), bank, h(r, half), ALU.mult)
    matmul_stream(c, [([(c.m("L3f_WvT"), h(k2, half))], P, S, "dve", gate(half)) for half in range(2)])
    add_and_norm(c, add=turn_back(c, c.outT), out=c.XN, store=out_dram)



def decoder(nc, dram, out_dram, q_dram, k_dram, q_wide, k_wide):
    with ExitStack() as ctx:
        c = Core(nc, ctx)
        c.dram, c.q_dram, c.k_dram, c.q_wide, c.k_wide = dram, q_dram, k_dram, q_wide, k_wide
        tiles = lambda t: t[:].rearrange("p (t f) -> p t f", t=NT)
        X, XT, XN, total = (c.sb(n, [P, TOK]) for n in ("x", "xT", "normed", "total"))
        c.X, c.XT, c.XN, c.total = tiles(X), XT, tiles(XN), tiles(total)
        c.rest_q, c.rest_k = XN[:], total[:]
        c.big = [c.sb("big1", [P, 8 * TOK]), c.sb("big2", [P, 4 * TOK]), c.sb("big3", [P, 8 * TOK])]
        c.VH = c.sb("v_heads", [P, NT * HEADS * 33])
        moe_w, late_w = c.sb("moe_weights", [P, max(width(p) for p in ("moe0", "moe1"))]), c.sb("late_weights", [P, 4 * TOK])
        mid_w = c.sb("mid_weights", [P, width("mid")])
        c.rows, c.cols = c.sb("rows", [P, P * len(row_names())]), c.sb("cols", [P, sum(n for _, n in col_names())])
        c.memories = {"const": (c.big[1], 0), "first": (late_w, width("turned")), "early": (late_w, width("turned") + width("first")), "moe0": (moe_w, 0),
                      "moe1": (moe_w, 0), "moe2": (moe_w, 0), "l3": (moe_w, width("moe2")), "mid": (mid_w, 0),
                      "turned": (late_w, 0), "l2x": (late_w, 0), "l3x": (moe_w, 0)}
        c.matrices = {}
        for pack, (memory, at) in c.memories.items():
            for name, rows, cols in MATRICES[pack]:
                c.matrices[name] = memory[0:rows, at:at + cols]
                at += cols
        c.loaded = {pack: ctx.enter_context(nc.semaphore(f"loaded_{pack}")) for pack in c.memories}
        vectors_loaded = ctx.enter_context(nc.semaphore("vectors_loaded"))
        x_loaded = ctx.enter_context(nc.semaphore("x_loaded"))
        c.stored = ctx.enter_context(nc.semaphore("out_stored"))
        c.stored_parts = ctx.enter_context(nc.semaphore("parts_in_dram"))
        c.nparts = 0

        c.ident, c.key_later, c.minus_later, c.ones = (c.sb(n, [P, P]) for n in ("ident", "key_later", "minus_later", "ones"))
        c.ident_bf = c.sb("ident_bf", [P, P], BF16)
        c.before_key, c.after_query = (c.sb(n, [P, S], BF16) for n in ("before_key", "after_query"))
        pick = c.sb("pick", [P, 4 * P], BF16)
        c.pick = pick[:].rearrange("p (j m) -> p j m", j=4)
        c.zeros_bf = c.sb("zeros_bf", [P, P], BF16)
        c.pick_id = c.sb("pick_id", [96, 32], BF16)
        c.minus_half = c.sb("minus_half", [P, 8])

        E, EM = c.big3(0, 4 * TOK), c.sb("masked_weights", [P, 8 * P])
        c.E = [E[:, i * TOK:(i + 1) * TOK].rearrange("p (x t) -> p x t", x=2) for i in range(4)]
        c.EM = [EM[:, i * 2 * P:(i + 1) * 2 * P].rearrange("p (x t) -> p x t", x=2) for i in range(4)]
        c.OT = c.sb("heads_out", [P, 2 * S])[:].rearrange("p (z t) -> p z t", z=2)
        c.MX = c.sb("maxima", [P, ST * 4])[:].rearrange("p (j t) -> p j t", t=ST)
        c.NM = c.sb("negmax", [P, 2 * ST * P], BF16)[:].rearrange("p (z t r) -> p z t r", z=2, t=ST)
        c.NMT = c.sb("negmaxT", [P, 2 * S], BF16)[:].rearrange("p (z t) -> p z t", z=2)
        c.RC = c.sb("reciprocals", [P, 2 * ST * 4])[:].rearrange("p (z t j) -> p z t j", z=2, t=ST)

        c.stats = c.sb("stats", [P, NT * 6])[:].rearrange("p (t s) -> p t s", t=NT)
        c.mv = c.sb("mean_var", [P, NT * 2])[:].rearrange("p (t s) -> p t s", t=NT)
        c.rstd, c.amax = c.sb("rstd", [P, NT]), c.sb("amax", [P, NT])[:]
        c.small, c.negA = c.sb("small", [P, 8]), c.sb("negA", [P, 16])[:]
        c.small8 = c.sb("small8", [P, 8 * NT])[:].rearrange("p (i t) -> p i t", i=8)
        c.ckT = c.sb("ctx_kT", [P, B * SK])
        bf = lambda ap: ap.bitcast(BF16)
        spare = width("turned") + width("first") + width("early")
        late = lambda a, n: late_w[:, spare + a:spare + a + n]
        c.signT = bf(late(0, P)).rearrange("p (z m) -> p z m", z=2)
        c.tern = bf(late(P, P)).rearrange("p (z m) -> p z m", z=2)
        c.alpha = late(2 * P, 2 * P).rearrange("p (z m) -> p z m", z=2)
        c.headmat = c.sb("headmat", [P, P])[:]

        c.Y8f, c.Y8 = c.big2(3 * TOK, TOK), c.big2(3 * TOK, TOK).rearrange("p (t f) -> p t f", t=NT)
        c.q_parts = bf(c.big2(0, 1536)).rearrange("p (z t) -> p z t", z=3)
        c.k_parts = bf(c.big2(1536, 1536)).rearrange("p (z t) -> p z t", z=3)
        c.qk32 = c.big1(0, 2 * TOK).rearrange("p (z t) -> p z t", z=2)
        c.QH = bf(c.big1(0, 8 * TOK)).rearrange("p (h x t) -> p h x t", h=HEADS // 2, x=2)
        c.KH = bf(c.big3(4 * TOK, 4 * TOK))
        c.qT, c.yT8 = c.big3(0, TOK), c.big1(0, TOK).rearrange("p (k t) -> p k t", k=1)
        c.q_bf, c.qT_bf = bf(c.big1(4 * TOK, TOK // 2)).rearrange("p (t f) -> p t f", t=NT), bf(c.big1(5 * TOK, TOK // 2))
        c.moe_sg, c.moe_h = (c.big1(i * TOK, TOK).rearrange("p (z t) -> p z t", z=2) for i in (0, 1))
        c.outT = c.big1(2 * TOK, TOK)
        c.cwT = bf(c.big3(0, TOK // 2))[0:96]
        c.cw_parts = bf(c.big3(512, 384)).rearrange("p (t r) -> p t r", t=NT)
        c.cw_rest = c.big3(1024, 256).rearrange("p (t e) -> p t e", t=NT)
        c.rt = c.big3(1280, 6 * 256).rearrange("p (i t e) -> p i t e", i=6, t=NT)
        c.top_v = c.big3(2816, 64).rearrange("p (t k) -> p t k", t=NT)
        c.top_i = c.big3(2880, 64).bitcast(U32).rearrange("p (t k) -> p t k", t=NT)
        c.top_f = c.big3(2944, 64).rearrange("p (t k) -> p t k", t=NT)
        c.pick_flat = bf(c.big3(4096, 1024))[0:96]
        c.x3 = c.big3(7 * TOK, TOK).rearrange("p (t f) -> p t f", t=NT)
        c.ctx_tmp = c.VH[:, 0:3 * B * SK].rearrange("p (z t) -> p z t", z=3)
        c.ctxnT = c.sb("ctx_normed", [CTX, B * SK])

        psum = c.ps("banks", [P, 8 * 512])
        c.banks = psum[:].rearrange("p (i t) -> p i t", i=8)
        c.bank = [psum[:, i * 512:(i + 1) * 512] for i in range(8)]
        c.banks_bf = [b[:, 0:256].bitcast(BF16) for b in c.bank]
        c.bank_bf = c.banks_bf[7]
        c.key_stack = bf(c.big2(0, 3 * TOK)).rearrange("p (u d z) -> p u d z", z=6, d=8)

        x_in = dram["x"].rearrange("(t p) f -> p t f", p=P)
        with nc.Block() as block:
            @block.sync
            def _(sp):
                sp.dma_start(c.X[:], x_in).then_inc(x_loaded, 16)
                for pack in ("const", "first"):
                    c.fetch(sp, pack)
                sp.dma_start(c.rows[:], dram["rows"].partition_broadcast(P)).then_inc(vectors_loaded, 16)
                sp.dma_start(c.cols[:], dram["cols"]).then_inc(vectors_loaded, 16)
                for pack in ("mid", "early", "moe0"):
                    c.fetch(sp, pack)
                sp.wait_ge(x_loaded, 16)
                sp.wait_ge(vectors_loaded, 32)
                for pack in ("first", "mid", "early"):
                    sp.wait_ge(c.loaded[pack], 16)

            @block.vector
            def _(dve):
                dve.wait_ge(c.loaded["const"], 16)
                nc.vector.tensor_copy(c.ident[:], c.m("ident"))
                nc.vector.tensor_copy(c.ident_bf[:], c.m("ident"))
                nc.vector.tensor_copy(c.key_later[:], c.m("later"))
                nc.vector.tensor_scalar(c.minus_later[:], c.m("later"), -1.0, None, ALU.mult)
                nc.vector.tensor_scalar(c.before_key[:, 0:P], c.m("later"), NEG, None, ALU.mult)
                nc.vector.tensor_scalar(c.after_query[:, S - P:S], c.m("later_t"), NEG, None, ALU.mult)
                nc.vector.tensor_copy(pick[:], c.m("pick"))
                nc.vector.tensor_copy(c.pick_id[:], c.m("pick_id"))

            @block.gpsimd
            def _(pool):
                nc.gpsimd.memset(c.ones[:], 1.0)
                nc.gpsimd.memset(c.before_key[:, P:S], 0.0)
                nc.gpsimd.memset(c.after_query[:, 0:S - P], 0.0)
                nc.gpsimd.memset(c.NM[:], 0.0)
                nc.gpsimd.memset(c.zeros_bf[:], 0.0)
                nc.gpsimd.memset(c.minus_half[:], -0.5)

        stages = [
            lambda: layer0_attention(c),
            lambda: cross_attention_8(c, c.m("L0x_WqT"), c.m("L0x_WkvT")[:, 0:P], c.m("L0x_WkvT")[:, P:2 * P], c.m("L0x_WoT"),
                                      None, None, None, None),
            lambda: (fill_pick(c, P), c.await_loads("moe0"), layer0_moe(c)),
            lambda: layer1_scan(c),
            lambda: cross_attention_8(c, c.m("L1x_Wq"), c.m("L1x_Wk"), c.m("L1x_Wv"), c.m("L1x_Wo"), c.col("L1_xattn_bq"),
                                      c.col("L1_xattn_bk"), c.row("L1_xattn_bv"), c.row("L1_xattn_bo")),
            lambda: (c.await_loads("moe1", "turned"), layer1_ffn(c)),
            lambda: layer2_attention(c),
            lambda: (c.await_loads("l2x"), layer2_cross(c)),
            lambda: (c.await_loads("moe2", "l3"), layer2_moe(c)),
            lambda: layer3_attention(c),
            lambda: (c.await_loads("l3x"), layer3_xattn(c)),
            lambda: layer3_ffn(c, out_dram),
        ]
        for stage in stages:
            stage()



def constants():
    p, f = np.arange(P)[:, None], np.arange(P)[None, :]
    pos = np.arange(S, dtype=np.float32)
    inv4 = (1.0 / 10000.0 ** (np.arange(4, dtype=np.float32) / np.float32(4))).astype(np.float32)
    tile_pos = pos.reshape(ST, P).T
    aq = tile_pos[:, :, None] * inv4
    ak = (16 * (np.arange(P) % 32)[:, None] + np.arange(16)[None, :]).astype(np.float32)[:, :, None] * inv4
    inv32 = (10000.0 ** (-np.arange(0, 64, 2, dtype=np.float32) / 64)).astype(np.float32)
    ticks = inv32[np.arange(P) % 32][:, None] * pos[None, :]
    sign = np.where(np.arange(P) % 64 < 32, -1.0, 1.0)[:, None]
    block = np.zeros((P, 36))
    for h in range(4):
        block[32 * h:32 * h + 32, 8 * h:8 * h + 8] = 1.0
        block[32 * h:32 * h + 32, 32 + h] = 1.0
    out = {
        "ident": p == f, "later": p > f, "later_t": f > p,
        "pick": np.concatenate([np.repeat(p // 2 == 16 * j, P, axis=1) for j in range(4)], axis=1),
        "pick_id": np.arange(96)[:, None] % 32 == np.arange(32)[None, :],
        "same_head": p // 8 == f // 8,
        "iota": np.repeat(np.arange(32)[None, :], P, axis=0),
        "rope_q": np.concatenate([np.cos(aq).reshape(P, -1), np.sin(aq).reshape(P, -1)], axis=1),
        "rope_k": np.concatenate([np.cos(ak).reshape(P, -1), np.sin(ak).reshape(P, -1)], axis=1),
        "cos": np.cos(ticks), "sin": np.sin(ticks) * sign, "block_kv": block,
    }
    return {k: v.astype(np.float32) for k, v in out.items()}


def by_rows(w):
    k = w.shape[0] // P
    return w.reshape(k, P, -1).transpose(1, 0, 2).reshape(P, -1)


def lay_out(a):
    m = constants()
    every = lambda v: np.broadcast_to(v[None, :], (P, v.shape[0]))
    heads8 = lambda u: np.concatenate([u] * HEADS, axis=1)
    m["L0_Wqkv"], m["L0_Wo"] = a["L0_attn_Wqkv_w"], a["L0_attn_Wo_w"]
    m["L0_UT"] = heads8(a["L0_attn_U"].T)
    m["ctxT"] = a["ctx_512"].reshape(B * SK, CTX).T
    m["L0x_WqT"], m["L0x_WkvT"], m["L0x_WoT"] = a["L0_xattn_Wq"].T, a["L0_xattn_Wkv"].T, a["L0_xattn_Wo"].T
    m["L0_gateT"] = np.concatenate([a["L0_ffn_gate_weight"], a["L0_ffn_new_gate_weight"]]).T
    m["gate_bias"] = every(np.concatenate([np.zeros(8, np.float32), a["L0_ffn_gate_bias"]]))
    for n, new in (("w1", "new_w1"), ("w3", "new_w3")):
        w = np.concatenate([a[f"L0_ffn_{n}"], a[f"L0_ffn_{new}"]])
        m[n + "T"] = w.transpose(2, 0, 1).reshape(P, -1)
    w = np.concatenate([a["L0_ffn_w2"], a["L0_ffn_new_w2"]]).transpose(0, 2, 1)
    padded = np.zeros((L0E, 3 * P, P), np.float32)
    padded[:, 0:L0HID] = w
    m["w2T"] = padded.reshape(L0E, 3, P, P).transpose(2, 0, 1, 3).reshape(P, -1)
    m["L1_WdtT"], m["L1_WBT"], m["L1_WCT"], m["L1_A_log"] = a["L1_attn_W_dt"].T, a["L1_attn_W_B"].T, a["L1_attn_W_C"].T, a["L1_attn_A_log"]
    for n in ("Wq", "Wk", "Wv", "Wo"):
        m["L1x_" + n] = a["L1_xattn_" + n]
    m["L1f_router"], m["router_b"] = a["L1_ffn_router_w"], every(a["L1_ffn_router_b"])
    for n in ("WQ", "WK", "WV", "WO"):
        m["L2_" + n] = a["L2_attn_" + n]
    m["L2_WQrT"], m["L2_WKrT"] = heads8(a["L2_attn_WQr"].T), heads8(a["L2_attn_WKr"].T)
    m["L2_routerT"], m["L2_bias"] = a["L2_ffn_router_weight"].T, every(a["L2_ffn_router_bias"])
    m["w1"], m["w2"] = (a["L1_ffn_" + n].transpose(1, 0, 2).reshape(P, -1) for n in ("w1", "w2"))
    m["w3"] = by_rows(a["L1_ffn_w3"].reshape(L1E * L1HID, P))
    m["wq"], m["wk"], m["wv"], m["wo"] = a["L1_ffn_wq"], a["L1_ffn_wk"], a["L1_ffn_wv"], by_rows(a["L1_ffn_wo"])
    swap = lambda w: w.reshape(P, -1, 2, 32)[:, :, ::-1, :].reshape(P, -1)
    m["wqs"], m["wks"] = swap(a["L1_ffn_wq"]), swap(a["L1_ffn_wk"])
    m["L2x_Wq"], m["L2x_Wk"], m["L2x_Wv"], m["L2x_Wo"] = a["L2_xattn_Wq"], a["L2_xattn_Wk"], a["L2_xattn_Wv"], by_rows(a["L2_xattn_Wo"])
    m["gateT"], m["upT"] = (a["L2_ffn_" + n].transpose(2, 0, 1).reshape(P, -1) for n in ("gate_w", "up_w"))
    m["downT"] = by_rows(a["L2_ffn_down_w"].transpose(0, 2, 1).reshape(L2E * L2HID, P))
    m["sgT"], m["suT"], m["sdT"] = (a[f"L2_ffn_shared_{n}_w"].T for n in ("gate", "up", "down"))
    m["L3_wqkvT"] = a["L3_attn_w_qkv"].T
    proj = np.zeros((HEADS, 8, HEADS, 32), np.float32)
    for h in range(HEADS):
        proj[h, :, h, :] = a["L3_attn_proj"][h]
    m["L3_proj"] = proj.reshape(P, 4 * P)
    m["L3_woutT"], m["L3_w1T"], m["L3_w2T"] = a["L3_attn_w_out"].T, a["L3_attn_w1"].T, by_rows(a["L3_attn_w2"].T)
    m["L3f_WrT"], m["L3f_WkT"], m["L3f_WvT"] = a["L3_ffn_W_r"].T, a["L3_ffn_W_k"].T, a["L3_ffn_W_v"].T
    for i in (1, 2):
        x = f"L3_xattn_a{i}_"
        for n in ("wq", "wk", "wv"):
            w = a[x + n]
            m[f"a{i}_{n}"] = w.transpose(1, 0, 2).reshape(w.shape[1], -1)
        m[f"a{i}_li1"], m[f"a{i}_li2"], m[f"a{i}_li3"] = by_rows(a[x + "li1_w"]), a[x + "li2_w"], by_rows(a[x + "li3_w"])

    out = {"x": a["x"].reshape(TOK, P)}
    for pack, names in MATRICES.items():
        whole = np.zeros((P, width(pack)), np.float32)
        at = 0
        for name, rows, cols in names:
            whole[0:rows, at:at + cols] = m[name]
            at += cols
        out[pack] = whole
    out["rows"] = np.concatenate([a[n] for n in row_names()]).reshape(1, -1)
    cols = np.zeros((P, sum(n for _, n in col_names())), np.float32)
    at = 0
    for name, n in col_names():
        v = a[name]
        if v.shape[0] < P:
            cols[0:v.shape[0], at] = v
        else:
            cols[:, at:at + n] = v.reshape(n, P).T
        at += n
    out["cols"] = cols
    return out


def build(nc, arrays):
    dram = {name: nc.dram_tensor("in_" + name, v.shape, F32, kind="ExternalInput").ap() for name, v in arrays.items()}
    out = nc.dram_tensor("out", (TOK, P), F32, kind="ExternalOutput").ap()
    q_dram = nc.dram_tensor("q_parts", (P, 6, TOK), BF16, kind="Internal").ap()
    k_dram = nc.dram_tensor("k_parts", (P, 6, TOK), BF16, kind="Internal").ap()
    q_wide, k_wide = (nc.dram_tensor(n, (P, 3, 8, TOK), BF16, kind="Internal").ap() for n in ("q_wide", "k_wide"))
    decoder(nc, dram, out.rearrange("(t p) f -> p t f", p=P), q_dram, k_dram, q_wide, k_wide)


def kernel(**inputs):
    import concourse.bacc as bacc
    from concourse.bass_utils import run_bass_kernel_spmd

    arrays = {k: np.ascontiguousarray(v) for k, v in lay_out({k: np.asarray(v) for k, v in inputs.items()}).items()}
    nc = bacc.Bacc("TRN2", target_bir_lowering=False, num_devices=1)
    build(nc, arrays)
    r = run_bass_kernel_spmd(nc, [{"in_" + k: v for k, v in arrays.items()}], core_ids=[0])
    return r.results[0]["out"].reshape(B, S, P)
```
